# Optimizing a Trainium2 kernel written in Bass

```python
import numpy as np
import jax
import jax.numpy as jnp

def _softmax(x, axis=-1):
    return jax.nn.softmax(x, axis=axis)

def _gelu(x):
    return jax.nn.gelu(x, approximate=True)

def _silu(x):
    return jax.nn.silu(x)

def _sigmoid(x):
    return jax.nn.sigmoid(x)

def _layernorm(x, axis=-1, eps=1e-05):
    m = jnp.mean(x, axis=axis, keepdims=True)
    v = jnp.var(x, axis=axis, keepdims=True)
    return (x - m) / jnp.sqrt(v + eps)

def _scatter_add(tgt, idx, src, axis=0):
    return tgt.at[idx].add(src)

def _segment_sum(src, seg, n):
    return jax.ops.segment_sum(src, seg, n)
kernel_name = 'mk_xattn_ffn_d4_seqx_r8_c1eb67'

def setup_inputs(seed: int=0):
    np.random.seed(seed)
    _w = jnp.asarray

    def _rec_inputs():
        import jax
        import jax.numpy as jnp
        _rk = jax.random.key(seed)
        x = -0.000125 + 0.9999 * jax.random.normal(jax.random.fold_in(_rk, 1), (4, 256, 256), jnp.float32)
        _lenS = 256 - jax.random.randint(jax.random.fold_in(_rk, 7), (4,), 0, max(1, 256 // 4) + 1, jnp.int32)
        _lenS2 = 1601 - jax.random.randint(jax.random.fold_in(_rk, 8), (4,), 0, max(1, 1601 // 4) + 1, jnp.int32)
        _ctx_2048P = jax.random.normal(jax.random.fold_in(_rk, 11), (4, 16, 256), jnp.float32)
        _ctx_2048c = jax.random.dirichlet(jax.random.fold_in(_rk, 511), 0.3 * jnp.ones((16,), jnp.float32), (4, 1601))
        _ctx_2048t = jnp.einsum('bsk,bkd->bsd', _ctx_2048c, _ctx_2048P)
        _ctx_2048t = _ctx_2048t * jax.lax.rsqrt(jnp.mean(jnp.square(_ctx_2048t)) + 1e-12) * 0.953939
        ctx_2048 = 0.00139358 + 0.999369 * (_ctx_2048t + 0.3 * jax.random.normal(jax.random.fold_in(_rk, 611), (4, 1601, 256), jnp.float32))
        pos_BxS2 = jnp.broadcast_to(jnp.arange(1601, dtype=jnp.int32), (4, 1601))
        itok_BxS_4096_4607 = jax.random.randint(jax.random.fold_in(_rk, 13), (4, 256), 512, 576, jnp.int32)
        return (x, ctx_2048, pos_BxS2, itok_BxS_4096_4607)
    x, ctx_2048, pos_BxS2, itok_BxS_4096_4607 = _rec_inputs()

    def _L0_xattn_setup():
        import jax, jax.numpy as jnp
        import numpy as np
        key = jax.random.key(seed)
        k = jax.random.split(key, 6)
        B, S, D, NKV = (4, 512, 256, 64)
        inv = D ** (-0.5)
        return {'x': jax.random.normal(k[0], (B, S, D), jnp.float32), 'W_qkv': jax.random.normal(k[1], (3 * D, D), jnp.float32) * inv, 'W_o': jax.random.normal(k[2], (D, D), jnp.float32) * inv, 'beta_q': jnp.array(1.0, jnp.float32), 'beta_k': jnp.array(1.0, jnp.float32), 'gate': jnp.array(0.0, jnp.float32), 'log_tau': jnp.array(0.0, jnp.float32), 'K_mem': jax.random.normal(k[3], (B, NKV, D), jnp.float32), 'V_mem': jax.random.normal(k[4], (B, NKV, D), jnp.float32), 'clip_k': 54}
    _L0_xattn_all = _L0_xattn_setup()
    _L0_xattn_in = {k: v for k, v in _L0_xattn_all.items() if k in ('W_qkv', 'W_o', 'beta_q', 'beta_k', 'gate', 'log_tau')}
    del _L0_xattn_all

    def _L0_ffn_setup():
        import jax, jax.numpy as jnp
        import numpy as np
        B, S, D = (4, 128, 256)
        H = 512
        NE = 8
        TOPK = 2
        key = jax.random.key(seed)
        ks = jax.random.split(key, 9)
        s = lambda fan_in: 1.0 / np.sqrt(fan_in)
        return {'x': jax.random.normal(ks[0], (B, S, D), dtype=jnp.float32), 'W1': jax.random.normal(ks[1], (NE, D, H), dtype=jnp.float32) * s(D), 'b1': jnp.zeros((NE, H), dtype=jnp.float32), 'W2': jax.random.normal(ks[2], (NE, H, H), dtype=jnp.float32) * s(H), 'b2': jnp.zeros((NE, H), dtype=jnp.float32), 'W3': jax.random.normal(ks[3], (NE, H, D), dtype=jnp.float32) * s(H), 'b3': jnp.zeros((NE, D), dtype=jnp.float32), 'Wg': jax.random.normal(ks[4], (D, NE), dtype=jnp.float32) * s(D), 'bg': jnp.zeros((NE,), dtype=jnp.float32)}
    _L0_ffn_all = _L0_ffn_setup()
    _L0_ffn_in = {k: v for k, v in _L0_ffn_all.items() if k in ('W1', 'b1', 'W2', 'b2', 'W3', 'b3', 'Wg', 'bg')}
    del _L0_ffn_all

    def _L1_xattn_setup():
        import jax, jax.numpy as jnp
        import numpy as np
        B, CTX, DRAFT, D = (2, 512, 64, 256)
        H, KVH, HD = (16, 4, 128)
        N_REP = H // KVH
        EPS = 1e-06
        THETA = 10000.0
        SCALE = 1.0 / np.sqrt(HD).astype(np.float32)

        def _rms_norm(x, w):
            v = jnp.mean(jnp.square(x.astype(jnp.float32)), axis=-1, keepdims=True)
            return (w * (x.astype(jnp.float32) * jax.lax.rsqrt(v + EPS))).astype(x.dtype)

        def _rotate_half(x):
            x1, x2 = jnp.split(x, 2, axis=-1)
            return jnp.concatenate((-x2, x1), axis=-1)

        def _rope(x, pos):
            inv_freq = 1.0 / THETA ** (jnp.arange(0, HD, 2, dtype=jnp.float32) / HD)
            freqs = pos.astype(jnp.float32)[:, None, :, None] * inv_freq
            emb = jnp.concatenate((freqs, freqs), axis=-1)
            return x * jnp.cos(emb) + _rotate_half(x) * jnp.sin(emb)
        key = jax.random.key(seed)
        ks = jax.random.split(key, 6)
        return {'draft_hidden': jax.random.normal(ks[0], (B, DRAFT, D), jnp.float32), 'context_hidden': jax.random.normal(ks[1], (B, CTX, D), jnp.float32), 'Wq': jax.random.normal(ks[2], (H * HD, D), jnp.float32) * 0.02, 'Wk': jax.random.normal(ks[3], (KVH * HD, D), jnp.float32) * 0.02, 'Wv': jax.random.normal(ks[4], (KVH * HD, D), jnp.float32) * 0.02, 'Wo': jax.random.normal(ks[5], (D, H * HD), jnp.float32) * 0.02, 'q_norm_w': jnp.ones((HD,), jnp.float32), 'k_norm_w': jnp.ones((HD,), jnp.float32), 'context_position_ids': jnp.broadcast_to(jnp.arange(CTX, dtype=jnp.int32), (B, CTX)), 'draft_position_ids': jnp.broadcast_to(CTX + jnp.arange(DRAFT, dtype=jnp.int32), (B, DRAFT))}
    _L1_xattn_all = _L1_xattn_setup()
    _L1_xattn_in = {k: v for k, v in _L1_xattn_all.items() if k in ('Wq', 'Wk', 'Wv', 'Wo', 'q_norm_w', 'k_norm_w')}
    del _L1_xattn_all

    def _L1_ffn_setup():
        import jax, jax.numpy as jnp
        import numpy as np
        key = jax.random.key(seed)
        k1, k2, k3, k4 = jax.random.split(key, 4)
        B, S, D_IN, D_OUT = (4, 512, 256, 256)
        x = jax.random.normal(k1, (B, S, D_IN), dtype=jnp.float32)
        weight = jax.random.normal(k2, (D_OUT, D_IN), dtype=jnp.float32) * 0.02
        scale_weight = jax.random.uniform(k3, (D_OUT,), dtype=jnp.float32, minval=0.5, maxval=1.5)
        bias = jax.random.normal(k4, (D_OUT,), dtype=jnp.float32) * 0.02
        return {'x': x, 'weight': weight, 'scale_weight': scale_weight, 'bias': bias}
    _L1_ffn_all = _L1_ffn_setup()
    _L1_ffn_in = {k: v for k, v in _L1_ffn_all.items() if k in ('weight', 'scale_weight', 'bias')}
    del _L1_ffn_all

    def _L2_xattn_setup():
        import jax, jax.numpy as jnp
        import numpy as np
        DIM = 256
        NH = 16
        HD = DIM // NH
        EPS = 1e-06
        IMG_LEN = 257

        def rms_norm(x, w, eps=EPS):
            xf = x.astype(jnp.float32)
            y = xf * jax.lax.rsqrt(jnp.mean(xf * xf, axis=-1, keepdims=True) + eps)
            return y.astype(x.dtype) * w

        def linear(x, w, b):
            return jnp.einsum('blc,oc->blo', x, w) + b

        def attention(q, k, v):
            scale = 1.0 / jnp.sqrt(jnp.asarray(HD, q.dtype))
            scores = jnp.einsum('bqhd,bkhd->bhqk', q, k) * scale
            probs = jax.nn.softmax(scores, axis=-1)
            return jnp.einsum('bhqk,bkhd->bqhd', probs, v)
        key = jax.random.key(seed)
        ks = jax.random.split(key, 12)
        B, L = (2, 1024)
        s = 0.02
        inp = {'x': jax.random.normal(ks[0], (B, L, DIM), jnp.float32), 'context': jax.random.normal(ks[1], (B, 769, DIM), jnp.float32), 'q_w': jax.random.normal(ks[2], (DIM, DIM), jnp.float32) * s, 'q_b': jnp.zeros((DIM,), jnp.float32), 'k_w': jax.random.normal(ks[3], (DIM, DIM), jnp.float32) * s, 'k_b': jnp.zeros((DIM,), jnp.float32), 'v_w': jax.random.normal(ks[4], (DIM, DIM), jnp.float32) * s, 'v_b': jnp.zeros((DIM,), jnp.float32), 'k_img_w': jax.random.normal(ks[5], (DIM, DIM), jnp.float32) * s, 'k_img_b': jnp.zeros((DIM,), jnp.float32), 'v_img_w': jax.random.normal(ks[6], (DIM, DIM), jnp.float32) * s, 'v_img_b': jnp.zeros((DIM,), jnp.float32), 'o_w': jax.random.normal(ks[7], (DIM, DIM), jnp.float32) * s, 'o_b': jnp.zeros((DIM,), jnp.float32), 'norm_q_w': jnp.ones((DIM,), jnp.float32), 'norm_k_w': jnp.ones((DIM,), jnp.float32), 'norm_k_img_w': jnp.ones((DIM,), jnp.float32)}
        return inp
    _L2_xattn_all = _L2_xattn_setup()
    _L2_xattn_in = {k: v for k, v in _L2_xattn_all.items() if k in ('q_w', 'q_b', 'k_w', 'k_b', 'v_w', 'v_b', 'k_img_w', 'k_img_b', 'v_img_w', 'v_img_b', 'o_w', 'o_b', 'norm_q_w', 'norm_k_w', 'norm_k_img_w')}
    del _L2_xattn_all

    def _L2_ffn_setup():
        import jax, jax.numpy as jnp
        import numpy as np
        B, S, D = (4, 256, 256)
        E = 8
        H = 352
        CAP_F = 1.0

        def _moe(x, Wg, W1, W3, W2, sw1, sw3, sw2):
            b, sl, d = x.shape
            T = b * sl
            C = int(CAP_F * T / E)
            xt = x.reshape(T, d)
            probs = jax.nn.softmax(xt @ Wg, axis=-1)
            eidx = jnp.argmax(probs, axis=-1)
            gate = jnp.take_along_axis(probs, eidx[:, None], 1)[:, 0]
            oh = jax.nn.one_hot(eidx, E, dtype=jnp.int32)
            pos = (jnp.cumsum(oh, axis=0) * oh).sum(-1) - 1
            keep = pos < C
            flat = jnp.where(keep, eidx * C + pos, E * C)
            xd = jnp.zeros((E * C, d), x.dtype).at[flat].set(xt, mode='drop')
            xd = xd.reshape(E, C, d)
            h = jax.nn.silu(jnp.einsum('ecd,edh->ech', xd, W1)) * jnp.einsum('ecd,edh->ech', xd, W3)
            oe = jnp.einsum('ech,ehd->ecd', h, W2).reshape(E * C, d)
            out = jnp.take(oe, jnp.minimum(flat, E * C - 1), axis=0)
            out = out * (gate * keep.astype(x.dtype))[:, None]
            shared = jax.nn.silu(xt @ sw1) * (xt @ sw3) @ sw2
            return (out + shared).reshape(b, sl, d)
        key = jax.random.key(seed)
        ks = jax.random.split(key, 8)
        s = lambda fan: 1.0 / np.sqrt(fan)
        return {'x': jax.random.normal(ks[0], (B, S, D), jnp.float32), 'Wg': jax.random.normal(ks[1], (D, E), jnp.float32) * s(D), 'W1': jax.random.normal(ks[2], (E, D, H), jnp.float32) * s(D), 'W3': jax.random.normal(ks[3], (E, D, H), jnp.float32) * s(D), 'W2': jax.random.normal(ks[4], (E, H, D), jnp.float32) * s(H), 'sw1': jax.random.normal(ks[5], (D, H), jnp.float32) * s(D), 'sw3': jax.random.normal(ks[6], (D, H), jnp.float32) * s(D), 'sw2': jax.random.normal(ks[7], (H, D), jnp.float32) * s(H)}
    _L2_ffn_all = _L2_ffn_setup()
    _L2_ffn_in = {k: v for k, v in _L2_ffn_all.items() if k in ('Wg', 'W1', 'W3', 'W2', 'sw1', 'sw3', 'sw2')}
    del _L2_ffn_all

    def _L3_xattn_setup():
        import jax, jax.numpy as jnp
        import numpy as np
        HIDDEN = 256
        N_HEADS = 16
        N_KV_HEADS = 4
        HEAD_DIM = 128
        EPS = 1e-06

        def rms_norm(x, w, eps=EPS):
            xf = x.astype(jnp.float32)
            var = jnp.mean(xf * xf, axis=-1, keepdims=True)
            return w * (xf * jax.lax.rsqrt(var + eps)).astype(x.dtype)
        key = jax.random.key(seed)
        ks = jax.random.split(key, 8)
        B, S, S_ENC = (4, 256, 128)
        inner = N_HEADS * HEAD_DIM
        kv_dim = N_KV_HEADS * HEAD_DIM
        s = 0.02
        return {'hidden_states': jax.random.normal(ks[0], (B, S, HIDDEN), jnp.float32), 'encoder_hidden_states': jax.random.normal(ks[1], (B, S_ENC, HIDDEN), jnp.float32), 'Wq': jax.random.normal(ks[2], (HIDDEN, inner), jnp.float32) * s, 'Wk': jax.random.normal(ks[3], (HIDDEN, kv_dim), jnp.float32) * s, 'Wv': jax.random.normal(ks[4], (HIDDEN, kv_dim), jnp.float32) * s, 'Wo': jax.random.normal(ks[5], (inner, HIDDEN), jnp.float32) * s, 'q_norm_w': jnp.ones((HEAD_DIM,), jnp.float32), 'k_norm_w': jnp.ones((HEAD_DIM,), jnp.float32)}
    _L3_xattn_all = _L3_xattn_setup()
    _L3_xattn_in = {k: v for k, v in _L3_xattn_all.items() if k in ('Wq', 'Wk', 'Wv', 'Wo', 'q_norm_w', 'k_norm_w')}
    del _L3_xattn_all

    def _L3_ffn_setup():
        import jax, jax.numpy as jnp
        import numpy as np
        H = 256
        E = 8
        TOPK = 2
        I_MOE = 128
        I_SH = 512

        def _silu_and_mul(gu):
            g, u = jnp.split(gu, 2, axis=-1)
            return jax.nn.silu(g) * u
        key = jax.random.key(seed)
        ks = jax.random.split(key, 6)
        s = lambda *sh: 1.0 / np.sqrt(sh[-2])
        hidden_states = jax.random.normal(ks[0], (2, 128, H), dtype=jnp.float32)
        w_gate = jax.random.normal(ks[1], (H, E), dtype=jnp.float32) * (1.0 / np.sqrt(H))
        w_gate_up = jax.random.normal(ks[2], (E, H, 2 * I_MOE), dtype=jnp.float32) * (1.0 / np.sqrt(H))
        w_down = jax.random.normal(ks[3], (E, I_MOE, H), dtype=jnp.float32) * (1.0 / np.sqrt(I_MOE))
        w_sh_gate_up = jax.random.normal(ks[4], (H, 2 * I_SH), dtype=jnp.float32) * (1.0 / np.sqrt(H))
        w_sh_down = jax.random.normal(ks[5], (I_SH, H), dtype=jnp.float32) * (1.0 / np.sqrt(I_SH))
        return {'hidden_states': hidden_states, 'w_gate': w_gate, 'w_gate_up': w_gate_up, 'w_down': w_down, 'w_sh_gate_up': w_sh_gate_up, 'w_sh_down': w_sh_down}
    _L3_ffn_all = _L3_ffn_setup()
    _L3_ffn_in = {k: v for k, v in _L3_ffn_all.items() if k in ('w_gate', 'w_gate_up', 'w_down', 'w_sh_gate_up', 'w_sh_down')}
    del _L3_ffn_all
    return {'x': x, 'ctx_2048': ctx_2048, 'pos_BxS2': pos_BxS2, 'itok_BxS_4096_4607': itok_BxS_4096_4607, 'L0_xattn_W_qkv': _L0_xattn_in['W_qkv'], 'L0_xattn_W_o': _L0_xattn_in['W_o'], 'L0_xattn_beta_q': _L0_xattn_in['beta_q'], 'L0_xattn_beta_k': _L0_xattn_in['beta_k'], 'L0_xattn_gate': _L0_xattn_in['gate'], 'L0_xattn_log_tau': _L0_xattn_in['log_tau'], 'L0_ffn_W1': _L0_ffn_in['W1'], 'L0_ffn_b1': _L0_ffn_in['b1'], 'L0_ffn_W2': _L0_ffn_in['W2'], 'L0_ffn_b2': _L0_ffn_in['b2'], 'L0_ffn_W3': _L0_ffn_in['W3'], 'L0_ffn_b3': _L0_ffn_in['b3'], 'L0_ffn_Wg': _L0_ffn_in['Wg'], 'L0_ffn_bg': _L0_ffn_in['bg'], 'L1_xattn_Wq': _L1_xattn_in['Wq'], 'L1_xattn_Wk': _L1_xattn_in['Wk'], 'L1_xattn_Wv': _L1_xattn_in['Wv'], 'L1_xattn_Wo': _L1_xattn_in['Wo'], 'L1_xattn_q_norm_w': _L1_xattn_in['q_norm_w'], 'L1_xattn_k_norm_w': _L1_xattn_in['k_norm_w'], 'L1_ffn_weight': _L1_ffn_in['weight'], 'L1_ffn_scale_weight': _L1_ffn_in['scale_weight'], 'L1_ffn_bias': _L1_ffn_in['bias'], 'L2_xattn_q_w': _L2_xattn_in['q_w'], 'L2_xattn_q_b': _L2_xattn_in['q_b'], 'L2_xattn_k_w': _L2_xattn_in['k_w'], 'L2_xattn_k_b': _L2_xattn_in['k_b'], 'L2_xattn_v_w': _L2_xattn_in['v_w'], 'L2_xattn_v_b': _L2_xattn_in['v_b'], 'L2_xattn_k_img_w': _L2_xattn_in['k_img_w'], 'L2_xattn_k_img_b': _L2_xattn_in['k_img_b'], 'L2_xattn_v_img_w': _L2_xattn_in['v_img_w'], 'L2_xattn_v_img_b': _L2_xattn_in['v_img_b'], 'L2_xattn_o_w': _L2_xattn_in['o_w'], 'L2_xattn_o_b': _L2_xattn_in['o_b'], 'L2_xattn_norm_q_w': _L2_xattn_in['norm_q_w'], 'L2_xattn_norm_k_w': _L2_xattn_in['norm_k_w'], 'L2_xattn_norm_k_img_w': _L2_xattn_in['norm_k_img_w'], 'L2_ffn_Wg': _L2_ffn_in['Wg'], 'L2_ffn_W1': _L2_ffn_in['W1'], 'L2_ffn_W3': _L2_ffn_in['W3'], 'L2_ffn_W2': _L2_ffn_in['W2'], 'L2_ffn_sw1': _L2_ffn_in['sw1'], 'L2_ffn_sw3': _L2_ffn_in['sw3'], 'L2_ffn_sw2': _L2_ffn_in['sw2'], 'L3_xattn_Wq': _L3_xattn_in['Wq'], 'L3_xattn_Wk': _L3_xattn_in['Wk'], 'L3_xattn_Wv': _L3_xattn_in['Wv'], 'L3_xattn_Wo': _L3_xattn_in['Wo'], 'L3_xattn_q_norm_w': _L3_xattn_in['q_norm_w'], 'L3_xattn_k_norm_w': _L3_xattn_in['k_norm_w'], 'L3_ffn_w_gate': _L3_ffn_in['w_gate'], 'L3_ffn_w_gate_up': _L3_ffn_in['w_gate_up'], 'L3_ffn_w_down': _L3_ffn_in['w_down'], 'L3_ffn_w_sh_gate_up': _L3_ffn_in['w_sh_gate_up'], 'L3_ffn_w_sh_down': _L3_ffn_in['w_sh_down']}

def reference(x, ctx_2048, pos_BxS2, itok_BxS_4096_4607, L0_xattn_W_qkv, L0_xattn_W_o, L0_xattn_beta_q, L0_xattn_beta_k, L0_xattn_gate, L0_xattn_log_tau, L0_ffn_W1, L0_ffn_b1, L0_ffn_W2, L0_ffn_b2, L0_ffn_W3, L0_ffn_b3, L0_ffn_Wg, L0_ffn_bg, L1_xattn_Wq, L1_xattn_Wk, L1_xattn_Wv, L1_xattn_Wo, L1_xattn_q_norm_w, L1_xattn_k_norm_w, L1_ffn_weight, L1_ffn_scale_weight, L1_ffn_bias, L2_xattn_q_w, L2_xattn_q_b, L2_xattn_k_w, L2_xattn_k_b, L2_xattn_v_w, L2_xattn_v_b, L2_xattn_k_img_w, L2_xattn_k_img_b, L2_xattn_v_img_w, L2_xattn_v_img_b, L2_xattn_o_w, L2_xattn_o_b, L2_xattn_norm_q_w, L2_xattn_norm_k_w, L2_xattn_norm_k_img_w, L2_ffn_Wg, L2_ffn_W1, L2_ffn_W3, L2_ffn_W2, L2_ffn_sw1, L2_ffn_sw3, L2_ffn_sw2, L3_xattn_Wq, L3_xattn_Wk, L3_xattn_Wv, L3_xattn_Wo, L3_xattn_q_norm_w, L3_xattn_k_norm_w, L3_ffn_w_gate, L3_ffn_w_gate_up, L3_ffn_w_down, L3_ffn_w_sh_gate_up, L3_ffn_w_sh_down):
    import jax
    import jax.numpy as jnp

    def _L0_xattn_ref(x, W_qkv, W_o, beta_q, beta_k, gate, log_tau, K_mem, V_mem, clip_k):
        import jax, jax.numpy as jnp
        import numpy as np
        D = x.shape[-1]
        scale = D ** (-0.5)
        qkv = x @ W_qkv.T
        Q = qkv[..., :D]
        alpha = jax.nn.sigmoid(gate)
        tau = jnp.exp(log_tau)
        coef = (alpha * beta_q + (1.0 - alpha) * beta_k) * scale * tau
        scores = coef * jnp.einsum('bsd,bnd->bsn', Q, K_mem)
        scores = scores - jnp.max(scores, axis=-1, keepdims=True)
        thr = jax.lax.top_k(scores, clip_k)[0][..., -1:]
        scores = jnp.where(scores < thr, -jnp.inf, scores)
        att = jax.nn.softmax(scores, axis=-1)
        out = jnp.einsum('bsn,bnd->bsd', att, V_mem)
        return out @ W_o.T

    def _L0_ffn_ref(x, W1, b1, W2, b2, W3, b3, Wg, bg):
        import jax, jax.numpy as jnp
        import numpy as np
        B, S, D = (4, 128, 256)
        H = 512
        NE = 8
        TOPK = 2
        gate_logits = jnp.einsum('bsd,dn->bsn', x, Wg) + bg
        gate_weights = jax.nn.softmax(gate_logits, axis=-1)
        topv, topi = jax.lax.top_k(gate_weights, TOPK)
        h = jax.nn.gelu(jnp.einsum('bsd,ndh->nbsh', x, W1) + b1[:, None, None, :], approximate=False)
        h = jax.nn.gelu(jnp.einsum('nbsh,nhf->nbsf', h, W2) + b2[:, None, None, :], approximate=False)
        eo = jnp.einsum('nbsf,nfd->nbsd', h, W3) + b3[:, None, None, :]
        comb = jnp.sum(jax.nn.one_hot(topi, NE, dtype=x.dtype) * topv[..., None], axis=-2)
        out = jnp.einsum('nbsd,bsn->bsd', eo, comb)
        return out

    def _L1_xattn_ref(draft_hidden, context_hidden, Wq, Wk, Wv, Wo, q_norm_w, k_norm_w, context_position_ids, draft_position_ids):
        import jax, jax.numpy as jnp
        import numpy as np
        B, CTX, DRAFT, D = (2, 512, 64, 256)
        H, KVH, HD = (16, 4, 128)
        N_REP = H // KVH
        EPS = 1e-06
        THETA = 10000.0
        SCALE = 1.0 / np.sqrt(HD).astype(np.float32)

        def _rms_norm(x, w):
            v = jnp.mean(jnp.square(x.astype(jnp.float32)), axis=-1, keepdims=True)
            return (w * (x.astype(jnp.float32) * jax.lax.rsqrt(v + EPS))).astype(x.dtype)

        def _rotate_half(x):
            x1, x2 = jnp.split(x, 2, axis=-1)
            return jnp.concatenate((-x2, x1), axis=-1)

        def _rope(x, pos):
            inv_freq = 1.0 / THETA ** (jnp.arange(0, HD, 2, dtype=jnp.float32) / HD)
            freqs = pos.astype(jnp.float32)[:, None, :, None] * inv_freq
            emb = jnp.concatenate((freqs, freqs), axis=-1)
            return x * jnp.cos(emb) + _rotate_half(x) * jnp.sin(emb)
        bsz, draft_len, _ = draft_hidden.shape
        ctx_len = context_hidden.shape[1]
        total_len = ctx_len + draft_len
        q = (draft_hidden @ Wq.T).reshape(bsz, draft_len, H, HD)
        q = _rms_norm(q, q_norm_w).transpose(0, 2, 1, 3)
        kv_in = jnp.concatenate([context_hidden, draft_hidden], axis=1)
        k = (kv_in @ Wk.T).reshape(bsz, total_len, KVH, HD)
        v = (kv_in @ Wv.T).reshape(bsz, total_len, KVH, HD).transpose(0, 2, 1, 3)
        k = _rms_norm(k, k_norm_w).transpose(0, 2, 1, 3)
        full_position_ids = jnp.concatenate([context_position_ids, draft_position_ids], axis=1)
        q = _rope(q, draft_position_ids)
        k = _rope(k, full_position_ids)
        k = jnp.repeat(k, N_REP, axis=1)
        v = jnp.repeat(v, N_REP, axis=1)
        scores = jnp.einsum('bhqd,bhkd->bhqk', q, k) * SCALE
        probs = jax.nn.softmax(scores, axis=-1)
        attn = jnp.einsum('bhqk,bhkd->bhqd', probs, v)
        attn = attn.transpose(0, 2, 1, 3).reshape(bsz, draft_len, H * HD)
        return attn @ Wo.T

    def _L1_ffn_ref(x, weight, scale_weight, bias):
        import jax, jax.numpy as jnp
        import numpy as np
        w = weight * scale_weight[:, None]
        out = jnp.einsum('bsi,oi->bso', x, w) + bias
        return out

    def _L2_xattn_ref(x, context, q_w, q_b, k_w, k_b, v_w, v_b, k_img_w, k_img_b, v_img_w, v_img_b, o_w, o_b, norm_q_w, norm_k_w, norm_k_img_w):
        import jax, jax.numpy as jnp
        import numpy as np
        DIM = 256
        NH = 16
        HD = DIM // NH
        EPS = 1e-06
        IMG_LEN = 257

        def rms_norm(x, w, eps=EPS):
            xf = x.astype(jnp.float32)
            y = xf * jax.lax.rsqrt(jnp.mean(xf * xf, axis=-1, keepdims=True) + eps)
            return y.astype(x.dtype) * w

        def linear(x, w, b):
            return jnp.einsum('blc,oc->blo', x, w) + b

        def attention(q, k, v):
            scale = 1.0 / jnp.sqrt(jnp.asarray(HD, q.dtype))
            scores = jnp.einsum('bqhd,bkhd->bhqk', q, k) * scale
            probs = jax.nn.softmax(scores, axis=-1)
            return jnp.einsum('bhqk,bkhd->bqhd', probs, v)
        B, L, _ = x.shape
        ctx_img = context[:, :IMG_LEN]
        ctx_txt = context[:, IMG_LEN:]
        q = rms_norm(linear(x, q_w, q_b), norm_q_w).reshape(B, L, NH, HD)
        k = rms_norm(linear(ctx_txt, k_w, k_b), norm_k_w).reshape(B, -1, NH, HD)
        v = linear(ctx_txt, v_w, v_b).reshape(B, -1, NH, HD)
        k_img = rms_norm(linear(ctx_img, k_img_w, k_img_b), norm_k_img_w).reshape(B, -1, NH, HD)
        v_img = linear(ctx_img, v_img_w, v_img_b).reshape(B, -1, NH, HD)
        img_x = attention(q, k_img, v_img)
        txt_x = attention(q, k, v)
        out = (txt_x + img_x).reshape(B, L, DIM)
        return linear(out, o_w, o_b)

    def _L2_ffn_ref(x, Wg, W1, W3, W2, sw1, sw3, sw2):
        import jax, jax.numpy as jnp
        import numpy as np
        B, S, D = (4, 256, 256)
        E = 8
        H = 352
        CAP_F = 1.0

        def _moe(x, Wg, W1, W3, W2, sw1, sw3, sw2):
            b, sl, d = x.shape
            T = b * sl
            C = int(CAP_F * T / E)
            xt = x.reshape(T, d)
            probs = jax.nn.softmax(xt @ Wg, axis=-1)
            eidx = jnp.argmax(probs, axis=-1)
            gate = jnp.take_along_axis(probs, eidx[:, None], 1)[:, 0]
            oh = jax.nn.one_hot(eidx, E, dtype=jnp.int32)
            pos = (jnp.cumsum(oh, axis=0) * oh).sum(-1) - 1
            keep = pos < C
            flat = jnp.where(keep, eidx * C + pos, E * C)
            xd = jnp.zeros((E * C, d), x.dtype).at[flat].set(xt, mode='drop')
            xd = xd.reshape(E, C, d)
            h = jax.nn.silu(jnp.einsum('ecd,edh->ech', xd, W1)) * jnp.einsum('ecd,edh->ech', xd, W3)
            oe = jnp.einsum('ech,ehd->ecd', h, W2).reshape(E * C, d)
            out = jnp.take(oe, jnp.minimum(flat, E * C - 1), axis=0)
            out = out * (gate * keep.astype(x.dtype))[:, None]
            shared = jax.nn.silu(xt @ sw1) * (xt @ sw3) @ sw2
            return (out + shared).reshape(b, sl, d)
        return _moe(x, Wg, W1, W3, W2, sw1, sw3, sw2)

    def _L3_xattn_ref(hidden_states, encoder_hidden_states, Wq, Wk, Wv, Wo, q_norm_w, k_norm_w):
        import jax, jax.numpy as jnp
        import numpy as np
        HIDDEN = 256
        N_HEADS = 16
        N_KV_HEADS = 4
        HEAD_DIM = 128
        EPS = 1e-06

        def rms_norm(x, w, eps=EPS):
            xf = x.astype(jnp.float32)
            var = jnp.mean(xf * xf, axis=-1, keepdims=True)
            return w * (xf * jax.lax.rsqrt(var + eps)).astype(x.dtype)
        B, S, _ = hidden_states.shape
        S_enc = encoder_hidden_states.shape[1]
        groups = N_HEADS // N_KV_HEADS
        scale = 1.0 / HEAD_DIM ** 0.5
        q = (hidden_states @ Wq).reshape(B, S, N_HEADS, HEAD_DIM)
        k = (encoder_hidden_states @ Wk).reshape(B, S_enc, N_KV_HEADS, HEAD_DIM)
        v = (encoder_hidden_states @ Wv).reshape(B, S_enc, N_KV_HEADS, HEAD_DIM)
        q = rms_norm(q, q_norm_w)
        k = rms_norm(k, k_norm_w)
        k = jnp.repeat(k, groups, axis=2)
        v = jnp.repeat(v, groups, axis=2)
        scores = jnp.einsum('bqhd,bkhd->bhqk', q, k) * scale
        probs = jax.nn.softmax(scores, axis=-1)
        out = jnp.einsum('bhqk,bkhd->bqhd', probs, v)
        out = out.reshape(B, S, N_HEADS * HEAD_DIM)
        return out @ Wo

    def _L3_ffn_ref(hidden_states, w_gate, w_gate_up, w_down, w_sh_gate_up, w_sh_down):
        import jax, jax.numpy as jnp
        import numpy as np
        H = 256
        E = 8
        TOPK = 2
        I_MOE = 128
        I_SH = 512

        def _silu_and_mul(gu):
            g, u = jnp.split(gu, 2, axis=-1)
            return jax.nn.silu(g) * u
        orig_shape = hidden_states.shape
        x = hidden_states.reshape(-1, orig_shape[-1])
        router_logits = x @ w_gate
        probs = jax.nn.softmax(router_logits, axis=-1)
        topk_w, topk_ids = jax.lax.top_k(probs, TOPK)
        topk_w = topk_w / jnp.sum(topk_w, axis=-1, keepdims=True)
        combine = jnp.sum(topk_w[..., None] * jax.nn.one_hot(topk_ids, E, dtype=x.dtype), axis=1)
        gu = jnp.einsum('th,ehf->etf', x, w_gate_up)
        act = _silu_and_mul(gu)
        eo = jnp.einsum('eti,eih->eth', act, w_down)
        routed = jnp.einsum('te,eth->th', combine, eo)
        shared = _silu_and_mul(x @ w_sh_gate_up) @ w_sh_down
        return (routed + shared).reshape(orig_shape)
    x = x + _L0_xattn_ref(_layernorm(x, axis=-1), L0_xattn_W_qkv, L0_xattn_W_o, L0_xattn_beta_q, L0_xattn_beta_k, L0_xattn_gate, L0_xattn_log_tau, ctx_2048, ctx_2048, 54)
    x = x + _L0_ffn_ref(_layernorm(x, axis=-1), L0_ffn_W1, L0_ffn_b1, L0_ffn_W2, L0_ffn_b2, L0_ffn_W3, L0_ffn_b3, L0_ffn_Wg, L0_ffn_bg)
    x = x + _L1_xattn_ref(_layernorm(x, axis=-1), ctx_2048, L1_xattn_Wq, L1_xattn_Wk, L1_xattn_Wv, L1_xattn_Wo, L1_xattn_q_norm_w, L1_xattn_k_norm_w, pos_BxS2, itok_BxS_4096_4607)
    x = x + _L1_ffn_ref(_layernorm(x, axis=-1), L1_ffn_weight, L1_ffn_scale_weight, L1_ffn_bias)
    x = x + _L2_xattn_ref(_layernorm(x, axis=-1), ctx_2048, L2_xattn_q_w, L2_xattn_q_b, L2_xattn_k_w, L2_xattn_k_b, L2_xattn_v_w, L2_xattn_v_b, L2_xattn_k_img_w, L2_xattn_k_img_b, L2_xattn_v_img_w, L2_xattn_v_img_b, L2_xattn_o_w, L2_xattn_o_b, L2_xattn_norm_q_w, L2_xattn_norm_k_w, L2_xattn_norm_k_img_w)
    x = x + _L2_ffn_ref(_layernorm(x, axis=-1), L2_ffn_Wg, L2_ffn_W1, L2_ffn_W3, L2_ffn_W2, L2_ffn_sw1, L2_ffn_sw3, L2_ffn_sw2)
    x = x + _L3_xattn_ref(_layernorm(x, axis=-1), ctx_2048, L3_xattn_Wq, L3_xattn_Wk, L3_xattn_Wv, L3_xattn_Wo, L3_xattn_q_norm_w, L3_xattn_k_norm_w)
    x = x + _L3_ffn_ref(_layernorm(x, axis=-1), L3_ffn_w_gate, L3_ffn_w_gate_up, L3_ffn_w_down, L3_ffn_w_sh_gate_up, L3_ffn_w_sh_down)
    return x

_drawn_inputs = setup_inputs


def setup_inputs(seed=0):
    import zlib

    import numpy as np

    out = dict(_drawn_inputs(seed))
    spreads = {'L0_ffn_b1': (0.0, 0.1),
     'L0_ffn_b2': (0.0, 0.1),
     'L0_ffn_b3': (0.0, 0.1),
     'L0_ffn_bg': (0.0, 0.1),
     'L1_xattn_q_norm_w': (1.0, 0.6),
     'L1_xattn_k_norm_w': (1.0, 0.6),
     'L2_xattn_q_b': (0.0, 1.095),
     'L2_xattn_k_b': (0.0, 0.8),
     'L2_xattn_v_b': (0.0, 0.1),
     'L2_xattn_k_img_b': (0.0, 0.8),
     'L2_xattn_v_img_b': (0.0, 0.1),
     'L2_xattn_o_b': (0.0, 0.1),
     'L2_xattn_norm_q_w': (1.0, 0.6),
     'L2_xattn_norm_k_w': (1.0, 0.6),
     'L2_xattn_norm_k_img_w': (1.0, 0.6),
     'L3_xattn_q_norm_w': (1.0, 0.6),
     'L3_xattn_k_norm_w': (1.0, 0.6)}
    factors = {}
    for name, (base, spread) in spreads.items():
        noise = np.random.default_rng([zlib.crc32(name.encode()), seed]).standard_normal(out[name].shape)
        drawn = base * np.exp(spread * noise) if base else spread * noise
        out[name] = jnp.asarray(drawn.astype(out[name].dtype))
    for name, factor in factors.items():
        out[name] = (out[name] * factor).astype(out[name].dtype)
    return out
```

```python
from contextlib import ExitStack

import concourse.bass as bass
import numpy as np
from concourse import mybir
from concourse.alu_op_type import AluOpType as ALU

F32 = mybir.dt.float32
F32R = mybir.dt.float32r
I32 = mybir.dt.int32
U32 = mybir.dt.uint32
ACT = mybir.ActivationFunctionType
AX = mybir.AxisListType

P = 128
B, S, D = 4, 256, 256
CTX = 1601
CTXP = CTX + 1
DC = D // P
QT = S // P
TT = B * QT
CTILES = -(-CTX // P)
CLAST = CTX - (CTILES - 1) * P
TOPK_CTX = 54


def flat2(a):
    return a.rearrange("p a b -> p (a b)")


class Step:

    def __init__(self, eng, sem):
        self.eng, self.sem, self.n = eng, sem, 0

    def __call__(self, ins):
        self.n += 1
        ins.then_inc(self.sem, 1)
        self.eng.wait_ge(self.sem, self.n)


class Stage:

    def __init__(self, nc, name):
        self.nc, self.name, self.ctx, self.sems = nc, name, ExitStack(), []

    def __enter__(self):
        return self

    def __exit__(self, *exc):
        self.clear()
        self.ctx.close()

    def sb(self, name, shape, dt=F32):
        return self.ctx.enter_context(self.nc.sbuf_tensor(f"{self.name}_{name}", shape, dt))

    def sem(self, name):
        s = self.ctx.enter_context(self.nc.semaphore(f"{self.name}_{name}"))
        self.sems.append(s)
        return s

    def clear(self):
        nums = sorted(s.num for s in self.sems)
        starts = [n for n in nums if n - 1 not in nums]
        for a in starts:
            e = next(n for n in range(a, a + len(nums) + 1) if n not in nums)
            self.nc.sync.sem_clear(range(a, e))
        self.nc.all_engine_barrier()


def make_constants(nc, m):
    with Stage(nc, "const") as st:
        made = st.sem("made")
        with nc.Block(name="constants") as block:
            @block.gpsimd
            def _(pool):
                pool.memset(m.ident[:, :], 0.0).then_inc(made, 1)
                pool.wait_ge(made, 1)
                pool.affine_select(out=m.ident[:, :], in_=m.ident[:, :], compare_op=ALU.not_equal, fill=1.0,
                                   base=0, pattern=[[-1, P]], channel_multiplier=1).then_inc(made, 1)
                pool.memset(m.nhalf[:, :], -0.5).then_inc(made, 1)
                pool.memset(m.onesf[:, :], 1.0).then_inc(made, 1)
                pool.wait_ge(made, 4)

            @block.scalar
            def _(act):
                act.wait_ge(made, 4)
                act.activation(m.ident_r[:, :], m.ident[:, :], ACT.Copy).then_inc(made, 1)
                act.activation(m.ones_r[:, :], m.onesf[:, :], ACT.Copy).then_inc(made, 1)


def copy_x_in(nc, m, x_in):
    with Stage(nc, "xin") as st:
        moved = st.sem("moved")
        with nc.Block(name="x_in") as block:
            @block.sync
            def _(sp):
                sp.dma_start(m.x_dram[:, :], x_in).then_inc(moved, 16)
                sp.wait_ge(moved, 16)


def transpose_context(nc, m, ctx_in):
    with Stage(nc, "ctxt") as st:
        rows = st.sb("rows", [P, CTILES, D])
        hi = st.sb("hi", [P, DC, CTXP], F32R)
        lo = st.sb("lo", [P, DC, CTXP], F32R)
        loaded, zeroed, turned, hi_done, lo_done, stored = [
            st.sem(n) for n in ("loaded", "zeroed", "turned", "hi_done", "lo_done", "stored")]
        banks = [(c, t0, min(t0 + 4, CTILES)) for c in range(DC) for t0 in range(0, CTILES, 4)]

        def cols(t0, t1):
            return t0 * P, min(t1 * P, CTX)

        with nc.Fori(0, B) as b:
            with nc.Block(name="ctx_turn") as block:
                @block.sync
                def _(sp):
                    full = (CTILES - 1) * P
                    sp.dma_start(rows[:, 0:CTILES - 1, :], ctx_in[bass.ds(b, 1), 0:full, :]
                                 .rearrange("a (t p) d -> p (a t) d", p=P)).then_inc(loaded, 16)
                    sp.dma_start(rows[0:CLAST, CTILES - 1, :], ctx_in[bass.ds(b, 1), full:CTX, :]
                                 .rearrange("a p d -> p (a d)")).then_inc(loaded, 16)
                    sp.wait_ge(zeroed, 2)
                    sp.wait_ge(hi_done, len(banks))
                    sp.dma_start(m.ctx_hi[bass.ds(b, 1), :, :].rearrange("a p n -> p (a n)"),
                                 hi[:, :, :].rearrange("p c n -> p (c n)").bitcast(F32)).then_inc(stored, 16)
                    sp.wait_ge(lo_done, len(banks))
                    sp.dma_start(m.ctx_lo[bass.ds(b, 1), :, :].rearrange("a p n -> p (a n)"),
                                 lo[:, :, :].rearrange("p c n -> p (c n)").bitcast(F32)).then_inc(stored, 16)
                    sp.wait_ge(stored, 32)

                @block.gpsimd
                def _(pool):
                    pool.memset(hi[:, :, CTX:CTXP].bitcast(F32), 0.0).then_inc(zeroed, 1)
                    pool.memset(lo[:, :, CTX:CTXP].bitcast(F32), 0.0).then_inc(zeroed, 1)

                @block.tensor
                def _(pe):
                    pe.wait_ge(loaded, 32)
                    for k, (c, t0, t1) in enumerate(banks):
                        for t in range(t0, t1):
                            r = P if t < CTILES - 1 else CLAST
                            ins = pe.transpose(m.ps[:, k, (t - t0) * P:(t - t0) * P + r],
                                               rows[0:r, t, c * P:(c + 1) * P], m.ident[0:r, 0:r])
                        ins.then_inc(turned, 1)

                @block.scalar
                def _(act):
                    for k, (c, t0, t1) in enumerate(banks):
                        a, z = cols(t0, t1)
                        act.wait_ge(turned, k + 1)
                        act.activation(hi[:, c, a:z], m.ps[:, k, 0:z - a], ACT.Copy).then_inc(hi_done, 1)

                @block.vector
                def _(dve):
                    for k, (c, t0, t1) in enumerate(banks):
                        a, z = cols(t0, t1)
                        dve.wait_ge(hi_done, k + 1)
                        dve.tensor_tensor(lo[:, c, a:z], m.ps[:, k, 0:z - a], hi[:, c, a:z].bitcast(F32),
                                          ALU.subtract).then_inc(lo_done, 1)
            st.clear()


def norm_block(nc, st, m, x_sb, zt_hi, zt_lo, tiles, x_src, sems, scratch, extra_loads=(), name="norm"):
    loaded, dstep, var_ok, rstd_ok, turned, hi_done, lo_done = sems
    stats, mv, rstd, z = scratch
    n_banks = DC * tiles * P // 512
    per = 512 // P
    slots = [(c, t) for c in range(DC) for t in range(tiles)]
    with nc.Block(name=name) as block:
        @block.sync
        def _(sp):
            sp.dma_start(x_sb[:, :, :], x_src).then_inc(loaded, 16)
            for dst, src in extra_loads:
                sp.dma_start(dst, src).then_inc(loaded, 16)
            sp.wait_ge(loaded, 16 * (1 + len(extra_loads)))

        @block.vector
        def _(dve):
            step = Step(dve, dstep)
            dve.wait_ge(loaded, 16 * (1 + len(extra_loads)))
            for t in range(tiles):
                dve.bn_stats(stats[:, t, :], x_sb[:, t, :]).then_inc(dstep, 1)
            step.n += tiles
            dve.wait_ge(dstep, step.n)
            for t in range(tiles):
                dve.bn_aggr(mv[:, t, :], stats[:, t, :]).then_inc(dstep, 1)
            step.n += tiles
            dve.wait_ge(dstep, step.n)
            dve.tensor_scalar(rstd[:, 0, :], mv[:, :, 1], 1e-5, None, ALU.add).then_inc(var_ok, 1)
            dve.wait_ge(rstd_ok, 1)
            for t in range(tiles):
                dve.tensor_scalar(z[:, t, :], x_sb[:, t, :], mv[:, t, 0:1], rstd[:, 1, t:t + 1],
                                  ALU.subtract, ALU.mult).then_inc(dstep, 1)
            step.n += tiles
            for k in range(n_banks):
                dve.wait_ge(hi_done, k + 1)
                dve.tensor_tensor(zt_lo[:, :, :].rearrange("p c n -> p (c n)")[:, k * 512:(k + 1) * 512],
                                  m.ps[:, k, :],
                                  zt_hi[:, :, :].rearrange("p c n -> p (c n)")[:, k * 512:(k + 1) * 512]
                                  .bitcast(F32), ALU.subtract).then_inc(lo_done, 1)

        @block.gpsimd
        def _(pool):
            pool.wait_ge(var_ok, 1)
            pool.tensor_tensor(rstd[:, 1, :], rstd[:, 0, :], m.nhalf[:, 0:1].to_broadcast([P, tiles]),
                               ALU.pow).then_inc(rstd_ok, 1)

        @block.tensor
        def _(pe):
            for i, (c, t) in enumerate(slots):
                pe.wait_ge(dstep, 3 * tiles)
                ins = pe.transpose(m.ps[:, i // per, (i % per) * P:(i % per + 1) * P],
                                   z[:, t, c * P:(c + 1) * P], m.ident[:, :])
                if i % per == per - 1:
                    ins.then_inc(turned, 1)

        @block.scalar
        def _(act):
            for k in range(n_banks):
                act.wait_ge(turned, k + 1)
                act.activation(zt_hi[:, :, :].rearrange("p c n -> p (c n)")[:, k * 512:(k + 1) * 512],
                               m.ps[:, k, :], ACT.Copy).then_inc(hi_done, 1)
def split_weights(nc, st, name, parts, arrived, w_hi, w_lo):
    with nc.Block(name=name) as block:
        @block.sync
        def _(sp):
            for (full, _halves, src), got in zip(parts, arrived):
                sp.dma_start(full, src).then_inc(got, 16)

        @block.scalar
        def _(act):
            for (full, halves, _src), got in zip(parts, arrived):
                act.wait_ge(got, 16)
                act.activation(halves[0], full, ACT.Copy).then_inc(w_hi, 1)

        @block.vector
        def _(dve):
            for i, (full, halves, _src) in enumerate(parts):
                dve.wait_ge(w_hi, i + 1)
                dve.tensor_tensor(halves[1], full, halves[0].bitcast(F32), ALU.subtract).then_inc(w_lo, 1)
    st.clear()


HALVES = ((0, 0), (0, 1), (1, 0))


def memory_attention(nc, m, w):
    CH = [(a, min(a + 512, CTXP)) for a in range(0, CTXP, 512)]
    ROUNDS = -(-TOPK_CTX // 8)
    with Stage(nc, "a0") as st:
        x_b = st.sb("x_b", [P, QT, D])
        zt = [st.sb(f"zt{i}", [P, DC, S], F32R) for i in range(2)]
        ct = [st.sb(f"ct{i}", [P, DC, CTXP], F32R) for i in range(2)]
        scratch = (st.sb("stats", [P, QT, 6]), st.sb("mv", [P, QT, 2]), st.sb("rstd", [P, 2, QT]),
                   st.sb("z", [P, QT, D]))
        rows = st.sb("rows", [P, CTILES, D])
        wf = st.sb("wf", [P, 2, DC * D])
        wr = [st.sb(f"wr{i}", [P, 2, DC * D], F32R) for i in range(2)]
        knob = st.sb("knob", [P, 12])
        qt = [st.sb(f"qt{i}", [P, DC, S], F32R) for i in range(2)]
        negm = st.sb("negm", [P, QT])
        shifted = st.sb("shifted", [P, QT, CTX])
        work = st.sb("work", [P, CTX])
        best = st.sb("best", [P, 8])
        expd = st.sb("expd", [P, QT, CTX])
        rsum = st.sb("rsum", [P, 2, QT])
        pt = st.sb("pt", [P, CTILES, S])
        ot = [st.sb(f"ot{i}", [P, DC, S], F32R) for i in range(2)]
        nsem = [st.sem("n_" + n) for n in ("loaded", "step", "var", "rstd", "turned", "hi", "lo")]
        w_in = [st.sem("wq_in"), st.sem("wo_in")]
        w_hi, w_lo, knobs_in, kact, dstep = [st.sem(n) for n in "w_hi w_lo knobs_in kact dstep".split()]
        (q_ready, q_hi, q_lo, s_ready, neg_ok, shift_ok, exp_ok, mask_ok, pt_turned, pt_ok, o_ready, o_hi,
         o_lo, y_ready) = [st.sem(n) for n in (
             "q_ready q_hi q_lo s_ready neg_ok shift_ok exp_ok mask_ok pt_turned pt_ok o_ready o_hi "
             "o_lo y_ready").split()]

        split_weights(nc, st, "a0_weights",
                      [(wf[:, i, :], (wr[0][:, i, :], wr[1][:, i, :]), w[n]) for i, n in enumerate(("wq", "wo"))],
                      w_in, w_hi, w_lo)
        GATE, TAU, BQ, BK = range(4)
        with nc.Block(name="a0_knobs") as block:
            @block.sync
            def _(sp):
                for i, n in enumerate(("gate", "log_tau", "beta_q", "beta_k")):
                    sp.dma_start(knob[:, i:i + 1], w[n].partition_broadcast(P)).then_inc(knobs_in, 16)

            @block.scalar
            def _(act):
                act.wait_ge(knobs_in, 64)
                act.activation(knob[:, 4:5], knob[:, GATE:GATE + 1], ACT.Exp, scale=-1.0).then_inc(kact, 1)
                act.activation(knob[:, 5:6], knob[:, TAU:TAU + 1], ACT.Exp).then_inc(kact, 1)

            @block.vector
            def _(dve):
                step = Step(dve, dstep)
                dve.wait_ge(kact, 2)
                step(dve.tensor_scalar(knob[:, 6:7], knob[:, 4:5], 1.0, None, ALU.add))
                step(dve.reciprocal(knob[:, 7:8], knob[:, 6:7]))
                step(dve.tensor_scalar(knob[:, 8:9], knob[:, 7:8], -1.0, 1.0, ALU.mult, ALU.add))
                step(dve.tensor_tensor(knob[:, 9:10], knob[:, 8:9], knob[:, BK:BK + 1], ALU.mult))
                step(dve.scalar_tensor_tensor(out=knob[:, 10:11], in0=knob[:, 7:8], scalar=knob[:, BQ:BQ + 1],
                                              in1=knob[:, 9:10], op0=ALU.mult, op1=ALU.add))
                step(dve.scalar_tensor_tensor(out=knob[:, 11:12], in0=knob[:, 10:11], scalar=D ** -0.5,
                                              in1=knob[:, 5:6], op0=ALU.mult, op1=ALU.mult))
        st.clear()
        coef = knob[:, 11:12]

        with nc.Fori(0, B) as b:
            x_rows = m.x_dram[bass.ds(b * QT, QT), :].rearrange("t (p d) -> p t d", p=P)
            full = (CTILES - 1) * P
            norm_block(nc, st, m, x_b, zt[0], zt[1], QT, x_rows, nsem, scratch, [
                (flat2(ct[0][:, :, :]).bitcast(F32), m.ctx_hi[bass.ds(b, 1), :, :].rearrange("a p n -> p (a n)")),
                (flat2(ct[1][:, :, :]).bitcast(F32), m.ctx_lo[bass.ds(b, 1), :, :].rearrange("a p n -> p (a n)")),
                (rows[:, 0:CTILES - 1, :], w["ctx"][bass.ds(b, 1), 0:full, :].rearrange("a (t p) d -> p (a t) d", p=P)),
                (rows[0:CLAST, CTILES - 1, :], w["ctx"][bass.ds(b, 1), full:CTX, :].rearrange("a p d -> p (a d)")),
            ], name="a0_norm")
            st.clear()
            with nc.Block(name="a0_attend") as block:
                @block.tensor
                def _(pe):
                    for o in range(DC):
                        n = 0
                        for c in range(DC):
                            for s, v in HALVES:
                                ins = pe.matmul(m.ps[:, 4 + o, 0:S], wr[v][:, 0, c * D + o * P:c * D + (o + 1) * P],
                                                zt[s][:, c, :], start=(n == 0), stop=(n == 3 * DC - 1))
                                n += 1
                        ins.then_inc(q_ready, 1)
                    pe.wait_ge(q_lo, DC)
                    for q in range(QT):
                        for k, (a, e) in enumerate(CH):
                            n = 0
                            for c in range(DC):
                                for s, v in HALVES:
                                    ins = pe.matmul(m.ps[:, 4 * q + k, 0:e - a], qt[s][:, c, q * P:(q + 1) * P],
                                                    ct[v][:, c, a:e], start=(n == 0), stop=(n == 3 * DC - 1))
                                    n += 1
                        ins.then_inc(s_ready, 1)
                    for q in range(QT):
                        pe.wait_ge(mask_ok, q + 1)
                        for k in range(0, CTILES, 4):
                            for t in range(k, min(k + 4, CTILES)):
                                r = P if t < CTILES - 1 else CLAST
                                ins = pe.transpose(m.ps[0:r, 4 * q + k // 4, (t - k) * P:(t - k + 1) * P],
                                                   expd[:, q, t * P:t * P + r], m.ident[:, :])
                            ins.then_inc(pt_turned, 1)
                    pe.wait_ge(pt_ok, 8)
                    for o in range(DC):
                        for t in range(CTILES):
                            r = P if t < CTILES - 1 else CLAST
                            ins = pe.matmul(m.ps[:, o, 0:S], rows[0:r, t, o * P:(o + 1) * P], pt[0:r, t, :],
                                            start=(t == 0), stop=(t == CTILES - 1))
                        ins.then_inc(o_ready, 1)
                    pe.wait_ge(o_lo, DC)
                    for q in range(QT):
                        n = 0
                        for c in range(DC):
                            for s, v in HALVES:
                                ins = pe.matmul(m.ps[:, 2 + q, 0:D], ot[s][:, c, q * P:(q + 1) * P],
                                                wr[v][:, 1, c * D:(c + 1) * D], start=(n == 0), stop=(n == 3 * DC - 1))
                                n += 1
                        ins.then_inc(y_ready, 1)

                @block.scalar
                def _(act):
                    for o in range(DC):
                        act.wait_ge(q_ready, o + 1)
                        act.activation(qt[0][:, o, :], m.ps[:, 4 + o, 0:S], ACT.Copy, scale=coef).then_inc(q_hi, 1)
                    for q in range(QT):
                        act.wait_ge(neg_ok, q + 1)
                        act.activation(shifted[:, q, :], m.ps[:, 4 * q:4 * q + 4, :]
                                       .rearrange("p b n -> p (b n)")[:, 0:CTX], ACT.Identity,
                                       bias=negm[:, q:q + 1]).then_inc(shift_ok, 1)
                        act.wait_ge(shift_ok, q + 1)
                        act.activation(expd[:, q, :], shifted[:, q, :], ACT.Exp).then_inc(exp_ok, 1)
                    for q in range(QT):
                        for k in range(0, CTILES, 4):
                            e = min(k + 4, CTILES)
                            i = q * 4 + k // 4
                            r = P if e < CTILES else CLAST
                            act.wait_ge(pt_turned, i + 1)
                            act.activation(pt[0:r, k:e, q * P:(q + 1) * P],
                                           m.ps[0:r, 4 * q + k // 4, 0:(e - k) * P].rearrange("p (t n) -> p t n", n=P),
                                           ACT.Copy).then_inc(pt_ok, 1)
                    for o in range(DC):
                        act.wait_ge(o_ready, o + 1)
                        act.activation(ot[0][:, o, :], m.ps[:, o, 0:S], ACT.Copy).then_inc(o_hi, 1)

                @block.vector
                def _(dve):
                    step = Step(dve, dstep)
                    for o in range(DC):
                        dve.wait_ge(q_hi, o + 1)
                        dve.scalar_tensor_tensor(out=qt[1][:, o, :], in0=m.ps[:, 4 + o, 0:S], scalar=coef,
                                                 in1=qt[0][:, o, :].bitcast(F32), op0=ALU.mult,
                                                 op1=ALU.subtract).then_inc(q_lo, 1)
                    for q in range(QT):
                        dve.wait_ge(s_ready, q + 1)
                        dve.tensor_reduce(negm[:, q:q + 1], m.ps[:, 4 * q:4 * q + 4, :]
                                          .rearrange("p b n -> p (b n)")[:, 0:CTX], AX.X, ALU.max, negate=True)\
                           .then_inc(neg_ok, 1)
                    for q in range(QT):
                        dve.wait_ge(shift_ok, q + 1)
                        left = shifted[:, q, :]
                        for r in range(ROUNDS):
                            step(dve.max(out=best[:, :], in_=left))
                            if r < ROUNDS - 1:
                                step(dve.match_replace(out=work[:, :], in_to_replace=best[:, :], in_values=left,
                                                       imm_value=-3.0e38))
                                left = work[:, :]
                        at = (TOPK_CTX - 1) % 8
                        dve.wait_ge(exp_ok, q + 1)
                        step(dve.scalar_tensor_tensor(out=expd[:, q, :], in0=shifted[:, q, :],
                                                      scalar=best[:, at:at + 1], in1=expd[:, q, :],
                                                      op0=ALU.is_ge, op1=ALU.mult, accum_out=rsum[:, 0, q:q + 1]))
                        dve.reciprocal(rsum[:, 1, q:q + 1], rsum[:, 0, q:q + 1]).then_inc(mask_ok, 1)
                    for o in range(DC):
                        dve.wait_ge(o_hi, o + 1)
                        dve.tensor_tensor(ot[1][:, o, :], m.ps[:, o, 0:S], ot[0][:, o, :].bitcast(F32),
                                          ALU.subtract).then_inc(o_lo, 1)
                    for q in range(QT):
                        dve.wait_ge(y_ready, q + 1)
                        dve.scalar_tensor_tensor(out=x_b[:, q, :], in0=m.ps[:, 2 + q, 0:D], scalar=rsum[:, 1, q:q + 1],
                                                 in1=x_b[:, q, :], op0=ALU.mult, op1=ALU.add).then_inc(dstep, 1)
            st.clear()
            with nc.Block(name="a0_out") as block:
                @block.sync
                def _(sp):
                    sp.dma_start(x_rows, x_b[:, :, :]).then_inc(nsem[0], 16)
                    sp.wait_ge(nsem[0], 16)
            st.clear()
HD = 128
KVH, REP = 4, 4
VW = HD + 1


def reduce_angle(dve, step, f, n, r):
    c1 = 6.28125
    c2 = float(np.float32(0.0019353071795864769))
    c3 = 2 * np.pi - c1 - c2
    magic = 12582912.0
    step(dve.tensor_scalar(n, f, 1.0 / (2 * np.pi), magic, ALU.mult, ALU.add))
    step(dve.tensor_scalar(n, n, -magic, None, ALU.add))
    step(dve.scalar_tensor_tensor(out=r, in0=n, scalar=-c1, in1=f, op0=ALU.mult, op1=ALU.add))
    step(dve.scalar_tensor_tensor(out=r, in0=n, scalar=-c2, in1=r, op0=ALU.mult, op1=ALU.add))
    step(dve.scalar_tensor_tensor(out=r, in0=n, scalar=-c3, in1=r, op0=ALU.mult, op1=ALU.add))


def grouped_attention(nc, m, name, w, rope):
    tiles = [(t * P, P if t < CTILES - 1 else CLAST, None) for t in range(CTILES)]
    if rope:
        tiles += [(CTX + q * P, P, q) for q in range(QT)]
    KT = len(tiles)
    NK = CTX + (S if rope else 0)
    NKP = NK + NK % 2
    GQ = REP * S
    NJ = GQ // P
    NG = 2
    JG = NJ // NG
    CH = [(a, min(a + 512, NKP)) for a in range(0, NKP, 512)]
    KB = [(t0, min(t0 + 4, KT)) for t0 in range(0, KT, 4)]
    KEND = [t[0] for t in tiles] + [NK]
    SCALE = HD ** -0.5

    with Stage(nc, name) as st:
        x_b = st.sb("x_b", [P, QT, D])
        zt_hi = st.sb("zt_hi", [P, DC, S], F32R)
        zt_lo = st.sb("zt_lo", [P, DC, S], F32R)
        ct_hi = st.sb("ct_hi", [P, DC, CTXP], F32R)
        ct_lo = st.sb("ct_lo", [P, DC, CTXP], F32R)
        stats = st.sb("stats", [P, QT, 6])
        mv = st.sb("mv", [P, QT, 2])
        rstd = st.sb("rstd", [P, 2, QT])
        z = st.sb("z", [P, QT, D])
        qw = st.sb("qw", [P, HD])
        kw = st.sb("kw", [P, HD])
        wq_f = st.sb("wq_f", [P, DC, REP * HD])
        wkv_f = st.sb("wkv_f", [P, DC, 2 * HD])
        wo_f = st.sb("wo_f", [P, REP, D])
        wq = [st.sb(f"wq{i}", [P, DC, REP * HD], F32R) for i in range(2)]
        wkv = [st.sb(f"wkv{i}", [P, DC, 2 * HD], F32R) for i in range(2)]
        wo = [st.sb(f"wo{i}", [P, REP, D], F32R) for i in range(2)]
        k_rows = st.sb("k_rows", [P, KT, HD])
        v_rows = st.sb("v_rows", [P, KT, VW])
        q_rows = st.sb("q_rows", [P, QT, REP, HD])
        k_sq = st.sb("k_sq", [P, 3, KT])
        q_sq = st.sb("q_sq", [P, 3, QT * REP])
        square = st.sb("square", [P, 8, HD])
        kt = [st.sb(f"kt{i}", [P, NKP], F32R) for i in range(2)]
        qt = [st.sb(f"qt{i}", [P, GQ], F32R) for i in range(2)]
        negmax = st.sb("negmax", [P, NJ])
        diag = st.sb("diag", [P, NJ, P], F32R)
        probs = st.sb("probs", [P, 3, 512])
        rsum = st.sb("rsum", [P, JG])
        o_rows = st.sb("o_rows", [P, NJ, HD])
        ot = [st.sb(f"ot{i}", [P, NJ * P], F32R) for i in range(2)]
        if rope:
            pos_i = st.sb("pos_i", [KT, P], I32)
            pos_rows = st.sb("pos_rows", [KT, P])
            pos_f = st.sb("pos_f", [P, KT])
            invf = st.sb("invf", [P, HD // 2])
            cos = st.sb("cos", [P, KT, HD // 2])
            sin = st.sb("sin", [P, KT, HD // 2])
            k_cos = st.sb("k_cos", [P, KT, HD])
            k_sin = st.sb("k_sin", [P, KT, HD])
            q_cos = st.sb("q_cos", [P, QT, REP, HD])
            q_sin = st.sb("q_sin", [P, QT, REP, HD])

        nsem = [st.sem("n_" + n) for n in ("loaded", "step", "var", "rstd", "turned", "hi", "lo")]
        (loaded, w_hi, w_lo, zeroed, dstep, kv_ready, sq_done, kv_taken, q_ready, qsq_done, q_taken,
         ksum_ok, qsum_ok, k_rstd, q_rstd, sin_half, k_ready, qr_ready, turned, hi_done, lo_done,
         smax_ready, neg_done, diag_done, st_ready, exp_done, pv_done, o_done, ot_turned, ot_hi,
         ot_lo, y_ready, angles, tables, pstep, wkv_in, wq_in, wo_in) = [st.sem(n) for n in (
             "loaded w_hi w_lo zeroed dstep kv_ready sq_done kv_taken q_ready qsq_done q_taken "
             "ksum_ok qsum_ok k_rstd q_rstd sin_half k_ready qr_ready turned hi_done lo_done "
             "smax_ready neg_done diag_done st_ready exp_done pv_done o_done ot_turned ot_hi "
             "ot_lo y_ready angles tables pstep wkv_in wq_in wo_in").split()]

        with nc.Block(name=f"{name}_once") as block:
            @block.sync
            def _(sp):
                sp.dma_start(qw[:, :], w["qw"].partition_broadcast(P)).then_inc(loaded, 16)
                sp.dma_start(kw[:, :], w["kw"].partition_broadcast(P)).then_inc(loaded, 16)
                n = 32
                if rope:
                    sp.dma_start(invf[:, :], w["inv_freq"].partition_broadcast(P)).then_inc(loaded, 16)
                    n += 16
                sp.wait_ge(loaded, n)

            @block.gpsimd
            def _(pool):
                pool.memset(v_rows[:, :, HD:VW], 1.0).then_inc(zeroed, 1)
                pool.memset(k_rows[:, :, :], 0.0).then_inc(zeroed, 1)
                pool.memset(k_sq[:, :, :], 1.0).then_inc(zeroed, 1)
                if NKP > NK:
                    pool.memset(kt[0][:, NK:NKP].bitcast(F32), 0.0).then_inc(zeroed, 1)
                if rope:
                    pool.memset(pos_i[:, :], 0).then_inc(zeroed, 1)
        st.clear()

        with nc.Fori(0, B) as b:
            x_rows = m.x_dram[bass.ds(b * QT, QT), :].rearrange("t (p d) -> p t d", p=P)
            extra = [(ct_hi[:, :, :].rearrange("p c n -> p (c n)").bitcast(F32),
                      m.ctx_hi[bass.ds(b, 1), :, :].rearrange("a p n -> p (a n)")),
                     (ct_lo[:, :, :].rearrange("p c n -> p (c n)").bitcast(F32),
                      m.ctx_lo[bass.ds(b, 1), :, :].rearrange("a p n -> p (a n)"))]
            if rope:
                full = (CTILES - 1) * P
                extra += [(pos_i[0:CTILES - 1, :], w["pos"][bass.ds(b, 1), 0:full]
                           .rearrange("a (t p) -> (a t) p", p=P)),
                          (pos_i[CTILES - 1:CTILES, 0:CLAST], w["pos"][bass.ds(b, 1), full:CTX]),
                          (pos_i[CTILES:KT, :], w["tok"][bass.ds(b, 1), :]
                           .rearrange("a (t p) -> (a t) p", p=P))]
            norm_block(nc, st, m, x_b, zt_hi, zt_lo, QT, x_rows, nsem, (stats, mv, rstd, z), extra,
                       name=f"{name}_norm")
            if rope:
                with nc.Block(name=f"{name}_rope") as block:
                    ang = k_cos[:, :, 0:HD // 2]
                    tmp = k_sin[:, :, 0:HD // 2]

                    @block.vector
                    def _(dve):
                        step = Step(dve, dstep)
                        dve.tensor_copy(pos_rows[:, :], pos_i[:, :]).then_inc(angles, 1)
                        dve.wait_ge(tables, 1)
                        step(dve.tensor_copy(pos_f[:, :], m.ps[:, 0, 0:KT]))
                        step(dve.tensor_tensor(ang, pos_f[:, :].unsqueeze(2).to_broadcast([P, KT, HD // 2]),
                                               invf[:, :].unsqueeze(1).to_broadcast([P, KT, HD // 2]), ALU.mult))
                        reduce_angle(dve, step, ang, tmp, sin[:, :, :])
                        step(dve.tensor_scalar(cos[:, :, :], sin[:, :, :], np.pi / 2, None, ALU.add))
                        step(dve.tensor_scalar(tmp, cos[:, :, :], np.pi, -2 * np.pi, ALU.is_gt, ALU.mult))
                        step(dve.tensor_tensor(cos[:, :, :], cos[:, :, :], tmp, ALU.add))
                        PI = 3.1415925
                        step(dve.tensor_scalar(cos[:, :, :], cos[:, :, :], PI, -PI, ALU.min, ALU.max))
                        dve.tensor_scalar(sin[:, :, :], sin[:, :, :], PI, -PI, ALU.min, ALU.max)\
                           .then_inc(angles, 1)

                    @block.tensor
                    def _(pe):
                        pe.wait_ge(angles, 1)
                        pe.transpose(m.ps[:, 0, 0:KT], pos_rows[:, :], m.ident[0:KT, 0:KT]).then_inc(tables, 1)

                    @block.scalar
                    def _(act):
                        act.wait_ge(angles, 2)
                        act.activation(sin[:, :, :], sin[:, :, :], ACT.Sin).then_inc(tables, 1)
                        act.activation(cos[:, :, :], cos[:, :, :], ACT.Sin).then_inc(tables, 1)
            st.clear()

            with nc.Fori(0, KVH) as g:
                with nc.Block(name=f"{name}_group") as block:
                    PVK = KT * NG

                    @block.sync
                    def _(sp):
                        for dst, src, arrived in ((wkv_f, w["wkv"], wkv_in), (wq_f, w["wq"], wq_in),
                                                  (wo_f, w["wo"], wo_in)):
                            sp.dma_start(dst[:, :, :].rearrange("p c n -> p (c n)"),
                                         src[bass.ds(g, 1), :, :].rearrange("a p n -> p (a n)"))\
                              .then_inc(arrived, 16)

                    @block.tensor
                    def _(pe):
                        def halves(c, hi, lo):
                            return [(hi[0], hi[1]), (hi[0], lo[1]), (lo[0], hi[1])]

                        pe.wait_ge(w_hi, 1)
                        pe.wait_ge(w_lo, 1)
                        for t, (at, r, own) in enumerate(tiles):
                            if t >= 8:
                                pe.wait_ge(sq_done, t - 7)
                                pe.wait_ge(kv_taken, t - 7)
                            n = 0
                            for c in range(DC):
                                src = ([a[:, c, at:at + r] for a in (ct_hi, ct_lo)] if own is None else
                                       [a[:, c, own * P:own * P + r] for a in (zt_hi, zt_lo)])
                                for s, v in ((0, 0), (0, 1), (1, 0)):
                                    ins = pe.matmul(m.ps[0:r, t % 8, 0:2 * HD], src[s], wkv[v][:, c, :],
                                                    start=(n == 0), stop=(n == 3 * DC - 1))
                                    n += 1
                            ins.then_inc(kv_ready, 1)
                        pe.wait_ge(w_hi, 2)
                        pe.wait_ge(w_lo, 2)
                        for q in range(QT):
                            pe.wait_ge(sq_done, KT + q - 7)
                            pe.wait_ge(kv_taken, KT + q - 7)
                            n = 0
                            for c in range(DC):
                                for s, v in ((0, 0), (0, 1), (1, 0)):
                                    src = (zt_hi, zt_lo)[s][:, c, q * P:(q + 1) * P]
                                    ins = pe.matmul(m.ps[:, (KT + q) % 8, :], src, wq[v][:, c, :],
                                                    start=(n == 0), stop=(n == 3 * DC - 1))
                                    n += 1
                            ins.then_inc(q_ready, 1)
                        pe.wait_ge(sq_done, KT)
                        pe.wait_ge(qsq_done, QT)
                        pe.wait_ge(q_taken, QT)
                        pe.wait_ge(k_ready, 1)
                        for k, (t0, t1) in enumerate(KB):
                            for t in range(t0, t1):
                                at, r, _own = tiles[t]
                                ins = pe.transpose(m.ps[:, k, at - KEND[t0]:at - KEND[t0] + r],
                                                   k_rows[0:r, t, :], m.ident[0:r, 0:r])
                            ins.then_inc(turned, 1)
                        pe.wait_ge(qr_ready, 1)
                        for j in range(NJ):
                            ins = pe.transpose(m.ps[:, len(KB) + j // 4, (j % 4) * P:(j % 4 + 1) * P],
                                               q_rows[:, j % QT, j // QT, :], m.ident[:, :])
                            if j % 4 == 3:
                                ins.then_inc(turned, 1)
                        pe.wait_ge(hi_done, len(KB) + 2)
                        pe.wait_ge(lo_done, len(KB) + 2)

                        def rough_scores(j):
                            if j:
                                pe.wait_ge(neg_done, j)
                            for k, (a, e) in enumerate(CH):
                                ins = pe.matmul(m.ps[:, k, 0:e - a], qt[0][:, j * P:(j + 1) * P],
                                                kt[0][:, a:e], start=True, stop=True)
                            ins.then_inc(smax_ready, 1)

                        def scores(n):
                            G, t = divmod(n, KT)
                            at, r, _own = tiles[t]
                            if t == 0:
                                pe.wait_ge(diag_done, JG * (G + 1))
                            if n >= 2:
                                pe.wait_ge(exp_done, n - 1)
                            out = m.ps[0:r, 4 + n % 2, :]
                            cols = slice(G * 512, (G + 1) * 512)
                            pe.matmul(out, m.ones_r[:, 0:r],
                                      diag[:, G * JG:(G + 1) * JG, :].rearrange("p j n -> p (j n)"),
                                      start=True, stop=False)
                            pe.matmul(out, kt[0][:, at:at + r], qt[0][:, cols], start=False, stop=False)
                            pe.matmul(out, kt[0][:, at:at + r], qt[1][:, cols], start=False, stop=False)
                            pe.matmul(out, kt[1][:, at:at + r], qt[0][:, cols], start=False, stop=True)\
                              .then_inc(st_ready, 1)

                        def values(n):
                            G, t = divmod(n, KT)
                            r = tiles[t][1]
                            pe.wait_ge(exp_done, n + 1)
                            if t == 0 and G:
                                pe.wait_ge(o_done, G)
                            for i in range(JG):
                                ins = pe.matmul(m.ps[:, 6 + i // 2, (i % 2) * 256:(i % 2) * 256 + VW],
                                                probs[0:r, n % 3, i * P:(i + 1) * P],
                                                v_rows[0:r, t, :], start=(t == 0 and i % 2 == 0),
                                                stop=(t == KT - 1), skip_group_check=True)
                            ins.then_inc(pv_done, 1)

                        for j in range(JG):
                            rough_scores(j)
                        for n in range(PVK):
                            scores(n)
                            if n < KT and n % 3 == 2 and JG + n // 3 < NJ:
                                rough_scores(JG + n // 3)
                            if n:
                                values(n - 1)
                        values(PVK - 1)
                        pe.wait_ge(o_done, NG)
                        for j in range(NJ):
                            ins = pe.transpose(m.ps[:, j // 4, (j % 4) * P:(j % 4 + 1) * P],
                                               o_rows[:, j, :], m.ident[:, :])
                            if j % 4 == 3:
                                ins.then_inc(ot_turned, 1)
                        pe.wait_ge(ot_hi, 2)
                        pe.wait_ge(ot_lo, 2)
                        pe.wait_ge(w_hi, 3)
                        pe.wait_ge(w_lo, 3)
                        for q in range(QT):
                            n = 0
                            for h in range(REP):
                                j = h * QT + q
                                for s, v in ((0, 0), (0, 1), (1, 0)):
                                    ins = pe.matmul(m.ps[:, 2 + q, 0:D], ot[s][:, j * P:(j + 1) * P],
                                                    wo[v][:, h, :], start=(n == 0), stop=(n == 3 * REP - 1))
                                    n += 1
                            ins.then_inc(y_ready, 1)

                    @block.scalar
                    def _(act):
                        for dst, src, arrived in ((wkv, wkv_f, wkv_in), (wq, wq_f, wq_in), (wo, wo_f, wo_in)):
                            act.wait_ge(arrived, 16)
                            act.activation(dst[0][:, :, :], src[:, :, :], ACT.Copy).then_inc(w_hi, 1)
                        for t, (_at, r, _own) in enumerate(tiles):
                            act.wait_ge(kv_ready, t + 1)
                            if t >= 4:
                                act.wait_ge(sq_done, t - 3)
                            act.activation(square[0:r, t % 4, :], m.ps[0:r, t % 8, 0:HD], ACT.Square,
                                           accum_out=k_sq[0:r, 0, t:t + 1]).then_inc(sq_done, 1)
                        for q in range(QT):
                            act.wait_ge(q_ready, q + 1)
                            if q:
                                act.wait_ge(qsq_done, q)
                            for h in range(REP):
                                i = q * REP + h
                                ins = act.activation(square[:, 4 + h, :], m.ps[:, (KT + q) % 8, h * HD:(h + 1) * HD],
                                                     ACT.Square, accum_out=q_sq[:, 0, i:i + 1])
                            ins.then_inc(qsq_done, 1)
                        for k, (t0, t1) in enumerate(KB):
                            a, e = KEND[t0], KEND[t1]
                            act.wait_ge(turned, k + 1)
                            act.activation(kt[0][:, a:e], m.ps[:, k, 0:e - a], ACT.Copy).then_inc(hi_done, 1)
                        for k in range(2):
                            act.wait_ge(turned, len(KB) + k + 1)
                            act.activation(qt[0][:, k * 512:(k + 1) * 512], m.ps[:, len(KB) + k, :], ACT.Copy)\
                               .then_inc(hi_done, 1)
                        for n in range(PVK):
                            r = tiles[n % KT][1]
                            act.wait_ge(st_ready, n + 1)
                            if n >= 3:
                                act.wait_ge(pv_done, n - 2)
                            act.activation(probs[0:r, n % 3, :], m.ps[0:r, 4 + n % 2, :], ACT.Exp)\
                               .then_inc(exp_done, 1)
                        for k in range(2):
                            act.wait_ge(ot_turned, k + 1)
                            act.activation(ot[0][:, k * 512:(k + 1) * 512], m.ps[:, k, :], ACT.Copy)\
                               .then_inc(ot_hi, 1)

                    @block.gpsimd
                    def _(pool):
                        step = Step(pool, pstep)
                        pool.wait_ge(sq_done, KT)
                        step(pool.tensor_scalar(k_sq[:, 1, :], k_sq[:, 0, :], 1.0 / HD, 1e-6, ALU.mult, ALU.add))
                        pool.tensor_tensor(k_sq[:, 2, :], k_sq[:, 1, :], m.nhalf[:, 0:1].to_broadcast([P, KT]),
                                           ALU.pow).then_inc(k_rstd, 1)
                        pool.wait_ge(qsq_done, QT)
                        step(pool.tensor_scalar(q_sq[:, 1, :], q_sq[:, 0, :], 1.0 / HD, 1e-6, ALU.mult, ALU.add))
                        step(pool.tensor_tensor(q_sq[:, 2, :], q_sq[:, 1, :],
                                                m.nhalf[:, 0:1].to_broadcast([P, QT * REP]), ALU.pow))
                        pool.tensor_scalar(q_sq[:, 2, :], q_sq[:, 2, :], SCALE, None, ALU.mult)\
                            .then_inc(q_rstd, 1)
                        if rope:
                            half = HD // 2
                            pool.wait_ge(k_ready, 0 + 1)
                        for j in range(NJ):
                            pool.wait_ge(neg_done, j + 1)
                            pool.tensor_scalar(diag[:, j, :], m.ident[:, :], negmax[:, j:j + 1], None, ALU.mult)\
                                .then_inc(diag_done, 1)

                    @block.vector
                    def _(dve):
                        step = Step(dve, dstep)
                        for k, (dst, src) in enumerate(((wkv, wkv_f), (wq, wq_f), (wo, wo_f))):
                            dve.wait_ge(w_hi, k + 1)
                            dve.tensor_tensor(dst[1][:, :, :], src[:, :, :], dst[0][:, :, :].bitcast(F32),
                                              ALU.subtract).then_inc(w_lo, 1)
                        for t, (_at, r, _own) in enumerate(tiles):
                            dve.wait_ge(sq_done, t + 1)
                            dve.tensor_tensor(k_rows[0:r, t, :], m.ps[0:r, t % 8, 0:HD], kw[0:r, :], ALU.mult)
                            dve.tensor_copy(v_rows[0:r, t, 0:HD], m.ps[0:r, t % 8, HD:2 * HD])\
                               .then_inc(kv_taken, 1)
                        for q in range(QT):
                            dve.wait_ge(qsq_done, q + 1)
                            dve.tensor_tensor(q_rows[:, q, :, :],
                                              m.ps[:, (KT + q) % 8, :].rearrange("p (h n) -> p h n", h=REP),
                                              qw[:, :].unsqueeze(1).to_broadcast([P, REP, HD]), ALU.mult)\
                               .then_inc(q_taken, 1)
                        dve.wait_ge(k_rstd, 1)
                        dve.wait_ge(kv_taken, KT)

                        def rotate(rows, by_cos, by_sin, c4, s4, n, done):
                            step(dve.tensor_tensor(by_sin, rows, s4, ALU.mult))
                            step(dve.tensor_tensor(by_cos, rows, c4, ALU.mult))
                            dve.tensor_tensor(rows[:, :, 0, :], by_cos[:, :, 0, :], by_sin[:, :, 1, :],
                                              ALU.subtract).then_inc(dstep, 1)
                            step.n += 1
                            dve.tensor_tensor(rows[:, :, 1, :], by_cos[:, :, 1, :], by_sin[:, :, 0, :],
                                              ALU.add).then_inc(dstep, 1)
                            step.n += 1
                            dve.wait_ge(dstep, step.n)

                        step(dve.tensor_tensor(k_rows[:, :, :], k_rows[:, :, :],
                                               k_sq[:, 2, :].unsqueeze(2).to_broadcast([P, KT, HD]), ALU.mult))
                        if rope:
                            half = HD // 2

                            def pairs(a):
                                return a.rearrange("p n (i d) -> p n i d", i=2)

                            rotate(pairs(k_rows[:, :, :]), pairs(k_cos[:, :, :]), pairs(k_sin[:, :, :]),
                                   cos[:, :, :].unsqueeze(2).to_broadcast([P, KT, 2, half]),
                                   sin[:, :, :].unsqueeze(2).to_broadcast([P, KT, 2, half]), KT, k_ready)
                        dve.engine_nop().then_inc(k_ready, 1)
                        dve.wait_ge(q_rstd, 1)
                        dve.wait_ge(q_taken, QT)
                        step(dve.tensor_tensor(q_rows[:, :, :, :].rearrange("p q h n -> p (q h) n"),
                                               q_rows[:, :, :, :].rearrange("p q h n -> p (q h) n"),
                                               q_sq[:, 2, :].unsqueeze(2).to_broadcast([P, QT * REP, HD]), ALU.mult))
                        if rope:
                            for q in range(QT):
                                rotate(pairs(q_rows[:, q, :, :]), pairs(q_cos[:, q, :, :]),
                                       pairs(q_sin[:, q, :, :]),
                                       cos[:, CTILES + q, :].unsqueeze(1).unsqueeze(1)
                                       .to_broadcast([P, REP, 2, half]),
                                       sin[:, CTILES + q, :].unsqueeze(1).unsqueeze(1)
                                       .to_broadcast([P, REP, 2, half]), REP, None)
                        dve.engine_nop().then_inc(qr_ready, 1)
                        for k, (t0, t1) in enumerate(KB):
                            a, e = KEND[t0], KEND[t1]
                            dve.wait_ge(hi_done, k + 1)
                            dve.tensor_tensor(kt[1][:, a:e], m.ps[:, k, 0:e - a], kt[0][:, a:e].bitcast(F32),
                                              ALU.subtract).then_inc(lo_done, 1)
                        for k in range(2):
                            dve.wait_ge(hi_done, len(KB) + k + 1)
                            dve.tensor_tensor(qt[1][:, k * 512:(k + 1) * 512], m.ps[:, len(KB) + k, :],
                                              qt[0][:, k * 512:(k + 1) * 512].bitcast(F32),
                                              ALU.subtract).then_inc(lo_done, 1)
                        for j in range(NJ):
                            dve.wait_ge(smax_ready, j + 1)
                            dve.tensor_reduce(negmax[:, j:j + 1],
                                              m.ps[:, 0:4, :].rearrange("p b n -> p (b n)")[:, 0:NK],
                                              AX.X, ALU.max, negate=True).then_inc(neg_done, 1)
                        for G in range(NG):
                            dve.wait_ge(pv_done, KT * (G + 1))
                            o = m.ps[:, 6:8, :].rearrange("p b (i n) -> p (b i) n", i=2)
                            step(dve.reciprocal(rsum[:, :].unsqueeze(2), o[:, :, HD:VW]))
                            dve.tensor_tensor(o_rows[:, G * JG:(G + 1) * JG, :], o[:, :, 0:HD],
                                              rsum[:, :].unsqueeze(2).to_broadcast([P, JG, HD]), ALU.mult)\
                               .then_inc(o_done, 1)
                        for k in range(2):
                            dve.wait_ge(ot_hi, k + 1)
                            dve.tensor_tensor(ot[1][:, k * 512:(k + 1) * 512], m.ps[:, k, :],
                                              ot[0][:, k * 512:(k + 1) * 512].bitcast(F32),
                                              ALU.subtract).then_inc(ot_lo, 1)
                        for q in range(QT):
                            dve.wait_ge(y_ready, q + 1)
                            dve.tensor_tensor(x_b[:, q, :], x_b[:, q, :], m.ps[:, 2 + q, 0:D], ALU.add)\
                               .then_inc(dstep, 1)
                st.clear()
            with nc.Block(name=f"{name}_out") as block:
                @block.sync
                def _(sp):
                    sp.dma_start(x_rows, x_b[:, :, :]).then_inc(loaded, 16)
                    sp.wait_ge(loaded, 16)
            st.clear()
NE = 8
TOK = B * S
HALF = 512


class FfnBase:

    def __init__(self, st, keep_z=False):
        self.x = st.sb("x", [P, TT, D])
        self.z = st.sb("z", [P, TT, D])
        self.zt = [st.sb(f"zt{i}", [P, DC, TOK], F32R) for i in range(2)]
        self.scratch = (st.sb("stats", [P, TT, 6]), st.sb("mv", [P, TT, 2]), st.sb("rstd", [P, 2, TT]), self.z)
        self.nsem = [st.sem("n_" + n) for n in ("loaded", "step", "var", "rstd", "turned", "hi", "lo")]

    def norm(self, nc, st, m, extra=()):
        norm_block(nc, st, m, self.x, self.zt[0], self.zt[1], TT,
                   m.x_dram[:, :].rearrange("t (p d) -> p t d", p=P), self.nsem, self.scratch, extra,
                   name=f"{st.name}_norm")
        st.clear()

    def store(self, nc, st, m):
        with nc.Block(name=f"{st.name}_out") as block:
            @block.sync
            def _(sp):
                sp.dma_start(m.x_dram[:, :].rearrange("t (p d) -> p t d", p=P), self.x[:, :, :])\
                  .then_inc(self.nsem[0], 16)
                sp.wait_ge(self.nsem[0], 16)
        st.clear()


class Gates:

    def __init__(self, st):
        self.wg_f = st.sb("wg_f", [P, DC, NE])
        self.wg = [st.sb(f"wg{i}", [P, DC, NE], F32R) for i in range(2)]
        self.bias = st.sb("gate_bias", [P, NE])
        self.logit = st.sb("logit", [P, TT, NE])
        self.prob = st.sb("prob", [P, TT, NE])
        self.row = st.sb("gate_row", [P, 2, TT])
        self.top = st.sb("top", [P, TT, 8])
        self.index = st.sb("index", [P, TT, 8], U32)
        self.index_f = st.sb("index_f", [P, TT, 8])
        self.iota_i = st.sb("iota_i", [P, NE], I32)
        self.iota = st.sb("iota", [P, NE])
        self.hot = st.sb("hot", [P, 2, TT, NE])
        self.sems = [st.sem("g_" + n) for n in ("split", "logits", "step", "shifted", "exped", "iota")]

    def route(self, nc, st, m, zt, comb, bias, topk, renorm):
        split, logits, dstep, shifted, exped, iota_ok = self.sems
        with nc.Block(name=f"{st.name}_route") as block:
            @block.scalar
            def _(act):
                act.activation(self.wg[0][:, :, :], self.wg_f[:, :, :], ACT.Copy).then_inc(split, 1)
                act.wait_ge(shifted, 1)
                act.activation(self.prob[:, :, :], self.logit[:, :, :], ACT.Exp).then_inc(exped, 1)

            @block.gpsimd
            def _(pool):
                pool.iota(self.iota_i[:, :], pattern=[[1, NE]], base=0, channel_multiplier=0).then_inc(iota_ok, 1)

            @block.tensor
            def _(pe):
                pe.wait_ge(split, 2)
                for t in range(TT):
                    n = 0
                    for c in range(DC):
                        for s, v in ((0, 0), (0, 1), (1, 0)):
                            ins = pe.matmul(m.ps[:, 0, t * NE:(t + 1) * NE], zt[s][:, c, t * P:(t + 1) * P],
                                            self.wg[v][:, c, :], start=(n == 0), stop=(n == 3 * DC - 1))
                            n += 1
                ins.then_inc(logits, 1)

            @block.vector
            def _(dve):
                step = Step(dve, dstep)

                def each(a):
                    return a.unsqueeze(2).to_broadcast([P, TT, NE])

                dve.wait_ge(split, 1)
                dve.tensor_tensor(self.wg[1][:, :, :], self.wg_f[:, :, :], self.wg[0][:, :, :].bitcast(F32),
                                  ALU.subtract).then_inc(split, 1)
                dve.wait_ge(iota_ok, 1)
                step(dve.tensor_copy(self.iota[:, :], self.iota_i[:, :]))
                dve.wait_ge(logits, 1)
                ps = m.ps[:, 0, 0:TT * NE].rearrange("p (t e) -> p t e", e=NE)
                if bias:
                    step(dve.tensor_tensor(self.logit[:, :, :], ps,
                                           self.bias[:, :].unsqueeze(1).to_broadcast([P, TT, NE]), ALU.add))
                else:
                    step(dve.tensor_copy(self.logit[:, :, :], ps))
                step(dve.tensor_reduce(self.row[:, 0, :], self.logit[:, :, :], AX.X, ALU.max))
                dve.tensor_tensor(self.logit[:, :, :], self.logit[:, :, :], each(self.row[:, 0, :]),
                                  ALU.subtract).then_inc(shifted, 1)
                dve.wait_ge(exped, 1)
                step(dve.tensor_reduce(self.row[:, 0, :], self.prob[:, :, :], AX.X, ALU.add))
                step(dve.reciprocal(self.row[:, 1, :], self.row[:, 0, :]))
                step(dve.tensor_tensor(self.prob[:, :, :], self.prob[:, :, :], each(self.row[:, 1, :]), ALU.mult))
                for t in range(TT):
                    ins = dve.max(out=self.top[:, t, :], in_=self.prob[:, t, :])
                step(ins)
                for t in range(TT):
                    ins = dve.max_index(out=self.index[:, t, :], in_max=self.top[:, t, :],
                                        in_values=self.prob[:, t, :])
                step(ins)
                step(dve.tensor_copy(self.index_f[:, :, :], self.index[:, :, :]))
                if renorm:
                    step(dve.tensor_tensor(self.row[:, 0, :], self.top[:, :, 0], self.top[:, :, 1], ALU.add))
                    step(dve.reciprocal(self.row[:, 1, :], self.row[:, 0, :]))
                    step(dve.tensor_tensor(self.top[:, :, 0:2], self.top[:, :, 0:2],
                                           self.row[:, 1, :].unsqueeze(2).to_broadcast([P, TT, 2]), ALU.mult))
                for k in range(topk):
                    step(dve.tensor_tensor(self.hot[:, k, :, :],
                                           self.iota[:, :].unsqueeze(1).to_broadcast([P, TT, NE]),
                                           each(self.index_f[:, :, k]), ALU.is_equal))
                if comb is not None:
                    for k in range(topk):
                        step(dve.tensor_tensor(self.hot[:, k, :, :], self.hot[:, k, :, :],
                                               each(self.top[:, :, k]), ALU.mult))
                    step(dve.tensor_tensor(comb[:, :, 0:NE], self.hot[:, 0, :, :], self.hot[:, 1, :, :], ALU.add))
        st.clear()


def gelu_experts(nc, m, w):
    H = 512
    HC = H // P
    with Stage(nc, "f0") as st:
        f = FfnBase(st)
        gates = Gates(st)
        comb = st.sb("comb", [P, TT, NE])
        comb_t = st.sb("comb_t", [NE, TOK])
        b3 = st.sb("b3", [NE, D])
        comb_e = st.sb("comb_e", [P, TT])
        wf = st.sb("wf", [P, 2 * H + HC * H + HC * D])
        wr = [st.sb(f"wr{i}", [P, 2 * H + HC * H + HC * D], F32R) for i in range(2)]
        cuts = [0, DC * H, DC * H + HC * H, DC * H + HC * H + HC * D]
        bias = st.sb("bias", [P, 2 * HC])
        full = st.sb("full", [P, 3, HALF])
        h = [[st.sb(f"h{l}{i}", [P, HC, TOK], F32R) for i in range(2)] for l in range(2)]
        turned, copied, b3_ready, b3_done = [st.sem(n) for n in ("turned", "copied", "b3_ready", "b3_done")]
        w_in = [st.sem(f"w_in{i}") for i in range(3)]
        bias_in, w_hi, w_lo, comb_ok, h_ready, full_done, hi_done, lo_done, y_ready, y_done = [
            st.sem(n) for n in ("bias_in w_hi w_lo comb_ok h_ready full_done hi_done lo_done y_ready y_done").split()]
        f.norm(nc, st, m, [(flat2(gates.wg_f[:, :, :]), w["wg"]),
                           (gates.bias[:, :], w["bg"].partition_broadcast(P)), (b3[:, :], w["b3"])])
        gates.route(nc, st, m, f.zt, comb, True, 2, False)

        with nc.Block(name="f0_b3") as block:
            @block.tensor
            def _(pe):
                for t in range(TT):
                    ins = pe.transpose(m.ps[0:NE, t // 4, (t % 4) * P:(t % 4 + 1) * P], comb[:, t, :], m.ident[:, :])
                ins.then_inc(turned, 1)
                pe.wait_ge(copied, 1)
                for t in range(TT):
                    if t >= 4:
                        pe.wait_ge(b3_done, t - 3)
                    pe.matmul(m.ps[:, 4 + t % 4, 0:D], comb_t[:, t * P:(t + 1) * P], b3[:, :],
                              start=True, stop=True).then_inc(b3_ready, 1)

            @block.vector
            def _(dve):
                dve.wait_ge(turned, 1)
                dve.tensor_copy(comb_t[:, :], flat2(m.ps[0:NE, 0:2, :])).then_inc(copied, 1)
                for t in range(TT):
                    dve.wait_ge(b3_ready, t + 1)
                    dve.tensor_tensor(f.x[:, t, :], f.x[:, t, :], m.ps[:, 4 + t % 4, 0:D], ALU.add)\
                       .then_inc(b3_done, 1)
        st.clear()

        units = [(l, hf, o) for l in range(2) for hf in range(2) for o in range(HC)]

        def done_by(layer, hf):
            return (layer * 2 + hf + 1) * HC

        with nc.Fori(0, NE) as e:
            with nc.Block(name="f0_expert") as block:
                @block.sync
                def _(sp):
                    for i in range(3):
                        sp.dma_start(wf[:, cuts[i]:cuts[i + 1]], w[f"w{i + 1}"][bass.ds(e, 1), :, :]
                                     .rearrange("a p n -> p (a n)")).then_inc(w_in[i], 16)
                    sp.dma_start(bias[:, :], w["b12"][bass.ds(e, 1), :, :].rearrange("a p n -> p (a n)"))\
                      .then_inc(bias_in, 16)

                @block.tensor
                def _(pe):
                    def wpart(v, l, k, o, n):
                        at = cuts[l] + k * (D if l == 2 else H) + o
                        return wr[v][:, at:at + n]

                    for u, (l, hf, o) in enumerate(units):
                        pe.wait_ge(w_hi, l + 1)
                        pe.wait_ge(w_lo, l + 1)
                        if u >= 6:
                            pe.wait_ge(lo_done, u - 5)
                        if l == 1:
                            pe.wait_ge(lo_done, done_by(0, hf))
                        src = f.zt if l == 0 else h[0]
                        K = DC if l == 0 else HC
                        n = 0
                        for k in range(K):
                            for s, v in ((0, 0), (1, 0), (0, 1)):
                                ins = pe.matmul(m.ps[:, u % 6, :], wpart(v, l, k, o * P, P),
                                                src[s][:, k, hf * HALF:(hf + 1) * HALF],
                                                start=(n == 0), stop=(n == 3 * K - 1))
                                n += 1
                        ins.then_inc(h_ready, 1)
                    pe.wait_ge(w_hi, 3)
                    pe.wait_ge(w_lo, 3)
                    for t in range(TT):
                        pe.wait_ge(lo_done, done_by(1, t * P // HALF))
                        if t >= 2:
                            pe.wait_ge(y_done, t - 1)
                        n = 0
                        for k in range(HC):
                            for s, v in ((0, 0), (0, 1), (1, 0)):
                                ins = pe.matmul(m.ps[:, 6 + t % 2, 0:D], h[1][s][:, k, t * P:(t + 1) * P],
                                                wpart(v, 2, k, 0, D), start=(n == 0), stop=(n == 3 * HC - 1))
                                n += 1
                        ins.then_inc(y_ready, 1)

                @block.scalar
                def _(act):
                    for i in range(3):
                        act.wait_ge(w_in[i], 16)
                        act.activation(wr[0][:, cuts[i]:cuts[i + 1]], wf[:, cuts[i]:cuts[i + 1]], ACT.Copy)\
                           .then_inc(w_hi, 1)
                    act.wait_ge(bias_in, 16)
                    for u, (l, hf, o) in enumerate(units):
                        act.wait_ge(h_ready, u + 1)
                        if u >= 3:
                            act.wait_ge(lo_done, u - 2)
                        b = bias[:, l * HC + o:l * HC + o + 1]
                        act.activation(full[:, u % 3, :], m.ps[:, u % 6, :], ACT.Gelu, bias=b).then_inc(full_done, 1)
                        act.activation(h[l][0][:, o, hf * HALF:(hf + 1) * HALF], m.ps[:, u % 6, :], ACT.Gelu,
                                       bias=b).then_inc(hi_done, 1)

                @block.vector
                def _(dve):
                    dve.tensor_copy(comb_e[:, :], comb[:, :, bass.ds(e, 1)].rearrange("p t a -> p (t a)"))\
                       .then_inc(comb_ok, 1)
                    for i in range(3):
                        dve.wait_ge(w_hi, i + 1)
                        dve.tensor_tensor(wr[1][:, cuts[i]:cuts[i + 1]], wf[:, cuts[i]:cuts[i + 1]],
                                          wr[0][:, cuts[i]:cuts[i + 1]].bitcast(F32), ALU.subtract)\
                           .then_inc(w_lo, 1)
                    for u, (l, hf, o) in enumerate(units):
                        dve.wait_ge(hi_done, u + 1)
                        cols = slice(hf * HALF, (hf + 1) * HALF)
                        dve.tensor_tensor(h[l][1][:, o, cols], full[:, u % 3, :],
                                          h[l][0][:, o, cols].bitcast(F32), ALU.subtract).then_inc(lo_done, 1)
                    dve.wait_ge(comb_ok, 1)
                    for t in range(TT):
                        dve.wait_ge(y_ready, t + 1)
                        dve.scalar_tensor_tensor(out=f.x[:, t, :], in0=m.ps[:, 6 + t % 2, 0:D],
                                                 scalar=comb_e[:, t:t + 1], in1=f.x[:, t, :],
                                                 op0=ALU.mult, op1=ALU.add).then_inc(y_done, 1)
            st.clear()
        f.store(nc, st, m)


def scaled_linear(nc, m, w):
    with Stage(nc, "f1") as st:
        f = FfnBase(st)
        wf = st.sb("wf", [P, DC, D])
        wr = [st.sb(f"wr{i}", [P, DC, D], F32R) for i in range(2)]
        scale = st.sb("scale", [P, D])
        bias = st.sb("bias", [P, D])
        w_full, w_hi, w_lo, y_ready, y_done, dstep = [
            st.sem(n) for n in ("w_full", "w_hi", "w_lo", "y_ready", "y_done", "dstep")]
        f.norm(nc, st, m, [(flat2(wf[:, :, :]), w["w"]), (scale[:, :], w["scale"].partition_broadcast(P)),
                           (bias[:, :], w["bias"].partition_broadcast(P))])
        with nc.Block(name="f1_linear") as block:
            @block.vector
            def _(dve):
                dve.tensor_tensor(wf[:, :, :], wf[:, :, :], scale[:, :].unsqueeze(1).to_broadcast([P, DC, D]),
                                  ALU.mult).then_inc(w_full, 1)
                dve.wait_ge(w_hi, 1)
                dve.tensor_tensor(wr[1][:, :, :], wf[:, :, :], wr[0][:, :, :].bitcast(F32),
                                  ALU.subtract).then_inc(w_lo, 1)
                step = Step(dve, dstep)
                step(dve.tensor_tensor(f.x[:, :, :], f.x[:, :, :],
                                       bias[:, :].unsqueeze(1).to_broadcast([P, TT, D]), ALU.add))
                for t in range(TT):
                    dve.wait_ge(y_ready, t + 1)
                    dve.tensor_tensor(f.x[:, t, :], f.x[:, t, :], m.ps[:, t, 0:D], ALU.add).then_inc(y_done, 1)

            @block.scalar
            def _(act):
                act.wait_ge(w_full, 1)
                act.activation(wr[0][:, :, :], wf[:, :, :], ACT.Copy).then_inc(w_hi, 1)

            @block.tensor
            def _(pe):
                pe.wait_ge(w_lo, 1)
                for t in range(TT):
                    n = 0
                    for c in range(DC):
                        for s, v in ((0, 0), (0, 1), (1, 0)):
                            ins = pe.matmul(m.ps[:, t, 0:D], f.zt[s][:, c, t * P:(t + 1) * P], wr[v][:, c, :],
                                            start=(n == 0), stop=(n == 3 * DC - 1))
                            n += 1
                    ins.then_inc(y_ready, 1)
        st.clear()
        f.store(nc, st, m)


class GatedUnits:

    def __init__(self, st, per):
        self.per = per
        self.wf = st.sb("u_wf", [P, 2, (DC * 2 + 2) * P])
        self.wr = [st.sb(f"u_wr{i}", [P, 2, (DC * 2 + 2) * P], F32R) for i in range(2)]
        self.act = st.sb("u_act", [P, 2, HALF])
        self.full = st.sb("u_full", [P, 2, HALF])
        self.h = [st.sb(f"u_h{i}", [P, 2, TOK], F32R) for i in range(2)]
        self.weight = st.sb("u_weight", [P, per, TT])
        self.sems = [st.sem("u_" + n) for n in
                     "in0 in1 w_hi w_lo weight gu_ready silu_done full_done hi_done lo_done y_ready y_done".split()]

    def block(self, nc, m, f, src, weight, name, sizes):
        (in0, in1, w_hi, w_lo, weight_ok, gu_ready, silu_done, full_done, hi_done, lo_done, y_ready,
         y_done) = self.sems
        per, GU = self.per, DC * 2 * P
        halves = [(u, hf) for u in range(per) for hf in range(2)]
        with nc.Block(name=name) as block:
            @block.sync
            def _(sp):
                for u in range(per):
                    if u >= 2:
                        sp.wait_ge(w_hi, u - 1)
                        sp.wait_ge(w_lo, u - 1)
                    sp.dma_start(self.wf[:, u % 2, :], src(u)).then_inc((in0, in1)[u % 2], 16)

            @block.scalar
            def _(act):
                def split(u):
                    act.wait_ge((in0, in1)[u % 2], 16 * (u // 2 + 1))
                    if u >= 2:
                        act.wait_ge(y_ready, TT * (u - 1))
                    act.activation(self.wr[0][:, u % 2, :], self.wf[:, u % 2, :], ACT.Copy).then_inc(w_hi, 1)

                split(0)
                if per > 1:
                    split(1)
                for i, (u, hf) in enumerate(halves):
                    r = sizes[u]
                    bank = 2 * (i % 3)
                    act.wait_ge(gu_ready, i + 1)
                    if i >= 2:
                        act.wait_ge(full_done, i - 1)
                    act.activation(self.act[0:r, i % 2, :], m.ps[0:r, bank, :], ACT.Silu).then_inc(silu_done, 1)
                    act.wait_ge(full_done, i + 1)
                    if i >= 4:
                        act.wait_ge(y_ready, TT * (u - 1))
                    act.activation(self.h[0][0:r, u % 2, hf * HALF:(hf + 1) * HALF], self.full[0:r, i % 2, :],
                                   ACT.Copy).then_inc(hi_done, 1)
                    if hf and u + 1 < per and u >= 1:
                        split(u + 1)

            @block.vector
            def _(dve):
                if weight is not None:
                    dve.tensor_copy(self.weight[:, :, :], weight).then_inc(weight_ok, 1)

                def split(u):
                    dve.wait_ge(w_hi, u + 1)
                    dve.tensor_tensor(self.wr[1][:, u % 2, :], self.wf[:, u % 2, :],
                                      self.wr[0][:, u % 2, :].bitcast(F32), ALU.subtract).then_inc(w_lo, 1)

                def outputs(u):
                    for t in range(TT):
                        dve.wait_ge(y_ready, u * TT + t + 1)
                        y = m.ps[:, 6 + t % 2, 0:D]
                        if u and not t:
                            dve.wait_ge(y_done, u * TT)
                        if weight is None:
                            ins = dve.tensor_tensor(f.x[:, t, :], f.x[:, t, :], y, ALU.add)
                        else:
                            ins = dve.scalar_tensor_tensor(out=f.x[:, t, :], in0=y,
                                                           scalar=self.weight[:, u, t:t + 1],
                                                           in1=f.x[:, t, :], op0=ALU.mult, op1=ALU.add)
                        ins.then_inc(y_done, 1)

                split(0)
                if per > 1:
                    split(1)
                if weight is not None:
                    dve.wait_ge(weight_ok, 1)
                for i, (u, hf) in enumerate(halves):
                    r = sizes[u]
                    bank = 2 * (i % 3)
                    dve.wait_ge(silu_done, i + 1)
                    if i >= 2:
                        dve.wait_ge(lo_done, i - 1)
                        dve.wait_ge(hi_done, i - 1)
                    dve.tensor_tensor(self.full[0:r, i % 2, :], self.act[0:r, i % 2, :], m.ps[0:r, bank + 1, :],
                                      ALU.mult).then_inc(full_done, 1)
                    dve.wait_ge(hi_done, i + 1)
                    cols = slice(hf * HALF, (hf + 1) * HALF)
                    dve.tensor_tensor(self.h[1][0:r, u % 2, cols], self.full[0:r, i % 2, :],
                                      self.h[0][0:r, u % 2, cols].bitcast(F32), ALU.subtract).then_inc(lo_done, 1)
                    if hf and u >= 1:
                        outputs(u - 1)
                        if u + 1 < per:
                            split(u + 1)
                outputs(per - 1)

            @block.tensor
            def _(pe):
                def down(u):
                    pe.wait_ge(lo_done, 2 * u + 2)
                    r = sizes[u]
                    for t in range(TT):
                        if u * TT + t >= 2:
                            pe.wait_ge(y_done, u * TT + t - 1)
                        for n, (s, v) in enumerate(((0, 0), (0, 1), (1, 0))):
                            ins = pe.matmul(m.ps[:, 6 + t % 2, 0:D], self.h[s][0:r, u % 2, t * P:(t + 1) * P],
                                            self.wr[v][0:r, u % 2, GU:GU + D], start=(n == 0), stop=(n == 2))
                        ins.then_inc(y_ready, 1)

                for i, (u, hf) in enumerate(halves):
                    r = sizes[u]
                    bank = 2 * (i % 3)
                    pe.wait_ge(w_hi, u + 1)
                    pe.wait_ge(w_lo, u + 1)
                    if i >= 3:
                        pe.wait_ge(full_done, i - 2)
                    for part in range(2):
                        n = 0
                        for c in range(DC):
                            at = c * 2 * P + part * P
                            for s, v in ((0, 0), (1, 0), (0, 1)):
                                ins = pe.matmul(m.ps[0:r, bank + part, :], self.wr[v][:, u % 2, at:at + r],
                                                f.zt[s][:, c, hf * HALF:(hf + 1) * HALF],
                                                start=(n == 0), stop=(n == 3 * DC - 1))
                                n += 1
                    ins.then_inc(gu_ready, 1)
                    if hf and u:
                        down(u - 1)
                down(per - 1)


def silu_experts(nc, m, w):
    SHARED, PER = 4, 4
    with Stage(nc, "f3") as st:
        f = FfnBase(st)
        gates = Gates(st)
        comb = st.sb("comb", [P, TT, NE + SHARED])
        units = GatedUnits(st, PER)
        ones_ok = st.sem("ones_ok")
        f.norm(nc, st, m, [(flat2(gates.wg_f[:, :, :]), w["wg"])])
        with nc.Block(name="f3_ones") as block:
            @block.gpsimd
            def _(pool):
                pool.memset(comb[:, :, NE:], 1.0).then_inc(ones_ok, 1)
        gates.route(nc, st, m, f.zt, comb, False, 2, True)
        with nc.Fori(0, (NE + SHARED) // PER) as e:
            units.block(nc, m, f, lambda u: w["units"][bass.ds(e * PER + u, 1), :, :].rearrange("a p n -> p (a n)"),
                        comb[:, :, bass.ds(e * PER, PER)].rearrange("p t e -> p e t"), "f3_units", [P] * PER)
            st.clear()
        f.store(nc, st, m)


def capacity_experts(nc, m, w):
    C = TOK // NE
    H = 352
    SIZES = [min(P, H - a) for a in range(0, H, P)]
    HC = len(SIZES)
    DROPPED = 4.0 * TOK
    with Stage(nc, "f2") as st:
        f = FfnBase(st)
        gates = Gates(st)
        units = GatedUnits(st, HC)
        upper = st.sb("upper", [P, P])
        slot_i = st.sb("slot_i", [P, NE * C], I32)
        slot = st.sb("slot", [P, NE * C])
        row_i = st.sb("row_i", [P, NE], I32)
        row_f = st.sb("row_f", [P, NE])
        place = st.sb("place", [P, TT, NE])
        flat = st.sb("flat", [P, 3, TT])
        hot = st.sb("hot_slots", [P, 2, NE * C])
        wf = st.sb("wf", [P, 2 * DC * H + HC * D])
        xd = st.sb("xd", [P, DC, NE * C])
        xe = st.sb("xe", [P, DC, C])
        act_g = st.sb("act_g", [P, HC, C])
        hid = st.sb("hid", [P, HC, C])
        oe = st.sb("oe", [P, NE, D])
        oe_e = st.sb("oe_e", [P, D])
        flat_b = st.sb("flat_b", [P, TOK])
        taken = st.sb("taken", [P, 2, TOK])
        made, rstep, ranked, flat_ok, hot_ok, disp, xd_ok, fb_ready, fb_ok = [
            st.sem(n) for n in "made rstep ranked flat_ok hot_ok disp xd_ok fb_ready fb_ok".split()]
        w_in, xe_ok, g_ready, silu_ok, hid_ok, oe_ready, oe_ok = [
            st.sem(n) for n in "w_in xe_ok g_ready silu_ok hid_ok oe_ready oe_ok".split()]
        dt_ok, dt_used, y_done = [st.sem(n) for n in "dt_ok dt_used y_done".split()]
        f.norm(nc, st, m, [(flat2(gates.wg_f[:, :, :]), w["wg"])])
        gates.route(nc, st, m, f.zt, None, False, 1, False)
        first = gates.hot[:, 0, :, :]

        with nc.Block(name="f2_dispatch") as block:
            @block.gpsimd
            def _(pool):
                pool.memset(upper[:, :], 1.0).then_inc(made, 1)
                pool.wait_ge(made, 1)
                pool.affine_select(out=upper[:, :], in_=upper[:, :], compare_op=ALU.is_ge, fill=0.0, base=0,
                                   pattern=[[1, P]], channel_multiplier=-1).then_inc(made, 1)
                pool.iota(slot_i[:, :], pattern=[[1, NE * C]], base=0, channel_multiplier=0).then_inc(made, 1)
                pool.iota(row_i[:, :], pattern=[[C, NE]], base=0, channel_multiplier=1).then_inc(made, 1)

            @block.tensor
            def _(pe):
                pe.wait_ge(made, 2)
                for t in range(TT):
                    for k in range(t + 1):
                        ins = pe.matmul(m.ps[:, 0, t * NE:(t + 1) * NE], upper[:, :] if k == t else m.onesf[:, :],
                                        first[:, k, :], start=(k == 0), stop=(k == t))
                ins.then_inc(ranked, 1)
                pe.wait_ge(flat_ok, 1)
                for t in range(TT):
                    ins = pe.matmul(m.ps[:, 5 + t // 4, (t % 4) * P:(t % 4 + 1) * P],
                                    flat[:, 1, t:t + 1].to_broadcast([P, P]), m.ident[:, :], start=True, stop=True)
                ins.then_inc(fb_ready, 1)
                for t in range(TT):
                    pe.wait_ge(hot_ok, t + 1)
                    for c in range(DC):
                        for s in range(2):
                            ins = pe.matmul(m.ps[:, 1 + 2 * c + s, :], f.z[:, t, c * P:(c + 1) * P],
                                            hot[:, t % 2, s * 512:(s + 1) * 512],
                                            start=(t == 0), stop=(t == TT - 1))
                    ins.then_inc(disp, 1)

            @block.vector
            def _(dve):
                step = Step(dve, rstep)
                dve.wait_ge(made, 4)
                step(dve.tensor_copy(slot[:, :], slot_i[:, :]))
                step(dve.tensor_copy(row_f[:, :], row_i[:, :]))
                dve.wait_ge(ranked, 1)
                step(dve.tensor_tensor(place[:, :, :], m.ps[:, 0, 0:TT * NE].rearrange("p (t e) -> p t e", e=NE),
                                       first, ALU.mult))
                step(dve.tensor_reduce(flat[:, 0, :], place[:, :, :], AX.X, ALU.add))
                step(dve.tensor_scalar(flat[:, 2, :], flat[:, 0, :], float(C), DROPPED, ALU.is_gt, ALU.mult))
                step(dve.tensor_tensor(flat[:, 2, :], flat[:, 2, :], flat[:, 0, :], ALU.add))
                step(dve.tensor_scalar(flat[:, 1, :], gates.index_f[:, :, 0], float(C), -1.0, ALU.mult, ALU.add))
                dve.tensor_tensor(flat[:, 1, :], flat[:, 1, :], flat[:, 2, :], ALU.add).then_inc(flat_ok, 1)
                dve.wait_ge(flat_ok, 1)
                for t in range(TT):
                    if t >= 2:
                        dve.wait_ge(disp, t - 1)
                    dve.tensor_scalar(hot[:, t % 2, :], slot[:, :], flat[:, 1, t:t + 1], None, ALU.is_equal)\
                       .then_inc(hot_ok, 1)
                dve.wait_ge(fb_ready, 1)
                dve.tensor_copy(flat_b[:, :], flat2(m.ps[:, 5:7, :])).then_inc(fb_ok, 1)

            @block.scalar
            def _(act):
                act.wait_ge(disp, TT)
                for c in range(DC):
                    act.activation(xd[:, c, :], flat2(m.ps[:, 1 + 2 * c:3 + 2 * c, :]), ACT.Copy).then_inc(xd_ok, 1)
        st.clear()

        units.block(nc, m, f, lambda u: w["units"][u, :, :], None, "f2_shared", SIZES)
        st.clear()

        with nc.Fori(0, NE) as e:
            with nc.Block(name="f2_expert") as block:
                @block.sync
                def _(sp):
                    sp.dma_start(wf[:, :], w["experts"][bass.ds(e, 1), :, :].rearrange("a p n -> p (a n)"))\
                      .then_inc(w_in, 16)

                @block.tensor
                def _(pe):
                    pe.wait_ge(w_in, 16)
                    pe.wait_ge(xe_ok, 1)
                    for part in range(2):
                        for o, r in enumerate(SIZES):
                            for c in range(DC):
                                at = (part * DC + c) * H + o * P
                                ins = pe.matmul(m.ps[0:r, part, o * P:o * P + C], wf[:, at:at + r], xe[:, c, :],
                                                start=(c == 0), stop=(c == DC - 1))
                            if o == HC - 1:
                                ins.then_inc(g_ready, 1)
                    for o, r in enumerate(SIZES):
                        pe.wait_ge(hid_ok, o + 1)
                        at = 2 * DC * H + o * D
                        ins = pe.matmul(m.ps[:, 2, 0:D], hid[0:r, o, :], wf[0:r, at:at + D],
                                        start=(o == 0), stop=(o == HC - 1))
                    ins.then_inc(oe_ready, 1)

                @block.scalar
                def _(act):
                    act.wait_ge(g_ready, 1)
                    for o, r in enumerate(SIZES):
                        act.activation(act_g[0:r, o, :], m.ps[0:r, 0, o * P:o * P + C], ACT.Silu).then_inc(silu_ok, 1)

                @block.vector
                def _(dve):
                    dve.tensor_copy(xe[:, :, :], xd[:, :, bass.ds(e * C, C)]).then_inc(xe_ok, 1)
                    dve.wait_ge(g_ready, 2)
                    for o, r in enumerate(SIZES):
                        dve.wait_ge(silu_ok, o + 1)
                        dve.tensor_tensor(hid[0:r, o, :], act_g[0:r, o, :], m.ps[0:r, 1, o * P:o * P + C],
                                          ALU.mult).then_inc(hid_ok, 1)
                    dve.wait_ge(oe_ready, 1)
                    dve.tensor_copy(oe[:, bass.ds(e, 1), :].rearrange("p a d -> p (a d)"), m.ps[:, 2, 0:D])\
                       .then_inc(oe_ok, 1)
            st.clear()

        with nc.Block(name="f2_combine") as block:
            @block.vector
            def _(dve):
                for e in range(NE):
                    if e >= 2:
                        dve.wait_ge(dt_used, e - 1)
                    dve.tensor_scalar(taken[:, e % 2, :], flat_b[:, :], row_f[:, e:e + 1], None, ALU.is_equal)\
                       .then_inc(dt_ok, 1)
                for t in range(TT):
                    dve.wait_ge(dt_used, NE)
                    dve.scalar_tensor_tensor(out=f.x[:, t, :], in0=m.ps[:, t, 0:D], scalar=gates.top[:, t, 0:1],
                                             in1=f.x[:, t, :], op0=ALU.mult, op1=ALU.add).then_inc(y_done, 1)

            @block.tensor
            def _(pe):
                for e in range(NE):
                    pe.wait_ge(dt_ok, e + 1)
                    for t in range(TT):
                        ins = pe.matmul(m.ps[:, t, 0:D], taken[:, e % 2, t * P:(t + 1) * P], oe[:, e, :],
                                        start=(e == 0), stop=(e == NE - 1))
                    ins.then_inc(dt_used, 1)
        st.clear()
        f.store(nc, st, m)
def image_text_attention(nc, m, w):
    NH, HDS = 16, 16
    IMG = 257
    LEAST = 65
    K_HI, K_LO, NEG = 0, 2 * HDS, 3 * HDS
    STK = 64
    GRP_AT = (0, IMG)
    tiles = ([(a, min(P, IMG - a), 0) for a in range(0, IMG, P)]
             + [(a, min(P, CTX - a), 1) for a in range(IMG, CTX, P)])
    KT = len(tiles)
    FIRST = (0, next(i for i, t in enumerate(tiles) if t[2]))
    LAST = (FIRST[1] - 1, KT - 1)
    NKEY = (IMG, CTX - IMG)
    VW2 = HDS + 1
    HP = NH // 2
    SCALE = HDS ** -0.5
    with Stage(nc, "a2") as st:
        x_b = st.sb("x_b", [P, QT, D])
        zt = [st.sb(f"zt{i}", [P, DC, S], F32R) for i in range(2)]
        ct = [st.sb(f"ct{i}", [P, DC, CTXP], F32R) for i in range(2)]
        scratch = (st.sb("stats", [P, QT, 6]), st.sb("mv", [P, QT, 2]), st.sb("rstd", [P, 2, QT]),
                   st.sb("z", [P, QT, D]))
        wide = [DC * 2 * D, DC * 2 * D, DC * D, DC * D]
        wr = [[st.sb(f"wr{k}{i}", [P, n], F32R) for i in range(2)] for k, n in enumerate(wide)]
        kv_bias = st.sb("kv_bias", [P, 2, 2 * D])
        qo_bias = st.sb("qo_bias", [P, 2, D])
        norm_w = st.sb("norm_w", [P, 3, D])
        k_rows = st.sb("k_rows", [P, KT, D])
        v_rows = st.sb("v_rows", [P, KT, NH, VW2])
        sq = st.sb("sq", [P, 3, KT + QT])
        square = st.sb("square", [P, 2, D])
        k_st = [[st.sb(f"k_st{g}{i}", [P, NH, STK], F32R) for i in range(2)] for g in range(2)]
        kt = st.sb("kt", [P, HP, KT * P], F32R)
        q_rows = st.sb("q_rows", [P, QT, D])
        q_st = st.sb("q_st", [P, QT, NH, STK], F32R)
        qt_a = st.sb("qt_a", [P, HP, S], F32R)
        qt_b = st.sb("qt_b", [P, 2, S], F32R)
        probs = st.sb("probs", [P, 3, 512])
        rs = st.sb("rs", [P, 2, 4])
        o_n = st.sb("o_n", [P, 2, 4, HDS])
        o_rows = st.sb("o_rows", [P, QT, D])
        nsem = [st.sem("n_" + n) for n in ("loaded", "step", "var", "rstd", "turned", "hi", "lo")]
        w_in = [st.sem(f"w_in{i}") for i in range(4)]
        w_hi, w_lo, small_in, zeroed, dstep, pstep = [st.sem(n) for n in "w_hi w_lo small_in zeroed dstep pstep".split()]
        (kv_ready, kb_done, sq_done, rstd_ok, kn_done, hi_done, lo_done, turned, ev_a, ev_b) = [
            st.sem(n) for n in "kv_ready kb_done sq_done rstd_ok kn_done hi_done lo_done turned ev_a ev_b".split()]
        (s_ready, neg_done, qb_turned, qb_done, st_ready, exp_done, pv_done, o_done) = [
            st.sem(n) for n in "s_ready neg_done qb_turned qb_done st_ready exp_done pv_done o_done".split()]

        wf = k_rows[:, :, :].rearrange("p t d -> p (t d)")
        at = [sum(wide[:k]) for k in range(5)]
        names = ("wkv_img", "wkv_txt", "wq", "wo")
        for lot in ((0, 1), (2, 3)):
            base = at[lot[0]]
            split_weights(nc, st, f"a2_weights{lot[0]}",
                          [(wf[:, at[k] - base:at[k + 1] - base], (wr[k][0][:, :], wr[k][1][:, :]), w[names[k]])
                           for k in lot], w_in[0:2], w_hi, w_lo)
        with nc.Block(name="a2_once") as block:
            @block.sync
            def _(sp):
                for dst, n in ((kv_bias[:, 0, 0:D], "k_img_b"), (kv_bias[:, 0, D:], "v_img_b"),
                               (kv_bias[:, 1, 0:D], "k_b"), (kv_bias[:, 1, D:], "v_b"),
                               (qo_bias[:, 0, :], "q_b"), (qo_bias[:, 1, :], "o_b"),
                               (norm_w[:, 0, :], "norm_k_img_w"), (norm_w[:, 1, :], "norm_k_w"),
                               (norm_w[:, 2, :], "norm_q_w")):
                    sp.dma_start(dst, w[n].partition_broadcast(P)).then_inc(small_in, 16)
                sp.wait_ge(small_in, 144)

            @block.gpsimd
            def _(pool):
                pool.memset(v_rows[:, :, :, :], 0.0).then_inc(zeroed, 1)
                pool.wait_ge(zeroed, 1)
                for t, (_a, r, _g) in enumerate(tiles):
                    pool.memset(v_rows[0:r, t, :, HDS:VW2], 1.0).then_inc(zeroed, 1)
                n = 1 + KT
                pool.memset(sq[:, :, :], 1.0).then_inc(zeroed, 1)
                pool.memset(q_st[:, :, :, :].bitcast(F32), 0.0).then_inc(zeroed, 1)
                for g in range(2):
                    for i in range(2):
                        pool.memset(k_st[g][i][:, :, :].bitcast(F32), 0.0).then_inc(zeroed, 1)
                pool.wait_ge(zeroed, n + 6)
                for g in range(2):
                    for i in range(2):
                        pool.memset(k_st[g][i][:, :, NEG + g:NEG + g + 1].bitcast(F32), 1.0).then_inc(zeroed, 1)
        st.clear()

        with nc.Fori(0, B) as b:
            x_rows = m.x_dram[bass.ds(b * QT, QT), :].rearrange("t (p d) -> p t d", p=P)
            norm_block(nc, st, m, x_b, zt[0], zt[1], QT, x_rows, nsem, scratch, [
                (flat2(ct[0][:, :, :]).bitcast(F32), m.ctx_hi[bass.ds(b, 1), :, :].rearrange("a p n -> p (a n)")),
                (flat2(ct[1][:, :, :]).bitcast(F32), m.ctx_lo[bass.ds(b, 1), :, :].rearrange("a p n -> p (a n)")),
            ], name="a2_norm")
            st.clear()

            with nc.Block(name="a2_keys") as block:
                @block.tensor
                def _(pe):
                    for t, (a, r, g) in enumerate(tiles):
                        M = max(r, LEAST)
                        if t >= 8:
                            pe.wait_ge(kb_done, t - 7)
                        n = 0
                        for c in range(DC):
                            for s, v in HALVES:
                                ins = pe.matmul(m.ps[0:M, t % 8, :], ct[s][:, c, a:a + M],
                                                wr[g][v][:, c * 2 * D:(c + 1) * 2 * D],
                                                start=(n == 0), stop=(n == 3 * DC - 1))
                                n += 1
                        ins.then_inc(kv_ready, 1)
                    pe.wait_ge(kb_done, KT)
                    for t in range(KT):
                        g, i = tiles[t][2], (t - FIRST[tiles[t][2]]) % 2
                        pe.wait_ge(lo_done, t + 1)
                        if t >= 4:
                            pe.wait_ge(ev_a, t - 3)
                            pe.wait_ge(ev_b, t - 3)
                        for hp in range(HP):
                            ins = pe.transpose(m.ps[:, 2 * (t % 4) + hp // 4, (hp % 4) * P:(hp % 4 + 1) * P]
                                               .bitcast(F32R), k_st[g][i][:, 2 * hp:2 * hp + 2, :]
                                               .rearrange("p a n -> p (a n)"), m.ident_r[:, :])
                        ins.then_inc(turned, 1)

                def evacuate(eng, t, half, done):
                    eng.wait_ge(turned, t + 1)
                    dst = kt[:, 4 * half:4 * half + 4, t * P:(t + 1) * P]
                    src = m.ps[:, 2 * (t % 4) + half, :].rearrange("p (h n) -> p h n", n=P)
                    return dst, src

                @block.scalar
                def _(act):
                    for t, (_a, r, g) in enumerate(tiles):
                        act.wait_ge(kb_done, t + 1)
                        if t >= 2:
                            act.wait_ge(sq_done, t - 1)
                        act.activation(square[0:r, t % 2, :], k_rows[0:r, t, :], ACT.Square,
                                       accum_out=sq[0:r, 0, t:t + 1]).then_inc(sq_done, 1)
                    for t in range(KT + 1):
                        if t < KT:
                            _a, r, g = tiles[t]
                            i = (t - FIRST[g]) % 2
                            act.wait_ge(kn_done, t + 1)
                            if t - 2 >= FIRST[g]:
                                act.wait_ge(turned, t - 1)
                            act.activation(k_st[g][i][0:r, :, 0:2 * HDS].rearrange("p h (a d) -> p h a d", a=2),
                                           k_rows[0:r, t, :].rearrange("p (h d) -> p h d", h=NH)
                                           .unsqueeze(2).to_broadcast([r, NH, 2, HDS]), ACT.Copy).then_inc(hi_done, 1)
                        if t:
                            dst, src = evacuate(act, t - 1, 0, ev_a)
                            act.activation(dst, src, ACT.Copy).then_inc(ev_a, 1)

                @block.gpsimd
                def _(pool):
                    step = Step(pool, pstep)
                    pool.wait_ge(sq_done, KT)
                    step(pool.tensor_scalar(sq[:, 1, 0:KT], sq[:, 0, 0:KT], 1.0 / D, 1e-6, ALU.mult, ALU.add))
                    pool.tensor_tensor(sq[:, 2, 0:KT], sq[:, 1, 0:KT], m.nhalf[:, 0:1].to_broadcast([P, KT]),
                                       ALU.pow).then_inc(rstd_ok, 1)

                @block.vector
                def _(dve):
                    for t, (_a, r, g) in enumerate(tiles):
                        dve.wait_ge(kv_ready, t + 1)
                        dve.tensor_tensor(v_rows[0:r, t, :, 0:HDS],
                                          m.ps[0:r, t % 8, D:].rearrange("p (h d) -> p h d", h=NH),
                                          kv_bias[0:r, g, D:].rearrange("p (h d) -> p h d", h=NH), ALU.add)
                        dve.tensor_tensor(k_rows[0:r, t, :], m.ps[0:r, t % 8, 0:D], kv_bias[0:r, g, 0:D],
                                          ALU.add).then_inc(kb_done, 1)
                    dve.wait_ge(rstd_ok, 1)
                    for t in range(KT + 1):
                        if t < KT:
                            _a, r, g = tiles[t]
                            i = (t - FIRST[g]) % 2
                            dve.scalar_tensor_tensor(out=k_rows[0:r, t, :], in0=k_rows[0:r, t, :],
                                                     scalar=sq[0:r, 2, t:t + 1], in1=norm_w[0:r, g, :],
                                                     op0=ALU.mult, op1=ALU.mult).then_inc(kn_done, 1)
                        if t:
                            dst, src = evacuate(dve, t - 1, 1, ev_b)
                            dve.tensor_copy(dst, src).then_inc(ev_b, 1)
                        if t < KT:
                            dve.wait_ge(hi_done, t + 1)
                            dve.tensor_tensor(k_st[g][i][0:r, :, K_LO:K_LO + HDS],
                                              k_rows[0:r, t, :].rearrange("p (h d) -> p h d", h=NH),
                                              k_st[g][i][0:r, :, K_HI:K_HI + HDS].bitcast(F32),
                                              ALU.subtract).then_inc(lo_done, 1)
            st.clear()

            with nc.Block(name="a2_queries") as block:
                @block.tensor
                def _(pe):
                    for q in range(QT):
                        n = 0
                        for c in range(DC):
                            for s, v in HALVES:
                                ins = pe.matmul(m.ps[:, q, 0:D], zt[s][:, c, q * P:(q + 1) * P],
                                                wr[2][v][:, c * D:(c + 1) * D], start=(n == 0), stop=(n == 3 * DC - 1))
                                n += 1
                        ins.then_inc(kv_ready, 1)
                    pe.wait_ge(lo_done, QT)
                    for hp in range(HP):
                        for q in range(QT):
                            at_ = (hp % 2) * S + q * P
                            ins = pe.transpose(m.ps[:, 2 + hp // 2, at_:at_ + P].bitcast(F32R),
                                               q_st[:, q, 2 * hp:2 * hp + 2, :].rearrange("p a n -> p (a n)"),
                                               m.ident_r[:, :])
                        if hp % 2:
                            ins.then_inc(turned, 1)

                @block.scalar
                def _(act):
                    for q in range(QT):
                        act.wait_ge(kb_done, q + 1)
                        act.activation(square[:, q, :], q_rows[:, q, :], ACT.Square,
                                       accum_out=sq[:, 0, KT + q:KT + q + 1]).then_inc(sq_done, 1)
                    for q in range(QT):
                        act.wait_ge(kn_done, q + 1)
                        rows = q_rows[:, q, :].rearrange("p (h d) -> p h d", h=NH)
                        act.activation(q_st[:, q, :, 0:HDS], rows, ACT.Copy)
                        act.activation(q_st[:, q, :, 2 * HDS:3 * HDS], rows, ACT.Copy).then_inc(hi_done, 1)
                    for k in range(HP // 2):
                        act.wait_ge(turned, k + 1)
                        act.activation(flat2(qt_a[:, 2 * k:2 * k + 2, :]), m.ps[:, 2 + k, :], ACT.Copy)\
                           .then_inc(ev_a, 1)

                @block.gpsimd
                def _(pool):
                    step = Step(pool, pstep)
                    pool.wait_ge(sq_done, QT)
                    step(pool.tensor_scalar(sq[:, 1, KT:], sq[:, 0, KT:], 1.0 / D, 1e-6, ALU.mult, ALU.add))
                    step(pool.tensor_tensor(sq[:, 2, KT:], sq[:, 1, KT:], m.nhalf[:, 0:1].to_broadcast([P, QT]),
                                            ALU.pow))
                    pool.tensor_scalar(sq[:, 2, KT:], sq[:, 2, KT:], SCALE, None, ALU.mult).then_inc(rstd_ok, 1)

                @block.vector
                def _(dve):
                    for q in range(QT):
                        dve.wait_ge(kv_ready, q + 1)
                        dve.tensor_tensor(q_rows[:, q, :], m.ps[:, q, 0:D], qo_bias[:, 0, :], ALU.add)\
                           .then_inc(kb_done, 1)
                    dve.wait_ge(kb_done, QT)
                    dve.wait_ge(rstd_ok, 1)
                    for q in range(QT):
                        dve.scalar_tensor_tensor(out=q_rows[:, q, :], in0=q_rows[:, q, :],
                                                 scalar=sq[:, 2, KT + q:KT + q + 1], in1=norm_w[:, 2, :],
                                                 op0=ALU.mult, op1=ALU.mult).then_inc(kn_done, 1)
                    for q in range(QT):
                        dve.wait_ge(hi_done, q + 1)
                        dve.tensor_tensor(q_st[:, q, :, HDS:2 * HDS],
                                          q_rows[:, q, :].rearrange("p (h d) -> p h d", h=NH),
                                          q_st[:, q, :, 0:HDS].bitcast(F32), ALU.subtract).then_inc(lo_done, 1)
            st.clear()

            PAIRS = KT // 2
            TURNS = NH * PAIRS
            with nc.Block(name="a2_attend") as block:
                @block.tensor
                def _(pe):
                    def rough_scores(i):
                        h, q = divmod(i, QT)
                        lo_p = STK * (h % 2)
                        pe.wait_ge(neg_done, i) if i else None
                        if h % 2 == 0 and q == 0 and h:
                            pe.wait_ge(qb_done, h // 2)
                        lhs = qt_a[lo_p:lo_p + HDS, h // 2, q * P:(q + 1) * P]
                        img = NKEY[0] + NKEY[0] % 2
                        pe.matmul(m.ps[:, 0, 0:img], lhs, kt[lo_p:lo_p + HDS, h // 2, 0:img], start=True, stop=True)
                        a0 = FIRST[1] * P
                        for k, a in enumerate(range(0, NKEY[1], 512)):
                            e = min(a + 512, NKEY[1])
                            ins = pe.matmul(m.ps[:, 1 + k, 0:e - a], lhs, kt[lo_p:lo_p + HDS, h // 2, a0 + a:a0 + e],
                                            start=True, stop=True)
                        ins.then_inc(s_ready, 1)

                    def turn_queries(hp):
                        pe.wait_ge(neg_done, 4 * (hp + 1))
                        if hp >= 2:
                            pe.wait_ge(st_ready, (2 * hp - 2) * PAIRS)
                        for q in range(QT):
                            ins = pe.transpose(m.ps[:, 0, q * P:(q + 1) * P].bitcast(F32R),
                                               q_st[:, q, 2 * hp:2 * hp + 2, :].rearrange("p a n -> p (a n)"),
                                               m.ident_r[:, :])
                        ins.then_inc(qb_turned, 1)

                    def scores(n):
                        h, k2 = divmod(n, PAIRS)
                        lo_p = STK * (h % 2)
                        if k2 == 0 and h % 2 == 0:
                            pe.wait_ge(qb_done, h // 2 + 1)
                        if n >= 2:
                            pe.wait_ge(exp_done, n - 1)
                        for i in range(2):
                            t = 2 * k2 + i
                            ins = pe.matmul(m.ps[:, 4 + n % 2, i * S:(i + 1) * S],
                                            kt[lo_p:lo_p + STK, h // 2, t * P:(t + 1) * P],
                                            qt_b[lo_p:lo_p + STK, (h // 2) % 2, :], start=True, stop=True)
                        ins.then_inc(st_ready, 1)

                    def values(n):
                        h, k2 = divmod(n, PAIRS)
                        pe.wait_ge(exp_done, n + 1)
                        if k2 == 0 and h >= 2:
                            pe.wait_ge(o_done, h - 1)
                        for i in range(2):
                            t = 2 * k2 + i
                            g = tiles[t][2]
                            for q in range(QT):
                                at_ = (2 * q + g) * 32
                                ins = pe.matmul(m.ps[:, 6 + h % 2, at_:at_ + VW2],
                                                probs[:, n % 3, i * S + q * P:i * S + (q + 1) * P],
                                                v_rows[:, t, h, :], start=(t == 0 and q == 0), stop=(t == LAST[g]),
                                                skip_group_check=True)
                        ins.then_inc(pv_done, 1)

                    for i in range(4):
                        rough_scores(i)
                    turn_queries(0)
                    for n in range(TURNS):
                        scores(n)
                        hp, r = divmod(n, 2 * PAIRS)
                        if n:
                            values(n - 1)
                        if hp + 1 < HP and r % 3 == 0 and r // 3 < 4:
                            rough_scores(4 * (hp + 1) + r // 3)
                        if hp + 1 < HP and r == 2 * PAIRS - 1:
                            turn_queries(hp + 1)
                    values(TURNS - 1)

                @block.scalar
                def _(act):
                    def take_queries(hp):
                        act.wait_ge(qb_turned, hp + 1)
                        act.activation(qt_b[:, hp % 2, :], m.ps[:, 0, 0:S], ACT.Copy).then_inc(qb_done, 1)

                    take_queries(0)
                    for n in range(TURNS):
                        act.wait_ge(st_ready, n + 1)
                        if n >= 3:
                            act.wait_ge(pv_done, n - 2)
                        act.activation(probs[:, n % 3, :], m.ps[:, 4 + n % 2, :], ACT.Exp).then_inc(exp_done, 1)
                        hp, r = divmod(n, 2 * PAIRS)
                        if hp + 1 < HP and r == 2 * PAIRS - 1:
                            take_queries(hp + 1)

                @block.vector
                def _(dve):
                    step = Step(dve, dstep)

                    def maxima(i):
                        h, q = divmod(i, QT)
                        dve.wait_ge(s_ready, i + 1)
                        dve.tensor_reduce(q_st[:, q, h, NEG:NEG + 1], m.ps[:, 0, 0:NKEY[0]], AX.X, ALU.max,
                                          negate=True)
                        dve.tensor_reduce(q_st[:, q, h, NEG + 1:NEG + 2], m.ps[:, 1:4, :]
                                          .rearrange("p b n -> p (b n)")[:, 0:NKEY[1]], AX.X, ALU.max,
                                          negate=True).then_inc(neg_done, 1)

                    def outputs(h):
                        dve.wait_ge(pv_done, PAIRS * (h + 1))
                        o = m.ps[:, 6 + h % 2, 0:128].rearrange("p (i n) -> p i n", i=4)
                        step(dve.reciprocal(rs[:, h % 2, :].unsqueeze(2), o[:, :, HDS:VW2]))
                        dve.tensor_tensor(o_n[:, h % 2, :, :], o[:, :, 0:HDS],
                                          rs[:, h % 2, :].unsqueeze(2).to_broadcast([P, 4, HDS]), ALU.mult)\
                           .then_inc(o_done, 1)
                        dve.wait_ge(o_done, h + 1)
                        on = o_n[:, h % 2, :, :].rearrange("p (q g) d -> p q g d", g=2)
                        step(dve.tensor_tensor(o_rows[:, :, h * HDS:(h + 1) * HDS], on[:, :, 0, :], on[:, :, 1, :],
                                               ALU.add))

                    for i in range(4):
                        maxima(i)
                    for hp in range(HP):
                        if hp:
                            outputs(2 * hp - 1)
                        if hp + 1 < HP:
                            for i in range(4):
                                maxima(4 * (hp + 1) + i)
                        outputs(2 * hp)
                    outputs(NH - 1)
            st.clear()

            with nc.Block(name="a2_project") as block:
                @block.tensor
                def _(pe):
                    for c in range(DC):
                        for q in range(QT):
                            ins = pe.transpose(m.ps[:, 0, c * S + q * P:c * S + (q + 1) * P],
                                               o_rows[:, q, c * P:(c + 1) * P], m.ident[:, :])
                    ins.then_inc(turned, 1)
                    pe.wait_ge(lo_done, 1)
                    for q in range(QT):
                        n = 0
                        for c in range(DC):
                            for s, v in HALVES:
                                ins = pe.matmul(m.ps[:, 1 + q, 0:D], zt[s][:, c, q * P:(q + 1) * P],
                                                wr[3][v][:, c * D:(c + 1) * D], start=(n == 0), stop=(n == 3 * DC - 1))
                                n += 1
                        ins.then_inc(kv_ready, 1)

                @block.scalar
                def _(act):
                    act.wait_ge(turned, 1)
                    act.activation(flat2(zt[0][:, :, :]), m.ps[:, 0, :], ACT.Copy).then_inc(hi_done, 1)

                @block.vector
                def _(dve):
                    dve.tensor_tensor(x_b[:, :, :], x_b[:, :, :], qo_bias[:, 1, :].unsqueeze(1)
                                      .to_broadcast([P, QT, D]), ALU.add).then_inc(dstep, 1)
                    dve.wait_ge(hi_done, 1)
                    dve.tensor_tensor(flat2(zt[1][:, :, :]), m.ps[:, 0, :], flat2(zt[0][:, :, :]).bitcast(F32),
                                      ALU.subtract).then_inc(lo_done, 1)
                    dve.wait_ge(dstep, 1)
                    for q in range(QT):
                        dve.wait_ge(kv_ready, q + 1)
                        dve.tensor_tensor(x_b[:, q, :], x_b[:, q, :], m.ps[:, 1 + q, 0:D], ALU.add)\
                           .then_inc(dstep, 1)
                @block.sync
                def _(sp):
                    sp.wait_ge(dstep, 1 + QT)
                    sp.dma_start(x_rows, x_b[:, :, :]).then_inc(small_in, 16)
                    sp.wait_ge(small_in, 16)
            st.clear()


def chunked(w, groups):
    w = np.asarray(w)
    k, n = w.shape
    return w.reshape(k // P, P, groups, n // groups).transpose(2, 1, 0, 3).reshape(groups, P, -1)


def lay_gqa(wq, wk, wv, wo, qw, kw, name):
    kv = np.stack([np.asarray(wk).reshape(D, KVH, HD), np.asarray(wv).reshape(D, KVH, HD)], axis=2)
    return {
        f"{name}_wq": chunked(wq, KVH),
        f"{name}_wkv": chunked(kv.reshape(D, -1), KVH),
        f"{name}_wo": np.asarray(wo).reshape(KVH, REP, P, D).transpose(0, 2, 1, 3).reshape(KVH, P, -1),
        f"{name}_qw": np.asarray(qw), f"{name}_kw": np.asarray(kw),
    }


def by_partition(w):
    w = np.asarray(w)
    *lead, k, n = w.shape
    return np.moveaxis(w.reshape(*lead, k // P, P, n), -2, -3).reshape(*lead, P, -1)


def lay_units(gate, up, down):
    gate, up, down = (np.asarray(a) for a in (gate, up, down))
    n = -(-gate.shape[1] // P)
    out = np.zeros((n, P, 3 * 2 * P), np.float32)
    for u in range(n):
        a, e = u * P, min((u + 1) * P, gate.shape[1])
        for c in range(DC):
            out[u, :, c * 2 * P:c * 2 * P + e - a] = gate[c * P:(c + 1) * P, a:e]
            out[u, :, c * 2 * P + P:c * 2 * P + P + e - a] = up[c * P:(c + 1) * P, a:e]
        out[u, 0:e - a, 4 * P:] = down[a:e]
    return out


def lay_ffn(i):
    out = {"f0_w1": by_partition(i["L0_ffn_W1"]), "f0_w2": by_partition(i["L0_ffn_W2"]),
           "f0_w3": by_partition(i["L0_ffn_W3"]), "f0_b3": i["L0_ffn_b3"],
           "f0_wg": by_partition(i["L0_ffn_Wg"]), "f0_bg": i["L0_ffn_bg"]}
    b12 = np.stack([np.asarray(i["L0_ffn_b1"]), np.asarray(i["L0_ffn_b2"])], axis=1)
    out["f0_b12"] = b12.reshape(NE, 2, -1, P).transpose(0, 3, 1, 2).reshape(NE, P, -1)
    out |= {"f1_w": by_partition(i["L1_ffn_weight"].T), "f1_scale": i["L1_ffn_scale_weight"],
            "f1_bias": i["L1_ffn_bias"]}
    out["f2_wg"] = by_partition(i["L2_ffn_Wg"])
    out["f2_units"] = lay_units(i["L2_ffn_sw1"], i["L2_ffn_sw3"], i["L2_ffn_sw2"])
    w2 = np.asarray(i["L2_ffn_W2"])
    down = np.zeros((NE, 3 * P, D), np.float32)
    down[:, 0:w2.shape[1]] = w2
    out["f2_experts"] = np.concatenate([by_partition(i["L2_ffn_W1"]), by_partition(i["L2_ffn_W3"]),
                                        by_partition(down)], axis=2)
    out["f3_wg"] = by_partition(i["L3_ffn_w_gate"])
    gu, dn = np.asarray(i["L3_ffn_w_gate_up"]), np.asarray(i["L3_ffn_w_down"])
    sgu, sdn = np.asarray(i["L3_ffn_w_sh_gate_up"]), np.asarray(i["L3_ffn_w_sh_down"])
    I = sgu.shape[1] // 2
    out["f3_units"] = np.concatenate([lay_units(gu[e, :, 0:P], gu[e, :, P:], dn[e]) for e in range(NE)]
                                     + [lay_units(sgu[:, 0:I], sgu[:, I:], sdn)])
    return out


def lay_memory(i):
    wqkv = np.asarray(i["L0_xattn_W_qkv"])
    out = {"a0_wq": by_partition(wqkv[0:D].T), "a0_wo": by_partition(np.asarray(i["L0_xattn_W_o"]).T)}
    for n in ("gate", "log_tau", "beta_q", "beta_k"):
        out[f"a0_{n}"] = np.asarray(i[f"L0_xattn_{n}"]).reshape(1)
    return out


def lay_image_text(i):
    def t(n):
        return np.asarray(i[f"L2_xattn_{n}"]).T
    out = {"a2_wkv_img": by_partition(np.concatenate([t("k_img_w"), t("v_img_w")], axis=1)),
           "a2_wkv_txt": by_partition(np.concatenate([t("k_w"), t("v_w")], axis=1)),
           "a2_wq": by_partition(t("q_w")), "a2_wo": by_partition(t("o_w"))}
    for n in "q_b k_b v_b k_img_b v_img_b o_b norm_q_w norm_k_w norm_k_img_w".split():
        out[f"a2_{n}"] = i[f"L2_xattn_{n}"]
    return out


def lay_out(i):
    out = {"x": i["x"], "ctx": i["ctx_2048"], "pos": i["pos_BxS2"], "tok": i["itok_BxS_4096_4607"],
           "inv_freq": (1.0 / 10000.0 ** (np.arange(0, HD, 2, dtype=np.float64) / HD)).astype(np.float32)}
    out |= lay_memory(i) | lay_image_text(i) | lay_ffn(i)
    out |= lay_gqa(i["L1_xattn_Wq"].T, i["L1_xattn_Wk"].T, i["L1_xattn_Wv"].T, i["L1_xattn_Wo"].T,
                   i["L1_xattn_q_norm_w"], i["L1_xattn_k_norm_w"], "a1")
    out |= lay_gqa(i["L3_xattn_Wq"], i["L3_xattn_Wk"], i["L3_xattn_Wv"], i["L3_xattn_Wo"],
                   i["L3_xattn_q_norm_w"], i["L3_xattn_k_norm_w"], "a3")
    return out


def run_layers(nc, m, d):
    def of(name):
        return {k[3:]: v for k, v in d.items() if k.startswith(name)}

    memory_attention(nc, m, of("a0_") | {"ctx": d["ctx"]})
    gelu_experts(nc, m, of("f0_"))
    grouped_attention(nc, m, "a1", of("a1_") | {k: d[k] for k in ("pos", "tok", "inv_freq")}, True)
    scaled_linear(nc, m, of("f1_"))
    image_text_attention(nc, m, of("a2_"))
    capacity_experts(nc, m, of("f2_"))
    grouped_attention(nc, m, "a3", of("a3_"), False)
    silu_experts(nc, m, of("f3_"))


def build(nc, dram, out):
    class m:
        pass
    with ExitStack() as ctx:
        m.ident = ctx.enter_context(nc.sbuf_tensor("ident", [P, P], F32))
        m.ident_r = ctx.enter_context(nc.sbuf_tensor("ident_r", [P, P], F32R))
        m.ones_r = ctx.enter_context(nc.sbuf_tensor("ones_r", [P, P], F32R))
        m.onesf = ctx.enter_context(nc.sbuf_tensor("onesf", [P, P], F32))
        m.nhalf = ctx.enter_context(nc.sbuf_tensor("nhalf", [P, 1], F32))
        m.ps = ctx.enter_context(nc.psum_tensor("ps", [P, 8, 512], F32))
        m.x_dram = nc.dram_tensor("x_state", (TT, P * D), F32, kind="Internal").ap()
        m.ctx_hi = nc.dram_tensor("ctx_hi", (B, P, DC * CTXP), F32, kind="Internal").ap()
        m.ctx_lo = nc.dram_tensor("ctx_lo", (B, P, DC * CTXP), F32, kind="Internal").ap()
        make_constants(nc, m)
        copy_x_in(nc, m, dram["x"].rearrange("b (t p) d -> (b t) (p d)", p=P))
        transpose_context(nc, m, dram["ctx"])
        run_layers(nc, m, dram)
        with Stage(nc, "xout") as st:
            moved = st.sem("moved")
            with nc.Block(name="x_out") as block:
                @block.sync
                def _(sp):
                    sp.dma_start(out.rearrange("b (t p) d -> (b t) (p d)", p=P), m.x_dram[:, :]).then_inc(moved, 16)
                    sp.wait_ge(moved, 16)


def kernel(**inputs):
    import concourse.bacc as bacc
    from concourse.bass_utils import run_bass_kernel_spmd

    nc = bacc.Bacc("TRN2", target_bir_lowering=False, num_devices=1)
    arrays = {n: np.ascontiguousarray(a) for n, a in lay_out(inputs).items()}
    dram = {n: nc.dram_tensor(f"in_{n}", a.shape, mybir.dt.from_np(a.dtype), kind="ExternalInput").ap()
            for n, a in arrays.items()}
    out = nc.dram_tensor("out_0", (B, S, D), F32, kind="ExternalOutput").ap()
    build(nc, dram, out)
    r = run_bass_kernel_spmd(nc, [{f"in_{n}": a for n, a in arrays.items()}], core_ids=[0])
    return r.results[0]["out_0"]
```

```python
from contextlib import ExitStack

import concourse.bass as bass
import numpy as np
from concourse import mybir
from concourse.alu_op_type import AluOpType as ALU

F32 = mybir.dt.float32
F32R = mybir.dt.float32r
I32 = mybir.dt.int32
U32 = mybir.dt.uint32
ACT = mybir.ActivationFunctionType
AX = mybir.AxisListType

P = 128
B, S, D = 4, 256, 256
CTX = 1601
CTXP = CTX + 1
DC = D // P
QT = S // P
TT = B * QT
CTILES = -(-CTX // P)
CLAST = CTX - (CTILES - 1) * P
TOPK_CTX = 54
HALVES = ((0, 0), (0, 1), (1, 0))


def flat2(a):
    return a.rearrange("p a b -> p (a b)")


class Step:

    def __init__(self, eng, sem):
        self.eng, self.sem, self.n = eng, sem, 0

    def __call__(self, ins):
        self.n += 1
        ins.then_inc(self.sem, 1)
        self.eng.wait_ge(self.sem, self.n)


class Stage:

    def __init__(self, nc, name):
        self.nc, self.name, self.ctx, self.sems = nc, name, ExitStack(), []

    def __enter__(self):
        return self

    def __exit__(self, *exc):
        self.clear()
        self.ctx.close()

    def sb(self, name, shape, dt=F32):
        return self.ctx.enter_context(self.nc.sbuf_tensor(f"{self.name}_{name}", shape, dt))

    def sem(self, name):
        s = self.ctx.enter_context(self.nc.semaphore(f"{self.name}_{name}"))
        self.sems.append(s)
        return s

    def clear(self):
        nums = sorted(s.num for s in self.sems)
        starts = [n for n in nums if n - 1 not in nums]
        for a in starts:
            e = next(n for n in range(a, a + len(nums) + 1) if n not in nums)
            self.nc.sync.sem_clear(range(a, e))
        self.nc.all_engine_barrier()


def make_constants(nc, m):
    with Stage(nc, "const") as st:
        made = st.sem("made")
        with nc.Block(name="constants") as block:
            @block.gpsimd
            def _(pool):
                pool.memset(m.ident[:, :], 0.0).then_inc(made, 1)
                pool.wait_ge(made, 1)
                pool.affine_select(out=m.ident[:, :], in_=m.ident[:, :], compare_op=ALU.not_equal, fill=1.0,
                                   base=0, pattern=[[-1, P]], channel_multiplier=1).then_inc(made, 1)
                pool.memset(m.nhalf[:, :], -0.5).then_inc(made, 1)
                pool.memset(m.onesf[:, :], 1.0).then_inc(made, 1)
                pool.wait_ge(made, 4)

            @block.scalar
            def _(act):
                act.wait_ge(made, 4)
                act.activation(m.ident_r[:, :], m.ident[:, :], ACT.Copy).then_inc(made, 1)
                act.activation(m.ones_r[:, :], m.onesf[:, :], ACT.Copy).then_inc(made, 1)


def copy_x_in(nc, m, x_in):
    with Stage(nc, "xin") as st:
        moved = st.sem("moved")
        with nc.Block(name="x_in") as block:
            @block.sync
            def _(sp):
                sp.dma_start(m.x_dram[:, :], x_in).then_inc(moved, 16)
                sp.wait_ge(moved, 16)


def transpose_context(nc, m, ctx_in):
    with Stage(nc, "ctxt") as st:
        rows = st.sb("rows", [P, CTILES, D])
        hi = st.sb("hi", [P, DC, CTXP], F32R)
        lo = st.sb("lo", [P, DC, CTXP], F32R)
        loaded, zeroed, turned, hi_done, lo_done, stored = [
            st.sem(n) for n in ("loaded", "zeroed", "turned", "hi_done", "lo_done", "stored")]
        banks = [(c, t0, min(t0 + 4, CTILES)) for c in range(DC) for t0 in range(0, CTILES, 4)]

        def cols(t0, t1):
            return t0 * P, min(t1 * P, CTX)

        with nc.Fori(0, B) as b:
            with nc.Block(name="ctx_turn") as block:
                @block.sync
                def _(sp):
                    full = (CTILES - 1) * P
                    sp.dma_start(rows[:, 0:CTILES - 1, :], ctx_in[bass.ds(b, 1), 0:full, :]
                                 .rearrange("a (t p) d -> p (a t) d", p=P)).then_inc(loaded, 16)
                    sp.dma_start(rows[0:CLAST, CTILES - 1, :], ctx_in[bass.ds(b, 1), full:CTX, :]
                                 .rearrange("a p d -> p (a d)")).then_inc(loaded, 16)
                    sp.wait_ge(zeroed, 2)
                    sp.wait_ge(hi_done, len(banks))
                    sp.dma_start(m.ctx_hi[bass.ds(b, 1), :, :].rearrange("a p n -> p (a n)"),
                                 hi[:, :, :].rearrange("p c n -> p (c n)").bitcast(F32)).then_inc(stored, 16)
                    sp.wait_ge(lo_done, len(banks))
                    sp.dma_start(m.ctx_lo[bass.ds(b, 1), :, :].rearrange("a p n -> p (a n)"),
                                 lo[:, :, :].rearrange("p c n -> p (c n)").bitcast(F32)).then_inc(stored, 16)
                    sp.wait_ge(stored, 32)

                @block.gpsimd
                def _(pool):
                    pool.memset(hi[:, :, CTX:CTXP].bitcast(F32), 0.0).then_inc(zeroed, 1)
                    pool.memset(lo[:, :, CTX:CTXP].bitcast(F32), 0.0).then_inc(zeroed, 1)

                @block.tensor
                def _(pe):
                    pe.wait_ge(loaded, 32)
                    for k, (c, t0, t1) in enumerate(banks):
                        for t in range(t0, t1):
                            r = P if t < CTILES - 1 else CLAST
                            ins = pe.transpose(m.ps[:, k, (t - t0) * P:(t - t0) * P + r],
                                               rows[0:r, t, c * P:(c + 1) * P], m.ident[0:r, 0:r])
                        ins.then_inc(turned, 1)

                @block.scalar
                def _(act):
                    for k, (c, t0, t1) in enumerate(banks):
                        a, z = cols(t0, t1)
                        act.wait_ge(turned, k + 1)
                        act.activation(hi[:, c, a:z], m.ps[:, k, 0:z - a], ACT.Copy).then_inc(hi_done, 1)

                @block.vector
                def _(dve):
                    for k, (c, t0, t1) in enumerate(banks):
                        a, z = cols(t0, t1)
                        dve.wait_ge(hi_done, k + 1)
                        dve.tensor_tensor(lo[:, c, a:z], m.ps[:, k, 0:z - a], hi[:, c, a:z].bitcast(F32),
                                          ALU.subtract).then_inc(lo_done, 1)
            st.clear()


def norm_block(nc, st, m, x_sb, zt_hi, zt_lo, tiles, x_src, sems, scratch, extra_loads=(), name="norm"):
    loaded, dstep, var_ok, rstd_ok, turned, hi_done, lo_done = sems
    stats, mv, rstd, z = scratch
    n_banks = DC * tiles * P // 512
    per = 512 // P
    slots = [(c, t) for c in range(DC) for t in range(tiles)]
    with nc.Block(name=name) as block:
        @block.sync
        def _(sp):
            sp.dma_start(x_sb[:, :, :], x_src).then_inc(loaded, 16)
            for dst, src in extra_loads:
                sp.dma_start(dst, src).then_inc(loaded, 16)
            sp.wait_ge(loaded, 16 * (1 + len(extra_loads)))

        @block.vector
        def _(dve):
            step = Step(dve, dstep)
            dve.wait_ge(loaded, 16 * (1 + len(extra_loads)))
            for t in range(tiles):
                dve.bn_stats(stats[:, t, :], x_sb[:, t, :]).then_inc(dstep, 1)
            step.n += tiles
            dve.wait_ge(dstep, step.n)
            for t in range(tiles):
                dve.bn_aggr(mv[:, t, :], stats[:, t, :]).then_inc(dstep, 1)
            step.n += tiles
            dve.wait_ge(dstep, step.n)
            dve.tensor_scalar(rstd[:, 0, :], mv[:, :, 1], 1e-5, None, ALU.add).then_inc(var_ok, 1)
            dve.wait_ge(rstd_ok, 1)
            for t in range(tiles):
                dve.tensor_scalar(z[:, t, :], x_sb[:, t, :], mv[:, t, 0:1], rstd[:, 1, t:t + 1],
                                  ALU.subtract, ALU.mult).then_inc(dstep, 1)
            step.n += tiles
            for k in range(n_banks):
                dve.wait_ge(hi_done, k + 1)
                dve.tensor_tensor(zt_lo[:, :, :].rearrange("p c n -> p (c n)")[:, k * 512:(k + 1) * 512],
                                  m.ps[:, k, :],
                                  zt_hi[:, :, :].rearrange("p c n -> p (c n)")[:, k * 512:(k + 1) * 512]
                                  .bitcast(F32), ALU.subtract).then_inc(lo_done, 1)

        @block.gpsimd
        def _(pool):
            pool.wait_ge(var_ok, 1)
            pool.tensor_tensor(rstd[:, 1, :], rstd[:, 0, :], m.nhalf[:, 0:1].to_broadcast([P, tiles]),
                               ALU.pow).then_inc(rstd_ok, 1)

        @block.tensor
        def _(pe):
            for i, (c, t) in enumerate(slots):
                pe.wait_ge(dstep, 3 * tiles)
                ins = pe.transpose(m.ps[:, i // per, (i % per) * P:(i % per + 1) * P],
                                   z[:, t, c * P:(c + 1) * P], m.ident[:, :])
                if i % per == per - 1:
                    ins.then_inc(turned, 1)

        @block.scalar
        def _(act):
            for k in range(n_banks):
                act.wait_ge(turned, k + 1)
                act.activation(zt_hi[:, :, :].rearrange("p c n -> p (c n)")[:, k * 512:(k + 1) * 512],
                               m.ps[:, k, :], ACT.Copy).then_inc(hi_done, 1)
def split_weights(nc, st, name, parts, arrived, w_hi, w_lo):
    with nc.Block(name=name) as block:
        @block.sync
        def _(sp):
            for (full, _halves, src), got in zip(parts, arrived):
                sp.dma_start(full, src).then_inc(got, 16)

        @block.scalar
        def _(act):
            for (full, halves, _src), got in zip(parts, arrived):
                act.wait_ge(got, 16)
                act.activation(halves[0], full, ACT.Copy).then_inc(w_hi, 1)

        @block.vector
        def _(dve):
            for i, (full, halves, _src) in enumerate(parts):
                dve.wait_ge(w_hi, i + 1)
                dve.tensor_tensor(halves[1], full, halves[0].bitcast(F32), ALU.subtract).then_inc(w_lo, 1)
    st.clear()


def memory_attention(nc, m, w):
    CH = [(a, min(a + 512, CTXP)) for a in range(0, CTXP, 512)]
    ROUNDS = -(-TOPK_CTX // 8)
    with Stage(nc, "a0") as st:
        x_b = st.sb("x_b", [P, QT, D])
        zt = [st.sb(f"zt{i}", [P, DC, S], F32R) for i in range(2)]
        ct = [st.sb(f"ct{i}", [P, DC, CTXP], F32R) for i in range(2)]
        scratch = (st.sb("stats", [P, QT, 6]), st.sb("mv", [P, QT, 2]), st.sb("rstd", [P, 2, QT]),
                   st.sb("z", [P, QT, D]))
        rows = st.sb("rows", [P, CTILES, D])
        wf = st.sb("wf", [P, 2, DC * D])
        wr = [st.sb(f"wr{i}", [P, 2, DC * D], F32R) for i in range(2)]
        knob = st.sb("knob", [P, 12])
        qt = [st.sb(f"qt{i}", [P, DC, S], F32R) for i in range(2)]
        negm = st.sb("negm", [P, QT])
        shifted = st.sb("shifted", [P, QT, CTX])
        work = st.sb("work", [P, CTX])
        best = st.sb("best", [P, 8])
        expd = st.sb("expd", [P, QT, CTX])
        rsum = st.sb("rsum", [P, 2, QT])
        pt = st.sb("pt", [P, CTILES, S])
        ot = [st.sb(f"ot{i}", [P, DC, S], F32R) for i in range(2)]
        nsem = [st.sem("n_" + n) for n in ("loaded", "step", "var", "rstd", "turned", "hi", "lo")]
        w_in = [st.sem("wq_in"), st.sem("wo_in")]
        w_hi, w_lo, knobs_in, kact, dstep = [st.sem(n) for n in "w_hi w_lo knobs_in kact dstep".split()]
        (q_ready, q_hi, q_lo, s_ready, neg_ok, shift_ok, exp_ok, mask_ok, pt_turned, pt_ok, o_ready, o_hi,
         o_lo, y_ready) = [st.sem(n) for n in (
             "q_ready q_hi q_lo s_ready neg_ok shift_ok exp_ok mask_ok pt_turned pt_ok o_ready o_hi "
             "o_lo y_ready").split()]

        split_weights(nc, st, "a0_weights",
                      [(wf[:, i, :], (wr[0][:, i, :], wr[1][:, i, :]), w[n]) for i, n in enumerate(("wq", "wo"))],
                      w_in, w_hi, w_lo)
        GATE, TAU, BQ, BK = range(4)
        with nc.Block(name="a0_knobs") as block:
            @block.sync
            def _(sp):
                for i, n in enumerate(("gate", "log_tau", "beta_q", "beta_k")):
                    sp.dma_start(knob[:, i:i + 1], w[n].partition_broadcast(P)).then_inc(knobs_in, 16)

            @block.scalar
            def _(act):
                act.wait_ge(knobs_in, 64)
                act.activation(knob[:, 4:5], knob[:, GATE:GATE + 1], ACT.Exp, scale=-1.0).then_inc(kact, 1)
                act.activation(knob[:, 5:6], knob[:, TAU:TAU + 1], ACT.Exp).then_inc(kact, 1)

            @block.vector
            def _(dve):
                step = Step(dve, dstep)
                dve.wait_ge(kact, 2)
                step(dve.tensor_scalar(knob[:, 6:7], knob[:, 4:5], 1.0, None, ALU.add))
                step(dve.reciprocal(knob[:, 7:8], knob[:, 6:7]))
                step(dve.tensor_scalar(knob[:, 8:9], knob[:, 7:8], -1.0, 1.0, ALU.mult, ALU.add))
                step(dve.tensor_tensor(knob[:, 9:10], knob[:, 8:9], knob[:, BK:BK + 1], ALU.mult))
                step(dve.scalar_tensor_tensor(out=knob[:, 10:11], in0=knob[:, 7:8], scalar=knob[:, BQ:BQ + 1],
                                              in1=knob[:, 9:10], op0=ALU.mult, op1=ALU.add))
                step(dve.scalar_tensor_tensor(out=knob[:, 11:12], in0=knob[:, 10:11], scalar=D ** -0.5,
                                              in1=knob[:, 5:6], op0=ALU.mult, op1=ALU.mult))
        st.clear()
        coef = knob[:, 11:12]

        with nc.Fori(0, B) as b:
            x_rows = m.x_dram[bass.ds(b * QT, QT), :].rearrange("t (p d) -> p t d", p=P)
            full = (CTILES - 1) * P
            norm_block(nc, st, m, x_b, zt[0], zt[1], QT, x_rows, nsem, scratch, [
                (flat2(ct[0][:, :, :]).bitcast(F32), m.ctx_hi[bass.ds(b, 1), :, :].rearrange("a p n -> p (a n)")),
                (flat2(ct[1][:, :, :]).bitcast(F32), m.ctx_lo[bass.ds(b, 1), :, :].rearrange("a p n -> p (a n)")),
                (rows[:, 0:CTILES - 1, :], w["ctx"][bass.ds(b, 1), 0:full, :].rearrange("a (t p) d -> p (a t) d", p=P)),
                (rows[0:CLAST, CTILES - 1, :], w["ctx"][bass.ds(b, 1), full:CTX, :].rearrange("a p d -> p (a d)")),
            ], name="a0_norm")
            st.clear()
            with nc.Block(name="a0_attend") as block:
                @block.tensor
                def _(pe):
                    for o in range(DC):
                        n = 0
                        for c in range(DC):
                            for s, v in HALVES:
                                ins = pe.matmul(m.ps[:, 4 + o, 0:S], wr[v][:, 0, c * D + o * P:c * D + (o + 1) * P],
                                                zt[s][:, c, :], start=(n == 0), stop=(n == 3 * DC - 1))
                                n += 1
                        ins.then_inc(q_ready, 1)
                    pe.wait_ge(q_lo, DC)
                    for q in range(QT):
                        for k, (a, e) in enumerate(CH):
                            n = 0
                            for c in range(DC):
                                for s, v in HALVES:
                                    ins = pe.matmul(m.ps[:, 4 * q + k, 0:e - a], qt[s][:, c, q * P:(q + 1) * P],
                                                    ct[v][:, c, a:e], start=(n == 0), stop=(n == 3 * DC - 1))
                                    n += 1
                        ins.then_inc(s_ready, 1)
                    for q in range(QT):
                        pe.wait_ge(mask_ok, q + 1)
                        for k in range(0, CTILES, 4):
                            for t in range(k, min(k + 4, CTILES)):
                                r = P if t < CTILES - 1 else CLAST
                                ins = pe.transpose(m.ps[0:r, 4 * q + k // 4, (t - k) * P:(t - k + 1) * P],
                                                   expd[:, q, t * P:t * P + r], m.ident[:, :])
                            ins.then_inc(pt_turned, 1)
                    pe.wait_ge(pt_ok, 8)
                    for o in range(DC):
                        for t in range(CTILES):
                            r = P if t < CTILES - 1 else CLAST
                            ins = pe.matmul(m.ps[:, o, 0:S], rows[0:r, t, o * P:(o + 1) * P], pt[0:r, t, :],
                                            start=(t == 0), stop=(t == CTILES - 1))
                        ins.then_inc(o_ready, 1)
                    pe.wait_ge(o_lo, DC)
                    for q in range(QT):
                        n = 0
                        for c in range(DC):
                            for s, v in HALVES:
                                ins = pe.matmul(m.ps[:, 2 + q, 0:D], ot[s][:, c, q * P:(q + 1) * P],
                                                wr[v][:, 1, c * D:(c + 1) * D], start=(n == 0), stop=(n == 3 * DC - 1))
                                n += 1
                        ins.then_inc(y_ready, 1)

                @block.scalar
                def _(act):
                    for o in range(DC):
                        act.wait_ge(q_ready, o + 1)
                        act.activation(qt[0][:, o, :], m.ps[:, 4 + o, 0:S], ACT.Copy, scale=coef).then_inc(q_hi, 1)
                    for q in range(QT):
                        act.wait_ge(neg_ok, q + 1)
                        act.activation(shifted[:, q, :], m.ps[:, 4 * q:4 * q + 4, :]
                                       .rearrange("p b n -> p (b n)")[:, 0:CTX], ACT.Identity,
                                       bias=negm[:, q:q + 1]).then_inc(shift_ok, 1)
                        act.wait_ge(shift_ok, q + 1)
                        act.activation(expd[:, q, :], shifted[:, q, :], ACT.Exp).then_inc(exp_ok, 1)
                    for q in range(QT):
                        for k in range(0, CTILES, 4):
                            e = min(k + 4, CTILES)
                            i = q * 4 + k // 4
                            r = P if e < CTILES else CLAST
                            act.wait_ge(pt_turned, i + 1)
                            act.activation(pt[0:r, k:e, q * P:(q + 1) * P],
                                           m.ps[0:r, 4 * q + k // 4, 0:(e - k) * P].rearrange("p (t n) -> p t n", n=P),
                                           ACT.Copy).then_inc(pt_ok, 1)
                    for o in range(DC):
                        act.wait_ge(o_ready, o + 1)
                        act.activation(ot[0][:, o, :], m.ps[:, o, 0:S], ACT.Copy).then_inc(o_hi, 1)

                @block.vector
                def _(dve):
                    step = Step(dve, dstep)
                    for o in range(DC):
                        dve.wait_ge(q_hi, o + 1)
                        dve.scalar_tensor_tensor(out=qt[1][:, o, :], in0=m.ps[:, 4 + o, 0:S], scalar=coef,
                                                 in1=qt[0][:, o, :].bitcast(F32), op0=ALU.mult,
                                                 op1=ALU.subtract).then_inc(q_lo, 1)
                    for q in range(QT):
                        dve.wait_ge(s_ready, q + 1)
                        dve.tensor_reduce(negm[:, q:q + 1], m.ps[:, 4 * q:4 * q + 4, :]
                                          .rearrange("p b n -> p (b n)")[:, 0:CTX], AX.X, ALU.max, negate=True)\
                           .then_inc(neg_ok, 1)
                    for q in range(QT):
                        dve.wait_ge(shift_ok, q + 1)
                        left = shifted[:, q, :]
                        for r in range(ROUNDS):
                            step(dve.max(out=best[:, :], in_=left))
                            if r < ROUNDS - 1:
                                step(dve.match_replace(out=work[:, :], in_to_replace=best[:, :], in_values=left,
                                                       imm_value=-3.0e38))
                                left = work[:, :]
                        at = (TOPK_CTX - 1) % 8
                        dve.wait_ge(exp_ok, q + 1)
                        step(dve.scalar_tensor_tensor(out=expd[:, q, :], in0=shifted[:, q, :],
                                                      scalar=best[:, at:at + 1], in1=expd[:, q, :],
                                                      op0=ALU.is_ge, op1=ALU.mult, accum_out=rsum[:, 0, q:q + 1]))
                        dve.reciprocal(rsum[:, 1, q:q + 1], rsum[:, 0, q:q + 1]).then_inc(mask_ok, 1)
                    for o in range(DC):
                        dve.wait_ge(o_hi, o + 1)
                        dve.tensor_tensor(ot[1][:, o, :], m.ps[:, o, 0:S], ot[0][:, o, :].bitcast(F32),
                                          ALU.subtract).then_inc(o_lo, 1)
                    for q in range(QT):
                        dve.wait_ge(y_ready, q + 1)
                        dve.scalar_tensor_tensor(out=x_b[:, q, :], in0=m.ps[:, 2 + q, 0:D], scalar=rsum[:, 1, q:q + 1],
                                                 in1=x_b[:, q, :], op0=ALU.mult, op1=ALU.add).then_inc(dstep, 1)
            st.clear()
            with nc.Block(name="a0_out") as block:
                @block.sync
                def _(sp):
                    sp.dma_start(x_rows, x_b[:, :, :]).then_inc(nsem[0], 16)
                    sp.wait_ge(nsem[0], 16)
            st.clear()
HD = 128
KVH, REP = 4, 4
VW = HD + 1


def reduce_angle(dve, step, f, n, r):
    c1 = 6.28125
    c2 = float(np.float32(0.0019353071795864769))
    c3 = 2 * np.pi - c1 - c2
    magic = 12582912.0
    step(dve.tensor_scalar(n, f, 1.0 / (2 * np.pi), magic, ALU.mult, ALU.add))
    step(dve.tensor_scalar(n, n, -magic, None, ALU.add))
    step(dve.scalar_tensor_tensor(out=r, in0=n, scalar=-c1, in1=f, op0=ALU.mult, op1=ALU.add))
    step(dve.scalar_tensor_tensor(out=r, in0=n, scalar=-c2, in1=r, op0=ALU.mult, op1=ALU.add))
    step(dve.scalar_tensor_tensor(out=r, in0=n, scalar=-c3, in1=r, op0=ALU.mult, op1=ALU.add))


def rope_tables(nc, m, name, w, table, KT):
    half = HD // 2
    full = (CTILES - 1) * P
    with Stage(nc, name) as st:
        pos_i = st.sb("pos_i", [KT, P], I32)
        pos_rows = st.sb("pos_rows", [KT, P])
        pos_f = st.sb("pos_f", [P, KT])
        invf = st.sb("invf", [P, half])
        ang = st.sb("ang", [P, KT, half])
        tmp = st.sb("tmp", [P, KT, half])
        cs = st.sb("cs", [P, 2, KT, half])
        once, zeroed, loaded, dstep, rows_ok, turned, angles, stored, done = [
            st.sem(n) for n in "once zeroed loaded dstep rows_ok turned angles stored done".split()]
        with nc.Block(name=f"{name}_once") as block:
            @block.sync
            def _(sp):
                sp.dma_start(invf[:, :], w["inv_freq"].partition_broadcast(P)).then_inc(once, 16)
                sp.wait_ge(once, 16)

            @block.gpsimd
            def _(pool):
                pool.memset(pos_i[:, :], 0).then_inc(zeroed, 1)
        st.clear()
        with nc.Fori(0, B) as b:
            with nc.Block(name=f"{name}_batch") as block:
                @block.sync
                def _(sp):
                    sp.dma_start(pos_i[0:CTILES - 1, :], w["pos"][bass.ds(b, 1), 0:full]
                                 .rearrange("a (t p) -> (a t) p", p=P)).then_inc(loaded, 16)
                    sp.dma_start(pos_i[CTILES - 1:CTILES, 0:CLAST], w["pos"][bass.ds(b, 1), full:CTX])\
                      .then_inc(loaded, 16)
                    sp.dma_start(pos_i[CTILES:KT, :], w["tok"][bass.ds(b, 1), :]
                                 .rearrange("a (t p) -> (a t) p", p=P)).then_inc(loaded, 16)
                    sp.wait_ge(done, 2)
                    sp.dma_start(table[bass.ds(b, 1), :, :].rearrange("a p n -> p (a n)"),
                                 cs[:, :, :, :].rearrange("p a k n -> p (a k n)")).then_inc(stored, 16)
                    sp.wait_ge(stored, 16)

                @block.vector
                def _(dve):
                    step = Step(dve, dstep)
                    cos, sin = cs[:, 0, :, :], cs[:, 1, :, :]
                    dve.wait_ge(loaded, 48)
                    dve.tensor_copy(pos_rows[:, :], pos_i[:, :]).then_inc(rows_ok, 1)
                    dve.wait_ge(turned, 1)
                    step(dve.tensor_copy(pos_f[:, :], m.ps[:, 0, 0:KT]))
                    step(dve.tensor_tensor(ang[:, :, :], pos_f[:, :].unsqueeze(2).to_broadcast([P, KT, half]),
                                           invf[:, :].unsqueeze(1).to_broadcast([P, KT, half]), ALU.mult))
                    reduce_angle(dve, step, ang[:, :, :], tmp[:, :, :], sin)
                    step(dve.tensor_scalar(cos, sin, np.pi / 2, None, ALU.add))
                    step(dve.tensor_scalar(tmp[:, :, :], cos, np.pi, -2 * np.pi, ALU.is_gt, ALU.mult))
                    step(dve.tensor_tensor(cos, cos, tmp[:, :, :], ALU.add))
                    PI = 3.1415925
                    dve.tensor_scalar(cos, cos, PI, -PI, ALU.min, ALU.max).then_inc(angles, 1)
                    dve.tensor_scalar(sin, sin, PI, -PI, ALU.min, ALU.max).then_inc(angles, 1)

                @block.tensor
                def _(pe):
                    pe.wait_ge(rows_ok, 1)
                    pe.transpose(m.ps[:, 0, 0:KT], pos_rows[:, :], m.ident[0:KT, 0:KT]).then_inc(turned, 1)

                @block.scalar
                def _(act):
                    for i in range(2):
                        act.wait_ge(angles, i + 1)
                        act.activation(cs[:, i, :, :], cs[:, i, :, :], ACT.Sin).then_inc(done, 1)
            st.clear()


def plan_group(KT, KB, rope, attend, norm, prepare, tail):
    turns = [[] for _ in range(2 * KT)]

    def put(at, *tasks):
        turns[min(at, len(turns) - 1)].extend(tasks)

    if prepare:
        put(0, ("W", 0))
    if tail:
        put(0, ("OX", 0), ("OX", 1))
        put(1, ("W", 2))
        put(2, ("Y", 0), ("Y", 1))
    if norm:
        put(2, ("N", 0))
        put(4, ("NX", 0))
    if attend:
        for r in range(8):
            put(1 + r, ("R", r))
    if prepare:
        put(3, ("W", 1))
        at = 6 if norm else 3
        for t in range(0, KT, 2):
            put(at, *[("KV", i) for i in range(t, min(t + 2, KT))])
            at += 1
        put(at, ("Q", 0), ("Q", 1))
        at += 2
        chunks = 3 if rope else 1
        for c in range(chunks):
            put(at, ("KN", c))
            at += 1
        put(at, ("QN", 0))
        put(at + (1 if rope else 0), ("QN", 1))
        at += 1
        for k in range(len(KB)):
            put(at + k // 2, ("KX", k))
        at += 2
        put(at, ("QX", 0), ("QX", 1))
        at += 1
        left = len(turns) - at
        for r in range(8):
            put(at + (r * left) // 8, ("R", 8 + r))
    return turns


def grouped_attention(nc, m, name, w, rope):
    tiles = [(t * P, P if t < CTILES - 1 else CLAST, None) for t in range(CTILES)]
    if rope:
        tiles += [(CTX + q * P, P, q) for q in range(QT)]
    KT = len(tiles)
    NK = CTX + (S if rope else 0)
    NKP = NK + NK % 2
    GQ = REP * S
    NJ = GQ // P
    NG = 2
    JG = NJ // NG
    TURNS = KT * NG
    KB = [(t0, min(t0 + 4, KT)) for t0 in range(0, KT, 4)]
    KEND = [t[0] for t in tiles] + [NK]
    RH = [(0, 1024, 1024), (1024, NKP, NK)]
    SCALE = HD ** -0.5
    half = HD // 2
    table = nc.dram_tensor(f"{name}_table", (B, P, 2 * KT * half), F32, kind="Internal").ap() if rope else None
    if rope:
        rope_tables(nc, m, f"{name}t", w, table, KT)

    with Stage(nc, name) as st:
        x_b = st.sb("x_b", [P, QT, D])
        x_n = st.sb("x_n", [P, QT, D])
        zt = [st.sb(f"zt{i}", [P, DC, S], F32R) for i in range(2)]
        ct = [st.sb(f"ct{i}", [P, DC, CTXP], F32R) for i in range(2)]
        stats = st.sb("stats", [P, QT, 6])
        mv = st.sb("mv", [P, QT, 2])
        rstd = st.sb("rstd", [P, 2, QT])
        z = st.sb("z", [P, QT, D])
        qw = st.sb("qw", [P, HD])
        kw = st.sb("kw", [P, HD])
        wf = [st.sb(f"wf{k}", [P, n]) for k, n in enumerate((DC * 2 * HD, DC * REP * HD, REP * D))]
        wr = [[st.sb(f"wr{k}{i}", [P, n], F32R) for i in range(2)]
              for k, n in enumerate((DC * 2 * HD, DC * REP * HD, REP * D))]
        k_rows = st.sb("k_rows", [P, KT, HD])
        v_rows = [st.sb(f"v_rows{i}", [P, KT, VW]) for i in range(2)]
        q_rows = st.sb("q_rows", [P, QT, REP, HD])
        k_sq = st.sb("k_sq", [P, 3, KT])
        q_sq = st.sb("q_sq", [P, 3, QT * REP])
        square = st.sb("square", [P, 8, HD])
        kts = [[st.sb(f"kt{g}{i}", [P, NKP], F32R) for i in range(2)] for g in range(2)]
        qts = [[st.sb(f"qt{g}{i}", [P, GQ], F32R) for i in range(2)] for g in range(2)]
        neg2 = st.sb("neg2", [P, NJ, 2])
        negmax = st.sb("negmax", [P, NJ])
        diag = st.sb("diag", [P, NJ, P], F32R)
        probs = st.sb("probs", [P, 3, 512])
        rsum = st.sb("rsum", [P, JG])
        o_rows = st.sb("o_rows", [P, NJ, HD])
        ot = [st.sb(f"ot{i}", [P, NJ * P], F32R) for i in range(2)]
        if rope:
            cs = st.sb("cs", [P, 2, KT, half])
            by_cos = st.sb("by_cos", [P, 5 * HD])
            by_sin = st.sb("by_sin", [P, 5 * HD])

        once, zeroed = st.sem("once"), st.sem("zeroed")
        (x_in, ct_in, tab_in, pre0, pre1, pre2, stored, w_hi, w_lo, dstep, pstep, var_ok, nrstd_ok, z_ok,
         item_ready, item_act, item_free, k_rstd, q_rstd, k_ready, q_normed, r_ready, neg_done, diag_done,
         st_ready, exp_done, pv_done, o_done, x_done, x_copied) = [st.sem(n) for n in (
             "x_in ct_in tab_in pre0 pre1 pre2 stored w_hi w_lo dstep pstep var_ok nrstd_ok z_ok "
             "item_ready item_act item_free k_rstd q_rstd k_ready q_normed r_ready neg_done diag_done "
             "st_ready exp_done pv_done o_done x_done x_copied").split()]

        with nc.Block(name=f"{name}_once") as block:
            @block.sync
            def _(sp):
                loads = [(qw[:, :], w["qw"].partition_broadcast(P)), (kw[:, :], w["kw"].partition_broadcast(P)),
                         (wf[0][:, :], w["wkv"][0]), (wf[1][:, :], w["wq"][0])]
                for dst, src in loads:
                    sp.dma_start(dst, src).then_inc(once, 16)
                sp.wait_ge(once, 16 * len(loads))

            @block.gpsimd
            def _(pool):
                for i in range(2):
                    pool.memset(v_rows[i][:, :, HD:VW], 1.0).then_inc(zeroed, 1)
                    if NKP > NK:
                        pool.memset(kts[i][0][:, NK:NKP].bitcast(F32), 0.0).then_inc(zeroed, 1)
                pool.memset(k_rows[:, :, :], 0.0).then_inc(zeroed, 1)
                pool.memset(k_sq[:, :, :], 1.0).then_inc(zeroed, 1)
                pool.memset(o_rows[:, :, :], 0.0).then_inc(zeroed, 1)
                pool.memset(x_b[:, :, :], 0.0).then_inc(zeroed, 1)
        st.clear()

        def group_block(a, b_next, attend=True, norm=False, prepare=True, tail=True, store=None):
            kt, qt, v_cur = kts[a % 2], qts[a % 2], v_rows[a % 2]
            kt_n, qt_n, v_next = kts[(a + 1) % 2], qts[(a + 1) % 2], v_rows[(a + 1) % 2]
            turns = plan_group(KT, KB, rope, attend, norm, prepare, tail)
            flat = [task for turn in turns for task in turn]
            items = [task for task in flat if task[0] in ("NX", "KV", "Q", "KX", "QX", "OX", "Y")]
            number = {task: i for i, task in enumerate(items)}
            scalar_items = [task for task in items if task[0] != "Y"]
            acted = {task: i + 1 for i, task in enumerate(scalar_items)}
            weights = [task[1] for task in flat if task[0] == "W"]
            w_count = {k: i + 1 for i, k in enumerate(weights)}
            rough = [task[1] for task in flat if task[0] == "R"]
            r_count = {r: i for i, r in enumerate(rough)}

            def bank(task):
                return 2 + number[task] % 2

            def rough_block(r):
                return (4 + r // 2, kt, qt) if r < 8 else ((r - 8) // 2, kt_n, qt_n)

            with nc.Block(name=f"{name}_group{a + 1}") as block:
                @block.sync
                def _(sp):
                    if norm:
                        rows = m.x_dram[bass.ds(b_next * QT, QT), :].rearrange("t (p d) -> p t d", p=P)
                        sp.dma_start(x_n[:, :, :], rows).then_inc(x_in, 16)
                        if rope:
                            sp.dma_start(cs[:, :, :, :].rearrange("p a k n -> p (a k n)"),
                                         table[bass.ds(b_next, 1), :, :].rearrange("a p n -> p (a n)"))\
                              .then_inc(tab_in, 16)
                        for i, src in enumerate((m.ctx_hi, m.ctx_lo)):
                            sp.dma_start(flat2(ct[i][:, :, :]).bitcast(F32),
                                         src[bass.ds(b_next, 1), :, :].rearrange("a p n -> p (a n)"))\
                              .then_inc(ct_in, 16)
                    if prepare:
                        g_next = {0: (a + 2) % KVH, 1: (a + 2) % KVH, 2: a % KVH}
                        src = {0: w["wkv"], 1: w["wq"], 2: w["wo"]}
                        for k in sorted((0, 1, 2), key=lambda k: w_count.get(k, 0)):
                            if k in w_count:
                                sp.wait_ge(w_lo, w_count[k])
                            sp.dma_start(wf[k][:, :], src[k][g_next[k]]).then_inc((pre0, pre1, pre2)[k], 16)
                    if store is not None:
                        sp.wait_ge(x_done, QT)
                        sp.dma_start(store, x_b[:, :, :]).then_inc(stored, 16)
                        sp.wait_ge(stored, 16)
                    if prepare:
                        for s in (pre0, pre1, pre2):
                            sp.wait_ge(s, 16)

                @block.tensor
                def _(pe):
                    def begin(task):
                        i = number[task]
                        if i >= 2:
                            pe.wait_ge(item_free, i - 1)
                        return m.ps[:, bank(task), :]

                    def halves_ready(k):
                        pe.wait_ge(w_lo, w_count[k])

                    def NX(i):
                        pe.wait_ge(z_ok, QT)
                        out = begin(("NX", i))
                        for c in range(DC):
                            for q in range(QT):
                                ins = pe.transpose(out[:, (c * QT + q) * P:(c * QT + q + 1) * P],
                                                   z[:, q, c * P:(c + 1) * P], m.ident[:, :])
                        ins.then_inc(item_ready, 1)

                    def KV(t):
                        out = begin(("KV", t))
                        at, r, own = tiles[t]
                        if t == 0:
                            halves_ready(0)
                            if norm:
                                pe.wait_ge(ct_in, 32)
                        if own is not None and norm:
                            pe.wait_ge(item_free, number[("NX", 0)] + 1)
                        n = 0
                        for c in range(DC):
                            for s, v in HALVES:
                                src = (ct[s][:, c, at:at + r] if own is None
                                       else zt[s][:, c, own * P:(own + 1) * P])
                                ins = pe.matmul(out[0:r, 0:2 * HD], src, wr[0][v][:, c * 2 * HD:(c + 1) * 2 * HD],
                                                start=(n == 0), stop=(n == 3 * DC - 1))
                                n += 1
                        ins.then_inc(item_ready, 1)

                    def Q(q):
                        out = begin(("Q", q))
                        halves_ready(1)
                        if norm:
                            pe.wait_ge(item_free, number[("NX", 0)] + 1)
                        n = 0
                        for c in range(DC):
                            for s, v in HALVES:
                                ins = pe.matmul(out, zt[s][:, c, q * P:(q + 1) * P],
                                                wr[1][v][:, c * REP * HD:(c + 1) * REP * HD],
                                                start=(n == 0), stop=(n == 3 * DC - 1))
                                n += 1
                        ins.then_inc(item_ready, 1)

                    def KX(k):
                        out = begin(("KX", k))
                        pe.wait_ge(k_ready, 3 if rope else 1)
                        t0, t1 = KB[k]
                        for t in range(t0, t1):
                            at, r, _own = tiles[t]
                            ins = pe.transpose(out[:, at - KEND[t0]:at - KEND[t0] + r],
                                               k_rows[0:r, t, :], m.ident[0:r, 0:r])
                        ins.then_inc(item_ready, 1)

                    def QX(k):
                        out = begin(("QX", k))
                        pe.wait_ge(q_normed, QT)
                        for i in range(4):
                            j = 4 * k + i
                            ins = pe.transpose(out[:, i * P:(i + 1) * P], q_rows[:, j % QT, j // QT, :],
                                               m.ident[:, :])
                        ins.then_inc(item_ready, 1)

                    def OX(k):
                        out = begin(("OX", k))
                        for i in range(4):
                            ins = pe.transpose(out[:, i * P:(i + 1) * P], o_rows[:, 4 * k + i, :], m.ident[:, :])
                        ins.then_inc(item_ready, 1)

                    def Y(q):
                        out = begin(("Y", q))
                        halves_ready(2)
                        pe.wait_ge(item_free, number[("OX", 1)] + 1)
                        n = 0
                        for h in range(REP):
                            j = h * QT + q
                            for s, v in HALVES:
                                ins = pe.matmul(out[:, 0:D], ot[s][:, j * P:(j + 1) * P],
                                                wr[2][v][:, h * D:(h + 1) * D],
                                                start=(n == 0), stop=(n == 3 * REP - 1))
                                n += 1
                        ins.then_inc(item_ready, 1)

                    def R(r):
                        j, keys, queries = rough_block(r)
                        if r_count[r]:
                            pe.wait_ge(neg_done, r_count[r])
                        if r == 8:
                            pe.wait_ge(item_free, number[("QX", 1)] + 1)
                        a0, e0, _e = RH[r % 2]
                        for k, c0 in enumerate(range(a0, e0, 512)):
                            c1 = min(c0 + 512, e0)
                            ins = pe.matmul(m.ps[:, k, 0:c1 - c0], queries[0][:, j * P:(j + 1) * P],
                                            keys[0][:, c0:c1], start=True, stop=True)
                        ins.then_inc(r_ready, 1)

                    def scores(n):
                        G, t = divmod(n, KT)
                        at, r, _own = tiles[t]
                        if t == 0 and G:
                            pe.wait_ge(diag_done, JG)
                        if n >= 2:
                            pe.wait_ge(exp_done, n - 1)
                        out = m.ps[0:r, 4 + n % 2, :]
                        cols = slice(G * 512, (G + 1) * 512)
                        pe.matmul(out, m.ones_r[:, 0:r],
                                  diag[:, G * JG:(G + 1) * JG, :].rearrange("p j n -> p (j n)"),
                                  start=True, stop=False)
                        pe.matmul(out, kt[0][:, at:at + r], qt[0][:, cols], start=False, stop=False)
                        pe.matmul(out, kt[0][:, at:at + r], qt[1][:, cols], start=False, stop=False)
                        pe.matmul(out, kt[1][:, at:at + r], qt[0][:, cols], start=False, stop=True)\
                          .then_inc(st_ready, 1)

                    def values(n):
                        G, t = divmod(n, KT)
                        r = tiles[t][1]
                        pe.wait_ge(exp_done, n + 1)
                        if t == 0 and G:
                            pe.wait_ge(o_done, G)
                        for i in range(JG):
                            ins = pe.matmul(m.ps[:, 6 + i // 2, (i % 2) * 256:(i % 2) * 256 + VW],
                                            probs[0:r, n % 3, i * P:(i + 1) * P],
                                            v_cur[0:r, t, :], start=(t == 0 and i % 2 == 0),
                                            stop=(t == KT - 1), skip_group_check=True)
                        ins.then_inc(pv_done, 1)

                    does = {"NX": NX, "KV": KV, "Q": Q, "KX": KX, "QX": QX, "OX": OX, "Y": Y, "R": R}
                    for n in range(TURNS):
                        if attend:
                            scores(n)
                        for task, i in turns[n]:
                            if task in does:
                                does[task](i)
                        if attend and n:
                            values(n - 1)
                    if attend:
                        values(TURNS - 1)

                @block.scalar
                def _(act):
                    def W(k):
                        act.activation(wr[k][0][:, :], wf[k][:, :], ACT.Copy).then_inc(w_hi, 1)

                    def begin(task):
                        act.wait_ge(item_ready, number[task] + 1)
                        return m.ps[:, bank(task), :]

                    def NX(i):
                        act.activation(flat2(zt[0][:, :, :]), begin(("NX", i)), ACT.Copy).then_inc(item_act, 1)

                    def KV(t):
                        r = tiles[t][1]
                        src = begin(("KV", t))
                        if t >= 4:
                            act.wait_ge(item_act, acted[("KV", t - 4)])
                        act.activation(square[0:r, t % 4, :], src[0:r, 0:HD], ACT.Square,
                                       accum_out=k_sq[0:r, 0, t:t + 1]).then_inc(item_act, 1)

                    def Q(q):
                        src = begin(("Q", q))
                        if q:
                            act.wait_ge(item_act, acted[("Q", q - 1)])
                        for h in range(REP):
                            i = q * REP + h
                            ins = act.activation(square[:, 4 + h, :], src[:, h * HD:(h + 1) * HD],
                                                 ACT.Square, accum_out=q_sq[:, 0, i:i + 1])
                        ins.then_inc(item_act, 1)

                    def KX(k):
                        a0, e0 = KEND[KB[k][0]], KEND[KB[k][1]]
                        act.activation(kt_n[0][:, a0:e0], begin(("KX", k))[:, 0:e0 - a0], ACT.Copy)\
                           .then_inc(item_act, 1)

                    def QX(k):
                        act.activation(qt_n[0][:, k * 512:(k + 1) * 512], begin(("QX", k)), ACT.Copy)\
                           .then_inc(item_act, 1)

                    def OX(k):
                        act.activation(ot[0][:, k * 512:(k + 1) * 512], begin(("OX", k)), ACT.Copy)\
                           .then_inc(item_act, 1)

                    def exp(n):
                        r = tiles[n % KT][1]
                        act.wait_ge(st_ready, n + 1)
                        if n >= 3:
                            act.wait_ge(pv_done, n - 2)
                        act.activation(probs[0:r, n % 3, :], m.ps[0:r, 4 + n % 2, :], ACT.Exp)\
                           .then_inc(exp_done, 1)

                    does = {"W": W, "NX": NX, "KV": KV, "Q": Q, "KX": KX, "QX": QX, "OX": OX}
                    for n in range(TURNS):
                        if attend:
                            exp(n)
                        for task, i in turns[n]:
                            if task in does:
                                does[task](i)

                @block.gpsimd
                def _(pool):
                    step = Step(pool, pstep)

                    def N(_i):
                        pool.wait_ge(var_ok, 1)
                        pool.tensor_tensor(rstd[:, 1, :], rstd[:, 0, :], m.nhalf[:, 0:1].to_broadcast([P, QT]),
                                           ALU.pow).then_inc(nrstd_ok, 1)

                    def KN(c):
                        if c == 0:
                            pool.wait_ge(item_act, acted[("KV", KT - 1)])
                            step(pool.tensor_scalar(k_sq[:, 1, :], k_sq[:, 0, :], 1.0 / HD, 1e-6, ALU.mult, ALU.add))
                            pool.tensor_tensor(k_sq[:, 2, :], k_sq[:, 1, :], m.nhalf[:, 0:1].to_broadcast([P, KT]),
                                               ALU.pow).then_inc(k_rstd, 1)

                    def QN(q):
                        if q == 0:
                            pool.wait_ge(item_act, acted[("Q", QT - 1)])
                            step(pool.tensor_scalar(q_sq[:, 1, :], q_sq[:, 0, :], 1.0 / HD, 1e-6, ALU.mult, ALU.add))
                            step(pool.tensor_tensor(q_sq[:, 2, :], q_sq[:, 1, :],
                                                    m.nhalf[:, 0:1].to_broadcast([P, QT * REP]), ALU.pow))
                            pool.tensor_scalar(q_sq[:, 2, :], q_sq[:, 2, :], SCALE, None, ALU.mult)\
                                .then_inc(q_rstd, 1)

                    def R(r):
                        if r % 2 == 0:
                            return
                        j = rough_block(r)[0]
                        pool.wait_ge(neg_done, r_count[r] + 1)
                        if attend and r == 9:
                            pool.wait_ge(st_ready, KT)
                        pool.tensor_scalar(diag[:, j, :], m.ident[:, :], negmax[:, j:j + 1], None, ALU.mult)\
                            .then_inc(diag_done, 1)

                    does = {"N": N, "KN": KN, "QN": QN, "R": R}
                    for turn in turns:
                        for task, i in turn:
                            if task in does:
                                does[task](i)

                @block.vector
                def _(dve):
                    step = Step(dve, dstep)

                    def W(k):
                        dve.wait_ge(w_hi, w_count[k])
                        dve.tensor_tensor(wr[k][1][:, :], wf[k][:, :], wr[k][0][:, :].bitcast(F32),
                                          ALU.subtract).then_inc(w_lo, 1)

                    def begin(task):
                        if task in acted:
                            dve.wait_ge(item_act, acted[task])
                        else:
                            dve.wait_ge(item_ready, number[task] + 1)
                        return m.ps[:, bank(task), :]

                    def low(task, dst, hi, width):
                        src = begin(task)
                        dve.tensor_tensor(dst, src[:, 0:width], hi.bitcast(F32), ALU.subtract)\
                           .then_inc(item_free, 1)

                    def N(_i):
                        dve.wait_ge(x_in, 16)
                        for q in range(QT):
                            ins = dve.bn_stats(stats[:, q, :], x_n[:, q, :])
                        step(ins)
                        for q in range(QT):
                            ins = dve.bn_aggr(mv[:, q, :], stats[:, q, :])
                        step(ins)
                        dve.tensor_scalar(rstd[:, 0, :], mv[:, :, 1], 1e-5, None, ALU.add).then_inc(var_ok, 1)

                    def NX(i):
                        low(("NX", i), flat2(zt[1][:, :, :]), flat2(zt[0][:, :, :]), 512)

                    def KV(t):
                        r = tiles[t][1]
                        src = begin(("KV", t))
                        dve.tensor_tensor(k_rows[0:r, t, :], src[0:r, 0:HD], kw[0:r, :], ALU.mult)
                        dve.tensor_copy(v_next[0:r, t, 0:HD], src[0:r, HD:2 * HD]).then_inc(item_free, 1)

                    def Q(q):
                        src = begin(("Q", q))
                        dve.tensor_tensor(q_rows[:, q, :, :], src.rearrange("p (h n) -> p h n", h=REP),
                                          qw[:, :].unsqueeze(1).to_broadcast([P, REP, HD]), ALU.mult)\
                           .then_inc(item_free, 1)

                    def rotate(rows, n, cos, sin):
                        bc = by_cos[:, 0:n * HD].rearrange("p (n i d) -> p n i d", n=n, i=2)
                        bs = by_sin[:, 0:n * HD].rearrange("p (n i d) -> p n i d", n=n, i=2)
                        dve.tensor_tensor(bs, rows, sin, ALU.mult)
                        step(dve.tensor_tensor(bc, rows, cos, ALU.mult))
                        dve.tensor_tensor(rows[:, :, 0, :], bc[:, :, 0, :], bs[:, :, 1, :], ALU.subtract)
                        step(dve.tensor_tensor(rows[:, :, 1, :], bc[:, :, 1, :], bs[:, :, 0, :], ALU.add))

                    def KN(c):
                        if c == 0:
                            dve.wait_ge(k_rstd, 1)
                            dve.wait_ge(item_free, number[("KV", KT - 1)] + 1)
                            if rope and norm:
                                dve.wait_ge(tab_in, 16)
                        n = 5 if rope else KT
                        t0 = n * c
                        rows = k_rows[:, t0:t0 + n, :]
                        step(dve.tensor_tensor(rows, rows, k_sq[:, 2, t0:t0 + n].unsqueeze(2)
                                               .to_broadcast([P, n, HD]), ALU.mult))
                        if rope:
                            rotate(rows.rearrange("p n (i d) -> p n i d", i=2), n,
                                   cs[:, 0, t0:t0 + n, :].unsqueeze(2).to_broadcast([P, n, 2, half]),
                                   cs[:, 1, t0:t0 + n, :].unsqueeze(2).to_broadcast([P, n, 2, half]))
                        dve.engine_nop().then_inc(k_ready, 1)

                    def QN(q):
                        if q == 0:
                            dve.wait_ge(q_rstd, 1)
                            dve.wait_ge(item_free, number[("Q", QT - 1)] + 1)
                        rows = q_rows[:, q, :, :]
                        step(dve.tensor_tensor(rows, rows, q_sq[:, 2, q * REP:(q + 1) * REP].unsqueeze(2)
                                               .to_broadcast([P, REP, HD]), ALU.mult))
                        if rope:
                            rotate(rows.rearrange("p n (i d) -> p n i d", i=2), REP,
                                   cs[:, 0, CTILES + q, :].unsqueeze(1).unsqueeze(1).to_broadcast([P, REP, 2, half]),
                                   cs[:, 1, CTILES + q, :].unsqueeze(1).unsqueeze(1).to_broadcast([P, REP, 2, half]))
                        dve.engine_nop().then_inc(q_normed, 1)

                    def KX(k):
                        a0, e0 = KEND[KB[k][0]], KEND[KB[k][1]]
                        low(("KX", k), kt_n[1][:, a0:e0], kt_n[0][:, a0:e0], e0 - a0)

                    def QX(k):
                        low(("QX", k), qt_n[1][:, k * 512:(k + 1) * 512], qt_n[0][:, k * 512:(k + 1) * 512], 512)

                    def OX(k):
                        low(("OX", k), ot[1][:, k * 512:(k + 1) * 512], ot[0][:, k * 512:(k + 1) * 512], 512)

                    def Y(q):
                        src = begin(("Y", q))
                        dve.tensor_tensor(x_b[:, q, :], x_b[:, q, :], src[:, 0:D], ALU.add).then_inc(item_free, 1)
                        dve.wait_ge(item_free, number[("Y", q)] + 1)
                        dve.engine_nop().then_inc(x_done, 1)

                    def R(r):
                        j = rough_block(r)[0]
                        a0, _e0, e = RH[r % 2]
                        dve.wait_ge(r_ready, r_count[r] + 1)
                        ins = dve.tensor_reduce(neg2[:, j, r % 2:r % 2 + 1],
                                                m.ps[:, 0:2, :].rearrange("p b n -> p (b n)")[:, 0:e - a0],
                                                AX.X, ALU.max, negate=True)
                        if r % 2 == 0:
                            ins.then_inc(neg_done, 1)
                            return
                        step(ins)
                        dve.wait_ge(neg_done, r_count[r])
                        dve.tensor_tensor(negmax[:, j:j + 1], neg2[:, j, 0:1], neg2[:, j, 1:2], ALU.min)\
                           .then_inc(neg_done, 1)

                    def outputs(G):
                        dve.wait_ge(pv_done, KT * (G + 1))
                        o = m.ps[:, 6:8, :].rearrange("p b (i n) -> p (b i) n", i=2)
                        step(dve.reciprocal(rsum[:, :].unsqueeze(2), o[:, :, HD:VW]))
                        if G == 0 and tail:
                            dve.wait_ge(item_free, number[("OX", 1)] + 1)
                        dve.tensor_tensor(o_rows[:, G * JG:(G + 1) * JG, :], o[:, :, 0:HD],
                                          rsum[:, :].unsqueeze(2).to_broadcast([P, JG, HD]), ALU.mult)\
                           .then_inc(o_done, 1)

                    def NZ(_i):
                        dve.wait_ge(nrstd_ok, 1)
                        for q in range(QT):
                            dve.tensor_scalar(z[:, q, :], x_n[:, q, :], mv[:, q, 0:1], rstd[:, 1, q:q + 1],
                                              ALU.subtract, ALU.mult).then_inc(z_ok, 1)

                    does = {"W": W, "N": N, "NX": NX, "KV": KV, "Q": Q, "KN": KN, "QN": QN, "KX": KX, "QX": QX,
                            "OX": OX, "Y": Y, "R": R}
                    for n in range(TURNS):
                        if attend and n == KT + 1:
                            outputs(0)
                        for task, i in turns[n]:
                            if task == "NX":
                                NZ(i)
                            does[task](i)
                    if attend:
                        outputs(1)
                    if store is not None and prepare:
                        dve.wait_ge(stored, 16)
                        dve.tensor_copy(x_b[:, :, :], x_n[:, :, :]).then_inc(x_copied, 1)
            st.clear()

        group_block(-1, 0, attend=False, norm=True, tail=False)
        with nc.Fori(0, B) as b:
            before = m.x_pad[bass.ds(b * QT, QT), :].rearrange("t (p d) -> p t d", p=P)
            for a in range(KVH):
                group_block(a, (b + 1) % B if a == KVH - 1 else None, norm=(a == KVH - 1),
                            store=before if a == 0 else None)
        last = m.x_dram[(B - 1) * QT:B * QT, :].rearrange("t (p d) -> p t d", p=P)
        group_block(KVH, None, attend=False, prepare=False, store=last)
NE = 8
TOK = B * S
HALF = 512


class FfnBase:

    def __init__(self, st, keep_z=False):
        self.x = st.sb("x", [P, TT, D])
        self.z = st.sb("z", [P, TT, D])
        self.zt = [st.sb(f"zt{i}", [P, DC, TOK], F32R) for i in range(2)]
        self.scratch = (st.sb("stats", [P, TT, 6]), st.sb("mv", [P, TT, 2]), st.sb("rstd", [P, 2, TT]), self.z)
        self.nsem = [st.sem("n_" + n) for n in ("loaded", "step", "var", "rstd", "turned", "hi", "lo")]

    def norm(self, nc, st, m, extra=()):
        norm_block(nc, st, m, self.x, self.zt[0], self.zt[1], TT,
                   m.x_dram[:, :].rearrange("t (p d) -> p t d", p=P), self.nsem, self.scratch, extra,
                   name=f"{st.name}_norm")
        st.clear()

    def store(self, nc, st, m):
        with nc.Block(name=f"{st.name}_out") as block:
            @block.sync
            def _(sp):
                sp.dma_start(m.x_dram[:, :].rearrange("t (p d) -> p t d", p=P), self.x[:, :, :])\
                  .then_inc(self.nsem[0], 16)
                sp.wait_ge(self.nsem[0], 16)
        st.clear()


class Gates:

    def __init__(self, st):
        self.wg_f = st.sb("wg_f", [P, DC, NE])
        self.wg = [st.sb(f"wg{i}", [P, DC, NE], F32R) for i in range(2)]
        self.bias = st.sb("gate_bias", [P, NE])
        self.logit = st.sb("logit", [P, TT, NE])
        self.prob = st.sb("prob", [P, TT, NE])
        self.row = st.sb("gate_row", [P, 2, TT])
        self.top = st.sb("top", [P, TT, 8])
        self.index = st.sb("index", [P, TT, 8], U32)
        self.index_f = st.sb("index_f", [P, TT, 8])
        self.iota_i = st.sb("iota_i", [P, NE], I32)
        self.iota = st.sb("iota", [P, NE])
        self.hot = st.sb("hot", [P, 2, TT, NE])
        self.sems = [st.sem("g_" + n) for n in ("split", "logits", "step", "shifted", "exped", "iota")]

    def route(self, nc, st, m, zt, comb, bias, topk, renorm):
        split, logits, dstep, shifted, exped, iota_ok = self.sems
        with nc.Block(name=f"{st.name}_route") as block:
            @block.scalar
            def _(act):
                act.activation(self.wg[0][:, :, :], self.wg_f[:, :, :], ACT.Copy).then_inc(split, 1)
                act.wait_ge(shifted, 1)
                act.activation(self.prob[:, :, :], self.logit[:, :, :], ACT.Exp).then_inc(exped, 1)

            @block.gpsimd
            def _(pool):
                pool.iota(self.iota_i[:, :], pattern=[[1, NE]], base=0, channel_multiplier=0).then_inc(iota_ok, 1)

            @block.tensor
            def _(pe):
                pe.wait_ge(split, 2)
                for t in range(TT):
                    n = 0
                    for c in range(DC):
                        for s, v in ((0, 0), (0, 1), (1, 0)):
                            ins = pe.matmul(m.ps[:, 0, t * NE:(t + 1) * NE], zt[s][:, c, t * P:(t + 1) * P],
                                            self.wg[v][:, c, :], start=(n == 0), stop=(n == 3 * DC - 1))
                            n += 1
                ins.then_inc(logits, 1)

            @block.vector
            def _(dve):
                step = Step(dve, dstep)

                def each(a):
                    return a.unsqueeze(2).to_broadcast([P, TT, NE])

                dve.wait_ge(split, 1)
                dve.tensor_tensor(self.wg[1][:, :, :], self.wg_f[:, :, :], self.wg[0][:, :, :].bitcast(F32),
                                  ALU.subtract).then_inc(split, 1)
                dve.wait_ge(iota_ok, 1)
                step(dve.tensor_copy(self.iota[:, :], self.iota_i[:, :]))
                dve.wait_ge(logits, 1)
                ps = m.ps[:, 0, 0:TT * NE].rearrange("p (t e) -> p t e", e=NE)
                if bias:
                    step(dve.tensor_tensor(self.logit[:, :, :], ps,
                                           self.bias[:, :].unsqueeze(1).to_broadcast([P, TT, NE]), ALU.add))
                else:
                    step(dve.tensor_copy(self.logit[:, :, :], ps))
                step(dve.tensor_reduce(self.row[:, 0, :], self.logit[:, :, :], AX.X, ALU.max))
                dve.tensor_tensor(self.logit[:, :, :], self.logit[:, :, :], each(self.row[:, 0, :]),
                                  ALU.subtract).then_inc(shifted, 1)
                dve.wait_ge(exped, 1)
                step(dve.tensor_reduce(self.row[:, 0, :], self.prob[:, :, :], AX.X, ALU.add))
                step(dve.reciprocal(self.row[:, 1, :], self.row[:, 0, :]))
                step(dve.tensor_tensor(self.prob[:, :, :], self.prob[:, :, :], each(self.row[:, 1, :]), ALU.mult))
                for t in range(TT):
                    ins = dve.max(out=self.top[:, t, :], in_=self.prob[:, t, :])
                step(ins)
                for t in range(TT):
                    ins = dve.max_index(out=self.index[:, t, :], in_max=self.top[:, t, :],
                                        in_values=self.prob[:, t, :])
                step(ins)
                step(dve.tensor_copy(self.index_f[:, :, :], self.index[:, :, :]))
                if renorm:
                    step(dve.tensor_tensor(self.row[:, 0, :], self.top[:, :, 0], self.top[:, :, 1], ALU.add))
                    step(dve.reciprocal(self.row[:, 1, :], self.row[:, 0, :]))
                    step(dve.tensor_tensor(self.top[:, :, 0:2], self.top[:, :, 0:2],
                                           self.row[:, 1, :].unsqueeze(2).to_broadcast([P, TT, 2]), ALU.mult))
                for k in range(topk):
                    step(dve.tensor_tensor(self.hot[:, k, :, :],
                                           self.iota[:, :].unsqueeze(1).to_broadcast([P, TT, NE]),
                                           each(self.index_f[:, :, k]), ALU.is_equal))
                if comb is not None:
                    for k in range(topk):
                        step(dve.tensor_tensor(self.hot[:, k, :, :], self.hot[:, k, :, :],
                                               each(self.top[:, :, k]), ALU.mult))
                    step(dve.tensor_tensor(comb[:, :, 0:NE], self.hot[:, 0, :, :], self.hot[:, 1, :, :], ALU.add))
        st.clear()


def gelu_experts(nc, m, w):
    H = 512
    HC = H // P
    with Stage(nc, "f0") as st:
        f = FfnBase(st)
        gates = Gates(st)
        comb = st.sb("comb", [P, TT, NE])
        comb_t = st.sb("comb_t", [NE, TOK])
        b3 = st.sb("b3", [NE, D])
        comb_e = st.sb("comb_e", [P, TT])
        wf = st.sb("wf", [P, 2 * H + HC * H + HC * D])
        wr = [st.sb(f"wr{i}", [P, 2 * H + HC * H + HC * D], F32R) for i in range(2)]
        cuts = [0, DC * H, DC * H + HC * H, DC * H + HC * H + HC * D]
        bias = st.sb("bias", [P, 2 * HC])
        full = st.sb("full", [P, 3, HALF])
        h = [[st.sb(f"h{l}{i}", [P, HC, TOK], F32R) for i in range(2)] for l in range(2)]
        turned, copied, b3_ready, b3_done = [st.sem(n) for n in ("turned", "copied", "b3_ready", "b3_done")]
        w_in = [st.sem(f"w_in{i}") for i in range(3)]
        bias_in, w_hi, w_lo, comb_ok, h_ready, full_done, hi_done, lo_done, y_ready, y_done = [
            st.sem(n) for n in ("bias_in w_hi w_lo comb_ok h_ready full_done hi_done lo_done y_ready y_done").split()]
        f.norm(nc, st, m, [(flat2(gates.wg_f[:, :, :]), w["wg"]),
                           (gates.bias[:, :], w["bg"].partition_broadcast(P)), (b3[:, :], w["b3"])])
        gates.route(nc, st, m, f.zt, comb, True, 2, False)

        with nc.Block(name="f0_b3") as block:
            @block.tensor
            def _(pe):
                for t in range(TT):
                    ins = pe.transpose(m.ps[0:NE, t // 4, (t % 4) * P:(t % 4 + 1) * P], comb[:, t, :], m.ident[:, :])
                ins.then_inc(turned, 1)
                pe.wait_ge(copied, 1)
                for t in range(TT):
                    if t >= 4:
                        pe.wait_ge(b3_done, t - 3)
                    pe.matmul(m.ps[:, 4 + t % 4, 0:D], comb_t[:, t * P:(t + 1) * P], b3[:, :],
                              start=True, stop=True).then_inc(b3_ready, 1)

            @block.vector
            def _(dve):
                dve.wait_ge(turned, 1)
                dve.tensor_copy(comb_t[:, :], flat2(m.ps[0:NE, 0:2, :])).then_inc(copied, 1)
                for t in range(TT):
                    dve.wait_ge(b3_ready, t + 1)
                    dve.tensor_tensor(f.x[:, t, :], f.x[:, t, :], m.ps[:, 4 + t % 4, 0:D], ALU.add)\
                       .then_inc(b3_done, 1)
        st.clear()

        units = [(l, hf, o) for l in range(2) for hf in range(2) for o in range(HC)]

        def done_by(layer, hf):
            return (layer * 2 + hf + 1) * HC

        with nc.Fori(0, NE) as e:
            with nc.Block(name="f0_expert") as block:
                @block.sync
                def _(sp):
                    for i in range(3):
                        sp.dma_start(wf[:, cuts[i]:cuts[i + 1]], w[f"w{i + 1}"][bass.ds(e, 1), :, :]
                                     .rearrange("a p n -> p (a n)")).then_inc(w_in[i], 16)
                    sp.dma_start(bias[:, :], w["b12"][bass.ds(e, 1), :, :].rearrange("a p n -> p (a n)"))\
                      .then_inc(bias_in, 16)

                @block.tensor
                def _(pe):
                    def wpart(v, l, k, o, n):
                        at = cuts[l] + k * (D if l == 2 else H) + o
                        return wr[v][:, at:at + n]

                    for u, (l, hf, o) in enumerate(units):
                        pe.wait_ge(w_hi, l + 1)
                        pe.wait_ge(w_lo, l + 1)
                        if u >= 6:
                            pe.wait_ge(lo_done, u - 5)
                        if l == 1:
                            pe.wait_ge(lo_done, done_by(0, hf))
                        src = f.zt if l == 0 else h[0]
                        K = DC if l == 0 else HC
                        n = 0
                        for k in range(K):
                            for s, v in ((0, 0), (1, 0), (0, 1)):
                                ins = pe.matmul(m.ps[:, u % 6, :], wpart(v, l, k, o * P, P),
                                                src[s][:, k, hf * HALF:(hf + 1) * HALF],
                                                start=(n == 0), stop=(n == 3 * K - 1))
                                n += 1
                        ins.then_inc(h_ready, 1)
                    pe.wait_ge(w_hi, 3)
                    pe.wait_ge(w_lo, 3)
                    for t in range(TT):
                        pe.wait_ge(lo_done, done_by(1, t * P // HALF))
                        if t >= 2:
                            pe.wait_ge(y_done, t - 1)
                        n = 0
                        for k in range(HC):
                            for s, v in ((0, 0), (0, 1), (1, 0)):
                                ins = pe.matmul(m.ps[:, 6 + t % 2, 0:D], h[1][s][:, k, t * P:(t + 1) * P],
                                                wpart(v, 2, k, 0, D), start=(n == 0), stop=(n == 3 * HC - 1))
                                n += 1
                        ins.then_inc(y_ready, 1)

                @block.scalar
                def _(act):
                    for i in range(3):
                        act.wait_ge(w_in[i], 16)
                        act.activation(wr[0][:, cuts[i]:cuts[i + 1]], wf[:, cuts[i]:cuts[i + 1]], ACT.Copy)\
                           .then_inc(w_hi, 1)
                    act.wait_ge(bias_in, 16)
                    for u, (l, hf, o) in enumerate(units):
                        act.wait_ge(h_ready, u + 1)
                        if u >= 3:
                            act.wait_ge(lo_done, u - 2)
                        b = bias[:, l * HC + o:l * HC + o + 1]
                        act.activation(full[:, u % 3, :], m.ps[:, u % 6, :], ACT.Gelu, bias=b).then_inc(full_done, 1)
                        act.activation(h[l][0][:, o, hf * HALF:(hf + 1) * HALF], m.ps[:, u % 6, :], ACT.Gelu,
                                       bias=b).then_inc(hi_done, 1)

                @block.vector
                def _(dve):
                    dve.tensor_copy(comb_e[:, :], comb[:, :, bass.ds(e, 1)].rearrange("p t a -> p (t a)"))\
                       .then_inc(comb_ok, 1)
                    for i in range(3):
                        dve.wait_ge(w_hi, i + 1)
                        dve.tensor_tensor(wr[1][:, cuts[i]:cuts[i + 1]], wf[:, cuts[i]:cuts[i + 1]],
                                          wr[0][:, cuts[i]:cuts[i + 1]].bitcast(F32), ALU.subtract)\
                           .then_inc(w_lo, 1)
                    for u, (l, hf, o) in enumerate(units):
                        dve.wait_ge(hi_done, u + 1)
                        cols = slice(hf * HALF, (hf + 1) * HALF)
                        dve.tensor_tensor(h[l][1][:, o, cols], full[:, u % 3, :],
                                          h[l][0][:, o, cols].bitcast(F32), ALU.subtract).then_inc(lo_done, 1)
                    dve.wait_ge(comb_ok, 1)
                    for t in range(TT):
                        dve.wait_ge(y_ready, t + 1)
                        dve.scalar_tensor_tensor(out=f.x[:, t, :], in0=m.ps[:, 6 + t % 2, 0:D],
                                                 scalar=comb_e[:, t:t + 1], in1=f.x[:, t, :],
                                                 op0=ALU.mult, op1=ALU.add).then_inc(y_done, 1)
            st.clear()
        f.store(nc, st, m)


def scaled_linear(nc, m, w):
    with Stage(nc, "f1") as st:
        f = FfnBase(st)
        wf = st.sb("wf", [P, DC, D])
        wr = [st.sb(f"wr{i}", [P, DC, D], F32R) for i in range(2)]
        scale = st.sb("scale", [P, D])
        bias = st.sb("bias", [P, D])
        w_full, w_hi, w_lo, y_ready, y_done, dstep = [
            st.sem(n) for n in ("w_full", "w_hi", "w_lo", "y_ready", "y_done", "dstep")]
        f.norm(nc, st, m, [(flat2(wf[:, :, :]), w["w"]), (scale[:, :], w["scale"].partition_broadcast(P)),
                           (bias[:, :], w["bias"].partition_broadcast(P))])
        with nc.Block(name="f1_linear") as block:
            @block.vector
            def _(dve):
                dve.tensor_tensor(wf[:, :, :], wf[:, :, :], scale[:, :].unsqueeze(1).to_broadcast([P, DC, D]),
                                  ALU.mult).then_inc(w_full, 1)
                dve.wait_ge(w_hi, 1)
                dve.tensor_tensor(wr[1][:, :, :], wf[:, :, :], wr[0][:, :, :].bitcast(F32),
                                  ALU.subtract).then_inc(w_lo, 1)
                step = Step(dve, dstep)
                step(dve.tensor_tensor(f.x[:, :, :], f.x[:, :, :],
                                       bias[:, :].unsqueeze(1).to_broadcast([P, TT, D]), ALU.add))
                for t in range(TT):
                    dve.wait_ge(y_ready, t + 1)
                    dve.tensor_tensor(f.x[:, t, :], f.x[:, t, :], m.ps[:, t, 0:D], ALU.add).then_inc(y_done, 1)

            @block.scalar
            def _(act):
                act.wait_ge(w_full, 1)
                act.activation(wr[0][:, :, :], wf[:, :, :], ACT.Copy).then_inc(w_hi, 1)

            @block.tensor
            def _(pe):
                pe.wait_ge(w_lo, 1)
                for t in range(TT):
                    n = 0
                    for c in range(DC):
                        for s, v in ((0, 0), (0, 1), (1, 0)):
                            ins = pe.matmul(m.ps[:, t, 0:D], f.zt[s][:, c, t * P:(t + 1) * P], wr[v][:, c, :],
                                            start=(n == 0), stop=(n == 3 * DC - 1))
                            n += 1
                    ins.then_inc(y_ready, 1)
        st.clear()
        f.store(nc, st, m)


class GatedUnits:

    def __init__(self, st, per):
        self.per = per
        self.wf = st.sb("u_wf", [P, 2, (DC * 2 + 2) * P])
        self.wr = [st.sb(f"u_wr{i}", [P, 2, (DC * 2 + 2) * P], F32R) for i in range(2)]
        self.act = st.sb("u_act", [P, 2, HALF])
        self.full = st.sb("u_full", [P, 2, HALF])
        self.h = [st.sb(f"u_h{i}", [P, 2, TOK], F32R) for i in range(2)]
        self.weight = st.sb("u_weight", [P, per, TT])
        self.sems = [st.sem("u_" + n) for n in
                     "in0 in1 w_hi w_lo weight gu_ready silu_done full_done hi_done lo_done y_ready y_done".split()]

    def block(self, nc, m, f, src, weight, name, sizes):
        (in0, in1, w_hi, w_lo, weight_ok, gu_ready, silu_done, full_done, hi_done, lo_done, y_ready,
         y_done) = self.sems
        per, GU = self.per, DC * 2 * P
        halves = [(u, hf) for u in range(per) for hf in range(2)]
        with nc.Block(name=name) as block:
            @block.sync
            def _(sp):
                for u in range(per):
                    if u >= 2:
                        sp.wait_ge(w_hi, u - 1)
                        sp.wait_ge(w_lo, u - 1)
                    sp.dma_start(self.wf[:, u % 2, :], src(u)).then_inc((in0, in1)[u % 2], 16)

            @block.scalar
            def _(act):
                def split(u):
                    act.wait_ge((in0, in1)[u % 2], 16 * (u // 2 + 1))
                    if u >= 2:
                        act.wait_ge(y_ready, TT * (u - 1))
                    act.activation(self.wr[0][:, u % 2, :], self.wf[:, u % 2, :], ACT.Copy).then_inc(w_hi, 1)

                split(0)
                if per > 1:
                    split(1)
                for i, (u, hf) in enumerate(halves):
                    r = sizes[u]
                    bank = 2 * (i % 3)
                    act.wait_ge(gu_ready, i + 1)
                    if i >= 2:
                        act.wait_ge(full_done, i - 1)
                    act.activation(self.act[0:r, i % 2, :], m.ps[0:r, bank, :], ACT.Silu).then_inc(silu_done, 1)
                    act.wait_ge(full_done, i + 1)
                    if i >= 4:
                        act.wait_ge(y_ready, TT * (u - 1))
                    act.activation(self.h[0][0:r, u % 2, hf * HALF:(hf + 1) * HALF], self.full[0:r, i % 2, :],
                                   ACT.Copy).then_inc(hi_done, 1)
                    if hf and u + 1 < per and u >= 1:
                        split(u + 1)

            @block.vector
            def _(dve):
                if weight is not None:
                    dve.tensor_copy(self.weight[:, :, :], weight).then_inc(weight_ok, 1)

                def split(u):
                    dve.wait_ge(w_hi, u + 1)
                    dve.tensor_tensor(self.wr[1][:, u % 2, :], self.wf[:, u % 2, :],
                                      self.wr[0][:, u % 2, :].bitcast(F32), ALU.subtract).then_inc(w_lo, 1)

                def outputs(u):
                    for t in range(TT):
                        dve.wait_ge(y_ready, u * TT + t + 1)
                        y = m.ps[:, 6 + t % 2, 0:D]
                        if u and not t:
                            dve.wait_ge(y_done, u * TT)
                        if weight is None:
                            ins = dve.tensor_tensor(f.x[:, t, :], f.x[:, t, :], y, ALU.add)
                        else:
                            ins = dve.scalar_tensor_tensor(out=f.x[:, t, :], in0=y,
                                                           scalar=self.weight[:, u, t:t + 1],
                                                           in1=f.x[:, t, :], op0=ALU.mult, op1=ALU.add)
                        ins.then_inc(y_done, 1)

                split(0)
                if per > 1:
                    split(1)
                if weight is not None:
                    dve.wait_ge(weight_ok, 1)
                for i, (u, hf) in enumerate(halves):
                    r = sizes[u]
                    bank = 2 * (i % 3)
                    dve.wait_ge(silu_done, i + 1)
                    if i >= 2:
                        dve.wait_ge(lo_done, i - 1)
                        dve.wait_ge(hi_done, i - 1)
                    dve.tensor_tensor(self.full[0:r, i % 2, :], self.act[0:r, i % 2, :], m.ps[0:r, bank + 1, :],
                                      ALU.mult).then_inc(full_done, 1)
                    dve.wait_ge(hi_done, i + 1)
                    cols = slice(hf * HALF, (hf + 1) * HALF)
                    dve.tensor_tensor(self.h[1][0:r, u % 2, cols], self.full[0:r, i % 2, :],
                                      self.h[0][0:r, u % 2, cols].bitcast(F32), ALU.subtract).then_inc(lo_done, 1)
                    if hf and u >= 1:
                        outputs(u - 1)
                        if u + 1 < per:
                            split(u + 1)
                outputs(per - 1)

            @block.tensor
            def _(pe):
                def down(u):
                    pe.wait_ge(lo_done, 2 * u + 2)
                    r = sizes[u]
                    for t in range(TT):
                        if u * TT + t >= 2:
                            pe.wait_ge(y_done, u * TT + t - 1)
                        for n, (s, v) in enumerate(((0, 0), (0, 1), (1, 0))):
                            ins = pe.matmul(m.ps[:, 6 + t % 2, 0:D], self.h[s][0:r, u % 2, t * P:(t + 1) * P],
                                            self.wr[v][0:r, u % 2, GU:GU + D], start=(n == 0), stop=(n == 2))
                        ins.then_inc(y_ready, 1)

                for i, (u, hf) in enumerate(halves):
                    r = sizes[u]
                    bank = 2 * (i % 3)
                    pe.wait_ge(w_hi, u + 1)
                    pe.wait_ge(w_lo, u + 1)
                    if i >= 3:
                        pe.wait_ge(full_done, i - 2)
                    for part in range(2):
                        n = 0
                        for c in range(DC):
                            at = c * 2 * P + part * P
                            for s, v in ((0, 0), (1, 0), (0, 1)):
                                ins = pe.matmul(m.ps[0:r, bank + part, :], self.wr[v][:, u % 2, at:at + r],
                                                f.zt[s][:, c, hf * HALF:(hf + 1) * HALF],
                                                start=(n == 0), stop=(n == 3 * DC - 1))
                                n += 1
                    ins.then_inc(gu_ready, 1)
                    if hf and u:
                        down(u - 1)
                down(per - 1)


def silu_experts(nc, m, w):
    SHARED, PER = 4, 4
    with Stage(nc, "f3") as st:
        f = FfnBase(st)
        gates = Gates(st)
        comb = st.sb("comb", [P, TT, NE + SHARED])
        units = GatedUnits(st, PER)
        ones_ok = st.sem("ones_ok")
        f.norm(nc, st, m, [(flat2(gates.wg_f[:, :, :]), w["wg"])])
        with nc.Block(name="f3_ones") as block:
            @block.gpsimd
            def _(pool):
                pool.memset(comb[:, :, NE:], 1.0).then_inc(ones_ok, 1)
        gates.route(nc, st, m, f.zt, comb, False, 2, True)
        with nc.Fori(0, (NE + SHARED) // PER) as e:
            units.block(nc, m, f, lambda u: w["units"][bass.ds(e * PER + u, 1), :, :].rearrange("a p n -> p (a n)"),
                        comb[:, :, bass.ds(e * PER, PER)].rearrange("p t e -> p e t"), "f3_units", [P] * PER)
            st.clear()
        f.store(nc, st, m)


def capacity_experts(nc, m, w):
    C = TOK // NE
    H = 352
    SIZES = [min(P, H - a) for a in range(0, H, P)]
    HC = len(SIZES)
    DROPPED = 4.0 * TOK
    with Stage(nc, "f2") as st:
        f = FfnBase(st)
        gates = Gates(st)
        units = GatedUnits(st, HC)
        upper = st.sb("upper", [P, P])
        slot_i = st.sb("slot_i", [P, NE * C], I32)
        slot = st.sb("slot", [P, NE * C])
        row_i = st.sb("row_i", [P, NE], I32)
        row_f = st.sb("row_f", [P, NE])
        place = st.sb("place", [P, TT, NE])
        flat = st.sb("flat", [P, 3, TT])
        hot = st.sb("hot_slots", [P, 2, NE * C])
        wf = st.sb("wf", [P, 2 * DC * H + HC * D])
        xd = st.sb("xd", [P, DC, NE * C])
        xe = st.sb("xe", [P, DC, C])
        act_g = st.sb("act_g", [P, HC, C])
        hid = st.sb("hid", [P, HC, C])
        oe = st.sb("oe", [P, NE, D])
        oe_e = st.sb("oe_e", [P, D])
        flat_b = st.sb("flat_b", [P, TOK])
        taken = st.sb("taken", [P, 2, TOK])
        made, rstep, ranked, flat_ok, hot_ok, disp, xd_ok, fb_ready, fb_ok = [
            st.sem(n) for n in "made rstep ranked flat_ok hot_ok disp xd_ok fb_ready fb_ok".split()]
        w_in, xe_ok, g_ready, silu_ok, hid_ok, oe_ready, oe_ok = [
            st.sem(n) for n in "w_in xe_ok g_ready silu_ok hid_ok oe_ready oe_ok".split()]
        dt_ok, dt_used, y_done = [st.sem(n) for n in "dt_ok dt_used y_done".split()]
        f.norm(nc, st, m, [(flat2(gates.wg_f[:, :, :]), w["wg"])])
        gates.route(nc, st, m, f.zt, None, False, 1, False)
        first = gates.hot[:, 0, :, :]

        with nc.Block(name="f2_dispatch") as block:
            @block.gpsimd
            def _(pool):
                pool.memset(upper[:, :], 1.0).then_inc(made, 1)
                pool.wait_ge(made, 1)
                pool.affine_select(out=upper[:, :], in_=upper[:, :], compare_op=ALU.is_ge, fill=0.0, base=0,
                                   pattern=[[1, P]], channel_multiplier=-1).then_inc(made, 1)
                pool.iota(slot_i[:, :], pattern=[[1, NE * C]], base=0, channel_multiplier=0).then_inc(made, 1)
                pool.iota(row_i[:, :], pattern=[[C, NE]], base=0, channel_multiplier=1).then_inc(made, 1)

            @block.tensor
            def _(pe):
                pe.wait_ge(made, 2)
                for t in range(TT):
                    for k in range(t + 1):
                        ins = pe.matmul(m.ps[:, 0, t * NE:(t + 1) * NE], upper[:, :] if k == t else m.onesf[:, :],
                                        first[:, k, :], start=(k == 0), stop=(k == t))
                ins.then_inc(ranked, 1)
                pe.wait_ge(flat_ok, 1)
                for t in range(TT):
                    ins = pe.matmul(m.ps[:, 5 + t // 4, (t % 4) * P:(t % 4 + 1) * P],
                                    flat[:, 1, t:t + 1].to_broadcast([P, P]), m.ident[:, :], start=True, stop=True)
                ins.then_inc(fb_ready, 1)
                for t in range(TT):
                    pe.wait_ge(hot_ok, t + 1)
                    for c in range(DC):
                        for s in range(2):
                            ins = pe.matmul(m.ps[:, 1 + 2 * c + s, :], f.z[:, t, c * P:(c + 1) * P],
                                            hot[:, t % 2, s * 512:(s + 1) * 512],
                                            start=(t == 0), stop=(t == TT - 1))
                    ins.then_inc(disp, 1)

            @block.vector
            def _(dve):
                step = Step(dve, rstep)
                dve.wait_ge(made, 4)
                step(dve.tensor_copy(slot[:, :], slot_i[:, :]))
                step(dve.tensor_copy(row_f[:, :], row_i[:, :]))
                dve.wait_ge(ranked, 1)
                step(dve.tensor_tensor(place[:, :, :], m.ps[:, 0, 0:TT * NE].rearrange("p (t e) -> p t e", e=NE),
                                       first, ALU.mult))
                step(dve.tensor_reduce(flat[:, 0, :], place[:, :, :], AX.X, ALU.add))
                step(dve.tensor_scalar(flat[:, 2, :], flat[:, 0, :], float(C), DROPPED, ALU.is_gt, ALU.mult))
                step(dve.tensor_tensor(flat[:, 2, :], flat[:, 2, :], flat[:, 0, :], ALU.add))
                step(dve.tensor_scalar(flat[:, 1, :], gates.index_f[:, :, 0], float(C), -1.0, ALU.mult, ALU.add))
                dve.tensor_tensor(flat[:, 1, :], flat[:, 1, :], flat[:, 2, :], ALU.add).then_inc(flat_ok, 1)
                dve.wait_ge(flat_ok, 1)
                for t in range(TT):
                    if t >= 2:
                        dve.wait_ge(disp, t - 1)
                    dve.tensor_scalar(hot[:, t % 2, :], slot[:, :], flat[:, 1, t:t + 1], None, ALU.is_equal)\
                       .then_inc(hot_ok, 1)
                dve.wait_ge(fb_ready, 1)
                dve.tensor_copy(flat_b[:, :], flat2(m.ps[:, 5:7, :])).then_inc(fb_ok, 1)

            @block.scalar
            def _(act):
                act.wait_ge(disp, TT)
                for c in range(DC):
                    act.activation(xd[:, c, :], flat2(m.ps[:, 1 + 2 * c:3 + 2 * c, :]), ACT.Copy).then_inc(xd_ok, 1)
        st.clear()

        units.block(nc, m, f, lambda u: w["units"][u, :, :], None, "f2_shared", SIZES)
        st.clear()

        with nc.Fori(0, NE) as e:
            with nc.Block(name="f2_expert") as block:
                @block.sync
                def _(sp):
                    sp.dma_start(wf[:, :], w["experts"][bass.ds(e, 1), :, :].rearrange("a p n -> p (a n)"))\
                      .then_inc(w_in, 16)

                @block.tensor
                def _(pe):
                    pe.wait_ge(w_in, 16)
                    pe.wait_ge(xe_ok, 1)
                    for part in range(2):
                        for o, r in enumerate(SIZES):
                            for c in range(DC):
                                at = (part * DC + c) * H + o * P
                                ins = pe.matmul(m.ps[0:r, part, o * P:o * P + C], wf[:, at:at + r], xe[:, c, :],
                                                start=(c == 0), stop=(c == DC - 1))
                            if o == HC - 1:
                                ins.then_inc(g_ready, 1)
                    for o, r in enumerate(SIZES):
                        pe.wait_ge(hid_ok, o + 1)
                        at = 2 * DC * H + o * D
                        ins = pe.matmul(m.ps[:, 2, 0:D], hid[0:r, o, :], wf[0:r, at:at + D],
                                        start=(o == 0), stop=(o == HC - 1))
                    ins.then_inc(oe_ready, 1)

                @block.scalar
                def _(act):
                    act.wait_ge(g_ready, 1)
                    for o, r in enumerate(SIZES):
                        act.activation(act_g[0:r, o, :], m.ps[0:r, 0, o * P:o * P + C], ACT.Silu).then_inc(silu_ok, 1)

                @block.vector
                def _(dve):
                    dve.tensor_copy(xe[:, :, :], xd[:, :, bass.ds(e * C, C)]).then_inc(xe_ok, 1)
                    dve.wait_ge(g_ready, 2)
                    for o, r in enumerate(SIZES):
                        dve.wait_ge(silu_ok, o + 1)
                        dve.tensor_tensor(hid[0:r, o, :], act_g[0:r, o, :], m.ps[0:r, 1, o * P:o * P + C],
                                          ALU.mult).then_inc(hid_ok, 1)
                    dve.wait_ge(oe_ready, 1)
                    dve.tensor_copy(oe[:, bass.ds(e, 1), :].rearrange("p a d -> p (a d)"), m.ps[:, 2, 0:D])\
                       .then_inc(oe_ok, 1)
            st.clear()

        with nc.Block(name="f2_combine") as block:
            @block.vector
            def _(dve):
                for e in range(NE):
                    if e >= 2:
                        dve.wait_ge(dt_used, e - 1)
                    dve.tensor_scalar(taken[:, e % 2, :], flat_b[:, :], row_f[:, e:e + 1], None, ALU.is_equal)\
                       .then_inc(dt_ok, 1)
                for t in range(TT):
                    dve.wait_ge(dt_used, NE)
                    dve.scalar_tensor_tensor(out=f.x[:, t, :], in0=m.ps[:, t, 0:D], scalar=gates.top[:, t, 0:1],
                                             in1=f.x[:, t, :], op0=ALU.mult, op1=ALU.add).then_inc(y_done, 1)

            @block.tensor
            def _(pe):
                for e in range(NE):
                    pe.wait_ge(dt_ok, e + 1)
                    for t in range(TT):
                        ins = pe.matmul(m.ps[:, t, 0:D], taken[:, e % 2, t * P:(t + 1) * P], oe[:, e, :],
                                        start=(e == 0), stop=(e == NE - 1))
                    ins.then_inc(dt_used, 1)
        st.clear()
        f.store(nc, st, m)
def image_text_attention(nc, m, w):
    NH, HDS = 16, 16
    IMG = 257
    LEAST = 65
    K_HI, K_LO, NEG = 0, 2 * HDS, 3 * HDS
    STK = 64
    GRP_AT = (0, IMG)
    tiles = ([(a, min(P, IMG - a), 0) for a in range(0, IMG, P)]
             + [(a, min(P, CTX - a), 1) for a in range(IMG, CTX, P)])
    KT = len(tiles)
    FIRST = (0, next(i for i, t in enumerate(tiles) if t[2]))
    LAST = (FIRST[1] - 1, KT - 1)
    NKEY = (IMG, CTX - IMG)
    VW2 = HDS + 1
    HP = NH // 2
    SCALE = HDS ** -0.5
    with Stage(nc, "a2") as st:
        x_b = st.sb("x_b", [P, QT, D])
        zt = [st.sb(f"zt{i}", [P, DC, S], F32R) for i in range(2)]
        ct = [st.sb(f"ct{i}", [P, DC, CTXP], F32R) for i in range(2)]
        scratch = (st.sb("stats", [P, QT, 6]), st.sb("mv", [P, QT, 2]), st.sb("rstd", [P, 2, QT]),
                   st.sb("z", [P, QT, D]))
        wide = [DC * 2 * D, DC * 2 * D, DC * D, DC * D]
        wr = [[st.sb(f"wr{k}{i}", [P, n], F32R) for i in range(2)] for k, n in enumerate(wide)]
        kv_bias = st.sb("kv_bias", [P, 2, 2 * D])
        qo_bias = st.sb("qo_bias", [P, 2, D])
        norm_w = st.sb("norm_w", [P, 3, D])
        k_rows = st.sb("k_rows", [P, KT, D])
        v_rows = st.sb("v_rows", [P, KT, NH, VW2])
        sq = st.sb("sq", [P, 3, KT + QT])
        square = st.sb("square", [P, 2, D])
        k_st = [[st.sb(f"k_st{g}{i}", [P, NH, STK], F32R) for i in range(2)] for g in range(2)]
        kt = st.sb("kt", [P, HP, KT * P], F32R)
        q_rows = st.sb("q_rows", [P, QT, D])
        q_st = st.sb("q_st", [P, QT, NH, STK], F32R)
        qt_a = st.sb("qt_a", [P, HP, S], F32R)
        qt_b = st.sb("qt_b", [P, 2, S], F32R)
        probs = st.sb("probs", [P, 3, 512])
        rs = st.sb("rs", [P, 2, 4])
        o_n = st.sb("o_n", [P, 2, 4, HDS])
        o_rows = st.sb("o_rows", [P, QT, D])
        nsem = [st.sem("n_" + n) for n in ("loaded", "step", "var", "rstd", "turned", "hi", "lo")]
        w_in = [st.sem(f"w_in{i}") for i in range(4)]
        w_hi, w_lo, small_in, zeroed, dstep, pstep = [st.sem(n) for n in "w_hi w_lo small_in zeroed dstep pstep".split()]
        (kv_ready, kb_done, sq_done, rstd_ok, kn_done, hi_done, lo_done, turned, ev_a, ev_b) = [
            st.sem(n) for n in "kv_ready kb_done sq_done rstd_ok kn_done hi_done lo_done turned ev_a ev_b".split()]
        (s_ready, neg_done, qb_turned, qb_done, st_ready, exp_done, pv_done, o_done) = [
            st.sem(n) for n in "s_ready neg_done qb_turned qb_done st_ready exp_done pv_done o_done".split()]

        wf = k_rows[:, :, :].rearrange("p t d -> p (t d)")
        at = [sum(wide[:k]) for k in range(5)]
        names = ("wkv_img", "wkv_txt", "wq", "wo")
        for lot in ((0, 1), (2, 3)):
            base = at[lot[0]]
            split_weights(nc, st, f"a2_weights{lot[0]}",
                          [(wf[:, at[k] - base:at[k + 1] - base], (wr[k][0][:, :], wr[k][1][:, :]), w[names[k]])
                           for k in lot], w_in[0:2], w_hi, w_lo)
        with nc.Block(name="a2_once") as block:
            @block.sync
            def _(sp):
                for dst, n in ((kv_bias[:, 0, 0:D], "k_img_b"), (kv_bias[:, 0, D:], "v_img_b"),
                               (kv_bias[:, 1, 0:D], "k_b"), (kv_bias[:, 1, D:], "v_b"),
                               (qo_bias[:, 0, :], "q_b"), (qo_bias[:, 1, :], "o_b"),
                               (norm_w[:, 0, :], "norm_k_img_w"), (norm_w[:, 1, :], "norm_k_w"),
                               (norm_w[:, 2, :], "norm_q_w")):
                    sp.dma_start(dst, w[n].partition_broadcast(P)).then_inc(small_in, 16)
                sp.wait_ge(small_in, 144)

            @block.gpsimd
            def _(pool):
                pool.memset(v_rows[:, :, :, :], 0.0).then_inc(zeroed, 1)
                pool.wait_ge(zeroed, 1)
                for t, (_a, r, _g) in enumerate(tiles):
                    pool.memset(v_rows[0:r, t, :, HDS:VW2], 1.0).then_inc(zeroed, 1)
                n = 1 + KT
                pool.memset(sq[:, :, :], 1.0).then_inc(zeroed, 1)
                pool.memset(q_st[:, :, :, :].bitcast(F32), 0.0).then_inc(zeroed, 1)
                for g in range(2):
                    for i in range(2):
                        pool.memset(k_st[g][i][:, :, :].bitcast(F32), 0.0).then_inc(zeroed, 1)
                pool.wait_ge(zeroed, n + 6)
                for g in range(2):
                    for i in range(2):
                        pool.memset(k_st[g][i][:, :, NEG + g:NEG + g + 1].bitcast(F32), 1.0).then_inc(zeroed, 1)
        st.clear()

        with nc.Fori(0, B) as b:
            x_rows = m.x_dram[bass.ds(b * QT, QT), :].rearrange("t (p d) -> p t d", p=P)
            norm_block(nc, st, m, x_b, zt[0], zt[1], QT, x_rows, nsem, scratch, [
                (flat2(ct[0][:, :, :]).bitcast(F32), m.ctx_hi[bass.ds(b, 1), :, :].rearrange("a p n -> p (a n)")),
                (flat2(ct[1][:, :, :]).bitcast(F32), m.ctx_lo[bass.ds(b, 1), :, :].rearrange("a p n -> p (a n)")),
            ], name="a2_norm")
            st.clear()

            with nc.Block(name="a2_keys") as block:
                @block.tensor
                def _(pe):
                    for t, (a, r, g) in enumerate(tiles):
                        M = max(r, LEAST)
                        if t >= 8:
                            pe.wait_ge(kb_done, t - 7)
                        n = 0
                        for c in range(DC):
                            for s, v in HALVES:
                                ins = pe.matmul(m.ps[0:M, t % 8, :], ct[s][:, c, a:a + M],
                                                wr[g][v][:, c * 2 * D:(c + 1) * 2 * D],
                                                start=(n == 0), stop=(n == 3 * DC - 1))
                                n += 1
                        ins.then_inc(kv_ready, 1)
                    pe.wait_ge(kb_done, KT)
                    for t in range(KT):
                        g, i = tiles[t][2], (t - FIRST[tiles[t][2]]) % 2
                        pe.wait_ge(lo_done, t + 1)
                        if t >= 4:
                            pe.wait_ge(ev_a, t - 3)
                            pe.wait_ge(ev_b, t - 3)
                        for hp in range(HP):
                            ins = pe.transpose(m.ps[:, 2 * (t % 4) + hp // 4, (hp % 4) * P:(hp % 4 + 1) * P]
                                               .bitcast(F32R), k_st[g][i][:, 2 * hp:2 * hp + 2, :]
                                               .rearrange("p a n -> p (a n)"), m.ident_r[:, :])
                        ins.then_inc(turned, 1)

                def evacuate(eng, t, half, done):
                    eng.wait_ge(turned, t + 1)
                    dst = kt[:, 4 * half:4 * half + 4, t * P:(t + 1) * P]
                    src = m.ps[:, 2 * (t % 4) + half, :].rearrange("p (h n) -> p h n", n=P)
                    return dst, src

                @block.scalar
                def _(act):
                    for t, (_a, r, g) in enumerate(tiles):
                        act.wait_ge(kb_done, t + 1)
                        if t >= 2:
                            act.wait_ge(sq_done, t - 1)
                        act.activation(square[0:r, t % 2, :], k_rows[0:r, t, :], ACT.Square,
                                       accum_out=sq[0:r, 0, t:t + 1]).then_inc(sq_done, 1)
                    for t in range(KT + 1):
                        if t < KT:
                            _a, r, g = tiles[t]
                            i = (t - FIRST[g]) % 2
                            act.wait_ge(kn_done, t + 1)
                            if t - 2 >= FIRST[g]:
                                act.wait_ge(turned, t - 1)
                            act.activation(k_st[g][i][0:r, :, 0:2 * HDS].rearrange("p h (a d) -> p h a d", a=2),
                                           k_rows[0:r, t, :].rearrange("p (h d) -> p h d", h=NH)
                                           .unsqueeze(2).to_broadcast([r, NH, 2, HDS]), ACT.Copy).then_inc(hi_done, 1)
                        if t:
                            dst, src = evacuate(act, t - 1, 0, ev_a)
                            act.activation(dst, src, ACT.Copy).then_inc(ev_a, 1)

                @block.gpsimd
                def _(pool):
                    step = Step(pool, pstep)
                    pool.wait_ge(sq_done, KT)
                    step(pool.tensor_scalar(sq[:, 1, 0:KT], sq[:, 0, 0:KT], 1.0 / D, 1e-6, ALU.mult, ALU.add))
                    pool.tensor_tensor(sq[:, 2, 0:KT], sq[:, 1, 0:KT], m.nhalf[:, 0:1].to_broadcast([P, KT]),
                                       ALU.pow).then_inc(rstd_ok, 1)

                @block.vector
                def _(dve):
                    for t, (_a, r, g) in enumerate(tiles):
                        dve.wait_ge(kv_ready, t + 1)
                        dve.tensor_tensor(v_rows[0:r, t, :, 0:HDS],
                                          m.ps[0:r, t % 8, D:].rearrange("p (h d) -> p h d", h=NH),
                                          kv_bias[0:r, g, D:].rearrange("p (h d) -> p h d", h=NH), ALU.add)
                        dve.tensor_tensor(k_rows[0:r, t, :], m.ps[0:r, t % 8, 0:D], kv_bias[0:r, g, 0:D],
                                          ALU.add).then_inc(kb_done, 1)
                    dve.wait_ge(rstd_ok, 1)
                    for t in range(KT + 1):
                        if t < KT:
                            _a, r, g = tiles[t]
                            i = (t - FIRST[g]) % 2
                            dve.scalar_tensor_tensor(out=k_rows[0:r, t, :], in0=k_rows[0:r, t, :],
                                                     scalar=sq[0:r, 2, t:t + 1], in1=norm_w[0:r, g, :],
                                                     op0=ALU.mult, op1=ALU.mult).then_inc(kn_done, 1)
                        if t:
                            dst, src = evacuate(dve, t - 1, 1, ev_b)
                            dve.tensor_copy(dst, src).then_inc(ev_b, 1)
                        if t < KT:
                            dve.wait_ge(hi_done, t + 1)
                            dve.tensor_tensor(k_st[g][i][0:r, :, K_LO:K_LO + HDS],
                                              k_rows[0:r, t, :].rearrange("p (h d) -> p h d", h=NH),
                                              k_st[g][i][0:r, :, K_HI:K_HI + HDS].bitcast(F32),
                                              ALU.subtract).then_inc(lo_done, 1)
            st.clear()

            with nc.Block(name="a2_queries") as block:
                @block.tensor
                def _(pe):
                    for q in range(QT):
                        n = 0
                        for c in range(DC):
                            for s, v in HALVES:
                                ins = pe.matmul(m.ps[:, q, 0:D], zt[s][:, c, q * P:(q + 1) * P],
                                                wr[2][v][:, c * D:(c + 1) * D], start=(n == 0), stop=(n == 3 * DC - 1))
                                n += 1
                        ins.then_inc(kv_ready, 1)
                    pe.wait_ge(lo_done, QT)
                    for hp in range(HP):
                        for q in range(QT):
                            at_ = (hp % 2) * S + q * P
                            ins = pe.transpose(m.ps[:, 2 + hp // 2, at_:at_ + P].bitcast(F32R),
                                               q_st[:, q, 2 * hp:2 * hp + 2, :].rearrange("p a n -> p (a n)"),
                                               m.ident_r[:, :])
                        if hp % 2:
                            ins.then_inc(turned, 1)

                @block.scalar
                def _(act):
                    for q in range(QT):
                        act.wait_ge(kb_done, q + 1)
                        act.activation(square[:, q, :], q_rows[:, q, :], ACT.Square,
                                       accum_out=sq[:, 0, KT + q:KT + q + 1]).then_inc(sq_done, 1)
                    for q in range(QT):
                        act.wait_ge(kn_done, q + 1)
                        rows = q_rows[:, q, :].rearrange("p (h d) -> p h d", h=NH)
                        act.activation(q_st[:, q, :, 0:HDS], rows, ACT.Copy)
                        act.activation(q_st[:, q, :, 2 * HDS:3 * HDS], rows, ACT.Copy).then_inc(hi_done, 1)
                    for k in range(HP // 2):
                        act.wait_ge(turned, k + 1)
                        act.activation(flat2(qt_a[:, 2 * k:2 * k + 2, :]), m.ps[:, 2 + k, :], ACT.Copy)\
                           .then_inc(ev_a, 1)

                @block.gpsimd
                def _(pool):
                    step = Step(pool, pstep)
                    pool.wait_ge(sq_done, QT)
                    step(pool.tensor_scalar(sq[:, 1, KT:], sq[:, 0, KT:], 1.0 / D, 1e-6, ALU.mult, ALU.add))
                    step(pool.tensor_tensor(sq[:, 2, KT:], sq[:, 1, KT:], m.nhalf[:, 0:1].to_broadcast([P, QT]),
                                            ALU.pow))
                    pool.tensor_scalar(sq[:, 2, KT:], sq[:, 2, KT:], SCALE, None, ALU.mult).then_inc(rstd_ok, 1)

                @block.vector
                def _(dve):
                    for q in range(QT):
                        dve.wait_ge(kv_ready, q + 1)
                        dve.tensor_tensor(q_rows[:, q, :], m.ps[:, q, 0:D], qo_bias[:, 0, :], ALU.add)\
                           .then_inc(kb_done, 1)
                    dve.wait_ge(kb_done, QT)
                    dve.wait_ge(rstd_ok, 1)
                    for q in range(QT):
                        dve.scalar_tensor_tensor(out=q_rows[:, q, :], in0=q_rows[:, q, :],
                                                 scalar=sq[:, 2, KT + q:KT + q + 1], in1=norm_w[:, 2, :],
                                                 op0=ALU.mult, op1=ALU.mult).then_inc(kn_done, 1)
                    for q in range(QT):
                        dve.wait_ge(hi_done, q + 1)
                        dve.tensor_tensor(q_st[:, q, :, HDS:2 * HDS],
                                          q_rows[:, q, :].rearrange("p (h d) -> p h d", h=NH),
                                          q_st[:, q, :, 0:HDS].bitcast(F32), ALU.subtract).then_inc(lo_done, 1)
            st.clear()

            PAIRS = KT // 2
            TURNS = NH * PAIRS
            with nc.Block(name="a2_attend") as block:
                @block.tensor
                def _(pe):
                    def rough_scores(i):
                        h, q = divmod(i, QT)
                        lo_p = STK * (h % 2)
                        pe.wait_ge(neg_done, i) if i else None
                        if h % 2 == 0 and q == 0 and h:
                            pe.wait_ge(qb_done, h // 2)
                        lhs = qt_a[lo_p:lo_p + HDS, h // 2, q * P:(q + 1) * P]
                        img = NKEY[0] + NKEY[0] % 2
                        pe.matmul(m.ps[:, 0, 0:img], lhs, kt[lo_p:lo_p + HDS, h // 2, 0:img], start=True, stop=True)
                        a0 = FIRST[1] * P
                        for k, a in enumerate(range(0, NKEY[1], 512)):
                            e = min(a + 512, NKEY[1])
                            ins = pe.matmul(m.ps[:, 1 + k, 0:e - a], lhs, kt[lo_p:lo_p + HDS, h // 2, a0 + a:a0 + e],
                                            start=True, stop=True)
                        ins.then_inc(s_ready, 1)

                    def turn_queries(hp):
                        pe.wait_ge(neg_done, 4 * (hp + 1))
                        if hp >= 2:
                            pe.wait_ge(st_ready, (2 * hp - 2) * PAIRS)
                        for q in range(QT):
                            ins = pe.transpose(m.ps[:, 0, q * P:(q + 1) * P].bitcast(F32R),
                                               q_st[:, q, 2 * hp:2 * hp + 2, :].rearrange("p a n -> p (a n)"),
                                               m.ident_r[:, :])
                        ins.then_inc(qb_turned, 1)

                    def scores(n):
                        h, k2 = divmod(n, PAIRS)
                        lo_p = STK * (h % 2)
                        if k2 == 0 and h % 2 == 0:
                            pe.wait_ge(qb_done, h // 2 + 1)
                        if n >= 2:
                            pe.wait_ge(exp_done, n - 1)
                        for i in range(2):
                            t = 2 * k2 + i
                            ins = pe.matmul(m.ps[:, 4 + n % 2, i * S:(i + 1) * S],
                                            kt[lo_p:lo_p + STK, h // 2, t * P:(t + 1) * P],
                                            qt_b[lo_p:lo_p + STK, (h // 2) % 2, :], start=True, stop=True)
                        ins.then_inc(st_ready, 1)

                    def values(n):
                        h, k2 = divmod(n, PAIRS)
                        pe.wait_ge(exp_done, n + 1)
                        if k2 == 0 and h >= 2:
                            pe.wait_ge(o_done, h - 1)
                        for i in range(2):
                            t = 2 * k2 + i
                            g = tiles[t][2]
                            for q in range(QT):
                                at_ = (2 * q + g) * 32
                                ins = pe.matmul(m.ps[:, 6 + h % 2, at_:at_ + VW2],
                                                probs[:, n % 3, i * S + q * P:i * S + (q + 1) * P],
                                                v_rows[:, t, h, :], start=(t == 0 and q == 0), stop=(t == LAST[g]),
                                                skip_group_check=True)
                        ins.then_inc(pv_done, 1)

                    for i in range(4):
                        rough_scores(i)
                    turn_queries(0)
                    for n in range(TURNS):
                        scores(n)
                        hp, r = divmod(n, 2 * PAIRS)
                        if n:
                            values(n - 1)
                        if hp + 1 < HP and r % 3 == 0 and r // 3 < 4:
                            rough_scores(4 * (hp + 1) + r // 3)
                        if hp + 1 < HP and r == 2 * PAIRS - 1:
                            turn_queries(hp + 1)
                    values(TURNS - 1)

                @block.scalar
                def _(act):
                    def take_queries(hp):
                        act.wait_ge(qb_turned, hp + 1)
                        act.activation(qt_b[:, hp % 2, :], m.ps[:, 0, 0:S], ACT.Copy).then_inc(qb_done, 1)

                    take_queries(0)
                    for n in range(TURNS):
                        act.wait_ge(st_ready, n + 1)
                        if n >= 3:
                            act.wait_ge(pv_done, n - 2)
                        act.activation(probs[:, n % 3, :], m.ps[:, 4 + n % 2, :], ACT.Exp).then_inc(exp_done, 1)
                        hp, r = divmod(n, 2 * PAIRS)
                        if hp + 1 < HP and r == 2 * PAIRS - 1:
                            take_queries(hp + 1)

                @block.vector
                def _(dve):
                    step = Step(dve, dstep)

                    def maxima(i):
                        h, q = divmod(i, QT)
                        dve.wait_ge(s_ready, i + 1)
                        dve.tensor_reduce(q_st[:, q, h, NEG:NEG + 1], m.ps[:, 0, 0:NKEY[0]], AX.X, ALU.max,
                                          negate=True)
                        dve.tensor_reduce(q_st[:, q, h, NEG + 1:NEG + 2], m.ps[:, 1:4, :]
                                          .rearrange("p b n -> p (b n)")[:, 0:NKEY[1]], AX.X, ALU.max,
                                          negate=True).then_inc(neg_done, 1)

                    def outputs(h):
                        dve.wait_ge(pv_done, PAIRS * (h + 1))
                        o = m.ps[:, 6 + h % 2, 0:128].rearrange("p (i n) -> p i n", i=4)
                        step(dve.reciprocal(rs[:, h % 2, :].unsqueeze(2), o[:, :, HDS:VW2]))
                        dve.tensor_tensor(o_n[:, h % 2, :, :], o[:, :, 0:HDS],
                                          rs[:, h % 2, :].unsqueeze(2).to_broadcast([P, 4, HDS]), ALU.mult)\
                           .then_inc(o_done, 1)
                        dve.wait_ge(o_done, h + 1)
                        on = o_n[:, h % 2, :, :].rearrange("p (q g) d -> p q g d", g=2)
                        step(dve.tensor_tensor(o_rows[:, :, h * HDS:(h + 1) * HDS], on[:, :, 0, :], on[:, :, 1, :],
                                               ALU.add))

                    for i in range(4):
                        maxima(i)
                    for hp in range(HP):
                        if hp:
                            outputs(2 * hp - 1)
                        if hp + 1 < HP:
                            for i in range(4):
                                maxima(4 * (hp + 1) + i)
                        outputs(2 * hp)
                    outputs(NH - 1)
            st.clear()

            with nc.Block(name="a2_project") as block:
                @block.tensor
                def _(pe):
                    for c in range(DC):
                        for q in range(QT):
                            ins = pe.transpose(m.ps[:, 0, c * S + q * P:c * S + (q + 1) * P],
                                               o_rows[:, q, c * P:(c + 1) * P], m.ident[:, :])
                    ins.then_inc(turned, 1)
                    pe.wait_ge(lo_done, 1)
                    for q in range(QT):
                        n = 0
                        for c in range(DC):
                            for s, v in HALVES:
                                ins = pe.matmul(m.ps[:, 1 + q, 0:D], zt[s][:, c, q * P:(q + 1) * P],
                                                wr[3][v][:, c * D:(c + 1) * D], start=(n == 0), stop=(n == 3 * DC - 1))
                                n += 1
                        ins.then_inc(kv_ready, 1)

                @block.scalar
                def _(act):
                    act.wait_ge(turned, 1)
                    act.activation(flat2(zt[0][:, :, :]), m.ps[:, 0, :], ACT.Copy).then_inc(hi_done, 1)

                @block.vector
                def _(dve):
                    dve.tensor_tensor(x_b[:, :, :], x_b[:, :, :], qo_bias[:, 1, :].unsqueeze(1)
                                      .to_broadcast([P, QT, D]), ALU.add).then_inc(dstep, 1)
                    dve.wait_ge(hi_done, 1)
                    dve.tensor_tensor(flat2(zt[1][:, :, :]), m.ps[:, 0, :], flat2(zt[0][:, :, :]).bitcast(F32),
                                      ALU.subtract).then_inc(lo_done, 1)
                    dve.wait_ge(dstep, 1)
                    for q in range(QT):
                        dve.wait_ge(kv_ready, q + 1)
                        dve.tensor_tensor(x_b[:, q, :], x_b[:, q, :], m.ps[:, 1 + q, 0:D], ALU.add)\
                           .then_inc(dstep, 1)
                @block.sync
                def _(sp):
                    sp.wait_ge(dstep, 1 + QT)
                    sp.dma_start(x_rows, x_b[:, :, :]).then_inc(small_in, 16)
                    sp.wait_ge(small_in, 16)
            st.clear()


def chunked(w, groups):
    w = np.asarray(w)
    k, n = w.shape
    return w.reshape(k // P, P, groups, n // groups).transpose(2, 1, 0, 3).reshape(groups, P, -1)


def lay_gqa(wq, wk, wv, wo, qw, kw, name):
    kv = np.stack([np.asarray(wk).reshape(D, KVH, HD), np.asarray(wv).reshape(D, KVH, HD)], axis=2)
    return {
        f"{name}_wq": chunked(wq, KVH),
        f"{name}_wkv": chunked(kv.reshape(D, -1), KVH),
        f"{name}_wo": np.asarray(wo).reshape(KVH, REP, P, D).transpose(0, 2, 1, 3).reshape(KVH, P, -1),
        f"{name}_qw": np.asarray(qw), f"{name}_kw": np.asarray(kw),
    }


def by_partition(w):
    w = np.asarray(w)
    *lead, k, n = w.shape
    return np.moveaxis(w.reshape(*lead, k // P, P, n), -2, -3).reshape(*lead, P, -1)


def lay_units(gate, up, down):
    gate, up, down = (np.asarray(a) for a in (gate, up, down))
    n = -(-gate.shape[1] // P)
    out = np.zeros((n, P, 3 * 2 * P), np.float32)
    for u in range(n):
        a, e = u * P, min((u + 1) * P, gate.shape[1])
        for c in range(DC):
            out[u, :, c * 2 * P:c * 2 * P + e - a] = gate[c * P:(c + 1) * P, a:e]
            out[u, :, c * 2 * P + P:c * 2 * P + P + e - a] = up[c * P:(c + 1) * P, a:e]
        out[u, 0:e - a, 4 * P:] = down[a:e]
    return out


def lay_ffn(i):
    out = {"f0_w1": by_partition(i["L0_ffn_W1"]), "f0_w2": by_partition(i["L0_ffn_W2"]),
           "f0_w3": by_partition(i["L0_ffn_W3"]), "f0_b3": i["L0_ffn_b3"],
           "f0_wg": by_partition(i["L0_ffn_Wg"]), "f0_bg": i["L0_ffn_bg"]}
    b12 = np.stack([np.asarray(i["L0_ffn_b1"]), np.asarray(i["L0_ffn_b2"])], axis=1)
    out["f0_b12"] = b12.reshape(NE, 2, -1, P).transpose(0, 3, 1, 2).reshape(NE, P, -1)
    out |= {"f1_w": by_partition(i["L1_ffn_weight"].T), "f1_scale": i["L1_ffn_scale_weight"],
            "f1_bias": i["L1_ffn_bias"]}
    out["f2_wg"] = by_partition(i["L2_ffn_Wg"])
    out["f2_units"] = lay_units(i["L2_ffn_sw1"], i["L2_ffn_sw3"], i["L2_ffn_sw2"])
    w2 = np.asarray(i["L2_ffn_W2"])
    down = np.zeros((NE, 3 * P, D), np.float32)
    down[:, 0:w2.shape[1]] = w2
    out["f2_experts"] = np.concatenate([by_partition(i["L2_ffn_W1"]), by_partition(i["L2_ffn_W3"]),
                                        by_partition(down)], axis=2)
    out["f3_wg"] = by_partition(i["L3_ffn_w_gate"])
    gu, dn = np.asarray(i["L3_ffn_w_gate_up"]), np.asarray(i["L3_ffn_w_down"])
    sgu, sdn = np.asarray(i["L3_ffn_w_sh_gate_up"]), np.asarray(i["L3_ffn_w_sh_down"])
    I = sgu.shape[1] // 2
    out["f3_units"] = np.concatenate([lay_units(gu[e, :, 0:P], gu[e, :, P:], dn[e]) for e in range(NE)]
                                     + [lay_units(sgu[:, 0:I], sgu[:, I:], sdn)])
    return out


def lay_memory(i):
    wqkv = np.asarray(i["L0_xattn_W_qkv"])
    out = {"a0_wq": by_partition(wqkv[0:D].T), "a0_wo": by_partition(np.asarray(i["L0_xattn_W_o"]).T)}
    for n in ("gate", "log_tau", "beta_q", "beta_k"):
        out[f"a0_{n}"] = np.asarray(i[f"L0_xattn_{n}"]).reshape(1)
    return out


def lay_image_text(i):
    def t(n):
        return np.asarray(i[f"L2_xattn_{n}"]).T
    out = {"a2_wkv_img": by_partition(np.concatenate([t("k_img_w"), t("v_img_w")], axis=1)),
           "a2_wkv_txt": by_partition(np.concatenate([t("k_w"), t("v_w")], axis=1)),
           "a2_wq": by_partition(t("q_w")), "a2_wo": by_partition(t("o_w"))}
    for n in "q_b k_b v_b k_img_b v_img_b o_b norm_q_w norm_k_w norm_k_img_w".split():
        out[f"a2_{n}"] = i[f"L2_xattn_{n}"]
    return out


def lay_out(i):
    out = {"x": i["x"], "ctx": i["ctx_2048"], "pos": i["pos_BxS2"], "tok": i["itok_BxS_4096_4607"],
           "inv_freq": (1.0 / 10000.0 ** (np.arange(0, HD, 2, dtype=np.float64) / HD)).astype(np.float32)}
    out |= lay_memory(i) | lay_image_text(i) | lay_ffn(i)
    out |= lay_gqa(i["L1_xattn_Wq"].T, i["L1_xattn_Wk"].T, i["L1_xattn_Wv"].T, i["L1_xattn_Wo"].T,
                   i["L1_xattn_q_norm_w"], i["L1_xattn_k_norm_w"], "a1")
    out |= lay_gqa(i["L3_xattn_Wq"], i["L3_xattn_Wk"], i["L3_xattn_Wv"], i["L3_xattn_Wo"],
                   i["L3_xattn_q_norm_w"], i["L3_xattn_k_norm_w"], "a3")
    return out


def run_layers(nc, m, d):
    def of(name):
        return {k[3:]: v for k, v in d.items() if k.startswith(name)}

    memory_attention(nc, m, of("a0_") | {"ctx": d["ctx"]})
    gelu_experts(nc, m, of("f0_"))
    grouped_attention(nc, m, "a1", of("a1_") | {k: d[k] for k in ("pos", "tok", "inv_freq")}, True)
    scaled_linear(nc, m, of("f1_"))
    image_text_attention(nc, m, of("a2_"))
    capacity_experts(nc, m, of("f2_"))
    grouped_attention(nc, m, "a3", of("a3_"), False)
    silu_experts(nc, m, of("f3_"))


def build(nc, dram, out):
    class m:
        pass
    with ExitStack() as ctx:
        m.ident = ctx.enter_context(nc.sbuf_tensor("ident", [P, P], F32))
        m.ident_r = ctx.enter_context(nc.sbuf_tensor("ident_r", [P, P], F32R))
        m.ones_r = ctx.enter_context(nc.sbuf_tensor("ones_r", [P, P], F32R))
        m.onesf = ctx.enter_context(nc.sbuf_tensor("onesf", [P, P], F32))
        m.nhalf = ctx.enter_context(nc.sbuf_tensor("nhalf", [P, 1], F32))
        m.ps = ctx.enter_context(nc.psum_tensor("ps", [P, 8, 512], F32))
        m.x_pad = nc.dram_tensor("x_state", (QT + TT, P * D), F32, kind="Internal").ap()
        m.x_dram = m.x_pad[QT:QT + TT, :]
        m.ctx_hi = nc.dram_tensor("ctx_hi", (B, P, DC * CTXP), F32, kind="Internal").ap()
        m.ctx_lo = nc.dram_tensor("ctx_lo", (B, P, DC * CTXP), F32, kind="Internal").ap()
        make_constants(nc, m)
        copy_x_in(nc, m, dram["x"].rearrange("b (t p) d -> (b t) (p d)", p=P))
        transpose_context(nc, m, dram["ctx"])
        run_layers(nc, m, dram)
        with Stage(nc, "xout") as st:
            moved = st.sem("moved")
            with nc.Block(name="x_out") as block:
                @block.sync
                def _(sp):
                    sp.dma_start(out.rearrange("b (t p) d -> (b t) (p d)", p=P), m.x_dram[:, :]).then_inc(moved, 16)
                    sp.wait_ge(moved, 16)


def kernel(**inputs):
    import concourse.bacc as bacc
    from concourse.bass_utils import run_bass_kernel_spmd

    nc = bacc.Bacc("TRN2", target_bir_lowering=False, num_devices=1)
    arrays = {n: np.ascontiguousarray(a) for n, a in lay_out(inputs).items()}
    dram = {n: nc.dram_tensor(f"in_{n}", a.shape, mybir.dt.from_np(a.dtype), kind="ExternalInput").ap()
            for n, a in arrays.items()}
    out = nc.dram_tensor("out_0", (B, S, D), F32, kind="ExternalOutput").ap()
    build(nc, dram, out)
    r = run_bass_kernel_spmd(nc, [{f"in_{n}": a for n, a in arrays.items()}], core_ids=[0])
    return r.results[0]["out_0"]
```

```python
from contextlib import ExitStack

import concourse.bass as bass
import numpy as np
from concourse import mybir
from concourse.alu_op_type import AluOpType as ALU

F32 = mybir.dt.float32
F32R = mybir.dt.float32r
I32 = mybir.dt.int32
U32 = mybir.dt.uint32
ACT = mybir.ActivationFunctionType
AX = mybir.AxisListType

P = 128
B, S, D = 4, 256, 256
CTX = 1601
CTXP = CTX + 1
DC = D // P
QT = S // P
TT = B * QT
CTILES = -(-CTX // P)
CLAST = CTX - (CTILES - 1) * P
TOPK_CTX = 54
HALVES = ((0, 0), (0, 1), (1, 0))


def flat2(a):
    return a.rearrange("p a b -> p (a b)")


class Step:

    def __init__(self, eng, sem):
        self.eng, self.sem, self.n = eng, sem, 0

    def __call__(self, ins):
        self.n += 1
        ins.then_inc(self.sem, 1)
        self.eng.wait_ge(self.sem, self.n)


class Stage:

    def __init__(self, nc, name):
        self.nc, self.name, self.ctx, self.sems = nc, name, ExitStack(), []

    def __enter__(self):
        return self

    def __exit__(self, *exc):
        self.clear()
        self.ctx.close()

    def sb(self, name, shape, dt=F32):
        return self.ctx.enter_context(self.nc.sbuf_tensor(f"{self.name}_{name}", shape, dt))

    def sem(self, name):
        s = self.ctx.enter_context(self.nc.semaphore(f"{self.name}_{name}"))
        self.sems.append(s)
        return s

    def clear(self):
        nums = sorted(s.num for s in self.sems)
        starts = [n for n in nums if n - 1 not in nums]
        for a in starts:
            e = next(n for n in range(a, a + len(nums) + 1) if n not in nums)
            self.nc.sync.sem_clear(range(a, e))
        self.nc.all_engine_barrier()


def make_constants(nc, m):
    with Stage(nc, "const") as st:
        made = st.sem("made")
        with nc.Block(name="constants") as block:
            @block.gpsimd
            def _(pool):
                pool.memset(m.ident[:, :], 0.0).then_inc(made, 1)
                pool.wait_ge(made, 1)
                pool.affine_select(out=m.ident[:, :], in_=m.ident[:, :], compare_op=ALU.not_equal, fill=1.0,
                                   base=0, pattern=[[-1, P]], channel_multiplier=1).then_inc(made, 1)
                pool.memset(m.nhalf[:, :], -0.5).then_inc(made, 1)
                pool.memset(m.onesf[:, :], 1.0).then_inc(made, 1)
                pool.wait_ge(made, 4)

            @block.scalar
            def _(act):
                act.wait_ge(made, 4)
                act.activation(m.ident_r[:, :], m.ident[:, :], ACT.Copy).then_inc(made, 1)
                act.activation(m.ones_r[:, :], m.onesf[:, :], ACT.Copy).then_inc(made, 1)


def copy_x_in(nc, m, x_in):
    with Stage(nc, "xin") as st:
        moved = st.sem("moved")
        with nc.Block(name="x_in") as block:
            @block.sync
            def _(sp):
                sp.dma_start(m.x_dram[:, :], x_in).then_inc(moved, 16)
                sp.wait_ge(moved, 16)


NORM_SEMS = "loaded0 loaded1 extra step var rstd turned hi lo".split()


def norm_block(nc, st, m, x_sb, zt_hi, zt_lo, tiles, x_src, sems, scratch, extra_loads=(), name="norm"):
    loaded0, loaded1, extra, dstep, var_ok, rstd_ok, turned, hi_done, lo_done = sems
    part = tiles // 2
    stats, mv, rstd, z = scratch
    n_banks = DC * tiles * P // 512
    per = 512 // P
    slots = [(c, t) for c in range(DC) for t in range(tiles)]
    with nc.Block(name=name) as block:
        @block.sync
        def _(sp):
            for i, got in enumerate((loaded0, loaded1)):
                sp.dma_start(x_sb[:, i * part:(i + 1) * part, :], x_src[:, i * part:(i + 1) * part, :])\
                  .then_inc(got, 16)
            for dst, src in extra_loads:
                sp.dma_start(dst, src).then_inc(extra, 16)
            if extra_loads:
                sp.wait_ge(extra, 16 * len(extra_loads))

        @block.vector
        def _(dve):
            step = Step(dve, dstep)
            for t in range(tiles):
                if t % part == 0:
                    dve.wait_ge((loaded0, loaded1)[t // part], 16)
                dve.bn_stats(stats[:, t, :], x_sb[:, t, :]).then_inc(dstep, 1)
            step.n += tiles
            dve.wait_ge(dstep, step.n)
            for t in range(tiles):
                dve.bn_aggr(mv[:, t, :], stats[:, t, :]).then_inc(dstep, 1)
            step.n += tiles
            dve.wait_ge(dstep, step.n)
            dve.tensor_scalar(rstd[:, 0, :], mv[:, :, 1], 1e-5, None, ALU.add).then_inc(var_ok, 1)
            dve.wait_ge(rstd_ok, 1)
            for t in range(tiles):
                dve.tensor_scalar(z[:, t, :], x_sb[:, t, :], mv[:, t, 0:1], rstd[:, 1, t:t + 1],
                                  ALU.subtract, ALU.mult).then_inc(dstep, 1)
            step.n += tiles
            for k in range(n_banks):
                dve.wait_ge(hi_done, k + 1)
                dve.tensor_tensor(zt_lo[:, :, :].rearrange("p c n -> p (c n)")[:, k * 512:(k + 1) * 512],
                                  m.ps[:, k, :],
                                  zt_hi[:, :, :].rearrange("p c n -> p (c n)")[:, k * 512:(k + 1) * 512]
                                  .bitcast(F32), ALU.subtract).then_inc(lo_done, 1)

        @block.gpsimd
        def _(pool):
            pool.wait_ge(var_ok, 1)
            pool.tensor_tensor(rstd[:, 1, :], rstd[:, 0, :], m.nhalf[:, 0:1].to_broadcast([P, tiles]),
                               ALU.pow).then_inc(rstd_ok, 1)

        @block.tensor
        def _(pe):
            for i, (c, t) in enumerate(slots):
                pe.wait_ge(dstep, 2 * tiles + t + 1)
                ins = pe.transpose(m.ps[:, i // per, (i % per) * P:(i % per + 1) * P],
                                   z[:, t, c * P:(c + 1) * P], m.ident[:, :])
                if i % per == per - 1:
                    ins.then_inc(turned, 1)

        @block.scalar
        def _(act):
            for k in range(n_banks):
                act.wait_ge(turned, k + 1)
                act.activation(zt_hi[:, :, :].rearrange("p c n -> p (c n)")[:, k * 512:(k + 1) * 512],
                               m.ps[:, k, :], ACT.Copy).then_inc(hi_done, 1)
def split_weights(nc, st, name, parts, arrived, w_hi, w_lo):
    with nc.Block(name=name) as block:
        @block.sync
        def _(sp):
            for (full, _halves, src), got in zip(parts, arrived):
                sp.dma_start(full, src).then_inc(got, 16)

        @block.scalar
        def _(act):
            for (full, halves, _src), got in zip(parts, arrived):
                act.wait_ge(got, 16)
                act.activation(halves[0], full, ACT.Copy).then_inc(w_hi, 1)

        @block.vector
        def _(dve):
            for i, (full, halves, _src) in enumerate(parts):
                dve.wait_ge(w_hi, i + 1)
                dve.tensor_tensor(halves[1], full, halves[0].bitcast(F32), ALU.subtract).then_inc(w_lo, 1)
    st.clear()


def memory_attention(nc, m, w):
    CH = [(a, min(a + 512, CTXP)) for a in range(0, CTXP, 512)]
    ROUNDS = -(-TOPK_CTX // 8)
    AT = (TOPK_CTX - 1) % 8
    TURN = [(c, t0, min(t0 + 4, CTILES)) for c in range(DC) for t0 in range(0, CTILES, 4)]
    NT = len(TURN)
    PT = [(t0, min(t0 + 4, CTILES)) for t0 in range(0, CTILES, 4)]
    with Stage(nc, "a0") as st:
        x_bs = [st.sb(f"x_b{i}", [P, QT, D]) for i in range(2)]
        zt = [st.sb(f"zt{i}", [P, DC, S], F32R) for i in range(2)]
        ct = [st.sb(f"ct{i}", [P, DC, CTXP], F32R) for i in range(2)]
        stats, mv, rstd, z = (st.sb("stats", [P, QT, 6]), st.sb("mv", [P, QT, 2]), st.sb("rstd", [P, 2, QT]),
                              st.sb("z", [P, QT, D]))
        rows2 = [st.sb(f"rows{i}", [P, CTILES, D]) for i in range(2)]
        wf = st.sb("wf", [P, 2, DC * D])
        wr = [st.sb(f"wr{i}", [P, 2, DC * D], F32R) for i in range(2)]
        knob = st.sb("knob", [P, 12])
        qt = [st.sb(f"qt{i}", [P, DC, S], F32R) for i in range(2)]
        negm = st.sb("negm", [P, QT])
        shifted2 = [st.sb(f"shifted{i}", [P, QT, CTX]) for i in range(2)]
        work = st.sb("work", [P, CTX])
        best = st.sb("best", [P, 8])
        expd = st.sb("expd", [P, QT, CTX])
        rsum = st.sb("rsum", [P, 2, QT])
        pt = st.sb("pt", [P, CTILES, S])
        ot = [st.sb(f"ot{i}", [P, DC, S], F32R) for i in range(2)]
        w_in = [st.sem("wq_in"), st.sem("wo_in")]
        w_hi, w_lo, knobs_in, kact, dstep, zeroed = [
            st.sem(n) for n in "w_hi w_lo knobs_in kact dstep zeroed".split()]
        (x_in, rows_in, ct_out, stored, var_ok, rstd_ok, z_ok, item_ready, item_act, item_free, s_ready,
         neg_ok, shift_ok, exp_ok, mask_ok, pt_turned, pt_ok, o_ready, o_hi, o_lo, y_ready, y_done) = [
            st.sem(n) for n in (
                "x_in rows_in ct_out stored var_ok rstd_ok z_ok item_ready item_act item_free s_ready "
                "neg_ok shift_ok exp_ok mask_ok pt_turned pt_ok o_ready o_hi o_lo y_ready y_done").split()]

        split_weights(nc, st, "a0_weights",
                      [(wf[:, i, :], (wr[0][:, i, :], wr[1][:, i, :]), w[n]) for i, n in enumerate(("wq", "wo"))],
                      w_in, w_hi, w_lo)
        GATE, TAU, BQ, BK = range(4)
        with nc.Block(name="a0_knobs") as block:
            @block.sync
            def _(sp):
                for i, n in enumerate(("gate", "log_tau", "beta_q", "beta_k")):
                    sp.dma_start(knob[:, i:i + 1], w[n].partition_broadcast(P)).then_inc(knobs_in, 16)

            @block.scalar
            def _(act):
                act.wait_ge(knobs_in, 64)
                act.activation(knob[:, 4:5], knob[:, GATE:GATE + 1], ACT.Exp, scale=-1.0).then_inc(kact, 1)
                act.activation(knob[:, 5:6], knob[:, TAU:TAU + 1], ACT.Exp).then_inc(kact, 1)

            @block.gpsimd
            def _(pool):
                for i in range(2):
                    pool.memset(ct[i][:, :, CTX:CTXP].bitcast(F32), 0.0).then_inc(zeroed, 1)

            @block.vector
            def _(dve):
                step = Step(dve, dstep)
                dve.wait_ge(kact, 2)
                step(dve.tensor_scalar(knob[:, 6:7], knob[:, 4:5], 1.0, None, ALU.add))
                step(dve.reciprocal(knob[:, 7:8], knob[:, 6:7]))
                step(dve.tensor_scalar(knob[:, 8:9], knob[:, 7:8], -1.0, 1.0, ALU.mult, ALU.add))
                step(dve.tensor_tensor(knob[:, 9:10], knob[:, 8:9], knob[:, BK:BK + 1], ALU.mult))
                step(dve.scalar_tensor_tensor(out=knob[:, 10:11], in0=knob[:, 7:8], scalar=knob[:, BQ:BQ + 1],
                                              in1=knob[:, 9:10], op0=ALU.mult, op1=ALU.add))
                step(dve.scalar_tensor_tensor(out=knob[:, 11:12], in0=knob[:, 10:11], scalar=D ** -0.5,
                                              in1=knob[:, 5:6], op0=ALU.mult, op1=ALU.mult))
        st.clear()
        coef = knob[:, 11:12]

        full = (CTILES - 1) * P
        items = [("CX", 0), ("NX", 0)] + [("CX", k) for k in range(1, NT)] + [("Q", o) for o in range(DC)]
        number = {task: i for i, task in enumerate(items)}

        def attention_block(par, b_prev, b_next, finish):
            x_b, x_n = x_bs[par], x_bs[1 - par]
            rows, rows_n = rows2[par], rows2[1 - par]
            shifted, shifted_n = shifted2[par], shifted2[1 - par]

            def x_rows(b):
                return m.x_dram[bass.ds(b * QT, QT), :].rearrange("t (p d) -> p t d", p=P)

            def bank(task):
                return m.ps[:, 4 + number[task] % 2, :]

            with nc.Block(name=f"a0_{'both' if finish else 'first'}{par}") as block:
                @block.sync
                def _(sp):
                    sp.dma_start(x_n[:, :, :], x_rows(b_next)).then_inc(x_in, 16)
                    sp.dma_start(rows_n[:, 0:CTILES - 1, :], w["ctx"][bass.ds(b_next, 1), 0:full, :]
                                 .rearrange("a (t p) d -> p (a t) d", p=P)).then_inc(rows_in, 16)
                    sp.dma_start(rows_n[0:CLAST, CTILES - 1, :], w["ctx"][bass.ds(b_next, 1), full:CTX, :]
                                 .rearrange("a p d -> p (a d)")).then_inc(rows_in, 16)
                    sp.wait_ge(item_free, number[("CX", NT - 1)] + 1)
                    for half, dst in zip(ct, (m.ctx_hi, m.ctx_lo)):
                        sp.dma_start(dst[bass.ds(b_next, 1), :, :].rearrange("a p n -> p (a n)"),
                                     flat2(half[:, :, :]).bitcast(F32)).then_inc(ct_out, 16)
                    if finish:
                        sp.wait_ge(y_done, QT)
                        sp.dma_start(x_rows(b_prev), x_b[:, :, :]).then_inc(stored, 16)
                        sp.wait_ge(stored, 16)
                    sp.wait_ge(ct_out, 32)

                @block.tensor
                def _(pe):
                    def begin(task):
                        if number[task] >= 2:
                            pe.wait_ge(item_free, number[task] - 1)
                        return bank(task)

                    def CX(k):
                        c, t0, t1 = TURN[k]
                        out = begin(("CX", k))
                        pe.wait_ge(rows_in, 32)
                        for t in range(t0, t1):
                            r = P if t < CTILES - 1 else CLAST
                            ins = pe.transpose(out[:, (t - t0) * P:(t - t0) * P + r],
                                               rows_n[0:r, t, c * P:(c + 1) * P], m.ident[0:r, 0:r])
                        ins.then_inc(item_ready, 1)

                    def NX():
                        out = begin(("NX", 0))
                        pe.wait_ge(z_ok, QT)
                        for c in range(DC):
                            for q in range(QT):
                                ins = pe.transpose(out[:, (c * QT + q) * P:(c * QT + q + 1) * P],
                                                   z[:, q, c * P:(c + 1) * P], m.ident[:, :])
                        ins.then_inc(item_ready, 1)

                    def Q(o):
                        out = begin(("Q", o))
                        pe.wait_ge(item_free, number[("NX", 0)] + 1)
                        n = 0
                        for c in range(DC):
                            for s, v in HALVES:
                                ins = pe.matmul(out[:, 0:S], wr[v][:, 0, c * D + o * P:c * D + (o + 1) * P],
                                                zt[s][:, c, :], start=(n == 0), stop=(n == 3 * DC - 1))
                                n += 1
                        ins.then_inc(item_ready, 1)

                    def scores(q):
                        if q == 0:
                            pe.wait_ge(item_free, len(items))
                        else:
                            pe.wait_ge(shift_ok, q)
                        for k, (a, e) in enumerate(CH):
                            n = 0
                            for c in range(DC):
                                for s, v in HALVES:
                                    ins = pe.matmul(m.ps[:, k, 0:e - a], qt[s][:, c, q * P:(q + 1) * P],
                                                    ct[v][:, c, a:e], start=(n == 0), stop=(n == 3 * DC - 1))
                                    n += 1
                        ins.then_inc(s_ready, 1)

                    def turn_weights(q):
                        pe.wait_ge(mask_ok, q + 1)
                        for k, (t0, t1) in enumerate(PT):
                            if k >= 2:
                                pe.wait_ge(pt_ok, q * len(PT) + k - 1)
                            elif q:
                                pe.wait_ge((o_lo, y_done)[k], q)
                            for t in range(t0, t1):
                                r = P if t < CTILES - 1 else CLAST
                                ins = pe.transpose(m.ps[0:r, 6 + k % 2, (t - t0) * P:(t - t0 + 1) * P],
                                                   expd[:, q, t * P:t * P + r], m.ident[:, :])
                            ins.then_inc(pt_turned, 1)

                    def weighted(q):
                        pe.wait_ge(pt_ok, len(PT) * (q + 1))
                        for o in range(DC):
                            for t in range(CTILES):
                                r = P if t < CTILES - 1 else CLAST
                                ins = pe.matmul(m.ps[:, 6, o * P:(o + 1) * P], rows[0:r, t, o * P:(o + 1) * P],
                                                pt[0:r, t, q * P:(q + 1) * P], start=(t == 0),
                                                stop=(t == CTILES - 1))
                        ins.then_inc(o_ready, 1)

                    def project(q):
                        pe.wait_ge(o_lo, q + 1)
                        n = 0
                        for c in range(DC):
                            for s, v in HALVES:
                                ins = pe.matmul(m.ps[:, 7, 0:D], ot[s][:, c, q * P:(q + 1) * P],
                                                wr[v][:, 1, c * D:(c + 1) * D], start=(n == 0), stop=(n == 3 * DC - 1))
                                n += 1
                        ins.then_inc(y_ready, 1)

                    CX(0)
                    NX()
                    for k in range(1, NT):
                        CX(k)
                    for o in range(DC):
                        Q(o)
                    scores(0)
                    if finish:
                        turn_weights(0)
                        weighted(0)
                    scores(1)
                    if finish:
                        project(0)
                        turn_weights(1)
                        weighted(1)
                        project(1)

                @block.scalar
                def _(act):
                    def exp(q):
                        act.activation(expd[:, q, :], shifted[:, q, :], ACT.Exp).then_inc(exp_ok, 1)

                    def item(task):
                        act.wait_ge(item_ready, number[task] + 1)
                        src = bank(task)
                        if task[0] == "CX":
                            c, t0, t1 = TURN[task[1]]
                            a, e = t0 * P, min(t1 * P, CTX)
                            ins = act.activation(ct[0][:, c, a:e], src[:, 0:e - a], ACT.Copy)
                        elif task[0] == "NX":
                            ins = act.activation(flat2(zt[0][:, :, :]), src, ACT.Copy)
                        else:
                            ins = act.activation(qt[0][:, task[1], :], src[:, 0:S], ACT.Copy, scale=coef)
                        ins.then_inc(item_act, 1)

                    def shift(q):
                        act.wait_ge(neg_ok, q + 1)
                        act.activation(shifted_n[:, q, :], flat2(m.ps[:, 0:4, :])[:, 0:CTX], ACT.Identity,
                                       bias=negm[:, q:q + 1]).then_inc(shift_ok, 1)

                    def take_weights(q):
                        for k, (t0, t1) in enumerate(PT):
                            r = P if t1 < CTILES else CLAST
                            act.wait_ge(pt_turned, q * len(PT) + k + 1)
                            act.activation(pt[0:r, t0:t1, q * P:(q + 1) * P],
                                           m.ps[0:r, 6 + k % 2, 0:(t1 - t0) * P]
                                           .rearrange("p (t n) -> p t n", n=P), ACT.Copy).then_inc(pt_ok, 1)

                    def take_output(q):
                        act.wait_ge(o_ready, q + 1)
                        act.activation(ot[0][:, :, q * P:(q + 1) * P], m.ps[:, 6, 0:D]
                                       .rearrange("p (c n) -> p c n", c=DC), ACT.Copy).then_inc(o_hi, 1)

                    if finish:
                        exp(0)
                        exp(1)
                    for task in items:
                        item(task)
                    if finish:
                        take_weights(0)
                    shift(0)
                    if finish:
                        take_output(0)
                        take_weights(1)
                    shift(1)
                    if finish:
                        take_output(1)

                @block.gpsimd
                def _(pool):
                    pool.wait_ge(var_ok, 1)
                    pool.tensor_tensor(rstd[:, 1, :], rstd[:, 0, :], m.nhalf[:, 0:1].to_broadcast([P, QT]),
                                       ALU.pow).then_inc(rstd_ok, 1)

                @block.vector
                def _(dve):
                    step = Step(dve, dstep)

                    def row_stats():
                        dve.wait_ge(x_in, 16)
                        for q in range(QT):
                            ins = dve.bn_stats(stats[:, q, :], x_n[:, q, :])
                        step(ins)
                        for q in range(QT):
                            ins = dve.bn_aggr(mv[:, q, :], stats[:, q, :])
                        step(ins)
                        dve.tensor_scalar(rstd[:, 0, :], mv[:, :, 1], 1e-5, None, ALU.add).then_inc(var_ok, 1)

                    def normalise():
                        dve.wait_ge(rstd_ok, 1)
                        for q in range(QT):
                            dve.tensor_scalar(z[:, q, :], x_n[:, q, :], mv[:, q, 0:1], rstd[:, 1, q:q + 1],
                                              ALU.subtract, ALU.mult).then_inc(z_ok, 1)

                    def item(task):
                        dve.wait_ge(item_act, number[task] + 1)
                        src = bank(task)
                        if task[0] == "CX":
                            c, t0, t1 = TURN[task[1]]
                            a, e = t0 * P, min(t1 * P, CTX)
                            ins = dve.tensor_tensor(ct[1][:, c, a:e], src[:, 0:e - a],
                                                    ct[0][:, c, a:e].bitcast(F32), ALU.subtract)
                        elif task[0] == "NX":
                            ins = dve.tensor_tensor(flat2(zt[1][:, :, :]), src, flat2(zt[0][:, :, :]).bitcast(F32),
                                                    ALU.subtract)
                        else:
                            o = task[1]
                            ins = dve.scalar_tensor_tensor(out=qt[1][:, o, :], in0=src[:, 0:S], scalar=coef,
                                                           in1=qt[0][:, o, :].bitcast(F32), op0=ALU.mult,
                                                           op1=ALU.subtract)
                        ins.then_inc(item_free, 1)

                    def largest(q, r):
                        left = shifted[:, q, :] if r == 0 else work[:, :]
                        step(dve.max(out=best[:, :], in_=left))
                        if r < ROUNDS - 1:
                            step(dve.match_replace(out=work[:, :], in_to_replace=best[:, :], in_values=left,
                                                   imm_value=-3.0e38))

                    def mask(q):
                        dve.wait_ge(exp_ok, q + 1)
                        step(dve.scalar_tensor_tensor(out=expd[:, q, :], in0=shifted[:, q, :],
                                                      scalar=best[:, AT:AT + 1], in1=expd[:, q, :],
                                                      op0=ALU.is_ge, op1=ALU.mult, accum_out=rsum[:, 0, q:q + 1]))
                        dve.reciprocal(rsum[:, 1, q:q + 1], rsum[:, 0, q:q + 1]).then_inc(mask_ok, 1)

                    def maximum(q):
                        dve.wait_ge(s_ready, q + 1)
                        dve.tensor_reduce(negm[:, q:q + 1], flat2(m.ps[:, 0:4, :])[:, 0:CTX], AX.X, ALU.max,
                                          negate=True).then_inc(neg_ok, 1)

                    def output_low(q):
                        dve.wait_ge(o_hi, q + 1)
                        dve.tensor_tensor(ot[1][:, :, q * P:(q + 1) * P],
                                          m.ps[:, 6, 0:D].rearrange("p (c n) -> p c n", c=DC),
                                          ot[0][:, :, q * P:(q + 1) * P].bitcast(F32), ALU.subtract)\
                           .then_inc(o_lo, 1)

                    def add_output(q):
                        dve.wait_ge(y_ready, q + 1)
                        dve.scalar_tensor_tensor(out=x_b[:, q, :], in0=m.ps[:, 7, 0:D], scalar=rsum[:, 1, q:q + 1],
                                                 in1=x_b[:, q, :], op0=ALU.mult, op1=ALU.add).then_inc(y_done, 1)

                    beside = {0: [], 1: [], 2: items[0:3]}
                    rest = items[3:]
                    for r in range(3, ROUNDS):
                        n = -(-len(rest) // (ROUNDS - r))
                        beside[r], rest = rest[:n], rest[n:]
                    row_stats()
                    if finish:
                        largest(0, 0)
                    normalise()
                    for r in range(ROUNDS):
                        if finish and r:
                            largest(0, r)
                        for task in beside[r]:
                            item(task)
                    if finish:
                        mask(0)
                        largest(1, 0)
                    maximum(0)
                    if finish:
                        for r in range(1, ROUNDS):
                            largest(1, r)
                            if r == 3:
                                output_low(0)
                            if r == 4:
                                add_output(0)
                        mask(1)
                    maximum(1)
                    if finish:
                        output_low(1)
                        add_output(1)
            st.clear()

        attention_block(1, None, 0, finish=False)
        with nc.Fori(0, B // 2) as pair:
            attention_block(0, pair * 2, pair * 2 + 1, finish=True)
            attention_block(1, pair * 2 + 1, (pair * 2 + 2) % B, finish=True)
HD = 128
KVH, REP = 4, 4
VW = HD + 1


def plan_group(KT, KB, rope, attend, norm, prepare, tail):
    turns = [[] for _ in range(2 * KT)]

    def put(at, *tasks):
        turns[min(at, len(turns) - 1)].extend(tasks)

    if prepare:
        put(0, ("W", 0))
    if tail:
        put(0, ("OX", 0), ("OX", 1))
        put(1, ("W", 2))
        put(2, ("Y", 0), ("Y", 1))
    if norm and rope:
        put(1, ("PR", 0))
        put(2, ("PX", 0))
        for i in range(3):
            put(3 + i, ("RA", i))
        put(5, ("RS", 0))
    if norm:
        put(2, ("N", 0))
        put(4, ("NX", 0))
    if attend:
        for r in range(8):
            put(1 + r, ("R", r))
    if prepare:
        put(3, ("W", 1))
        at = 7 if norm else 3
        for t in range(0, KT, 2):
            put(at, *[("KV", i) for i in range(t, min(t + 2, KT))])
            at += 1
        put(at, ("Q", 0), ("Q", 1))
        at += 2
        chunks = 3 if rope else 1
        for c in range(chunks):
            put(at, ("KN", c))
            at += 1
        put(at, ("QN", 0))
        put(at + (1 if rope else 0), ("QN", 1))
        at += 1
        for k in range(len(KB)):
            put(at + k // 2, ("KX", k))
        at += 2
        put(at, ("QX", 0), ("QX", 1))
        at += 1
        left = len(turns) - at
        for r in range(8):
            put(at + (r * left) // 8, ("R", 8 + r))
    return turns


def grouped_attention(nc, m, name, w, rope):
    tiles = [(t * P, P if t < CTILES - 1 else CLAST, None) for t in range(CTILES)]
    if rope:
        tiles += [(CTX + q * P, P, q) for q in range(QT)]
    KT = len(tiles)
    NK = CTX + (S if rope else 0)
    NKP = NK + NK % 2
    GQ = REP * S
    NJ = GQ // P
    NG = 2
    JG = NJ // NG
    TURNS = KT * NG
    KB = [(t0, min(t0 + 4, KT)) for t0 in range(0, KT, 4)]
    KEND = [t[0] for t in tiles] + [NK]
    RH = [(0, 1024, 1024), (1024, NKP, NK)]
    SCALE = HD ** -0.5
    half = HD // 2

    with Stage(nc, name) as st:
        x_b = st.sb("x_b", [P, QT, D])
        x_n = st.sb("x_n", [P, QT, D])
        zt = [st.sb(f"zt{i}", [P, DC, S], F32R) for i in range(2)]
        ct = [st.sb(f"ct{i}", [P, DC, CTXP], F32R) for i in range(2)]
        stats = st.sb("stats", [P, QT, 6])
        mv = st.sb("mv", [P, QT, 2])
        rstd = st.sb("rstd", [P, 2, QT])
        z = st.sb("z", [P, QT, D])
        qw = st.sb("qw", [P, HD])
        kw = st.sb("kw", [P, HD])
        wf = [st.sb(f"wf{k}", [P, n]) for k, n in enumerate((DC * 2 * HD, DC * REP * HD, REP * D))]
        wr = [[st.sb(f"wr{k}{i}", [P, n], F32R) for i in range(2)]
              for k, n in enumerate((DC * 2 * HD, DC * REP * HD, REP * D))]
        k_rows = st.sb("k_rows", [P, KT, HD])
        v_rows = [st.sb(f"v_rows{i}", [P, KT, VW]) for i in range(2)]
        q_rows = st.sb("q_rows", [P, QT, REP, HD])
        k_sq = st.sb("k_sq", [P, 3, KT])
        q_sq = st.sb("q_sq", [P, 3, QT * REP])
        square = st.sb("square", [P, 8, HD])
        kts = [[st.sb(f"kt{g}{i}", [P, NKP], F32R) for i in range(2)] for g in range(2)]
        qts = [[st.sb(f"qt{g}{i}", [P, GQ], F32R) for i in range(2)] for g in range(2)]
        neg2 = st.sb("neg2", [P, NJ, 2])
        negmax = st.sb("negmax", [P, NJ])
        diag = st.sb("diag", [P, NJ, P], F32R)
        probs = st.sb("probs", [P, 3, 512])
        rsum = st.sb("rsum", [P, JG])
        o_rows = st.sb("o_rows", [P, NJ, HD])
        ot = [st.sb(f"ot{i}", [P, NJ * P], F32R) for i in range(2)]
        if rope:
            cs = st.sb("cs", [P, 2, KT, half])
            pos_i = st.sb("pos_i", [KT, P], I32)
            pos_rows = st.sb("pos_rows", [KT, P])
            pos_f = st.sb("pos_f", [P, KT])
            invf = st.sb("invf", [P, half])
            ang, tmp = k_rows[:, :, 0:half], k_rows[:, :, half:HD]
            by_cos = st.sb("by_cos", [P, 5 * HD])
            by_sin = st.sb("by_sin", [P, 5 * HD])

        once, zeroed = st.sem("once"), st.sem("zeroed")
        pos_in, rows_ok, angles, tab_ok = [st.sem(n) for n in "pos_in rows_ok angles tab_ok".split()]
        (x_in, ct_in, pre0, pre1, pre2, stored, w_hi, w_lo, dstep, pstep, var_ok, nrstd_ok, z_ok,
         item_ready, item_act, item_free, k_rstd, q_rstd, k_ready, q_normed, r_ready, neg_done, diag_done,
         st_ready, exp_done, pv_done, o_done, x_done, x_copied) = [st.sem(n) for n in (
             "x_in ct_in pre0 pre1 pre2 stored w_hi w_lo dstep pstep var_ok nrstd_ok z_ok "
             "item_ready item_act item_free k_rstd q_rstd k_ready q_normed r_ready neg_done diag_done "
             "st_ready exp_done pv_done o_done x_done x_copied").split()]

        with nc.Block(name=f"{name}_once") as block:
            @block.sync
            def _(sp):
                loads = [(qw[:, :], w["qw"].partition_broadcast(P)), (kw[:, :], w["kw"].partition_broadcast(P)),
                         (wf[0][:, :], w["wkv"][0]), (wf[1][:, :], w["wq"][0])]
                if rope:
                    loads.append((invf[:, :], w["inv_freq"].partition_broadcast(P)))
                for dst, src in loads:
                    sp.dma_start(dst, src).then_inc(once, 16)
                sp.wait_ge(once, 16 * len(loads))

            @block.gpsimd
            def _(pool):
                for i in range(2):
                    pool.memset(v_rows[i][:, :, HD:VW], 1.0).then_inc(zeroed, 1)
                    if NKP > NK:
                        pool.memset(kts[i][0][:, NK:NKP].bitcast(F32), 0.0).then_inc(zeroed, 1)
                if rope:
                    pool.memset(pos_i[:, :], 0).then_inc(zeroed, 1)
                pool.memset(k_rows[:, :, :], 0.0).then_inc(zeroed, 1)
                pool.memset(k_sq[:, :, :], 1.0).then_inc(zeroed, 1)
                pool.memset(o_rows[:, :, :], 0.0).then_inc(zeroed, 1)
                pool.memset(x_b[:, :, :], 0.0).then_inc(zeroed, 1)
        st.clear()

        def group_block(a, b_next, attend=True, norm=False, prepare=True, tail=True, store=None):
            kt, qt, v_cur = kts[a % 2], qts[a % 2], v_rows[a % 2]
            kt_n, qt_n, v_next = kts[(a + 1) % 2], qts[(a + 1) % 2], v_rows[(a + 1) % 2]
            turns = plan_group(KT, KB, rope, attend, norm, prepare, tail)
            flat = [task for turn in turns for task in turn]
            items = [task for task in flat if task[0] in ("PX", "NX", "KV", "Q", "KX", "QX", "OX", "Y")]
            number = {task: i for i, task in enumerate(items)}
            scalar_items = [task for task in items if task[0] not in ("PX", "Y")]
            acted = {task: i + 1 for i, task in enumerate(scalar_items)}
            weights = [task[1] for task in flat if task[0] == "W"]
            w_count = {k: i + 1 for i, k in enumerate(weights)}
            rough = [task[1] for task in flat if task[0] == "R"]
            r_count = {r: i for i, r in enumerate(rough)}

            def bank(task):
                return 2 + number[task] % 2

            def rough_block(r):
                return (4 + r // 2, kt, qt) if r < 8 else ((r - 8) // 2, kt_n, qt_n)

            with nc.Block(name=f"{name}_group{a + 1}") as block:
                @block.sync
                def _(sp):
                    if norm:
                        rows = m.x_dram[bass.ds(b_next * QT, QT), :].rearrange("t (p d) -> p t d", p=P)
                        sp.dma_start(x_n[:, :, :], rows).then_inc(x_in, 16)
                        if rope:
                            full = (CTILES - 1) * P
                            sp.dma_start(pos_i[0:CTILES - 1, :], w["pos"][bass.ds(b_next, 1), 0:full]
                                         .rearrange("a (t p) -> (a t) p", p=P)).then_inc(pos_in, 16)
                            sp.dma_start(pos_i[CTILES - 1:CTILES, 0:CLAST],
                                         w["pos"][bass.ds(b_next, 1), full:CTX]).then_inc(pos_in, 16)
                            sp.dma_start(pos_i[CTILES:KT, :], w["tok"][bass.ds(b_next, 1), :]
                                         .rearrange("a (t p) -> (a t) p", p=P)).then_inc(pos_in, 16)
                        for i, src in enumerate((m.ctx_hi, m.ctx_lo)):
                            sp.dma_start(flat2(ct[i][:, :, :]).bitcast(F32),
                                         src[bass.ds(b_next, 1), :, :].rearrange("a p n -> p (a n)"))\
                              .then_inc(ct_in, 16)
                    if prepare:
                        g_next = {0: (a + 2) % KVH, 1: (a + 2) % KVH, 2: a % KVH}
                        src = {0: w["wkv"], 1: w["wq"], 2: w["wo"]}
                        for k in sorted((0, 1, 2), key=lambda k: w_count.get(k, 0)):
                            if k in w_count:
                                sp.wait_ge(w_lo, w_count[k])
                            sp.dma_start(wf[k][:, :], src[k][g_next[k]]).then_inc((pre0, pre1, pre2)[k], 16)
                    if store is not None:
                        sp.wait_ge(x_done, QT)
                        sp.dma_start(store, x_b[:, :, :]).then_inc(stored, 16)
                        sp.wait_ge(stored, 16)
                    if prepare:
                        for s in (pre0, pre1, pre2):
                            sp.wait_ge(s, 16)

                @block.tensor
                def _(pe):
                    def begin(task):
                        i = number[task]
                        if i >= 2:
                            pe.wait_ge(item_free, i - 1)
                        return m.ps[:, bank(task), :]

                    def halves_ready(k):
                        pe.wait_ge(w_lo, w_count[k])

                    def PX(_i):
                        out = begin(("PX", 0))
                        pe.wait_ge(rows_ok, 1)
                        pe.transpose(out[:, 0:KT], pos_rows[:, :], m.ident[0:KT, 0:KT]).then_inc(item_ready, 1)

                    def NX(i):
                        pe.wait_ge(z_ok, QT)
                        out = begin(("NX", i))
                        for c in range(DC):
                            for q in range(QT):
                                ins = pe.transpose(out[:, (c * QT + q) * P:(c * QT + q + 1) * P],
                                                   z[:, q, c * P:(c + 1) * P], m.ident[:, :])
                        ins.then_inc(item_ready, 1)

                    def KV(t):
                        out = begin(("KV", t))
                        at, r, own = tiles[t]
                        if t == 0:
                            halves_ready(0)
                            if norm:
                                pe.wait_ge(ct_in, 32)
                        if own is not None and norm:
                            pe.wait_ge(item_free, number[("NX", 0)] + 1)
                        n = 0
                        for c in range(DC):
                            for s, v in HALVES:
                                src = (ct[s][:, c, at:at + r] if own is None
                                       else zt[s][:, c, own * P:(own + 1) * P])
                                ins = pe.matmul(out[0:r, 0:2 * HD], src, wr[0][v][:, c * 2 * HD:(c + 1) * 2 * HD],
                                                start=(n == 0), stop=(n == 3 * DC - 1))
                                n += 1
                        ins.then_inc(item_ready, 1)

                    def Q(q):
                        out = begin(("Q", q))
                        halves_ready(1)
                        if norm:
                            pe.wait_ge(item_free, number[("NX", 0)] + 1)
                        n = 0
                        for c in range(DC):
                            for s, v in HALVES:
                                ins = pe.matmul(out, zt[s][:, c, q * P:(q + 1) * P],
                                                wr[1][v][:, c * REP * HD:(c + 1) * REP * HD],
                                                start=(n == 0), stop=(n == 3 * DC - 1))
                                n += 1
                        ins.then_inc(item_ready, 1)

                    def KX(k):
                        out = begin(("KX", k))
                        pe.wait_ge(k_ready, 3 if rope else 1)
                        t0, t1 = KB[k]
                        for t in range(t0, t1):
                            at, r, _own = tiles[t]
                            ins = pe.transpose(out[:, at - KEND[t0]:at - KEND[t0] + r],
                                               k_rows[0:r, t, :], m.ident[0:r, 0:r])
                        ins.then_inc(item_ready, 1)

                    def QX(k):
                        out = begin(("QX", k))
                        pe.wait_ge(q_normed, QT)
                        for i in range(4):
                            j = 4 * k + i
                            ins = pe.transpose(out[:, i * P:(i + 1) * P], q_rows[:, j % QT, j // QT, :],
                                               m.ident[:, :])
                        ins.then_inc(item_ready, 1)

                    def OX(k):
                        out = begin(("OX", k))
                        for i in range(4):
                            ins = pe.transpose(out[:, i * P:(i + 1) * P], o_rows[:, 4 * k + i, :], m.ident[:, :])
                        ins.then_inc(item_ready, 1)

                    def Y(q):
                        out = begin(("Y", q))
                        halves_ready(2)
                        pe.wait_ge(item_free, number[("OX", 1)] + 1)
                        n = 0
                        for h in range(REP):
                            j = h * QT + q
                            for s, v in HALVES:
                                ins = pe.matmul(out[:, 0:D], ot[s][:, j * P:(j + 1) * P],
                                                wr[2][v][:, h * D:(h + 1) * D],
                                                start=(n == 0), stop=(n == 3 * REP - 1))
                                n += 1
                        ins.then_inc(item_ready, 1)

                    def R(r):
                        j, keys, queries = rough_block(r)
                        if r_count[r]:
                            pe.wait_ge(neg_done, r_count[r])
                        if r == 8:
                            pe.wait_ge(item_free, number[("QX", 1)] + 1)
                        a0, e0, _e = RH[r % 2]
                        for k, c0 in enumerate(range(a0, e0, 512)):
                            c1 = min(c0 + 512, e0)
                            ins = pe.matmul(m.ps[:, k, 0:c1 - c0], queries[0][:, j * P:(j + 1) * P],
                                            keys[0][:, c0:c1], start=True, stop=True)
                        ins.then_inc(r_ready, 1)

                    def scores(n):
                        G, t = divmod(n, KT)
                        at, r, _own = tiles[t]
                        if t == 0 and G:
                            pe.wait_ge(diag_done, JG)
                        if n >= 2:
                            pe.wait_ge(exp_done, n - 1)
                        out = m.ps[0:r, 4 + n % 2, :]
                        cols = slice(G * 512, (G + 1) * 512)
                        pe.matmul(out, m.ones_r[:, 0:r],
                                  diag[:, G * JG:(G + 1) * JG, :].rearrange("p j n -> p (j n)"),
                                  start=True, stop=False)
                        pe.matmul(out, kt[0][:, at:at + r], qt[0][:, cols], start=False, stop=False)
                        pe.matmul(out, kt[0][:, at:at + r], qt[1][:, cols], start=False, stop=False)
                        pe.matmul(out, kt[1][:, at:at + r], qt[0][:, cols], start=False, stop=True)\
                          .then_inc(st_ready, 1)

                    def values(n):
                        G, t = divmod(n, KT)
                        r = tiles[t][1]
                        pe.wait_ge(exp_done, n + 1)
                        if t == 0 and G:
                            pe.wait_ge(o_done, G)
                        for i in range(JG):
                            ins = pe.matmul(m.ps[:, 6 + i // 2, (i % 2) * 256:(i % 2) * 256 + VW],
                                            probs[0:r, n % 3, i * P:(i + 1) * P],
                                            v_cur[0:r, t, :], start=(t == 0 and i % 2 == 0),
                                            stop=(t == KT - 1), skip_group_check=True)
                        ins.then_inc(pv_done, 1)

                    does = {"PX": PX, "NX": NX, "KV": KV, "Q": Q, "KX": KX, "QX": QX, "OX": OX, "Y": Y, "R": R}
                    for n in range(TURNS):
                        if attend:
                            scores(n)
                        for task, i in turns[n]:
                            if task in does:
                                does[task](i)
                        if attend and n:
                            values(n - 1)
                    if attend:
                        values(TURNS - 1)

                @block.scalar
                def _(act):
                    def W(k):
                        act.activation(wr[k][0][:, :], wf[k][:, :], ACT.Copy).then_inc(w_hi, 1)

                    def begin(task):
                        act.wait_ge(item_ready, number[task] + 1)
                        return m.ps[:, bank(task), :]

                    def NX(i):
                        act.activation(flat2(zt[0][:, :, :]), begin(("NX", i)), ACT.Copy).then_inc(item_act, 1)

                    def KV(t):
                        r = tiles[t][1]
                        src = begin(("KV", t))
                        if t >= 4:
                            act.wait_ge(item_act, acted[("KV", t - 4)])
                        act.activation(square[0:r, t % 4, :], src[0:r, 0:HD], ACT.Square,
                                       accum_out=k_sq[0:r, 0, t:t + 1]).then_inc(item_act, 1)

                    def Q(q):
                        src = begin(("Q", q))
                        if q:
                            act.wait_ge(item_act, acted[("Q", q - 1)])
                        for h in range(REP):
                            i = q * REP + h
                            ins = act.activation(square[:, 4 + h, :], src[:, h * HD:(h + 1) * HD],
                                                 ACT.Square, accum_out=q_sq[:, 0, i:i + 1])
                        ins.then_inc(item_act, 1)

                    def KX(k):
                        a0, e0 = KEND[KB[k][0]], KEND[KB[k][1]]
                        act.activation(kt_n[0][:, a0:e0], begin(("KX", k))[:, 0:e0 - a0], ACT.Copy)\
                           .then_inc(item_act, 1)

                    def QX(k):
                        act.activation(qt_n[0][:, k * 512:(k + 1) * 512], begin(("QX", k)), ACT.Copy)\
                           .then_inc(item_act, 1)

                    def OX(k):
                        act.activation(ot[0][:, k * 512:(k + 1) * 512], begin(("OX", k)), ACT.Copy)\
                           .then_inc(item_act, 1)

                    def exp(n):
                        r = tiles[n % KT][1]
                        act.wait_ge(st_ready, n + 1)
                        if n >= 3:
                            act.wait_ge(pv_done, n - 2)
                        act.activation(probs[0:r, n % 3, :], m.ps[0:r, 4 + n % 2, :], ACT.Exp)\
                           .then_inc(exp_done, 1)

                    def RS(_i):
                        for i in range(2):
                            act.wait_ge(angles, i + 1)
                            act.activation(cs[:, i, :, :], cs[:, i, :, :], ACT.Sin).then_inc(tab_ok, 1)

                    does = {"RS": RS, "W": W, "NX": NX, "KV": KV, "Q": Q, "KX": KX, "QX": QX, "OX": OX}
                    for n in range(TURNS):
                        if attend:
                            exp(n)
                        for task, i in turns[n]:
                            if task in does:
                                does[task](i)

                @block.gpsimd
                def _(pool):
                    step = Step(pool, pstep)

                    def N(_i):
                        pool.wait_ge(var_ok, 1)
                        pool.tensor_tensor(rstd[:, 1, :], rstd[:, 0, :], m.nhalf[:, 0:1].to_broadcast([P, QT]),
                                           ALU.pow).then_inc(nrstd_ok, 1)

                    def KN(c):
                        if c == 0:
                            pool.wait_ge(item_act, acted[("KV", KT - 1)])
                            step(pool.tensor_scalar(k_sq[:, 1, :], k_sq[:, 0, :], 1.0 / HD, 1e-6, ALU.mult, ALU.add))
                            pool.tensor_tensor(k_sq[:, 2, :], k_sq[:, 1, :], m.nhalf[:, 0:1].to_broadcast([P, KT]),
                                               ALU.pow).then_inc(k_rstd, 1)

                    def QN(q):
                        if q == 0:
                            pool.wait_ge(item_act, acted[("Q", QT - 1)])
                            step(pool.tensor_scalar(q_sq[:, 1, :], q_sq[:, 0, :], 1.0 / HD, 1e-6, ALU.mult, ALU.add))
                            step(pool.tensor_tensor(q_sq[:, 2, :], q_sq[:, 1, :],
                                                    m.nhalf[:, 0:1].to_broadcast([P, QT * REP]), ALU.pow))
                            pool.tensor_scalar(q_sq[:, 2, :], q_sq[:, 2, :], SCALE, None, ALU.mult)\
                                .then_inc(q_rstd, 1)

                    def R(r):
                        if r % 2 == 0:
                            return
                        j = rough_block(r)[0]
                        pool.wait_ge(neg_done, r_count[r] + 1)
                        if attend and r == 9:
                            pool.wait_ge(st_ready, KT)
                        pool.tensor_scalar(diag[:, j, :], m.ident[:, :], negmax[:, j:j + 1], None, ALU.mult)\
                            .then_inc(diag_done, 1)

                    does = {"N": N, "KN": KN, "QN": QN, "R": R}
                    for turn in turns:
                        for task, i in turn:
                            if task in does:
                                does[task](i)

                @block.vector
                def _(dve):
                    step = Step(dve, dstep)

                    def W(k):
                        dve.wait_ge(w_hi, w_count[k])
                        dve.tensor_tensor(wr[k][1][:, :], wf[k][:, :], wr[k][0][:, :].bitcast(F32),
                                          ALU.subtract).then_inc(w_lo, 1)

                    def begin(task):
                        if task in acted:
                            dve.wait_ge(item_act, acted[task])
                        else:
                            dve.wait_ge(item_ready, number[task] + 1)
                        return m.ps[:, bank(task), :]

                    def low(task, dst, hi, width):
                        src = begin(task)
                        dve.tensor_tensor(dst, src[:, 0:width], hi.bitcast(F32), ALU.subtract)\
                           .then_inc(item_free, 1)

                    def N(_i):
                        dve.wait_ge(x_in, 16)
                        for q in range(QT):
                            ins = dve.bn_stats(stats[:, q, :], x_n[:, q, :])
                        step(ins)
                        for q in range(QT):
                            ins = dve.bn_aggr(mv[:, q, :], stats[:, q, :])
                        step(ins)
                        dve.tensor_scalar(rstd[:, 0, :], mv[:, :, 1], 1e-5, None, ALU.add).then_inc(var_ok, 1)

                    def NX(i):
                        low(("NX", i), flat2(zt[1][:, :, :]), flat2(zt[0][:, :, :]), 512)

                    def KV(t):
                        r = tiles[t][1]
                        src = begin(("KV", t))
                        dve.tensor_tensor(k_rows[0:r, t, :], src[0:r, 0:HD], kw[0:r, :], ALU.mult)
                        dve.tensor_copy(v_next[0:r, t, 0:HD], src[0:r, HD:2 * HD]).then_inc(item_free, 1)

                    def Q(q):
                        src = begin(("Q", q))
                        dve.tensor_tensor(q_rows[:, q, :, :], src.rearrange("p (h n) -> p h n", h=REP),
                                          qw[:, :].unsqueeze(1).to_broadcast([P, REP, HD]), ALU.mult)\
                           .then_inc(item_free, 1)

                    def rotate(rows, n, cos, sin):
                        bc = by_cos[:, 0:n * HD].rearrange("p (n i d) -> p n i d", n=n, i=2)
                        bs = by_sin[:, 0:n * HD].rearrange("p (n i d) -> p n i d", n=n, i=2)
                        dve.tensor_tensor(bs, rows, sin, ALU.mult)
                        step(dve.tensor_tensor(bc, rows, cos, ALU.mult))
                        dve.tensor_tensor(rows[:, :, 0, :], bc[:, :, 0, :], bs[:, :, 1, :], ALU.subtract)
                        step(dve.tensor_tensor(rows[:, :, 1, :], bc[:, :, 1, :], bs[:, :, 0, :], ALU.add))

                    def KN(c):
                        if c == 0:
                            dve.wait_ge(k_rstd, 1)
                            dve.wait_ge(item_free, number[("KV", KT - 1)] + 1)
                            if rope and norm:
                                dve.wait_ge(tab_ok, 2)
                        n = 5 if rope else KT
                        t0 = n * c
                        rows = k_rows[:, t0:t0 + n, :]
                        step(dve.tensor_tensor(rows, rows, k_sq[:, 2, t0:t0 + n].unsqueeze(2)
                                               .to_broadcast([P, n, HD]), ALU.mult))
                        if rope:
                            rotate(rows.rearrange("p n (i d) -> p n i d", i=2), n,
                                   cs[:, 0, t0:t0 + n, :].unsqueeze(2).to_broadcast([P, n, 2, half]),
                                   cs[:, 1, t0:t0 + n, :].unsqueeze(2).to_broadcast([P, n, 2, half]))
                        dve.engine_nop().then_inc(k_ready, 1)

                    def QN(q):
                        if q == 0:
                            dve.wait_ge(q_rstd, 1)
                            dve.wait_ge(item_free, number[("Q", QT - 1)] + 1)
                        rows = q_rows[:, q, :, :]
                        step(dve.tensor_tensor(rows, rows, q_sq[:, 2, q * REP:(q + 1) * REP].unsqueeze(2)
                                               .to_broadcast([P, REP, HD]), ALU.mult))
                        if rope:
                            rotate(rows.rearrange("p n (i d) -> p n i d", i=2), REP,
                                   cs[:, 0, CTILES + q, :].unsqueeze(1).unsqueeze(1).to_broadcast([P, REP, 2, half]),
                                   cs[:, 1, CTILES + q, :].unsqueeze(1).unsqueeze(1).to_broadcast([P, REP, 2, half]))
                        dve.engine_nop().then_inc(q_normed, 1)

                    def KX(k):
                        a0, e0 = KEND[KB[k][0]], KEND[KB[k][1]]
                        low(("KX", k), kt_n[1][:, a0:e0], kt_n[0][:, a0:e0], e0 - a0)

                    def QX(k):
                        low(("QX", k), qt_n[1][:, k * 512:(k + 1) * 512], qt_n[0][:, k * 512:(k + 1) * 512], 512)

                    def OX(k):
                        low(("OX", k), ot[1][:, k * 512:(k + 1) * 512], ot[0][:, k * 512:(k + 1) * 512], 512)

                    def Y(q):
                        src = begin(("Y", q))
                        dve.tensor_tensor(x_b[:, q, :], x_b[:, q, :], src[:, 0:D], ALU.add).then_inc(item_free, 1)
                        dve.wait_ge(item_free, number[("Y", q)] + 1)
                        dve.engine_nop().then_inc(x_done, 1)

                    def R(r):
                        j = rough_block(r)[0]
                        a0, _e0, e = RH[r % 2]
                        dve.wait_ge(r_ready, r_count[r] + 1)
                        ins = dve.tensor_reduce(neg2[:, j, r % 2:r % 2 + 1],
                                                m.ps[:, 0:2, :].rearrange("p b n -> p (b n)")[:, 0:e - a0],
                                                AX.X, ALU.max, negate=True)
                        if r % 2 == 0:
                            ins.then_inc(neg_done, 1)
                            return
                        step(ins)
                        dve.wait_ge(neg_done, r_count[r])
                        dve.tensor_tensor(negmax[:, j:j + 1], neg2[:, j, 0:1], neg2[:, j, 1:2], ALU.min)\
                           .then_inc(neg_done, 1)

                    def outputs(G):
                        dve.wait_ge(pv_done, KT * (G + 1))
                        o = m.ps[:, 6:8, :].rearrange("p b (i n) -> p (b i) n", i=2)
                        step(dve.reciprocal(rsum[:, :].unsqueeze(2), o[:, :, HD:VW]))
                        if G == 0 and tail:
                            dve.wait_ge(item_free, number[("OX", 1)] + 1)
                        dve.tensor_tensor(o_rows[:, G * JG:(G + 1) * JG, :], o[:, :, 0:HD],
                                          rsum[:, :].unsqueeze(2).to_broadcast([P, JG, HD]), ALU.mult)\
                           .then_inc(o_done, 1)

                    def NZ(_i):
                        dve.wait_ge(nrstd_ok, 1)
                        for q in range(QT):
                            dve.tensor_scalar(z[:, q, :], x_n[:, q, :], mv[:, q, 0:1], rstd[:, 1, q:q + 1],
                                              ALU.subtract, ALU.mult).then_inc(z_ok, 1)

                    def PR(_i):
                        dve.wait_ge(pos_in, 48)
                        dve.tensor_copy(pos_rows[:, :], pos_i[:, :]).then_inc(rows_ok, 1)

                    def PX(_i):
                        src = begin(("PX", 0))
                        step(dve.tensor_copy(pos_f[:, :], src[:, 0:KT]))
                        dve.engine_nop().then_inc(item_free, 1)

                    def RA(i):
                        c1 = 6.28125
                        c2 = float(np.float32(0.0019353071795864769))
                        c3 = 2 * np.pi - c1 - c2
                        magic = 12582912.0
                        PI = 3.1415925
                        cos, sin = cs[:, 0, :, :], cs[:, 1, :, :]
                        if i == 0:
                            step(dve.tensor_tensor(ang, pos_f[:, :].unsqueeze(2).to_broadcast([P, KT, half]),
                                                   invf[:, :].unsqueeze(1).to_broadcast([P, KT, half]), ALU.mult))
                            step(dve.tensor_scalar(tmp, ang, 1.0 / (2 * np.pi), magic, ALU.mult, ALU.add))
                            step(dve.tensor_scalar(tmp, tmp, -magic, None, ALU.add))
                        if i == 1:
                            step(dve.scalar_tensor_tensor(out=sin, in0=tmp, scalar=-c1, in1=ang,
                                                          op0=ALU.mult, op1=ALU.add))
                            step(dve.scalar_tensor_tensor(out=sin, in0=tmp, scalar=-c2, in1=sin,
                                                          op0=ALU.mult, op1=ALU.add))
                            step(dve.scalar_tensor_tensor(out=sin, in0=tmp, scalar=-c3, in1=sin,
                                                          op0=ALU.mult, op1=ALU.add))
                        if i == 2:
                            step(dve.tensor_scalar(cos, sin, np.pi / 2, None, ALU.add))
                            step(dve.tensor_scalar(tmp, cos, np.pi, -2 * np.pi, ALU.is_gt, ALU.mult))
                            step(dve.tensor_tensor(cos, cos, tmp, ALU.add))
                            dve.tensor_scalar(cos, cos, PI, -PI, ALU.min, ALU.max).then_inc(angles, 1)
                            dve.tensor_scalar(sin, sin, PI, -PI, ALU.min, ALU.max).then_inc(angles, 1)

                    does = {"PR": PR, "PX": PX, "RA": RA, "W": W, "N": N, "NX": NX, "KV": KV, "Q": Q, "KN": KN, "QN": QN, "KX": KX, "QX": QX,
                            "OX": OX, "Y": Y, "R": R}
                    for n in range(TURNS):
                        if attend and n == KT + 1:
                            outputs(0)
                        for task, i in turns[n]:
                            if task == "NX":
                                NZ(i)
                            if task in does:
                                does[task](i)
                    if attend:
                        outputs(1)
                    if store is not None and prepare:
                        dve.wait_ge(stored, 16)
                        dve.tensor_copy(x_b[:, :, :], x_n[:, :, :]).then_inc(x_copied, 1)
            st.clear()

        group_block(-1, 0, attend=False, norm=True, tail=False)
        with nc.Fori(0, B) as b:
            before = m.x_pad[bass.ds(b * QT, QT), :].rearrange("t (p d) -> p t d", p=P)
            for a in range(KVH):
                group_block(a, (b + 1) % B if a == KVH - 1 else None, norm=(a == KVH - 1),
                            store=before if a == 0 else None)
        last = m.x_dram[(B - 1) * QT:B * QT, :].rearrange("t (p d) -> p t d", p=P)
        group_block(KVH, None, attend=False, prepare=False, store=last)
NE = 8
TOK = B * S
HALF = 512


class FfnBase:

    def __init__(self, st, keep_z=False):
        self.x = st.sb("x", [P, TT, D])
        self.z = st.sb("z", [P, TT, D])
        self.zt = [st.sb(f"zt{i}", [P, DC, TOK], F32R) for i in range(2)]
        self.scratch = (st.sb("stats", [P, TT, 6]), st.sb("mv", [P, TT, 2]), st.sb("rstd", [P, 2, TT]), self.z)
        self.nsem = [st.sem("n_" + n) for n in NORM_SEMS]

    def norm(self, nc, st, m, extra=()):
        norm_block(nc, st, m, self.x, self.zt[0], self.zt[1], TT,
                   m.x_dram[:, :].rearrange("t (p d) -> p t d", p=P), self.nsem, self.scratch, extra,
                   name=f"{st.name}_norm")
        st.clear()

    def store(self, nc, st, m):
        with nc.Block(name=f"{st.name}_out") as block:
            @block.sync
            def _(sp):
                sp.dma_start(m.x_dram[:, :].rearrange("t (p d) -> p t d", p=P), self.x[:, :, :])\
                  .then_inc(self.nsem[0], 16)
                sp.wait_ge(self.nsem[0], 16)
        st.clear()


class Gates:

    def __init__(self, st):
        self.wg_f = st.sb("wg_f", [P, DC, NE])
        self.wg = [st.sb(f"wg{i}", [P, DC, NE], F32R) for i in range(2)]
        self.bias = st.sb("gate_bias", [P, NE])
        self.logit = st.sb("logit", [P, TT, NE])
        self.prob = st.sb("prob", [P, TT, NE])
        self.row = st.sb("gate_row", [P, 2, TT])
        self.top = st.sb("top", [P, TT, 8])
        self.index = st.sb("index", [P, TT, 8], U32)
        self.index_f = st.sb("index_f", [P, TT, 8])
        self.iota_i = st.sb("iota_i", [P, NE], I32)
        self.iota = st.sb("iota", [P, NE])
        self.hot = st.sb("hot", [P, 2, TT, NE])
        self.sems = [st.sem("g_" + n) for n in ("split", "logits", "step", "shifted", "exped", "iota")]

    def route(self, nc, st, m, zt, comb, bias, topk, renorm):
        split, logits, dstep, shifted, exped, iota_ok = self.sems
        with nc.Block(name=f"{st.name}_route") as block:
            @block.scalar
            def _(act):
                act.activation(self.wg[0][:, :, :], self.wg_f[:, :, :], ACT.Copy).then_inc(split, 1)
                act.wait_ge(shifted, 1)
                act.activation(self.prob[:, :, :], self.logit[:, :, :], ACT.Exp).then_inc(exped, 1)

            @block.gpsimd
            def _(pool):
                pool.iota(self.iota_i[:, :], pattern=[[1, NE]], base=0, channel_multiplier=0).then_inc(iota_ok, 1)

            @block.tensor
            def _(pe):
                pe.wait_ge(split, 2)
                for t in range(TT):
                    n = 0
                    for c in range(DC):
                        for s, v in ((0, 0), (0, 1), (1, 0)):
                            ins = pe.matmul(m.ps[:, 0, t * NE:(t + 1) * NE], zt[s][:, c, t * P:(t + 1) * P],
                                            self.wg[v][:, c, :], start=(n == 0), stop=(n == 3 * DC - 1))
                            n += 1
                ins.then_inc(logits, 1)

            @block.vector
            def _(dve):
                step = Step(dve, dstep)

                def each(a):
                    return a.unsqueeze(2).to_broadcast([P, TT, NE])

                dve.wait_ge(split, 1)
                dve.tensor_tensor(self.wg[1][:, :, :], self.wg_f[:, :, :], self.wg[0][:, :, :].bitcast(F32),
                                  ALU.subtract).then_inc(split, 1)
                dve.wait_ge(iota_ok, 1)
                step(dve.tensor_copy(self.iota[:, :], self.iota_i[:, :]))
                dve.wait_ge(logits, 1)
                ps = m.ps[:, 0, 0:TT * NE].rearrange("p (t e) -> p t e", e=NE)
                if bias:
                    step(dve.tensor_tensor(self.logit[:, :, :], ps,
                                           self.bias[:, :].unsqueeze(1).to_broadcast([P, TT, NE]), ALU.add))
                else:
                    step(dve.tensor_copy(self.logit[:, :, :], ps))
                step(dve.tensor_reduce(self.row[:, 0, :], self.logit[:, :, :], AX.X, ALU.max))
                dve.tensor_tensor(self.logit[:, :, :], self.logit[:, :, :], each(self.row[:, 0, :]),
                                  ALU.subtract).then_inc(shifted, 1)
                dve.wait_ge(exped, 1)
                step(dve.tensor_reduce(self.row[:, 0, :], self.prob[:, :, :], AX.X, ALU.add))
                step(dve.reciprocal(self.row[:, 1, :], self.row[:, 0, :]))
                step(dve.tensor_tensor(self.prob[:, :, :], self.prob[:, :, :], each(self.row[:, 1, :]), ALU.mult))
                for t in range(TT):
                    ins = dve.max(out=self.top[:, t, :], in_=self.prob[:, t, :])
                step(ins)
                for t in range(TT):
                    ins = dve.max_index(out=self.index[:, t, :], in_max=self.top[:, t, :],
                                        in_values=self.prob[:, t, :])
                step(ins)
                step(dve.tensor_copy(self.index_f[:, :, :], self.index[:, :, :]))
                if renorm:
                    step(dve.tensor_tensor(self.row[:, 0, :], self.top[:, :, 0], self.top[:, :, 1], ALU.add))
                    step(dve.reciprocal(self.row[:, 1, :], self.row[:, 0, :]))
                    step(dve.tensor_tensor(self.top[:, :, 0:2], self.top[:, :, 0:2],
                                           self.row[:, 1, :].unsqueeze(2).to_broadcast([P, TT, 2]), ALU.mult))
                for k in range(topk):
                    step(dve.tensor_tensor(self.hot[:, k, :, :],
                                           self.iota[:, :].unsqueeze(1).to_broadcast([P, TT, NE]),
                                           each(self.index_f[:, :, k]), ALU.is_equal))
                if comb is not None:
                    for k in range(topk):
                        step(dve.tensor_tensor(self.hot[:, k, :, :], self.hot[:, k, :, :],
                                               each(self.top[:, :, k]), ALU.mult))
                    step(dve.tensor_tensor(comb[:, :, 0:NE], self.hot[:, 0, :, :], self.hot[:, 1, :, :], ALU.add))
        st.clear()


def gelu_experts(nc, m, w):
    H = 512
    HC = H // P
    with Stage(nc, "f0") as st:
        f = FfnBase(st)
        gates = Gates(st)
        comb = st.sb("comb", [P, TT, NE])
        comb_t = st.sb("comb_t", [NE, TOK])
        b3 = st.sb("b3", [NE, D])
        comb_e = st.sb("comb_e", [P, TT])
        wf = st.sb("wf", [P, 2 * H + HC * H + HC * D])
        wr = [st.sb(f"wr{i}", [P, 2 * H + HC * H + HC * D], F32R) for i in range(2)]
        cuts = [0, DC * H, DC * H + HC * H, DC * H + HC * H + HC * D]
        bias_all = st.sb("bias_all", [P, NE, 2 * HC])
        bias = st.sb("bias", [P, 2 * HC])
        full = st.sb("full", [P, 3, HALF])
        h = [[st.sb(f"h{l}{i}", [P, HC, TOK], F32R) for i in range(2)] for l in range(2)]
        turned, copied, b3_ready, b3_done = [st.sem(n) for n in ("turned", "copied", "b3_ready", "b3_done")]
        w_in = [st.sem(f"w_in{i}") for i in range(3)]
        bias_ok, w_hi, w_lo, comb_ok, h_ready, full_done, hi_done, lo_done, y_ready, y_done = [
            st.sem(n) for n in ("bias_ok w_hi w_lo comb_ok h_ready full_done hi_done lo_done y_ready y_done").split()]
        f.norm(nc, st, m, [(flat2(gates.wg_f[:, :, :]), w["wg"]),
                           (gates.bias[:, :], w["bg"].partition_broadcast(P)), (b3[:, :], w["b3"]),
                           (bias_all[:, :, :], w["b12"].rearrange("e p n -> p e n"))]
               + [(wf[:, cuts[i]:cuts[i + 1]], w[f"w{i + 1}"][0, :, :]) for i in range(3)])
        gates.route(nc, st, m, f.zt, comb, True, 2, False)

        def split_high(act, i):
            act.activation(wr[0][:, cuts[i]:cuts[i + 1]], wf[:, cuts[i]:cuts[i + 1]], ACT.Copy).then_inc(w_hi, 1)

        def split_low(dve, i, n):
            dve.wait_ge(w_hi, n)
            dve.tensor_tensor(wr[1][:, cuts[i]:cuts[i + 1]], wf[:, cuts[i]:cuts[i + 1]],
                              wr[0][:, cuts[i]:cuts[i + 1]].bitcast(F32), ALU.subtract).then_inc(w_lo, 1)

        with nc.Block(name="f0_b3") as block:
            @block.scalar
            def _(act):
                split_high(act, 0)

            @block.tensor
            def _(pe):
                for t in range(TT):
                    ins = pe.transpose(m.ps[0:NE, t // 4, (t % 4) * P:(t % 4 + 1) * P], comb[:, t, :], m.ident[:, :])
                ins.then_inc(turned, 1)
                pe.wait_ge(copied, 1)
                for t in range(TT):
                    if t >= 4:
                        pe.wait_ge(b3_done, t - 3)
                    pe.matmul(m.ps[:, 4 + t % 4, 0:D], comb_t[:, t * P:(t + 1) * P], b3[:, :],
                              start=True, stop=True).then_inc(b3_ready, 1)

            @block.vector
            def _(dve):
                split_low(dve, 0, 1)
                dve.wait_ge(turned, 1)
                dve.tensor_copy(comb_t[:, :], flat2(m.ps[0:NE, 0:2, :])).then_inc(copied, 1)
                for t in range(TT):
                    dve.wait_ge(b3_ready, t + 1)
                    dve.tensor_tensor(f.x[:, t, :], f.x[:, t, :], m.ps[:, 4 + t % 4, 0:D], ALU.add)\
                       .then_inc(b3_done, 1)
        st.clear()

        units = [(l, hf, o) for l in range(2) for hf in range(2) for o in range(HC)]

        def done_by(layer, hf):
            return (layer * 2 + hf + 1) * HC

        with nc.Fori(0, NE) as e:
            with nc.Block(name="f0_expert") as block:
                @block.sync
                def _(sp):
                    for i in range(3):
                        if i:
                            sp.wait_ge(w_lo, i)
                        sp.dma_start(wf[:, cuts[i]:cuts[i + 1]], w[f"w{i + 1}"][bass.ds((e + 1) % NE, 1), :, :]
                                     .rearrange("a p n -> p (a n)")).then_inc(w_in[i], 16)
                    for i in range(3):
                        sp.wait_ge(w_in[i], 16)

                @block.tensor
                def _(pe):
                    def wpart(v, l, k, o, n):
                        at = cuts[l] + k * (D if l == 2 else H) + o
                        return wr[v][:, at:at + n]

                    for u, (l, hf, o) in enumerate(units):
                        if l == 1:
                            pe.wait_ge(w_hi, 1)
                            pe.wait_ge(w_lo, 1)
                        if u >= 6:
                            pe.wait_ge(lo_done, u - 5)
                        if l == 1:
                            pe.wait_ge(lo_done, done_by(0, hf))
                        src = f.zt if l == 0 else h[0]
                        K = DC if l == 0 else HC
                        n = 0
                        for k in range(K):
                            for s, v in ((0, 0), (1, 0), (0, 1)):
                                ins = pe.matmul(m.ps[:, u % 6, :], wpart(v, l, k, o * P, P),
                                                src[s][:, k, hf * HALF:(hf + 1) * HALF],
                                                start=(n == 0), stop=(n == 3 * K - 1))
                                n += 1
                        ins.then_inc(h_ready, 1)
                    pe.wait_ge(w_hi, 2)
                    pe.wait_ge(w_lo, 2)
                    for t in range(TT):
                        pe.wait_ge(lo_done, done_by(1, t * P // HALF))
                        if t >= 2:
                            pe.wait_ge(y_done, t - 1)
                        n = 0
                        for k in range(HC):
                            for s, v in ((0, 0), (0, 1), (1, 0)):
                                ins = pe.matmul(m.ps[:, 6 + t % 2, 0:D], h[1][s][:, k, t * P:(t + 1) * P],
                                                wpart(v, 2, k, 0, D), start=(n == 0), stop=(n == 3 * HC - 1))
                                n += 1
                        ins.then_inc(y_ready, 1)

                @block.scalar
                def _(act):
                    split_high(act, 1)
                    split_high(act, 2)
                    act.wait_ge(bias_ok, 1)
                    for u, (l, hf, o) in enumerate(units):
                        act.wait_ge(h_ready, u + 1)
                        if u == done_by(0, 1) + 1:
                            act.wait_ge(w_in[0], 16)
                            split_high(act, 0)
                        if u >= 3:
                            act.wait_ge(lo_done, u - 2)
                        b = bias[:, l * HC + o:l * HC + o + 1]
                        act.activation(full[:, u % 3, :], m.ps[:, u % 6, :], ACT.Gelu, bias=b).then_inc(full_done, 1)
                        act.activation(h[l][0][:, o, hf * HALF:(hf + 1) * HALF], m.ps[:, u % 6, :], ACT.Gelu,
                                       bias=b).then_inc(hi_done, 1)

                @block.vector
                def _(dve):
                    dve.tensor_copy(comb_e[:, :], comb[:, :, bass.ds(e, 1)].rearrange("p t a -> p (t a)"))\
                       .then_inc(comb_ok, 1)
                    dve.tensor_copy(bias[:, :], bias_all[:, bass.ds(e, 1), :].rearrange("p a n -> p (a n)"))\
                       .then_inc(bias_ok, 1)
                    split_low(dve, 1, 1)
                    split_low(dve, 2, 2)
                    for u, (l, hf, o) in enumerate(units):
                        if u == done_by(0, 1) + 2:
                            split_low(dve, 0, 3)
                        dve.wait_ge(hi_done, u + 1)
                        cols = slice(hf * HALF, (hf + 1) * HALF)
                        dve.tensor_tensor(h[l][1][:, o, cols], full[:, u % 3, :],
                                          h[l][0][:, o, cols].bitcast(F32), ALU.subtract).then_inc(lo_done, 1)
                    dve.wait_ge(comb_ok, 1)
                    for t in range(TT):
                        dve.wait_ge(y_ready, t + 1)
                        dve.scalar_tensor_tensor(out=f.x[:, t, :], in0=m.ps[:, 6 + t % 2, 0:D],
                                                 scalar=comb_e[:, t:t + 1], in1=f.x[:, t, :],
                                                 op0=ALU.mult, op1=ALU.add).then_inc(y_done, 1)
            st.clear()
        f.store(nc, st, m)


def scaled_linear(nc, m, w):
    with Stage(nc, "f1") as st:
        f = FfnBase(st)
        wf = st.sb("wf", [P, DC, D])
        wr = [st.sb(f"wr{i}", [P, DC, D], F32R) for i in range(2)]
        scale = st.sb("scale", [P, D])
        bias = st.sb("bias", [P, D])
        w_full, w_hi, w_lo, y_ready, y_done, dstep = [
            st.sem(n) for n in ("w_full", "w_hi", "w_lo", "y_ready", "y_done", "dstep")]
        f.norm(nc, st, m, [(flat2(wf[:, :, :]), w["w"]), (scale[:, :], w["scale"].partition_broadcast(P)),
                           (bias[:, :], w["bias"].partition_broadcast(P))])
        with nc.Block(name="f1_linear") as block:
            @block.vector
            def _(dve):
                dve.tensor_tensor(wf[:, :, :], wf[:, :, :], scale[:, :].unsqueeze(1).to_broadcast([P, DC, D]),
                                  ALU.mult).then_inc(w_full, 1)
                dve.wait_ge(w_hi, 1)
                dve.tensor_tensor(wr[1][:, :, :], wf[:, :, :], wr[0][:, :, :].bitcast(F32),
                                  ALU.subtract).then_inc(w_lo, 1)
                step = Step(dve, dstep)
                step(dve.tensor_tensor(f.x[:, :, :], f.x[:, :, :],
                                       bias[:, :].unsqueeze(1).to_broadcast([P, TT, D]), ALU.add))
                for t in range(TT):
                    dve.wait_ge(y_ready, t + 1)
                    dve.tensor_tensor(f.x[:, t, :], f.x[:, t, :], m.ps[:, t, 0:D], ALU.add).then_inc(y_done, 1)

            @block.scalar
            def _(act):
                act.wait_ge(w_full, 1)
                act.activation(wr[0][:, :, :], wf[:, :, :], ACT.Copy).then_inc(w_hi, 1)

            @block.tensor
            def _(pe):
                pe.wait_ge(w_lo, 1)
                for t in range(TT):
                    n = 0
                    for c in range(DC):
                        for s, v in ((0, 0), (0, 1), (1, 0)):
                            ins = pe.matmul(m.ps[:, t, 0:D], f.zt[s][:, c, t * P:(t + 1) * P], wr[v][:, c, :],
                                            start=(n == 0), stop=(n == 3 * DC - 1))
                            n += 1
                    ins.then_inc(y_ready, 1)
        st.clear()
        f.store(nc, st, m)


class GatedUnits:

    def __init__(self, st, per):
        self.per = per
        self.wf = st.sb("u_wf", [P, 3, (DC * 2 + 2) * P])
        self.wr = [st.sb(f"u_wr{i}", [P, 3, (DC * 2 + 2) * P], F32R) for i in range(2)]
        self.act = st.sb("u_act", [P, 2, HALF])
        self.full = st.sb("u_full", [P, 2, HALF])
        self.h = [st.sb(f"u_h{i}", [P, 2, TOK], F32R) for i in range(2)]
        self.weight = st.sb("u_weight", [P, per, TT])
        self.sems = [st.sem("u_" + n) for n in
                     "in0 in1 in2 w_hi w_lo weight gu_ready silu_done full_done hi_done lo_done y_ready y_done".split()]

    def first_loads(self, w):
        return [(self.wf[:, u, :], w[u, :, :]) for u in range(2)]

    def block(self, nc, m, f, src, weight, name, sizes, ahead):
        (in0, in1, in2, w_hi, w_lo, weight_ok, gu_ready, silu_done, full_done, hi_done, lo_done, y_ready,
         y_done) = self.sems
        per, GU, HT = self.per, DC * 2 * P, TT // 2
        arrived = (in0, in1, in2)
        loads = list(range(2, per + (2 if ahead else 0)))

        def load_count(u):
            return 16 * len([k for k in loads if k <= u and k % 3 == u % 3])

        with nc.Block(name=name) as block:
            @block.sync
            def _(sp):
                for u in loads:
                    if u >= 3:
                        sp.wait_ge(w_lo, u - 2)
                    sp.dma_start(self.wf[:, u % 3, :], src(u)).then_inc(arrived[u % 3], 16)
                for u in loads[-2:] if ahead else []:
                    sp.wait_ge(arrived[u % 3], load_count(u))

            @block.scalar
            def _(act):
                def split(u):
                    if u >= 2:
                        act.wait_ge(arrived[u % 3], load_count(u))
                    if u >= 3:
                        act.wait_ge(y_ready, TT * (u - 2))
                    act.activation(self.wr[0][:, u % 3, :], self.wf[:, u % 3, :], ACT.Copy).then_inc(w_hi, 1)

                def hidden(u, hf):
                    i, r = 2 * u + hf, sizes[u]
                    act.wait_ge(gu_ready, i + 1)
                    if i >= 2:
                        act.wait_ge(full_done, i - 1)
                    act.activation(self.act[0:r, i % 2, :], m.ps[0:r, 2 * (i % 3), :], ACT.Silu).then_inc(silu_done, 1)
                    act.wait_ge(full_done, i + 1)
                    if u >= 2:
                        act.wait_ge(y_ready, TT * (u - 1))
                    act.activation(self.h[0][0:r, u % 2, hf * HALF:(hf + 1) * HALF], self.full[0:r, i % 2, :],
                                   ACT.Copy).then_inc(hi_done, 1)

                split(0)
                for u in range(per):
                    hidden(u, 0)
                    if u + 1 < per:
                        split(u + 1)
                    hidden(u, 1)

            @block.vector
            def _(dve):
                if weight is not None:
                    dve.tensor_copy(self.weight[:, :, :], weight).then_inc(weight_ok, 1)

                def split(u):
                    dve.wait_ge(w_hi, u + 1)
                    dve.tensor_tensor(self.wr[1][:, u % 3, :], self.wf[:, u % 3, :],
                                      self.wr[0][:, u % 3, :].bitcast(F32), ALU.subtract).then_inc(w_lo, 1)

                def hidden(u, hf):
                    i, r = 2 * u + hf, sizes[u]
                    dve.wait_ge(silu_done, i + 1)
                    if i >= 2:
                        dve.wait_ge(lo_done, i - 1)
                        dve.wait_ge(hi_done, i - 1)
                    dve.tensor_tensor(self.full[0:r, i % 2, :], self.act[0:r, i % 2, :],
                                      m.ps[0:r, 2 * (i % 3) + 1, :], ALU.mult).then_inc(full_done, 1)
                    dve.wait_ge(hi_done, i + 1)
                    cols = slice(hf * HALF, (hf + 1) * HALF)
                    dve.tensor_tensor(self.h[1][0:r, u % 2, cols], self.full[0:r, i % 2, :],
                                      self.h[0][0:r, u % 2, cols].bitcast(F32), ALU.subtract).then_inc(lo_done, 1)

                def outputs(u, hf):
                    for t in range(hf * HT, (hf + 1) * HT):
                        dve.wait_ge(y_ready, u * TT + t + 1)
                        y = m.ps[:, 6 + t % 2, 0:D]
                        if u and not t:
                            dve.wait_ge(y_done, u * TT)
                        if weight is None:
                            ins = dve.tensor_tensor(f.x[:, t, :], f.x[:, t, :], y, ALU.add)
                        else:
                            ins = dve.scalar_tensor_tensor(out=f.x[:, t, :], in0=y,
                                                           scalar=self.weight[:, u, t:t + 1],
                                                           in1=f.x[:, t, :], op0=ALU.mult, op1=ALU.add)
                        ins.then_inc(y_done, 1)

                split(0)
                if weight is not None:
                    dve.wait_ge(weight_ok, 1)
                for u in range(per):
                    if u:
                        outputs(u - 1, 0)
                    hidden(u, 0)
                    if u + 1 < per:
                        split(u + 1)
                    if u:
                        outputs(u - 1, 1)
                    hidden(u, 1)
                for hf in range(2):
                    outputs(per - 1, hf)

            @block.tensor
            def _(pe):
                def gate_up(u, hf):
                    i, r = 2 * u + hf, sizes[u]
                    pe.wait_ge(w_hi, u + 1)
                    pe.wait_ge(w_lo, u + 1)
                    if i >= 3:
                        pe.wait_ge(full_done, i - 2)
                    for part in range(2):
                        n = 0
                        for c in range(DC):
                            at = c * 2 * P + part * P
                            for s, v in ((0, 0), (1, 0), (0, 1)):
                                ins = pe.matmul(m.ps[0:r, 2 * (i % 3) + part, :], self.wr[v][:, u % 3, at:at + r],
                                                f.zt[s][:, c, hf * HALF:(hf + 1) * HALF],
                                                start=(n == 0), stop=(n == 3 * DC - 1))
                                n += 1
                    ins.then_inc(gu_ready, 1)

                def down(u, hf):
                    r = sizes[u]
                    pe.wait_ge(lo_done, 2 * u + hf + 1)
                    for t in range(hf * HT, (hf + 1) * HT):
                        if u * TT + t >= 2:
                            pe.wait_ge(y_done, u * TT + t - 1)
                        for n, (s, v) in enumerate(((0, 0), (0, 1), (1, 0))):
                            ins = pe.matmul(m.ps[:, 6 + t % 2, 0:D], self.h[s][0:r, u % 2, t * P:(t + 1) * P],
                                            self.wr[v][0:r, u % 3, GU:GU + D], start=(n == 0), stop=(n == 2))
                        ins.then_inc(y_ready, 1)

                for u in range(per):
                    for hf in range(2):
                        gate_up(u, hf)
                        if u:
                            down(u - 1, hf)
                for hf in range(2):
                    down(per - 1, hf)


def silu_experts(nc, m, w):
    SHARED, PER = 4, 6
    BLOCKS = (NE + SHARED) // PER
    with Stage(nc, "f3") as st:
        f = FfnBase(st)
        gates = Gates(st)
        comb = st.sb("comb", [P, TT, NE + SHARED])
        units = GatedUnits(st, PER)
        ones_ok = st.sem("ones_ok")
        f.norm(nc, st, m, [(flat2(gates.wg_f[:, :, :]), w["wg"])] + units.first_loads(w["units"]))
        with nc.Block(name="f3_ones") as block:
            @block.gpsimd
            def _(pool):
                pool.memset(comb[:, :, NE:], 1.0).then_inc(ones_ok, 1)
        gates.route(nc, st, m, f.zt, comb, False, 2, True)
        with nc.Fori(0, BLOCKS) as e:
            def weights_of(u):
                first = e * PER if u < PER else ((e + 1) % BLOCKS) * PER
                return w["units"][bass.ds(first + u % PER, 1), :, :].rearrange("a p n -> p (a n)")

            units.block(nc, m, f, weights_of, comb[:, :, bass.ds(e * PER, PER)].rearrange("p t e -> p e t"),
                        "f3_units", [P] * PER, ahead=True)
            st.clear()
        f.store(nc, st, m)


def capacity_experts(nc, m, w):
    C = TOK // NE
    H = 352
    SIZES = [min(P, H - a) for a in range(0, H, P)]
    HC = len(SIZES)
    DROPPED = 4.0 * TOK
    EPB = 4
    with Stage(nc, "f2") as st:
        f = FfnBase(st)
        gates = Gates(st)
        units = GatedUnits(st, HC)
        upper = st.sb("upper", [P, P])
        upper_r = st.sb("upper_r", [P, P], F32R)
        first_r = st.sb("first_r", [P, TT, NE], F32R)
        z_r = [st.sb(f"z_r{i}", [P, TT, D], F32R) for i in range(2)]
        slot_i = st.sb("slot_i", [P, NE * C], I32)
        slot = st.sb("slot", [P, NE * C])
        row_i = st.sb("row_i", [P, NE], I32)
        row_f = st.sb("row_f", [P, NE])
        place = st.sb("place", [P, TT, NE])
        flat = st.sb("flat", [P, 3, TT])
        hot = st.sb("hot_slots", [P, 2, NE * C], F32R)
        wf = st.sb("wf", [P, 2, 2 * DC * H + HC * D])
        xd = st.sb("xd", [P, DC, NE * C])
        xe = st.sb("xe", [P, DC, EPB * C])
        act_g = st.sb("act_g", [P, 2, HC, C])
        hid = st.sb("hid", [P, 2, HC, C])
        oe_b = [st.sb(f"oe_b{i}", [P, EPB, D], F32R) for i in range(2)]
        oe = [st.sb(f"oe{i}", [P, NE, D], F32R) for i in range(2)]
        flat_b = st.sb("flat_b", [P, TOK])
        taken = st.sb("taken", [P, 2, TOK], F32R)
        made, rstep, ranked, flat_ok, hot_ok, disp, xd_ok, fb_ready, fb_ok = [
            st.sem(n) for n in "made rstep ranked flat_ok hot_ok disp xd_ok fb_ready fb_ok".split()]
        w_in0, w_in1, xe_ok, g_ready, silu_ok, hid_ok, oe_ready, oe_hi, oe_lo, oe_kept, split_z, low_z, ones_ok = [
            st.sem(n) for n in ("w_in0 w_in1 xe_ok g_ready silu_ok hid_ok oe_ready oe_hi oe_lo oe_kept split_z "
                                "low_z ones_ok").split()]
        dt_ok, dt_used, y_done = [st.sem(n) for n in "dt_ok dt_used y_done".split()]
        f.norm(nc, st, m, [(flat2(gates.wg_f[:, :, :]), w["wg"])] + units.first_loads(w["units"])
               + [(wf[:, i, :], w["experts"][i, :, :]) for i in range(2)])
        gates.route(nc, st, m, f.zt, None, False, 1, False)
        first = gates.hot[:, 0, :, :]

        with nc.Block(name="f2_dispatch") as block:
            @block.gpsimd
            def _(pool):
                pool.memset(upper[:, :], 1.0).then_inc(made, 1)
                pool.wait_ge(made, 1)
                pool.affine_select(out=upper[:, :], in_=upper[:, :], compare_op=ALU.is_ge, fill=0.0, base=0,
                                   pattern=[[1, P]], channel_multiplier=-1).then_inc(made, 1)
                pool.iota(slot_i[:, :], pattern=[[1, NE * C]], base=0, channel_multiplier=0).then_inc(made, 1)
                pool.iota(row_i[:, :], pattern=[[C, NE]], base=0, channel_multiplier=1).then_inc(made, 1)

            @block.tensor
            def _(pe):
                pe.wait_ge(ones_ok, 2)
                for t in range(TT):
                    for k in range(t + 1):
                        ins = pe.matmul(m.ps[:, 0, t * NE:(t + 1) * NE], upper_r[:, :] if k == t else m.ones_r[:, :],
                                        first_r[:, k, :], start=(k == 0), stop=(k == t))
                ins.then_inc(ranked, 1)
                pe.wait_ge(flat_ok, 1)
                for t in range(TT):
                    ins = pe.matmul(m.ps[:, 5 + t // 4, (t % 4) * P:(t % 4 + 1) * P],
                                    flat[:, 1, t:t + 1].to_broadcast([P, P]), m.ident[:, :], start=True, stop=True)
                ins.then_inc(fb_ready, 1)
                pe.wait_ge(low_z, 1)
                for t in range(TT):
                    pe.wait_ge(hot_ok, t + 1)
                    for c in range(DC):
                        for i in range(2):
                            for s in range(2):
                                ins = pe.matmul(m.ps[:, 1 + 2 * c + s, :], z_r[i][:, t, c * P:(c + 1) * P],
                                                hot[:, t % 2, s * 512:(s + 1) * 512],
                                                start=(t == 0 and i == 0), stop=(t == TT - 1 and i == 1))
                    ins.then_inc(disp, 1)

            @block.vector
            def _(dve):
                step = Step(dve, rstep)
                dve.tensor_copy(first_r[:, :, :], first).then_inc(ones_ok, 1)
                dve.wait_ge(made, 4)
                dve.tensor_copy(upper_r[:, :], upper[:, :]).then_inc(ones_ok, 1)
                step(dve.tensor_copy(slot[:, :], slot_i[:, :]))
                step(dve.tensor_copy(row_f[:, :], row_i[:, :]))
                dve.wait_ge(ranked, 1)
                step(dve.tensor_tensor(place[:, :, :], m.ps[:, 0, 0:TT * NE].rearrange("p (t e) -> p t e", e=NE),
                                       first, ALU.mult))
                step(dve.tensor_reduce(flat[:, 0, :], place[:, :, :], AX.X, ALU.add))
                step(dve.tensor_scalar(flat[:, 2, :], flat[:, 0, :], float(C), DROPPED, ALU.is_gt, ALU.mult))
                step(dve.tensor_tensor(flat[:, 2, :], flat[:, 2, :], flat[:, 0, :], ALU.add))
                step(dve.tensor_scalar(flat[:, 1, :], gates.index_f[:, :, 0], float(C), -1.0, ALU.mult, ALU.add))
                dve.tensor_tensor(flat[:, 1, :], flat[:, 1, :], flat[:, 2, :], ALU.add).then_inc(flat_ok, 1)
                dve.wait_ge(split_z, 1)
                dve.tensor_tensor(z_r[1][:, :, :], f.z[:, :, :], z_r[0][:, :, :].bitcast(F32), ALU.subtract)\
                   .then_inc(low_z, 1)
                dve.wait_ge(flat_ok, 1)
                for t in range(TT):
                    if t >= 2:
                        dve.wait_ge(disp, t - 1)
                    dve.tensor_scalar(hot[:, t % 2, :], slot[:, :], flat[:, 1, t:t + 1], None, ALU.is_equal)\
                       .then_inc(hot_ok, 1)
                dve.wait_ge(fb_ready, 1)
                dve.tensor_copy(flat_b[:, :], flat2(m.ps[:, 5:7, :])).then_inc(fb_ok, 1)

            @block.scalar
            def _(act):
                act.activation(z_r[0][:, :, :], f.z[:, :, :], ACT.Copy).then_inc(split_z, 1)
                act.wait_ge(disp, TT)
                for c in range(DC):
                    act.activation(xd[:, c, :], flat2(m.ps[:, 1 + 2 * c:3 + 2 * c, :]), ACT.Copy).then_inc(xd_ok, 1)
        st.clear()

        units.block(nc, m, f, lambda u: w["units"][u, :, :], None, "f2_shared", SIZES,
                    ahead=False)
        st.clear()

        BLOCKS = NE // EPB
        arrived = (w_in0, w_in1)
        with nc.Fori(0, BLOCKS) as e:
            with nc.Block(name="f2_experts") as block:
                @block.sync
                def _(sp):
                    for u in range(2, EPB + 2):
                        sp.wait_ge(oe_ready, u - 1)
                        first_of = e * EPB if u < EPB else ((e + 1) % BLOCKS) * EPB
                        sp.dma_start(wf[:, u % 2, :], w["experts"][bass.ds(first_of + u % EPB, 1), :, :]
                                     .rearrange("a p n -> p (a n)")).then_inc(arrived[u % 2], 16)
                    for s in arrived:
                        sp.wait_ge(s, 16 * EPB // 2)

                @block.tensor
                def _(pe):
                    def gate_up(u):
                        if u == 0:
                            pe.wait_ge(xe_ok, 1)
                        if u >= 2:
                            pe.wait_ge(arrived[u % 2], 16 * (u // 2))
                            pe.wait_ge(hid_ok, HC * (u - 1))
                        for part in range(2):
                            for o, r in enumerate(SIZES):
                                for c in range(DC):
                                    at = (part * DC + c) * H + o * P
                                    ins = pe.matmul(m.ps[0:r, 2 * (u % 2) + part, o * P:o * P + C],
                                                    wf[:, u % 2, at:at + r], xe[:, c, u * C:(u + 1) * C],
                                                    start=(c == 0), stop=(c == DC - 1))
                            ins.then_inc(g_ready, 1)

                    def down(u):
                        if u >= 2:
                            pe.wait_ge(oe_lo, u - 1)
                        for o, r in enumerate(SIZES):
                            pe.wait_ge(hid_ok, HC * u + o + 1)
                            at = 2 * DC * H + o * D
                            ins = pe.matmul(m.ps[:, 4 + u % 2, 0:D], hid[0:r, u % 2, o, :], wf[0:r, u % 2, at:at + D],
                                            start=(o == 0), stop=(o == HC - 1))
                        ins.then_inc(oe_ready, 1)

                    for u in range(EPB):
                        gate_up(u)
                        if u:
                            down(u - 1)
                    down(EPB - 1)

                @block.scalar
                def _(act):
                    def gates_of(u):
                        act.wait_ge(g_ready, 2 * u + 1)
                        if u >= 2:
                            act.wait_ge(hid_ok, HC * (u - 1))
                        for o, r in enumerate(SIZES):
                            act.activation(act_g[0:r, u % 2, o, :], m.ps[0:r, 2 * (u % 2), o * P:o * P + C], ACT.Silu)\
                               .then_inc(silu_ok, 1)

                    def output(u):
                        act.wait_ge(oe_ready, u + 1)
                        act.activation(oe_b[0][:, u, :], m.ps[:, 4 + u % 2, 0:D], ACT.Copy).then_inc(oe_hi, 1)

                    for u in range(EPB):
                        gates_of(u)
                        if u:
                            output(u - 1)
                    output(EPB - 1)

                @block.vector
                def _(dve):
                    def hidden(u):
                        dve.wait_ge(g_ready, 2 * u + 2)
                        if u >= 2:
                            dve.wait_ge(oe_ready, u - 1)
                        for o, r in enumerate(SIZES):
                            dve.wait_ge(silu_ok, HC * u + o + 1)
                            dve.tensor_tensor(hid[0:r, u % 2, o, :], act_g[0:r, u % 2, o, :],
                                              m.ps[0:r, 2 * (u % 2) + 1, o * P:o * P + C], ALU.mult).then_inc(hid_ok, 1)

                    def output(u):
                        dve.wait_ge(oe_hi, u + 1)
                        dve.tensor_tensor(oe_b[1][:, u, :], m.ps[:, 4 + u % 2, 0:D], oe_b[0][:, u, :].bitcast(F32),
                                          ALU.subtract).then_inc(oe_lo, 1)

                    dve.tensor_copy(xe[:, :, :], xd[:, :, bass.ds(e * (EPB * C), EPB * C)]).then_inc(xe_ok, 1)
                    for u in range(EPB):
                        hidden(u)
                        if u:
                            output(u - 1)
                    output(EPB - 1)
                    dve.wait_ge(oe_lo, EPB)
                    for i in range(2):
                        dve.tensor_copy(oe[i][:, bass.ds(e * EPB, EPB), :], oe_b[i][:, :, :].bitcast(F32))\
                           .then_inc(oe_kept, 1)
            st.clear()

        with nc.Block(name="f2_combine") as block:
            @block.vector
            def _(dve):
                for e in range(NE):
                    if e >= 2:
                        dve.wait_ge(dt_used, e - 1)
                    dve.tensor_scalar(taken[:, e % 2, :], flat_b[:, :], row_f[:, e:e + 1], None, ALU.is_equal)\
                       .then_inc(dt_ok, 1)
                for t in range(TT):
                    dve.wait_ge(dt_used, NE)
                    dve.scalar_tensor_tensor(out=f.x[:, t, :], in0=m.ps[:, t, 0:D], scalar=gates.top[:, t, 0:1],
                                             in1=f.x[:, t, :], op0=ALU.mult, op1=ALU.add).then_inc(y_done, 1)

            @block.tensor
            def _(pe):
                for e in range(NE):
                    pe.wait_ge(dt_ok, e + 1)
                    for t in range(TT):
                        for i in range(2):
                            ins = pe.matmul(m.ps[:, t, 0:D], taken[:, e % 2, t * P:(t + 1) * P], oe[i][:, e, :],
                                            start=(e == 0 and i == 0), stop=(e == NE - 1 and i == 1))
                    ins.then_inc(dt_used, 1)
        st.clear()
        f.store(nc, st, m)
def image_text_attention(nc, m, w):
    NH, HDS = 16, 16
    IMG = 257
    LEAST = 65
    K_HI, K_LO, NEG = 0, 2 * HDS, 3 * HDS
    STK = 64
    GRP_AT = (0, IMG)
    tiles = ([(a, min(P, IMG - a), 0) for a in range(0, IMG, P)]
             + [(a, min(P, CTX - a), 1) for a in range(IMG, CTX, P)])
    KT = len(tiles)
    FIRST = (0, next(i for i, t in enumerate(tiles) if t[2]))
    LAST = (FIRST[1] - 1, KT - 1)
    NKEY = (IMG, CTX - IMG)
    VW2 = HDS + 1
    HP = NH // 2
    SCALE = HDS ** -0.5
    with Stage(nc, "a2") as st:
        x_b = st.sb("x_b", [P, QT, D])
        zt = [st.sb(f"zt{i}", [P, DC, S], F32R) for i in range(2)]
        ct = [st.sb(f"ct{i}", [P, DC, CTXP], F32R) for i in range(2)]
        x_n = st.sb("x_n", [P, QT, D])
        scratch = (st.sb("stats", [P, QT, 6]), st.sb("mv", [P, QT, 2]), st.sb("rstd", [P, 2, QT]),
                   st.sb("z", [P, QT, D]))
        stats, mv, rstd, z = scratch
        wide = [DC * 2 * D, DC * 2 * D, DC * D, DC * D]
        wr = [[st.sb(f"wr{k}{i}", [P, n], F32R) for i in range(2)] for k, n in enumerate(wide)]
        kv_bias = st.sb("kv_bias", [P, 2, 2 * D])
        qo_bias = st.sb("qo_bias", [P, 2, D])
        norm_w = st.sb("norm_w", [P, 3, D])
        k_rows = st.sb("k_rows", [P, KT, D])
        v_rows = st.sb("v_rows", [P, KT, NH, VW2])
        sq = st.sb("sq", [P, 3, KT + QT])
        square = st.sb("square", [P, 2, D])
        k_st = [[st.sb(f"k_st{g}{i}", [P, NH, STK], F32R) for i in range(2)] for g in range(2)]
        kt = st.sb("kt", [P, HP, KT * P], F32R)
        q_rows = st.sb("q_rows", [P, QT, D])
        q_st = st.sb("q_st", [P, QT, NH, STK], F32R)
        qt_a = st.sb("qt_a", [P, HP, S], F32R)
        qt_b = st.sb("qt_b", [P, 2, S], F32R)
        probs = st.sb("probs", [P, 3, 512])
        rs = st.sb("rs", [P, 8])
        o_t = st.sb("o_t", [P, S])
        o_n = st.sb("o_n", [P, 8, HDS])
        o_rows = st.sb("o_rows", [P, QT, D])
        ot = [qt_a[:, DC * i:DC * (i + 1), :] for i in range(2)]
        nsem = [st.sem("n_" + n) for n in NORM_SEMS]
        w_in = [st.sem(f"w_in{i}") for i in range(4)]
        w_hi, w_lo, small_in, zeroed, dstep, pstep = [st.sem(n) for n in "w_hi w_lo small_in zeroed dstep pstep".split()]
        (kv_ready, kb_done, sq_done, rstd_ok, kn_done, hi_done, lo_done, turned, ev_a, ev_b) = [
            st.sem(n) for n in "kv_ready kb_done sq_done rstd_ok kn_done hi_done lo_done turned ev_a ev_b".split()]
        (s_ready, neg_done, qb_turned, qb_done, st_ready, exp_done, pv_done, ot_zero, ot_done, o_turned,
         o_done) = [st.sem(n) for n in ("s_ready neg_done qb_turned qb_done st_ready exp_done pv_done ot_zero "
                                        "ot_done o_turned o_done").split()]
        (x_in, ct_in, x_moved, var_ok, nrstd_ok, z_ok, nx_ready, nx_hi, nx_lo, or_turned, or_hi, or_lo, y_ready,
         y_done, stored, rows_ok) = [st.sem(n) for n in ("x_in ct_in x_moved var_ok nrstd_ok z_ok nx_ready nx_hi nx_lo "
                                                "or_turned or_hi or_lo y_ready y_done stored rows_ok").split()]

        wf = k_rows[:, :, :].rearrange("p t d -> p (t d)")
        at = [sum(wide[:k]) for k in range(5)]
        names = ("wkv_img", "wkv_txt", "wq", "wo")
        for lot in ((0, 1), (2, 3)):
            base = at[lot[0]]
            split_weights(nc, st, f"a2_weights{lot[0]}",
                          [(wf[:, at[k] - base:at[k + 1] - base], (wr[k][0][:, :], wr[k][1][:, :]), w[names[k]])
                           for k in lot], w_in[0:2], w_hi, w_lo)
        with nc.Block(name="a2_once") as block:
            @block.sync
            def _(sp):
                for dst, n in ((kv_bias[:, 0, 0:D], "k_img_b"), (kv_bias[:, 0, D:], "v_img_b"),
                               (kv_bias[:, 1, 0:D], "k_b"), (kv_bias[:, 1, D:], "v_b"),
                               (qo_bias[:, 0, :], "q_b"), (qo_bias[:, 1, :], "o_b"),
                               (norm_w[:, 0, :], "norm_k_img_w"), (norm_w[:, 1, :], "norm_k_w"),
                               (norm_w[:, 2, :], "norm_q_w")):
                    sp.dma_start(dst, w[n].partition_broadcast(P)).then_inc(small_in, 16)
                sp.wait_ge(small_in, 144)

            @block.gpsimd
            def _(pool):
                pool.memset(v_rows[:, :, :, :], 0.0).then_inc(zeroed, 1)
                pool.wait_ge(zeroed, 1)
                for t, (_a, r, _g) in enumerate(tiles):
                    pool.memset(v_rows[0:r, t, :, HDS:VW2], 1.0).then_inc(zeroed, 1)
                n = 1 + KT
                pool.memset(sq[:, :, :], 1.0).then_inc(zeroed, 1)
                pool.memset(q_st[:, :, :, :].bitcast(F32), 0.0).then_inc(zeroed, 1)
                for g in range(2):
                    for i in range(2):
                        pool.memset(k_st[g][i][:, :, :].bitcast(F32), 0.0).then_inc(zeroed, 1)
                pool.wait_ge(zeroed, n + 6)
                for g in range(2):
                    for i in range(2):
                        pool.memset(k_st[g][i][:, :, NEG + g:NEG + g + 1].bitcast(F32), 1.0).then_inc(zeroed, 1)
        st.clear()

        norm_block(nc, st, m, x_n, zt[0], zt[1], QT, m.x_dram[0:QT, :].rearrange("t (p d) -> p t d", p=P), nsem,
                   scratch, [(flat2(ct[0][:, :, :]).bitcast(F32), m.ctx_hi[0, :, :]),
                             (flat2(ct[1][:, :, :]).bitcast(F32), m.ctx_lo[0, :, :])], name="a2_norm")
        st.clear()
        ALL = KT + QT
        LOT = 4
        LEAD = 6
        PIPE = range(ALL + LEAD + 2)

        with nc.Fori(0, B) as b:
            x_rows = m.x_dram[bass.ds(b * QT, QT), :].rearrange("t (p d) -> p t d", p=P)

            with nc.Block(name="a2_keys") as block:
                @block.tensor
                def _(pe):
                    def project(t):
                        if t >= 4:
                            pe.wait_ge(kb_done, t - 3)
                        n = 0
                        for c in range(DC):
                            for s, v in HALVES:
                                if t < KT:
                                    a, r, g = tiles[t]
                                    M = max(r, LEAST)
                                    ins = pe.matmul(m.ps[0:M, t % 4, :], ct[s][:, c, a:a + M],
                                                    wr[g][v][:, c * 2 * D:(c + 1) * 2 * D],
                                                    start=(n == 0), stop=(n == 3 * DC - 1))
                                else:
                                    q = t - KT
                                    ins = pe.matmul(m.ps[:, t % 4, 0:D], zt[s][:, c, q * P:(q + 1) * P],
                                                    wr[2][v][:, c * D:(c + 1) * D],
                                                    start=(n == 0), stop=(n == 3 * DC - 1))
                                n += 1
                        ins.then_inc(kv_ready, 1)

                    def turn(t):
                        g, i = tiles[t][2], (t - FIRST[tiles[t][2]]) % 2
                        pe.wait_ge(lo_done, t + 1)
                        if t >= 2:
                            pe.wait_ge(ev_a, t - 1)
                            pe.wait_ge(ev_b, t - 1)
                        for hp in range(HP):
                            ins = pe.transpose(m.ps[:, 4 + 2 * (t % 2) + hp // 4, (hp % 4) * P:(hp % 4 + 1) * P]
                                               .bitcast(F32R), k_st[g][i][:, 2 * hp:2 * hp + 2, :]
                                               .rearrange("p a n -> p (a n)"), m.ident_r[:, :])
                        ins.then_inc(turned, 1)

                    def turn_queries(k):
                        if k == 0:
                            pe.wait_ge(lo_done, ALL)
                        if k % 2 == 0:
                            pe.wait_ge(ev_a, KT - 1 + k // 2)
                            pe.wait_ge(ev_b, KT - 1 + k // 2)
                        for i in range(4):
                            hp, q = 2 * k + i // QT, i % QT
                            ins = pe.transpose(m.ps[:, 4 + k, i * P:(i + 1) * P].bitcast(F32R),
                                               q_st[:, q, 2 * hp:2 * hp + 2, :].rearrange("p a n -> p (a n)"),
                                               m.ident_r[:, :])
                        ins.then_inc(turned, 1)

                    for i in PIPE:
                        if i < ALL:
                            project(i)
                        if 0 <= i - LEAD - 1 < KT:
                            turn(i - LEAD - 1)
                    for k in range(HP // 2):
                        turn_queries(k)

                def evacuate(eng, t, half):
                    eng.wait_ge(turned, t + 1)
                    dst = kt[:, 4 * half:4 * half + 4, t * P:(t + 1) * P]
                    src = m.ps[:, 4 + 2 * (t % 2) + half, :].rearrange("p (h n) -> p h n", n=P)
                    return dst, src

                def rows_of(t):
                    return (k_rows[0:tiles[t][1], t, :], tiles[t][1]) if t < KT else (q_rows[:, t - KT, :], P)

                @block.scalar
                def _(act):
                    def squares(t):
                        rows, r = rows_of(t)
                        act.wait_ge(kb_done, t + 1)
                        if t >= 2:
                            act.wait_ge(sq_done, t - 1)
                        act.activation(square[0:r, t % 2, :], rows, ACT.Square,
                                       accum_out=sq[0:r, 0, t:t + 1]).then_inc(sq_done, 1)

                    def high(t):
                        rows, r = rows_of(t)
                        act.wait_ge(kn_done, t + 1)
                        heads = rows.rearrange("p (h d) -> p h d", h=NH)
                        if t < KT:
                            g = tiles[t][2]
                            i = (t - FIRST[g]) % 2
                            if t - 2 >= FIRST[g]:
                                act.wait_ge(turned, t - 1)
                            act.activation(k_st[g][i][0:r, :, 0:2 * HDS].rearrange("p h (a d) -> p h a d", a=2),
                                           heads.unsqueeze(2).to_broadcast([r, NH, 2, HDS]), ACT.Copy)\
                               .then_inc(hi_done, 1)
                        else:
                            q = t - KT
                            act.activation(q_st[:, q, :, 0:HDS], heads, ACT.Copy)
                            act.activation(q_st[:, q, :, 2 * HDS:3 * HDS], heads, ACT.Copy).then_inc(hi_done, 1)

                    for i in PIPE:
                        if i < ALL:
                            squares(i)
                        t = i - LEAD
                        if 0 <= t < ALL:
                            high(t)
                        if 0 <= t - 2 < KT:
                            dst, src = evacuate(act, t - 2, 0)
                            act.activation(dst, src, ACT.Copy).then_inc(ev_a, 1)
                    for k in range(HP // 2):
                        act.wait_ge(turned, KT + k + 1)
                        act.activation(flat2(qt_a[:, 2 * k:2 * k + 2, :]), m.ps[:, 4 + k, :], ACT.Copy)\
                           .then_inc(ev_a, 1)

                @block.gpsimd
                def _(pool):
                    step = Step(pool, pstep)
                    for t0 in range(0, ALL, LOT):
                        t1 = min(t0 + LOT, ALL)
                        pool.wait_ge(sq_done, t1)
                        step(pool.tensor_scalar(sq[:, 1, t0:t1], sq[:, 0, t0:t1], 1.0 / D, 1e-6, ALU.mult, ALU.add))
                        ins = pool.tensor_tensor(sq[:, 2, t0:t1], sq[:, 1, t0:t1],
                                                 m.nhalf[:, 0:1].to_broadcast([P, t1 - t0]), ALU.pow)
                        if t1 == ALL:
                            step(ins)
                            ins = pool.tensor_scalar(sq[:, 2, KT:], sq[:, 2, KT:], SCALE, None, ALU.mult)
                        ins.then_inc(rstd_ok, 1)

                @block.vector
                def _(dve):
                    def biased(t):
                        dve.wait_ge(kv_ready, t + 1)
                        if t < KT:
                            _a, r, g = tiles[t]
                            dve.tensor_tensor(v_rows[0:r, t, :, 0:HDS],
                                              m.ps[0:r, t % 4, D:].rearrange("p (h d) -> p h d", h=NH),
                                              kv_bias[0:r, g, D:].rearrange("p (h d) -> p h d", h=NH), ALU.add)
                            ins = dve.tensor_tensor(k_rows[0:r, t, :], m.ps[0:r, t % 4, 0:D], kv_bias[0:r, g, 0:D],
                                                    ALU.add)
                        else:
                            ins = dve.tensor_tensor(q_rows[:, t - KT, :], m.ps[:, t % 4, 0:D], qo_bias[:, 0, :],
                                                    ALU.add)
                        ins.then_inc(kb_done, 1)

                    def normed(t):
                        rows, r = rows_of(t)
                        if t % LOT == 0:
                            dve.wait_ge(rstd_ok, t // LOT + 1)
                        weight = norm_w[0:r, tiles[t][2] if t < KT else 2, :]
                        dve.scalar_tensor_tensor(out=rows, in0=rows, scalar=sq[0:r, 2, t:t + 1], in1=weight,
                                                 op0=ALU.mult, op1=ALU.mult).then_inc(kn_done, 1)

                    def low(t):
                        rows, r = rows_of(t)
                        heads = rows.rearrange("p (h d) -> p h d", h=NH)
                        dve.wait_ge(hi_done, t + 1)
                        if t < KT:
                            g = tiles[t][2]
                            i = (t - FIRST[g]) % 2
                            dst, hi = (k_st[g][i][0:r, :, at:at + HDS] for at in (K_LO, K_HI))
                        else:
                            dst, hi = (q_st[:, t - KT, :, at:at + HDS] for at in (HDS, 0))
                        dve.tensor_tensor(dst, heads, hi.bitcast(F32), ALU.subtract).then_inc(lo_done, 1)

                    for i in PIPE:
                        if i < ALL:
                            biased(i)
                        t = i - LEAD
                        if 0 <= t < ALL:
                            normed(t)
                        if 0 <= t - 2 < KT:
                            dst, src = evacuate(dve, t - 2, 1)
                            dve.tensor_copy(dst, src).then_inc(ev_b, 1)
                        if 0 <= t < ALL:
                            low(t)
                    dve.tensor_copy(x_b[:, :, :], x_n[:, :, :]).then_inc(x_moved, 1)
            st.clear()

            PAIRS = KT // 2
            TURNS = NH * PAIRS
            with nc.Block(name="a2_attend") as block:
                @block.sync
                def _(sp):
                    nxt = (b + 1) % B
                    sp.dma_start(x_n[:, :, :], m.x_dram[bass.ds(nxt * QT, QT), :]
                                 .rearrange("t (p d) -> p t d", p=P)).then_inc(x_in, 16)
                    for half, src in zip(ct, (m.ctx_hi, m.ctx_lo)):
                        sp.dma_start(flat2(half[:, :, :]).bitcast(F32), src[bass.ds(nxt, 1), :, :]
                                     .rearrange("a p n -> p (a n)")).then_inc(ct_in, 16)
                    sp.wait_ge(y_done, QT)
                    sp.dma_start(x_rows, x_b[:, :, :]).then_inc(stored, 16)
                    sp.wait_ge(ct_in, 32)
                    sp.wait_ge(stored, 16)

                @block.gpsimd
                def _(pool):
                    pool.wait_ge(var_ok, 1)
                    pool.tensor_tensor(rstd[:, 1, :], rstd[:, 0, :], m.nhalf[:, 0:1].to_broadcast([P, QT]),
                                       ALU.pow).then_inc(nrstd_ok, 1)

                @block.tensor
                def _(pe):
                    def rough_scores(i):
                        h, q = divmod(i, QT)
                        lo_p = STK * (h % 2)
                        pe.wait_ge(neg_done, i) if i else None
                        if h % 2 == 0 and q == 0 and h:
                            pe.wait_ge(qb_done, h // 2)
                        lhs = qt_a[lo_p:lo_p + HDS, h // 2, q * P:(q + 1) * P]
                        img = NKEY[0] + NKEY[0] % 2
                        pe.matmul(m.ps[:, 0, 0:img], lhs, kt[lo_p:lo_p + HDS, h // 2, 0:img], start=True, stop=True)
                        a0 = FIRST[1] * P
                        for k, a in enumerate(range(0, NKEY[1], 512)):
                            e = min(a + 512, NKEY[1])
                            ins = pe.matmul(m.ps[:, 1 + k, 0:e - a], lhs, kt[lo_p:lo_p + HDS, h // 2, a0 + a:a0 + e],
                                            start=True, stop=True)
                        ins.then_inc(s_ready, 1)

                    def turn_queries(hp):
                        pe.wait_ge(neg_done, 4 * (hp + 1))
                        if hp >= 2:
                            pe.wait_ge(st_ready, (2 * hp - 2) * PAIRS)
                        for q in range(QT):
                            ins = pe.transpose(m.ps[:, 0, q * P:(q + 1) * P].bitcast(F32R),
                                               q_st[:, q, 2 * hp:2 * hp + 2, :].rearrange("p a n -> p (a n)"),
                                               m.ident_r[:, :])
                        ins.then_inc(qb_turned, 1)

                    def scores(n):
                        h, k2 = divmod(n, PAIRS)
                        lo_p = STK * (h % 2)
                        if k2 == 0 and h % 2 == 0:
                            pe.wait_ge(qb_done, h // 2 + 1)
                        if n >= 2:
                            pe.wait_ge(exp_done, n - 1)
                        for i in range(2):
                            t = 2 * k2 + i
                            ins = pe.matmul(m.ps[:, 4 + n % 2, i * S:(i + 1) * S],
                                            kt[lo_p:lo_p + STK, h // 2, t * P:(t + 1) * P],
                                            qt_b[lo_p:lo_p + STK, (h // 2) % 2, :], start=True, stop=True)
                        ins.then_inc(st_ready, 1)

                    def values(n):
                        h, k2 = divmod(n, PAIRS)
                        hp = h // 2
                        pe.wait_ge(exp_done, n + 1)
                        if n == 0:
                            pe.wait_ge(ot_zero, 2)
                        if k2 == 0 and h % 2 == 0 and hp >= 2:
                            pe.wait_ge(o_done, hp - 1)
                        for i in range(2):
                            t = 2 * k2 + i
                            g = tiles[t][2]
                            at_ = 64 * (h % 2) + 32 * g
                            ins = pe.matmul(m.ps[at_:at_ + VW2, 6 + hp % 2, 0:S], v_rows[:, t, h, :],
                                            probs[:, n % 3, i * S:(i + 1) * S], start=(t == FIRST[g]),
                                            stop=(t == LAST[g]), skip_group_check=True)
                        ins.then_inc(pv_done, 1)

                    def turn_outputs(hp):
                        pe.wait_ge(ot_done, hp + 1)
                        for q in range(QT):
                            ins = pe.transpose(m.ps[:, 6 + hp % 2, S + q * P:S + (q + 1) * P],
                                               o_t[:, q * P:(q + 1) * P], m.ident[:, :])
                        ins.then_inc(o_turned, 1)

                    def turn_normed():
                        pe.wait_ge(neg_done, QT * NH)
                        pe.wait_ge(z_ok, QT)
                        for c in range(DC):
                            for q in range(QT):
                                ins = pe.transpose(m.ps[:, 1, c * S + q * P:c * S + (q + 1) * P],
                                                   z[:, q, c * P:(c + 1) * P], m.ident[:, :])
                        ins.then_inc(nx_ready, 1)

                    def project():
                        pe.wait_ge(rows_ok, HP)
                        pe.wait_ge(qb_done, HP)
                        for c in range(DC):
                            for q in range(QT):
                                ins = pe.transpose(m.ps[:, 0, c * S + q * P:c * S + (q + 1) * P],
                                                   o_rows[:, q, c * P:(c + 1) * P], m.ident[:, :])
                        ins.then_inc(or_turned, 1)
                        pe.wait_ge(or_lo, 1)
                        for q in range(QT):
                            n = 0
                            for c in range(DC):
                                for s, v in HALVES:
                                    ins = pe.matmul(m.ps[:, 2 + q, 0:D], ot[s][:, c, q * P:(q + 1) * P],
                                                    wr[3][v][:, c * D:(c + 1) * D],
                                                    start=(n == 0), stop=(n == 3 * DC - 1))
                                    n += 1
                            ins.then_inc(y_ready, 1)

                    for i in range(4):
                        rough_scores(i)
                    turn_queries(0)
                    for n in range(TURNS):
                        scores(n)
                        hp, r = divmod(n, 2 * PAIRS)
                        if n:
                            values(n - 1)
                        if hp + 1 < HP and r % 3 == 0 and r // 3 < 4:
                            rough_scores(4 * (hp + 1) + r // 3)
                        if hp and r == 3:
                            turn_outputs(hp - 1)
                        if hp == HP - 1 and r == 5:
                            turn_normed()
                        if hp + 1 < HP and r == 2 * PAIRS - 1:
                            turn_queries(hp + 1)
                    values(TURNS - 1)
                    turn_outputs(HP - 1)
                    project()

                @block.scalar
                def _(act):
                    def take_queries(hp):
                        act.wait_ge(qb_turned, hp + 1)
                        act.activation(qt_b[:, hp % 2, :], m.ps[:, 0, 0:S], ACT.Copy).then_inc(qb_done, 1)

                    take_queries(0)
                    for n in range(TURNS):
                        act.wait_ge(st_ready, n + 1)
                        if n >= 3:
                            act.wait_ge(pv_done, n - 2)
                        act.activation(probs[:, n % 3, :], m.ps[:, 4 + n % 2, :], ACT.Exp).then_inc(exp_done, 1)
                        hp, r = divmod(n, 2 * PAIRS)
                        if hp + 1 < HP and r == 2 * PAIRS - 1:
                            take_queries(hp + 1)
                        if hp == HP - 1 and r == 8:
                            act.wait_ge(nx_ready, 1)
                            act.activation(flat2(zt[0][:, :, :]), m.ps[:, 1, :], ACT.Copy).then_inc(nx_hi, 1)
                    act.wait_ge(or_turned, 1)
                    act.activation(flat2(ot[0]), m.ps[:, 0, :], ACT.Copy).then_inc(or_hi, 1)

                @block.vector
                def _(dve):
                    step = Step(dve, dstep)

                    def maxima(i):
                        h, q = divmod(i, QT)
                        dve.wait_ge(s_ready, i + 1)
                        dve.tensor_reduce(q_st[:, q, h, NEG:NEG + 1], m.ps[:, 0, 0:NKEY[0]], AX.X, ALU.max,
                                          negate=True)
                        dve.tensor_reduce(q_st[:, q, h, NEG + 1:NEG + 2], m.ps[:, 1:4, :]
                                          .rearrange("p b n -> p (b n)")[:, 0:NKEY[1]], AX.X, ALU.max,
                                          negate=True).then_inc(neg_done, 1)

                    def take_sums(hp):
                        dve.wait_ge(pv_done, 2 * PAIRS * (hp + 1))
                        if hp:
                            dve.wait_ge(o_turned, hp)
                        dve.tensor_copy(o_t[:, :], m.ps[:, 6 + hp % 2, 0:S]).then_inc(ot_done, 1)

                    def outputs(hp):
                        dve.wait_ge(o_turned, hp + 1)
                        o = m.ps[:, 6 + hp % 2, S:].rearrange("p (i n) -> p i n", n=32)
                        step(dve.reciprocal(rs[:, :].unsqueeze(2), o[:, :, HDS:VW2]))
                        dve.tensor_tensor(o_n[:, :, :], o[:, :, 0:HDS],
                                          rs[:, :].unsqueeze(2).to_broadcast([P, 8, HDS]), ALU.mult)\
                           .then_inc(o_done, 1)
                        dve.wait_ge(o_done, hp + 1)
                        on = o_n[:, :, :].rearrange("p (q h g) d -> p q h g d", q=QT, h=2)
                        dst = o_rows[:, :, hp * 2 * HDS:(hp + 1) * 2 * HDS].rearrange("p q (h d) -> p q h d", h=2)
                        dve.tensor_tensor(dst, on[:, :, :, 0, :], on[:, :, :, 1, :], ALU.add).then_inc(rows_ok, 1)

                    def row_stats():
                        dve.wait_ge(x_in, 16)
                        for q in range(QT):
                            ins = dve.bn_stats(stats[:, q, :], x_n[:, q, :])
                        step(ins)
                        for q in range(QT):
                            ins = dve.bn_aggr(mv[:, q, :], stats[:, q, :])
                        step(ins)
                        dve.tensor_scalar(rstd[:, 0, :], mv[:, :, 1], 1e-5, None, ALU.add).then_inc(var_ok, 1)

                    def normalise():
                        dve.wait_ge(nrstd_ok, 1)
                        for q in range(QT):
                            dve.tensor_scalar(z[:, q, :], x_n[:, q, :], mv[:, q, 0:1], rstd[:, 1, q:q + 1],
                                              ALU.subtract, ALU.mult).then_inc(z_ok, 1)

                    for i in range(2):
                        dve.memset(m.ps[:, 6 + i, 0:S], 0.0).then_inc(ot_zero, 1)
                    for i in range(4):
                        maxima(i)
                    for hp in range(HP):
                        if hp:
                            take_sums(hp - 1)
                        if hp + 1 < HP:
                            maxima(4 * (hp + 1))
                            maxima(4 * (hp + 1) + 1)
                        if hp:
                            outputs(hp - 1)
                        if hp == 1:
                            row_stats()
                        if hp == 2:
                            normalise()
                        if hp + 1 < HP:
                            maxima(4 * (hp + 1) + 2)
                            maxima(4 * (hp + 1) + 3)
                    dve.wait_ge(nx_hi, 1)
                    dve.tensor_tensor(flat2(zt[1][:, :, :]), m.ps[:, 1, :], flat2(zt[0][:, :, :]).bitcast(F32),
                                      ALU.subtract).then_inc(nx_lo, 1)
                    step(dve.tensor_tensor(x_b[:, :, :], x_b[:, :, :], qo_bias[:, 1, :].unsqueeze(1)
                                           .to_broadcast([P, QT, D]), ALU.add))
                    take_sums(HP - 1)
                    outputs(HP - 1)
                    dve.wait_ge(or_hi, 1)
                    dve.tensor_tensor(flat2(ot[1]), m.ps[:, 0, :], flat2(ot[0]).bitcast(F32), ALU.subtract)\
                       .then_inc(or_lo, 1)
                    for q in range(QT):
                        dve.wait_ge(y_ready, q + 1)
                        dve.tensor_tensor(x_b[:, q, :], x_b[:, q, :], m.ps[:, 2 + q, 0:D], ALU.add)\
                           .then_inc(y_done, 1)
            st.clear()


def chunked(w, groups):
    w = np.asarray(w)
    k, n = w.shape
    return w.reshape(k // P, P, groups, n // groups).transpose(2, 1, 0, 3).reshape(groups, P, -1)


def lay_gqa(wq, wk, wv, wo, qw, kw, name):
    kv = np.stack([np.asarray(wk).reshape(D, KVH, HD), np.asarray(wv).reshape(D, KVH, HD)], axis=2)
    return {
        f"{name}_wq": chunked(wq, KVH),
        f"{name}_wkv": chunked(kv.reshape(D, -1), KVH),
        f"{name}_wo": np.asarray(wo).reshape(KVH, REP, P, D).transpose(0, 2, 1, 3).reshape(KVH, P, -1),
        f"{name}_qw": np.asarray(qw), f"{name}_kw": np.asarray(kw),
    }


def by_partition(w):
    w = np.asarray(w)
    *lead, k, n = w.shape
    return np.moveaxis(w.reshape(*lead, k // P, P, n), -2, -3).reshape(*lead, P, -1)


def lay_units(gate, up, down):
    gate, up, down = (np.asarray(a) for a in (gate, up, down))
    n = -(-gate.shape[1] // P)
    out = np.zeros((n, P, 3 * 2 * P), np.float32)
    for u in range(n):
        a, e = u * P, min((u + 1) * P, gate.shape[1])
        for c in range(DC):
            out[u, :, c * 2 * P:c * 2 * P + e - a] = gate[c * P:(c + 1) * P, a:e]
            out[u, :, c * 2 * P + P:c * 2 * P + P + e - a] = up[c * P:(c + 1) * P, a:e]
        out[u, 0:e - a, 4 * P:] = down[a:e]
    return out


def lay_ffn(i):
    out = {"f0_w1": by_partition(i["L0_ffn_W1"]), "f0_w2": by_partition(i["L0_ffn_W2"]),
           "f0_w3": by_partition(i["L0_ffn_W3"]), "f0_b3": i["L0_ffn_b3"],
           "f0_wg": by_partition(i["L0_ffn_Wg"]), "f0_bg": i["L0_ffn_bg"]}
    b12 = np.stack([np.asarray(i["L0_ffn_b1"]), np.asarray(i["L0_ffn_b2"])], axis=1)
    out["f0_b12"] = b12.reshape(NE, 2, -1, P).transpose(0, 3, 1, 2).reshape(NE, P, -1)
    out |= {"f1_w": by_partition(i["L1_ffn_weight"].T), "f1_scale": i["L1_ffn_scale_weight"],
            "f1_bias": i["L1_ffn_bias"]}
    out["f2_wg"] = by_partition(i["L2_ffn_Wg"])
    out["f2_units"] = lay_units(i["L2_ffn_sw1"], i["L2_ffn_sw3"], i["L2_ffn_sw2"])
    w2 = np.asarray(i["L2_ffn_W2"])
    down = np.zeros((NE, 3 * P, D), np.float32)
    down[:, 0:w2.shape[1]] = w2
    out["f2_experts"] = np.concatenate([by_partition(i["L2_ffn_W1"]), by_partition(i["L2_ffn_W3"]),
                                        by_partition(down)], axis=2)
    out["f3_wg"] = by_partition(i["L3_ffn_w_gate"])
    gu, dn = np.asarray(i["L3_ffn_w_gate_up"]), np.asarray(i["L3_ffn_w_down"])
    sgu, sdn = np.asarray(i["L3_ffn_w_sh_gate_up"]), np.asarray(i["L3_ffn_w_sh_down"])
    I = sgu.shape[1] // 2
    out["f3_units"] = np.concatenate([lay_units(gu[e, :, 0:P], gu[e, :, P:], dn[e]) for e in range(NE)]
                                     + [lay_units(sgu[:, 0:I], sgu[:, I:], sdn)])
    return out


def lay_memory(i):
    wqkv = np.asarray(i["L0_xattn_W_qkv"])
    out = {"a0_wq": by_partition(wqkv[0:D].T), "a0_wo": by_partition(np.asarray(i["L0_xattn_W_o"]).T)}
    for n in ("gate", "log_tau", "beta_q", "beta_k"):
        out[f"a0_{n}"] = np.asarray(i[f"L0_xattn_{n}"]).reshape(1)
    return out


def lay_image_text(i):
    def t(n):
        return np.asarray(i[f"L2_xattn_{n}"]).T
    out = {"a2_wkv_img": by_partition(np.concatenate([t("k_img_w"), t("v_img_w")], axis=1)),
           "a2_wkv_txt": by_partition(np.concatenate([t("k_w"), t("v_w")], axis=1)),
           "a2_wq": by_partition(t("q_w")), "a2_wo": by_partition(t("o_w"))}
    for n in "q_b k_b v_b k_img_b v_img_b o_b norm_q_w norm_k_w norm_k_img_w".split():
        out[f"a2_{n}"] = i[f"L2_xattn_{n}"]
    return out


def lay_out(i):
    out = {"x": i["x"], "ctx": i["ctx_2048"], "pos": i["pos_BxS2"], "tok": i["itok_BxS_4096_4607"],
           "inv_freq": (1.0 / 10000.0 ** (np.arange(0, HD, 2, dtype=np.float64) / HD)).astype(np.float32)}
    out |= lay_memory(i) | lay_image_text(i) | lay_ffn(i)
    out |= lay_gqa(i["L1_xattn_Wq"].T, i["L1_xattn_Wk"].T, i["L1_xattn_Wv"].T, i["L1_xattn_Wo"].T,
                   i["L1_xattn_q_norm_w"], i["L1_xattn_k_norm_w"], "a1")
    out |= lay_gqa(i["L3_xattn_Wq"], i["L3_xattn_Wk"], i["L3_xattn_Wv"], i["L3_xattn_Wo"],
                   i["L3_xattn_q_norm_w"], i["L3_xattn_k_norm_w"], "a3")
    return out


def run_layers(nc, m, d):
    def of(name):
        return {k[3:]: v for k, v in d.items() if k.startswith(name)}

    memory_attention(nc, m, of("a0_") | {"ctx": d["ctx"]})
    gelu_experts(nc, m, of("f0_"))
    grouped_attention(nc, m, "a1", of("a1_") | {k: d[k] for k in ("pos", "tok", "inv_freq")}, True)
    scaled_linear(nc, m, of("f1_"))
    image_text_attention(nc, m, of("a2_"))
    capacity_experts(nc, m, of("f2_"))
    grouped_attention(nc, m, "a3", of("a3_"), False)
    silu_experts(nc, m, of("f3_"))


def build(nc, dram, out):
    class m:
        pass
    with ExitStack() as ctx:
        m.ident = ctx.enter_context(nc.sbuf_tensor("ident", [P, P], F32))
        m.ident_r = ctx.enter_context(nc.sbuf_tensor("ident_r", [P, P], F32R))
        m.ones_r = ctx.enter_context(nc.sbuf_tensor("ones_r", [P, P], F32R))
        m.onesf = ctx.enter_context(nc.sbuf_tensor("onesf", [P, P], F32))
        m.nhalf = ctx.enter_context(nc.sbuf_tensor("nhalf", [P, 1], F32))
        m.ps = ctx.enter_context(nc.psum_tensor("ps", [P, 8, 512], F32))
        m.x_pad = nc.dram_tensor("x_state", (QT + TT, P * D), F32, kind="Internal").ap()
        m.x_dram = m.x_pad[QT:QT + TT, :]
        m.ctx_hi = nc.dram_tensor("ctx_hi", (B, P, DC * CTXP), F32, kind="Internal").ap()
        m.ctx_lo = nc.dram_tensor("ctx_lo", (B, P, DC * CTXP), F32, kind="Internal").ap()
        make_constants(nc, m)
        copy_x_in(nc, m, dram["x"].rearrange("b (t p) d -> (b t) (p d)", p=P))
        run_layers(nc, m, dram)
        with Stage(nc, "xout") as st:
            moved = st.sem("moved")
            with nc.Block(name="x_out") as block:
                @block.sync
                def _(sp):
                    sp.dma_start(out.rearrange("b (t p) d -> (b t) (p d)", p=P), m.x_dram[:, :]).then_inc(moved, 16)
                    sp.wait_ge(moved, 16)


def kernel(**inputs):
    import concourse.bacc as bacc
    from concourse.bass_utils import run_bass_kernel_spmd

    nc = bacc.Bacc("TRN2", target_bir_lowering=False, num_devices=1)
    arrays = {n: np.ascontiguousarray(a) for n, a in lay_out(inputs).items()}
    dram = {n: nc.dram_tensor(f"in_{n}", a.shape, mybir.dt.from_np(a.dtype), kind="ExternalInput").ap()
            for n, a in arrays.items()}
    out = nc.dram_tensor("out_0", (B, S, D), F32, kind="ExternalOutput").ap()
    build(nc, dram, out)
    r = run_bass_kernel_spmd(nc, [{f"in_{n}": a for n, a in arrays.items()}], core_ids=[0])
    return r.results[0]["out_0"]
```
